# Optimizing a Trainium2 kernel written in Bass

```python
import numpy as np
import jax
import jax.numpy as jnp

def _softmax(x, axis=-1):
    return jax.nn.softmax(x, axis=axis)

def _gelu(x):
    return jax.nn.gelu(x, approximate=True)

def _silu(x):
    return jax.nn.silu(x)

def _sigmoid(x):
    return jax.nn.sigmoid(x)

def _layernorm(x, axis=-1, eps=1e-05):
    m = jnp.mean(x, axis=axis, keepdims=True)
    v = jnp.var(x, axis=axis, keepdims=True)
    return (x - m) / jnp.sqrt(v + eps)

def _scatter_add(tgt, idx, src, axis=0):
    return tgt.at[idx].add(src)

def _segment_sum(src, seg, n):
    return jax.ops.segment_sum(src, seg, n)
kernel_name = 'mk_flamingo_gated_d4_seqx_r8_8ba167'

def setup_inputs(seed: int=0):
    np.random.seed(seed)
    _w = jnp.asarray

    def _rec_inputs():
        import jax
        import jax.numpy as jnp
        _rk = jax.random.key(seed)
        x = -0.0002928 + 1 * jax.random.normal(jax.random.fold_in(_rk, 1), (8, 100, 128), jnp.float32)
        _lenS = 100 - jax.random.randint(jax.random.fold_in(_rk, 7), (8,), 0, max(1, 100 // 4) + 1, jnp.int32)
        _lenS2 = 1444 - jax.random.randint(jax.random.fold_in(_rk, 8), (8,), 0, max(1, 1444 // 4) + 1, jnp.int32)
        _ctx_1024P = jax.random.normal(jax.random.fold_in(_rk, 11), (8, 16, 128), jnp.float32)
        _ctx_1024c = jax.random.dirichlet(jax.random.fold_in(_rk, 511), 0.3 * jnp.ones((16,), jnp.float32), (8, 1444))
        _ctx_1024t = jnp.einsum('bsk,bkd->bsd', _ctx_1024c, _ctx_1024P)
        _ctx_1024t = _ctx_1024t * jax.lax.rsqrt(jnp.mean(jnp.square(_ctx_1024t)) + 1e-12) * 0.953939
        ctx_1024 = -1.39393e-06 + 0.999914 * (_ctx_1024t + 0.3 * jax.random.normal(jax.random.fold_in(_rk, 611), (8, 1444, 128), jnp.float32))
        _validS = jnp.arange(100)[None, :] < _lenS[:, None]
        _validS2 = jnp.arange(1444)[None, :] < _lenS2[:, None]
        _causal = jnp.tril(jnp.ones((100, 100), dtype=bool))
        mask_1x1xSxS2_ik0 = jnp.where(jnp.broadcast_to(_validS2[0:1, None, None, :], (1, 1, 100, 1444)), 0, 1).astype(jnp.int32)
        mask_BxS2_bf1 = jnp.ones((8, 1444), dtype=bool)
        _g = jax.random.normal(jax.random.fold_in(_rk, 9001), (2, 4), jnp.float32)
        _g = jnp.sign(_g) * jnp.maximum(jnp.abs(_g), 1.0) + (_g == 0) * 1.0
        g_xattn = _g[0]
        g_ffn = _g[1]
        return (x, ctx_1024, mask_1x1xSxS2_ik0, mask_BxS2_bf1, g_xattn, g_ffn)
    x, ctx_1024, mask_1x1xSxS2_ik0, mask_BxS2_bf1, g_xattn, g_ffn = _rec_inputs()

    def _L0_xattn_setup():
        import jax, jax.numpy as jnp
        import numpy as np
        B, N, DIM, H = (2, 256, 128, 16)
        HD = DIM // H
        SCALE = HD ** (-0.5)

        def _split_heads(x):
            b, n, _ = x.shape
            return x.reshape(b, n, H, HD).transpose(0, 2, 1, 3)
        key = jax.random.key(seed)
        ks = jax.random.split(key, 11)
        std = DIM ** (-0.5)
        inp = {'q': jax.random.normal(ks[0], (B, N, DIM), jnp.float32), 'k': jax.random.normal(ks[1], (B, N, DIM), jnp.float32), 'v': jax.random.normal(ks[2], (B, N, DIM), jnp.float32), 'mask': jnp.tril(jnp.ones((N, N), jnp.int32))[None, None], 'Wq': jax.random.normal(ks[3], (DIM, DIM), jnp.float32) * std, 'bq': jnp.zeros((DIM,), jnp.float32), 'Wk': jax.random.normal(ks[4], (DIM, DIM), jnp.float32) * std, 'bk': jnp.zeros((DIM,), jnp.float32), 'Wv': jax.random.normal(ks[5], (DIM, DIM), jnp.float32) * std, 'bv': jnp.zeros((DIM,), jnp.float32), 'Wo': jax.random.normal(ks[6], (DIM, DIM), jnp.float32) * std, 'bo': jnp.zeros((DIM,), jnp.float32)}
        return inp
    _L0_xattn_all = _L0_xattn_setup()
    _L0_xattn_in = {k: v for k, v in _L0_xattn_all.items() if k in ('Wq', 'bq', 'Wk', 'bk', 'Wv', 'bv', 'Wo', 'bo')}
    del _L0_xattn_all

    def _L0_ffn_setup():
        import jax, jax.numpy as jnp
        import numpy as np
        CAPACITY_FACTOR = 0.5
        key = jax.random.key(seed)
        ks = jax.random.split(key, 5)
        B, S, D, F = (4, 512, 128, 512)
        scale_in = 1.0 / np.sqrt(D)
        scale_ff = 1.0 / np.sqrt(F)
        return {'hidden_states': jax.random.normal(ks[0], (B, S, D), dtype=jnp.float32), 'w_router': jax.random.normal(ks[1], (D,), dtype=jnp.float32) * scale_in, 'W1': jax.random.normal(ks[2], (D, F), dtype=jnp.float32) * scale_in, 'b1': jnp.zeros((F,), dtype=jnp.float32), 'W2': jax.random.normal(ks[3], (F, D), dtype=jnp.float32) * scale_ff, 'b2': jnp.zeros((D,), dtype=jnp.float32)}
    _L0_ffn_all = _L0_ffn_setup()
    _L0_ffn_in = {k: v for k, v in _L0_ffn_all.items() if k in ('w_router', 'W1', 'b1', 'W2', 'b2')}
    del _L0_ffn_all

    def _L1_xattn_setup():
        import jax, jax.numpy as jnp
        import numpy as np
        D, H = (128, 16)
        DH = D // H

        def _split_heads(z):
            b, t, _ = z.shape
            return z.reshape(b, t, H, DH).transpose(0, 2, 1, 3)
        key = jax.random.key(seed)
        ks = jax.random.split(key, 11)
        b, t, ta = (2, 256, 1500)
        s = 1.0 / np.sqrt(D)
        return {'x': jax.random.normal(ks[0], (b, t, D), dtype=jnp.float32), 'xa': jax.random.normal(ks[1], (b, ta, D), dtype=jnp.float32), 'Wqkv': jax.random.normal(ks[2], (D, 3 * D), dtype=jnp.float32) * s, 'bqkv': jax.random.normal(ks[3], (3 * D,), dtype=jnp.float32) * 0.01, 'Wqkv_aux': jax.random.normal(ks[4], (D, 3 * D), dtype=jnp.float32) * s, 'bqkv_aux': jax.random.normal(ks[5], (3 * D,), dtype=jnp.float32) * 0.01, 'Wo': jax.random.normal(ks[6], (D, D), dtype=jnp.float32) * s, 'bo': jax.random.normal(ks[7], (D,), dtype=jnp.float32) * 0.01, 'g': jnp.zeros((H,), dtype=jnp.float32)}
    _L1_xattn_all = _L1_xattn_setup()
    _L1_xattn_in = {k: v for k, v in _L1_xattn_all.items() if k in ('Wqkv', 'bqkv', 'Wqkv_aux', 'bqkv_aux', 'Wo', 'bo', 'g')}
    del _L1_xattn_all

    def _L1_ffn_setup():
        import jax, jax.numpy as jnp
        import numpy as np
        D_MODEL = 128
        NUM_SLOTS = 64
        TOP_K = 8
        B, T = (4, 512)

        def _forward(x, slot_init, slot_scale, w1, b1, w2, b2, gru_wih, gru_whh, gru_bih, gru_bhh, wv, bv, wo, bo, tau):
            Bn, Tn, D = x.shape
            Sn = slot_init.shape[0]
            S = jnp.broadcast_to((slot_init * slot_scale)[None], (Bn, Sn, D)).astype(x.dtype)
            slot_mean = S.mean(axis=1, keepdims=True)
            ctx = jnp.concatenate([x, jnp.broadcast_to(slot_mean, x.shape)], axis=-1)
            h = jax.nn.gelu(ctx @ w1.T + b1, approximate=False)
            route_logits = (h @ w2.T + b2) / (jnp.abs(tau) + 0.1)
            topk_vals, topk_idx = jax.lax.top_k(route_logits, TOP_K)
            topk_w = jax.nn.softmax(topk_vals, axis=-1)
            alpha = jnp.sum(topk_w[..., None] * jax.nn.one_hot(topk_idx, Sn, dtype=x.dtype), axis=-2)
            slot_input = jnp.einsum('bts,btd->bsd', alpha, x)
            slot_wsum = alpha.sum(axis=1) + 1e-08
            gi = (slot_input / slot_wsum[..., None]).reshape(Bn * Sn, D)
            hs = S.reshape(Bn * Sn, D)
            gx = gi @ gru_wih.T + gru_bih
            gh = hs @ gru_whh.T + gru_bhh
            xr, xz, xn = jnp.split(gx, 3, axis=-1)
            hr, hz, hn = jnp.split(gh, 3, axis=-1)
            r = jax.nn.sigmoid(xr + hr)
            z = jax.nn.sigmoid(xz + hz)
            n = jnp.tanh(xn + r * hn)
            h_new = (1.0 - z) * n + z * hs
            S_new = h_new.reshape(Bn, Sn, D)
            slot_values = S_new @ wv.T + bv
            out = jnp.einsum('bts,bsd->btd', alpha, slot_values)
            return out @ wo.T + bo
        key = jax.random.key(seed)
        ks = jax.random.split(key, 16)
        D, S = (D_MODEL, NUM_SLOTS)
        H = D // 2
        sc = lambda fan_in: 1.0 / np.sqrt(fan_in)
        inp = {'x': jax.random.normal(ks[0], (B, T, D), dtype=jnp.float32), 'slot_init': jax.random.normal(ks[1], (S, D), dtype=jnp.float32) * 0.1, 'slot_scale': jnp.ones((S, 1), dtype=jnp.float32), 'w1': jax.random.normal(ks[2], (H, 2 * D), dtype=jnp.float32) * sc(2 * D), 'b1': jnp.zeros((H,), dtype=jnp.float32), 'w2': jax.random.normal(ks[3], (S, H), dtype=jnp.float32) * sc(H), 'b2': jnp.zeros((S,), dtype=jnp.float32), 'gru_wih': jax.random.normal(ks[4], (3 * D, D), dtype=jnp.float32) * sc(D), 'gru_whh': jax.random.normal(ks[5], (3 * D, D), dtype=jnp.float32) * sc(D), 'gru_bih': jnp.zeros((3 * D,), dtype=jnp.float32), 'gru_bhh': jnp.zeros((3 * D,), dtype=jnp.float32), 'wv': jax.random.normal(ks[6], (D, D), dtype=jnp.float32) * sc(D), 'bv': jnp.zeros((D,), dtype=jnp.float32), 'wo': jax.random.normal(ks[7], (D, D), dtype=jnp.float32) * sc(D), 'bo': jnp.zeros((D,), dtype=jnp.float32), 'tau': jnp.ones((1,), dtype=jnp.float32)}
        return inp
    _L1_ffn_all = _L1_ffn_setup()
    _L1_ffn_in = {k: v for k, v in _L1_ffn_all.items() if k in ('slot_init', 'slot_scale', 'w1', 'b1', 'w2', 'b2', 'gru_wih', 'gru_whh', 'gru_bih', 'gru_bhh', 'wv', 'bv', 'wo', 'bo', 'tau')}
    del _L1_ffn_all

    def _L2_xattn_setup():
        import jax, jax.numpy as jnp
        import numpy as np
        DIM = 128
        DIM_LATENT = 128
        DIM_HEAD = 64
        HEADS = 16
        INNER = HEADS * DIM_HEAD

        def layernorm(x, g, b, eps=1e-05):
            m = jnp.mean(x, axis=-1, keepdims=True)
            v = jnp.mean((x - m) ** 2, axis=-1, keepdims=True)
            return (x - m) / jnp.sqrt(v + eps) * g + b

        def rmsnorm(x, gamma, eps=1e-08):
            n = jnp.linalg.norm(x, axis=-1, keepdims=True) * x.shape[-1] ** (-0.5)
            return x / jnp.maximum(n, eps) * gamma
        key = jax.random.key(seed)
        ks = jax.random.split(key, 8)
        b, n, m = (4, 512, 64)
        x = jax.random.normal(ks[0], (b, n, DIM), dtype=jnp.float32)
        latents = jax.random.normal(ks[1], (b, m, DIM_LATENT), dtype=jnp.float32)
        mask = jnp.ones((b, n), dtype=bool)
        s = 0.02
        return {'x': x, 'latents': latents, 'mask': mask, 'ln_x_g': jnp.ones((DIM,), jnp.float32), 'ln_x_b': jnp.zeros((DIM,), jnp.float32), 'ln_l_g': jnp.ones((DIM_LATENT,), jnp.float32), 'ln_l_b': jnp.zeros((DIM_LATENT,), jnp.float32), 'qn_g': jnp.ones((DIM_HEAD,), jnp.float32), 'kn_g': jnp.ones((DIM_HEAD,), jnp.float32), 'Wq': jax.random.normal(ks[2], (DIM_LATENT, INNER), jnp.float32) * s, 'Wkv': jax.random.normal(ks[3], (DIM, 2 * INNER), jnp.float32) * s, 'Wout': jax.random.normal(ks[4], (INNER, DIM_LATENT), jnp.float32) * s, 'bout': jnp.zeros((DIM_LATENT,), jnp.float32)}
    _L2_xattn_all = _L2_xattn_setup()
    _L2_xattn_in = {k: v for k, v in _L2_xattn_all.items() if k in ('ln_x_g', 'ln_x_b', 'ln_l_g', 'ln_l_b', 'qn_g', 'kn_g', 'Wq', 'Wkv', 'Wout', 'bout')}
    del _L2_xattn_all

    def _L2_ffn_setup():
        import jax, jax.numpy as jnp
        import numpy as np
        EPS = 1e-06
        LN_EPS = 1e-05

        def _absmean_core(W):
            gamma = jnp.mean(jnp.abs(W)) + EPS
            Ws = W / gamma
            Wq = jnp.sign(Ws) * jnp.minimum(jnp.round(jnp.abs(Ws)), 1.0)
            return (Wq, gamma)

        @jax.custom_vjp
        def absmean(W):
            return _absmean_core(W)[0]

        def _absmean_fwd(W):
            Wq, gamma = _absmean_core(W)
            return (Wq, gamma)

        def _absmean_bwd(gamma, g):
            return (g / gamma,)
        absmean.defvjp(_absmean_fwd, _absmean_bwd)

        def layernorm(x, w, b, eps=LN_EPS):
            mu = jnp.mean(x, axis=-1, keepdims=True)
            var = jnp.mean((x - mu) ** 2, axis=-1, keepdims=True)
            return (x - mu) * jax.lax.rsqrt(var + eps) * w + b
        key = jax.random.key(seed)
        k1, k2, k3 = jax.random.split(key, 3)
        d, h = (128, 512)
        B, T = (8, 256)
        return {'x': jax.random.normal(k1, (B, T, d), jnp.float32), 'W_fc': jax.random.normal(k2, (h, d), jnp.float32), 'ln_w': jnp.ones((h,), jnp.float32), 'ln_b': jnp.zeros((h,), jnp.float32), 'W_proj': jax.random.normal(k3, (d, h), jnp.float32)}
    _L2_ffn_all = _L2_ffn_setup()
    _L2_ffn_in = {k: v for k, v in _L2_ffn_all.items() if k in ('W_fc', 'ln_w', 'ln_b', 'W_proj')}
    del _L2_ffn_all

    def _L3_xattn_setup():
        import jax, jax.numpy as jnp
        import numpy as np
        B, S, E, H = (4, 256, 64, 128)
        key = jax.random.key(seed)
        ks = jax.random.split(key, 8)
        s = 1.0 / np.sqrt(H)
        return {'hidden_states': jax.random.normal(ks[0], (B, S, H), jnp.float32), 'external_embeddings': jax.random.normal(ks[1], (B, E, H), jnp.float32), 'Wq': jax.random.normal(ks[2], (H, H), jnp.float32) * s, 'bq': jax.random.normal(ks[3], (H,), jnp.float32) * 0.02, 'Wk': jax.random.normal(ks[4], (H, H), jnp.float32) * s, 'bk': jax.random.normal(ks[5], (H,), jnp.float32) * 0.02, 'Wv': jax.random.normal(ks[6], (H, H), jnp.float32) * s, 'bv': jax.random.normal(ks[7], (H,), jnp.float32) * 0.02}
    _L3_xattn_all = _L3_xattn_setup()
    _L3_xattn_in = {k: v for k, v in _L3_xattn_all.items() if k in ('Wq', 'bq', 'Wk', 'bk', 'Wv', 'bv')}
    del _L3_xattn_all

    def _L3_ffn_setup():
        import jax, jax.numpy as jnp
        import numpy as np
        from jax import lax
        LOKAL_GRUP = 7
        TOP_K = 2
        EPS = 1e-08
        CACHE_BONUS = 0.1

        def _route(tokens, uzman_embeddings, onbellek_durumu):
            sim = tokens @ uzman_embeddings.T
            _, local_idx = lax.top_k(sim, LOKAL_GRUP)
            t_norm = tokens / (jnp.linalg.norm(tokens, axis=-1, keepdims=True) + EPS)
            e_norm = uzman_embeddings / (jnp.linalg.norm(uzman_embeddings, axis=-1, keepdims=True) + EPS)
            local_embs = e_norm[local_idx]
            scores = jnp.einsum('nld,nd->nl', local_embs, t_norm)
            scores = scores + CACHE_BONUS * onbellek_durumu[local_idx]
            top_scores, top_local = lax.top_k(scores, TOP_K)
            global_idx = jnp.take_along_axis(local_idx, top_local, axis=1)
            weights = jax.nn.softmax(top_scores, axis=-1)
            return (global_idx, lax.stop_gradient(weights))
        key = jax.random.key(seed)
        ks = jax.random.split(key, 6)
        B, S, D, E, H = (2, 256, 128, 8, 512)
        return {'x': jax.random.normal(ks[0], (B, S, D), jnp.float32), 'uzman_embeddings': jax.random.normal(ks[1], (E, D), jnp.float32) * 0.01, 'W1': jax.random.normal(ks[2], (E, D, H), jnp.float32) * 0.02, 'b1': jax.random.normal(ks[3], (E, H), jnp.float32) * 0.02, 'W2': jax.random.normal(ks[4], (E, H, D), jnp.float32) * 0.02, 'b2': jax.random.normal(ks[5], (E, D), jnp.float32) * 0.02, 'onbellek_durumu': jnp.ones((E,), jnp.float32)}
    _L3_ffn_all = _L3_ffn_setup()
    _L3_ffn_in = {k: v for k, v in _L3_ffn_all.items() if k in ('uzman_embeddings', 'W1', 'b1', 'W2', 'b2', 'onbellek_durumu')}
    del _L3_ffn_all
    return {'x': x, 'ctx_1024': ctx_1024, 'mask_1x1xSxS2_ik0': mask_1x1xSxS2_ik0, 'mask_BxS2_bf1': mask_BxS2_bf1, 'g_xattn': g_xattn, 'g_ffn': g_ffn, 'L0_xattn_Wq': _L0_xattn_in['Wq'], 'L0_xattn_bq': _L0_xattn_in['bq'], 'L0_xattn_Wk': _L0_xattn_in['Wk'], 'L0_xattn_bk': _L0_xattn_in['bk'], 'L0_xattn_Wv': _L0_xattn_in['Wv'], 'L0_xattn_bv': _L0_xattn_in['bv'], 'L0_xattn_Wo': _L0_xattn_in['Wo'], 'L0_xattn_bo': _L0_xattn_in['bo'], 'L0_ffn_w_router': _L0_ffn_in['w_router'], 'L0_ffn_W1': _L0_ffn_in['W1'], 'L0_ffn_b1': _L0_ffn_in['b1'], 'L0_ffn_W2': _L0_ffn_in['W2'], 'L0_ffn_b2': _L0_ffn_in['b2'], 'L1_xattn_Wqkv': _L1_xattn_in['Wqkv'], 'L1_xattn_bqkv': _L1_xattn_in['bqkv'], 'L1_xattn_Wqkv_aux': _L1_xattn_in['Wqkv_aux'], 'L1_xattn_bqkv_aux': _L1_xattn_in['bqkv_aux'], 'L1_xattn_Wo': _L1_xattn_in['Wo'], 'L1_xattn_bo': _L1_xattn_in['bo'], 'L1_xattn_g': _L1_xattn_in['g'], 'L1_ffn_slot_init': _L1_ffn_in['slot_init'], 'L1_ffn_slot_scale': _L1_ffn_in['slot_scale'], 'L1_ffn_w1': _L1_ffn_in['w1'], 'L1_ffn_b1': _L1_ffn_in['b1'], 'L1_ffn_w2': _L1_ffn_in['w2'], 'L1_ffn_b2': _L1_ffn_in['b2'], 'L1_ffn_gru_wih': _L1_ffn_in['gru_wih'], 'L1_ffn_gru_whh': _L1_ffn_in['gru_whh'], 'L1_ffn_gru_bih': _L1_ffn_in['gru_bih'], 'L1_ffn_gru_bhh': _L1_ffn_in['gru_bhh'], 'L1_ffn_wv': _L1_ffn_in['wv'], 'L1_ffn_bv': _L1_ffn_in['bv'], 'L1_ffn_wo': _L1_ffn_in['wo'], 'L1_ffn_bo': _L1_ffn_in['bo'], 'L1_ffn_tau': _L1_ffn_in['tau'], 'L2_xattn_ln_x_g': _L2_xattn_in['ln_x_g'], 'L2_xattn_ln_x_b': _L2_xattn_in['ln_x_b'], 'L2_xattn_ln_l_g': _L2_xattn_in['ln_l_g'], 'L2_xattn_ln_l_b': _L2_xattn_in['ln_l_b'], 'L2_xattn_qn_g': _L2_xattn_in['qn_g'], 'L2_xattn_kn_g': _L2_xattn_in['kn_g'], 'L2_xattn_Wq': _L2_xattn_in['Wq'], 'L2_xattn_Wkv': _L2_xattn_in['Wkv'], 'L2_xattn_Wout': _L2_xattn_in['Wout'], 'L2_xattn_bout': _L2_xattn_in['bout'], 'L2_ffn_W_fc': _L2_ffn_in['W_fc'], 'L2_ffn_ln_w': _L2_ffn_in['ln_w'], 'L2_ffn_ln_b': _L2_ffn_in['ln_b'], 'L2_ffn_W_proj': _L2_ffn_in['W_proj'], 'L3_xattn_Wq': _L3_xattn_in['Wq'], 'L3_xattn_bq': _L3_xattn_in['bq'], 'L3_xattn_Wk': _L3_xattn_in['Wk'], 'L3_xattn_bk': _L3_xattn_in['bk'], 'L3_xattn_Wv': _L3_xattn_in['Wv'], 'L3_xattn_bv': _L3_xattn_in['bv'], 'L3_ffn_uzman_embeddings': _L3_ffn_in['uzman_embeddings'], 'L3_ffn_W1': _L3_ffn_in['W1'], 'L3_ffn_b1': _L3_ffn_in['b1'], 'L3_ffn_W2': _L3_ffn_in['W2'], 'L3_ffn_b2': _L3_ffn_in['b2'], 'L3_ffn_onbellek_durumu': _L3_ffn_in['onbellek_durumu']}

def reference(x, ctx_1024, mask_1x1xSxS2_ik0, mask_BxS2_bf1, g_xattn, g_ffn, L0_xattn_Wq, L0_xattn_bq, L0_xattn_Wk, L0_xattn_bk, L0_xattn_Wv, L0_xattn_bv, L0_xattn_Wo, L0_xattn_bo, L0_ffn_w_router, L0_ffn_W1, L0_ffn_b1, L0_ffn_W2, L0_ffn_b2, L1_xattn_Wqkv, L1_xattn_bqkv, L1_xattn_Wqkv_aux, L1_xattn_bqkv_aux, L1_xattn_Wo, L1_xattn_bo, L1_xattn_g, L1_ffn_slot_init, L1_ffn_slot_scale, L1_ffn_w1, L1_ffn_b1, L1_ffn_w2, L1_ffn_b2, L1_ffn_gru_wih, L1_ffn_gru_whh, L1_ffn_gru_bih, L1_ffn_gru_bhh, L1_ffn_wv, L1_ffn_bv, L1_ffn_wo, L1_ffn_bo, L1_ffn_tau, L2_xattn_ln_x_g, L2_xattn_ln_x_b, L2_xattn_ln_l_g, L2_xattn_ln_l_b, L2_xattn_qn_g, L2_xattn_kn_g, L2_xattn_Wq, L2_xattn_Wkv, L2_xattn_Wout, L2_xattn_bout, L2_ffn_W_fc, L2_ffn_ln_w, L2_ffn_ln_b, L2_ffn_W_proj, L3_xattn_Wq, L3_xattn_bq, L3_xattn_Wk, L3_xattn_bk, L3_xattn_Wv, L3_xattn_bv, L3_ffn_uzman_embeddings, L3_ffn_W1, L3_ffn_b1, L3_ffn_W2, L3_ffn_b2, L3_ffn_onbellek_durumu):
    import jax
    import jax.numpy as jnp

    def _L0_xattn_ref(q, k, v, mask, Wq, bq, Wk, bk, Wv, bv, Wo, bo):
        import jax, jax.numpy as jnp
        import numpy as np
        B, N, DIM, H = (2, 256, 128, 16)
        HD = DIM // H
        SCALE = HD ** (-0.5)

        def _split_heads(x):
            b, n, _ = x.shape
            return x.reshape(b, n, H, HD).transpose(0, 2, 1, 3)
        qh = _split_heads(q @ Wq.T + bq)
        kh = _split_heads(k @ Wk.T + bk)
        vh = _split_heads(v @ Wv.T + bv)
        attn = jnp.einsum('bhqc,bhkc->bhqk', qh, kh) * SCALE
        attn = jnp.where(mask == 0, -jnp.inf, attn)
        attn = jax.nn.softmax(attn, axis=-1)
        out = jnp.einsum('bhqk,bhkc->bhqc', attn, vh)
        b, h, n, c = out.shape
        out = out.transpose(0, 2, 1, 3).reshape(b, n, h * c)
        return out @ Wo.T + bo

    def _L0_ffn_ref(hidden_states, w_router, W1, b1, W2, b2):
        import jax, jax.numpy as jnp
        import numpy as np
        CAPACITY_FACTOR = 0.5
        'Mixture-of-Depths block: route top-k tokens through an FFN inner block,\n            scatter back with sigmoid router weights; bypassed tokens pass through.'
        B, S, D = hidden_states.shape
        k = int(S * CAPACITY_FACTOR)
        scores = jnp.einsum('bsd,d->bs', hidden_states, w_router)
        top_scores, top_idx = jax.lax.top_k(scores, k)
        weights = jax.nn.sigmoid(top_scores)
        selected = jnp.take_along_axis(hidden_states, top_idx[:, :, None], axis=1)
        h = jax.nn.gelu(jnp.einsum('bkd,df->bkf', selected, W1) + b1)
        processed = jnp.einsum('bkf,fd->bkd', h, W2) + b2
        update = weights[:, :, None] * processed

        def scatter_one(xb, ib, ub):
            return xb.at[ib].add(ub)
        output = jax.vmap(scatter_one)(hidden_states, top_idx, update)
        return output

    def _L1_xattn_ref(x, xa, Wqkv, bqkv, Wqkv_aux, bqkv_aux, Wo, bo, g):
        import jax, jax.numpy as jnp
        import numpy as np
        D, H = (128, 16)
        DH = D // H

        def _split_heads(z):
            b, t, _ = z.shape
            return z.reshape(b, t, H, DH).transpose(0, 2, 1, 3)
        qkv = x @ Wqkv + bqkv
        qkv_a = xa @ Wqkv_aux + bqkv_aux
        q, k, v = (_split_heads(c) for c in jnp.split(qkv, 3, axis=-1))
        qa, ka, va = (_split_heads(c) for c in jnp.split(qkv_a, 3, axis=-1))
        scale = 1.0 / jnp.sqrt(jnp.float32(DH))
        dots = jnp.einsum('bhqd,bhkd->bhqk', q, k) * scale
        dots_aux = jnp.einsum('bhqd,bhkd->bhqk', q, ka) * scale
        p = jax.nn.softmax(dots, axis=-1)
        pa = jax.nn.softmax(dots_aux, axis=-1)
        h_main = jnp.einsum('bhqk,bhkd->bhqd', p, v)
        h_aux = jnp.einsum('bhqk,bhkd->bhqd', pa, va)
        gate = jax.nn.sigmoid(g).reshape(1, H, 1, 1)
        out = h_main * (1.0 - gate) + h_aux * gate
        b, _, t, _ = out.shape
        out = out.transpose(0, 2, 1, 3).reshape(b, t, H * DH)
        return out @ Wo + bo

    def _L1_ffn_ref(x, slot_init, slot_scale, w1, b1, w2, b2, gru_wih, gru_whh, gru_bih, gru_bhh, wv, bv, wo, bo, tau):
        import jax, jax.numpy as jnp
        import numpy as np
        D_MODEL = 128
        NUM_SLOTS = 64
        TOP_K = 8
        B, T = (4, 512)

        def _forward(x, slot_init, slot_scale, w1, b1, w2, b2, gru_wih, gru_whh, gru_bih, gru_bhh, wv, bv, wo, bo, tau):
            Bn, Tn, D = x.shape
            Sn = slot_init.shape[0]
            S = jnp.broadcast_to((slot_init * slot_scale)[None], (Bn, Sn, D)).astype(x.dtype)
            slot_mean = S.mean(axis=1, keepdims=True)
            ctx = jnp.concatenate([x, jnp.broadcast_to(slot_mean, x.shape)], axis=-1)
            h = jax.nn.gelu(ctx @ w1.T + b1, approximate=False)
            route_logits = (h @ w2.T + b2) / (jnp.abs(tau) + 0.1)
            topk_vals, topk_idx = jax.lax.top_k(route_logits, TOP_K)
            topk_w = jax.nn.softmax(topk_vals, axis=-1)
            alpha = jnp.sum(topk_w[..., None] * jax.nn.one_hot(topk_idx, Sn, dtype=x.dtype), axis=-2)
            slot_input = jnp.einsum('bts,btd->bsd', alpha, x)
            slot_wsum = alpha.sum(axis=1) + 1e-08
            gi = (slot_input / slot_wsum[..., None]).reshape(Bn * Sn, D)
            hs = S.reshape(Bn * Sn, D)
            gx = gi @ gru_wih.T + gru_bih
            gh = hs @ gru_whh.T + gru_bhh
            xr, xz, xn = jnp.split(gx, 3, axis=-1)
            hr, hz, hn = jnp.split(gh, 3, axis=-1)
            r = jax.nn.sigmoid(xr + hr)
            z = jax.nn.sigmoid(xz + hz)
            n = jnp.tanh(xn + r * hn)
            h_new = (1.0 - z) * n + z * hs
            S_new = h_new.reshape(Bn, Sn, D)
            slot_values = S_new @ wv.T + bv
            out = jnp.einsum('bts,bsd->btd', alpha, slot_values)
            return out @ wo.T + bo
        return _forward(x, slot_init, slot_scale, w1, b1, w2, b2, gru_wih, gru_whh, gru_bih, gru_bhh, wv, bv, wo, bo, tau)

    def _L2_xattn_ref(x, latents, mask, ln_x_g, ln_x_b, ln_l_g, ln_l_b, qn_g, kn_g, Wq, Wkv, Wout, bout):
        import jax, jax.numpy as jnp
        import numpy as np
        DIM = 128
        DIM_LATENT = 128
        DIM_HEAD = 64
        HEADS = 16
        INNER = HEADS * DIM_HEAD

        def layernorm(x, g, b, eps=1e-05):
            m = jnp.mean(x, axis=-1, keepdims=True)
            v = jnp.mean((x - m) ** 2, axis=-1, keepdims=True)
            return (x - m) / jnp.sqrt(v + eps) * g + b

        def rmsnorm(x, gamma, eps=1e-08):
            n = jnp.linalg.norm(x, axis=-1, keepdims=True) * x.shape[-1] ** (-0.5)
            return x / jnp.maximum(n, eps) * gamma
        b, n, _ = x.shape
        m = latents.shape[1]
        h, d = (HEADS, DIM_HEAD)
        scale = d ** (-0.5)
        xn = layernorm(x, ln_x_g, ln_x_b)
        ln = layernorm(latents, ln_l_g, ln_l_b)
        q = (ln @ Wq).reshape(b, m, h, d).transpose(0, 2, 1, 3)
        kv = jnp.concatenate([xn @ Wkv, ln @ Wkv], axis=1)
        kv = kv.reshape(b, n + m, 2, h, d)
        k = kv[:, :, 0].transpose(0, 2, 1, 3)
        v = kv[:, :, 1].transpose(0, 2, 1, 3)
        qn = rmsnorm(q, qn_g) * scale
        kn = rmsnorm(k, kn_g)
        sim = jnp.einsum('bhid,bhjd->bhij', qn, kn)
        max_neg = -jnp.finfo(sim.dtype).max
        padded_mask = jnp.concatenate([mask, jnp.ones((b, m), bool)], axis=1)
        sim = jnp.where(padded_mask[:, None, None, :], sim, max_neg)
        attn = jax.nn.softmax(sim.astype(jnp.float32), axis=-1).astype(sim.dtype)
        out = jnp.einsum('bhij,bhjd->bhid', attn, v)
        out = out.transpose(0, 2, 1, 3).reshape(b, m, h * d)
        return out @ Wout + bout

    def _L2_ffn_ref(x, W_fc, ln_w, ln_b, W_proj):
        import jax, jax.numpy as jnp
        import numpy as np
        EPS = 1e-06
        LN_EPS = 1e-05

        def _absmean_core(W):
            gamma = jnp.mean(jnp.abs(W)) + EPS
            Ws = W / gamma
            Wq = jnp.sign(Ws) * jnp.minimum(jnp.round(jnp.abs(Ws)), 1.0)
            return (Wq, gamma)

        @jax.custom_vjp
        def absmean(W):
            return _absmean_core(W)[0]

        def _absmean_fwd(W):
            Wq, gamma = _absmean_core(W)
            return (Wq, gamma)

        def _absmean_bwd(gamma, g):
            return (g / gamma,)
        absmean.defvjp(_absmean_fwd, _absmean_bwd)

        def layernorm(x, w, b, eps=LN_EPS):
            mu = jnp.mean(x, axis=-1, keepdims=True)
            var = jnp.mean((x - mu) ** 2, axis=-1, keepdims=True)
            return (x - mu) * jax.lax.rsqrt(var + eps) * w + b
        h = jnp.einsum('btd,hd->bth', x, absmean(W_fc))
        h = jax.nn.gelu(h, approximate=False)
        h = layernorm(h, ln_w, ln_b)
        return jnp.einsum('bth,dh->btd', h, absmean(W_proj))

    def _L3_xattn_ref(hidden_states, external_embeddings, Wq, bq, Wk, bk, Wv, bv):
        import jax, jax.numpy as jnp
        import numpy as np
        B, S, E, H = (4, 256, 64, 128)
        q = hidden_states @ Wq + bq
        k_tok = hidden_states @ Wk + bk
        v_tok = hidden_states @ Wv + bv
        k_ext = external_embeddings @ Wk + bk
        v_ext = external_embeddings @ Wv + bv
        s_self = jnp.einsum('bsh,bsh->bs', q, k_tok)[..., None]
        s_ext = jnp.einsum('bsh,beh->bse', q, k_ext)
        scores = jnp.concatenate([s_self, s_ext], axis=-1)
        probs = jax.nn.softmax(scores, axis=-1)
        ctx = probs[..., :1] * v_tok + jnp.einsum('bse,beh->bsh', probs[..., 1:], v_ext)
        return ctx

    def _L3_ffn_ref(x, uzman_embeddings, W1, b1, W2, b2, onbellek_durumu):
        import jax, jax.numpy as jnp
        import numpy as np
        from jax import lax
        LOKAL_GRUP = 7
        TOP_K = 2
        EPS = 1e-08
        CACHE_BONUS = 0.1

        def _route(tokens, uzman_embeddings, onbellek_durumu):
            sim = tokens @ uzman_embeddings.T
            _, local_idx = lax.top_k(sim, LOKAL_GRUP)
            t_norm = tokens / (jnp.linalg.norm(tokens, axis=-1, keepdims=True) + EPS)
            e_norm = uzman_embeddings / (jnp.linalg.norm(uzman_embeddings, axis=-1, keepdims=True) + EPS)
            local_embs = e_norm[local_idx]
            scores = jnp.einsum('nld,nd->nl', local_embs, t_norm)
            scores = scores + CACHE_BONUS * onbellek_durumu[local_idx]
            top_scores, top_local = lax.top_k(scores, TOP_K)
            global_idx = jnp.take_along_axis(local_idx, top_local, axis=1)
            weights = jax.nn.softmax(top_scores, axis=-1)
            return (global_idx, lax.stop_gradient(weights))
        B, S, D = x.shape
        tokens = x.reshape(-1, D)
        global_idx, weights = _route(tokens, uzman_embeddings, onbellek_durumu)
        h = jnp.einsum('nd,edh->enh', tokens, W1) + b1[:, None, :]
        h = jax.nn.gelu(h, approximate=False)
        out_all = jnp.einsum('enh,ehd->end', h, W2) + b2[:, None, :]
        N = tokens.shape[0]
        out_sel = out_all[global_idx, jnp.arange(N)[:, None]]
        out = jnp.sum(weights[..., None] * out_sel, axis=1)
        return out.reshape(B, S, D)
    x = x + jnp.tanh(g_xattn[0]) * _L0_xattn_ref(_layernorm(x, axis=-1), ctx_1024, ctx_1024, mask_1x1xSxS2_ik0, L0_xattn_Wq, L0_xattn_bq, L0_xattn_Wk, L0_xattn_bk, L0_xattn_Wv, L0_xattn_bv, L0_xattn_Wo, L0_xattn_bo)
    x = x + jnp.tanh(g_ffn[0]) * _L0_ffn_ref(_layernorm(x, axis=-1), L0_ffn_w_router, L0_ffn_W1, L0_ffn_b1, L0_ffn_W2, L0_ffn_b2)
    x = x + jnp.tanh(g_xattn[1]) * _L1_xattn_ref(_layernorm(x, axis=-1), ctx_1024, L1_xattn_Wqkv, L1_xattn_bqkv, L1_xattn_Wqkv_aux, L1_xattn_bqkv_aux, L1_xattn_Wo, L1_xattn_bo, L1_xattn_g)
    x = x + jnp.tanh(g_ffn[1]) * _L1_ffn_ref(_layernorm(x, axis=-1), L1_ffn_slot_init, L1_ffn_slot_scale, L1_ffn_w1, L1_ffn_b1, L1_ffn_w2, L1_ffn_b2, L1_ffn_gru_wih, L1_ffn_gru_whh, L1_ffn_gru_bih, L1_ffn_gru_bhh, L1_ffn_wv, L1_ffn_bv, L1_ffn_wo, L1_ffn_bo, L1_ffn_tau)
    x = x + jnp.tanh(g_xattn[2]) * _L2_xattn_ref(ctx_1024, _layernorm(x, axis=-1), mask_BxS2_bf1, L2_xattn_ln_x_g, L2_xattn_ln_x_b, L2_xattn_ln_l_g, L2_xattn_ln_l_b, L2_xattn_qn_g, L2_xattn_kn_g, L2_xattn_Wq, L2_xattn_Wkv, L2_xattn_Wout, L2_xattn_bout)
    x = x + jnp.tanh(g_ffn[2]) * _L2_ffn_ref(_layernorm(x, axis=-1), L2_ffn_W_fc, L2_ffn_ln_w, L2_ffn_ln_b, L2_ffn_W_proj)
    x = x + jnp.tanh(g_xattn[3]) * _L3_xattn_ref(_layernorm(x, axis=-1), ctx_1024, L3_xattn_Wq, L3_xattn_bq, L3_xattn_Wk, L3_xattn_bk, L3_xattn_Wv, L3_xattn_bv)
    x = x + jnp.tanh(g_ffn[3]) * _L3_ffn_ref(_layernorm(x, axis=-1), L3_ffn_uzman_embeddings, L3_ffn_W1, L3_ffn_b1, L3_ffn_W2, L3_ffn_b2, L3_ffn_onbellek_durumu)
    return x

_drawn_inputs = setup_inputs


def setup_inputs(seed=0):
    import zlib

    import numpy as np

    out = dict(_drawn_inputs(seed))
    spreads = {'L0_xattn_bq': (0.0, 0.1),
     'L0_xattn_bk': (0.0, 2.0),
     'L0_xattn_bv': (0.0, 0.1),
     'L0_xattn_bo': (0.0, 0.1),
     'L0_ffn_b1': (0.0, 0.1),
     'L0_ffn_b2': (0.0, 0.1),
     'L1_xattn_g': (0.0, 0.1),
     'L1_ffn_slot_scale': (1.0, 0.6),
     'L1_ffn_b1': (0.0, 0.1),
     'L1_ffn_b2': (0.0, 0.1),
     'L1_ffn_gru_bih': (0.0, 0.1),
     'L1_ffn_gru_bhh': (0.0, 0.1),
     'L1_ffn_bv': (0.0, 0.1),
     'L1_ffn_bo': (0.0, 0.1),
     'L2_xattn_ln_x_g': (1.0, 0.6),
     'L2_xattn_ln_x_b': (0.0, 0.366),
     'L2_xattn_ln_l_g': (1.0, 0.6),
     'L2_xattn_ln_l_b': (0.0, 0.8),
     'L2_xattn_qn_g': (1.0, 0.6),
     'L2_xattn_kn_g': (1.0, 0.6),
     'L2_xattn_bout': (0.0, 0.1),
     'L2_ffn_ln_w': (1.0, 0.2),
     'L2_ffn_ln_b': (0.0, 0.1),
     'L3_ffn_onbellek_durumu': (1.0, 0.6)}
    factors = {'g_ffn': 23.44,
     'L1_xattn_bqkv': 4.404,
     'L1_xattn_bqkv_aux': 3.53,
     'L1_ffn_gru_whh': 3.724,
     'L3_xattn_bq': 24.389,
     'L3_xattn_bk': 64.0,
     'L3_xattn_bv': 42.727,
     'L3_ffn_uzman_embeddings': 8.0,
     'L3_ffn_W1': 8.0,
     'L3_ffn_b1': 30.564,
     'L3_ffn_W2': 8.0,
     'L3_ffn_b2': 64.0}
    for name, (base, spread) in spreads.items():
        noise = np.random.default_rng([zlib.crc32(name.encode()), seed]).standard_normal(out[name].shape)
        drawn = base * np.exp(spread * noise) if base else spread * noise
        out[name] = jnp.asarray(drawn.astype(out[name].dtype))
    for name, factor in factors.items():
        out[name] = (out[name] * factor).astype(out[name].dtype)
    return out
```

```python
from contextlib import ExitStack

import concourse.bass as bass
from concourse import mybir

F32 = mybir.dt.float32
BF16 = mybir.dt.bfloat16
I32 = mybir.dt.int32
U8 = mybir.dt.uint8
ALU = mybir.AluOpType
ACT = mybir.ActivationFunctionType
AX = mybir.AxisListType

B, T, D = 8, 100, 128
H = 16
S2 = 1444
NCH = 12
CK = 121
LAST = S2 - (NCH - 1) * CK
KQ = S2 // 4
HD = 8
DH = 64
F0 = 512
NSLOT = 64
E3, H3 = 8, 512
BT = B * T
HALF = BT // 2
BANK = 512
LN_EPS = 1e-5
OFF = -1e30
GROUP = 4 * T
ROWS = [CK] * (NCH - 1) + [LAST]


def flamingo(nc, A, out):
    ctx = ExitStack()
    with ctx:
        def sb(name, shape, dt=F32):
            return ctx.enter_context(nc.sbuf_tensor(name, shape, dt))

        sems = {}

        def sem(name):
            if name not in sems:
                sems[name] = ctx.enter_context(nc.semaphore(name))
            return sems[name]

        x = sb("x", [T, B, D])
        xn = sb("xn", [T, B, D])
        xnT = sb("xnT", [D, BT])
        wideA = sb("wideA", [T, B, D])
        wideB = sb("wideB", [T, B, D])
        small = sb("small", [128, 64])
        stat = sb("stat", [128, 8, 32])
        gates = sb("gates", [128, 8])

        ident = sb("ident", [128, 128])
        identb = sb("identb", [128, 128], BF16)
        low_rows = sb("low_rows", [32, 1])
        before = sb("before", [T, T])
        ones = sb("ones", [128, 128])

        W = {}
        for name, ap in A.items():
            if name.startswith("w_"):
                W[name[2:]] = sb(name, list(ap.shape))
        wr_bc = sb("wr_bc", [D, T])
        bv1 = sb("bv1", [128, 1])
        head_gates = sb("head_gates", [128, 2, H])
        ctxT = sb("ctxT", [D, S2])
        ctxk = sb("ctxk", [128, NCH + 1, D])
        M = sb("M", [128, 4 * GROUP])
        arena = sb("arena", [128, 13 * 1600])

        psum = ctx.enter_context(nc.psum_tensor("psum", [128, 8, BANK], F32))

        def carve(off, shape):
            n = 1
            for s in shape[1:]:
                n *= s
            v = arena[0:shape[0], off:off + n]
            if len(shape) == 3:
                v = v.rearrange("p (a b) -> p a b", a=shape[1])
            if len(shape) == 4:
                v = v.rearrange("p (a b c) -> p a b c", a=shape[1], b=shape[2])
            return v, off + n

        kst_w, o = carve(0, [128, 8 * S2 // 2])
        own_kst_w, o = carve(o, [128, 8 * T // 2])
        q1_w, o = carve(o, [128, 8 * T // 2])
        q2_w, o = carve(o, [128, 8 * T // 2])
        own_q2_w, o = carve(o, [128, 8 * T // 2])
        kparts_w, o = carve(o, [128, 3 * S2 // 2])
        qparts_w, o = carve(o, [128, 3 * (BT + T) // 2])
        own_kparts_w, o = carve(o, [128, 3 * (BT + T) // 2])
        Vo_w, o = carve(o, [128, NCH * H * 9])
        own_Vo_w, o = carve(o, [128, H * 9])
        P3, o = carve(o, [128, 3, 2 * GROUP])
        summed, o = carve(o, [128, GROUP])
        own_summed, o = carve(o, [128, GROUP])
        shares, o = carve(o, [T, 2, H])
        heads, o = carve(o, [T, D])
        own_heads, o = carve(o, [T, D])
        headsT, o = carve(o, [D, T])
        attended, o = carve(o, [T, (B + 1) * D])
        mx, o = carve(o, [T, 2, 32])
        flag, o = carve(o, [T, 32])
        hl_w, o = carve(o, [32, 2 * T // 2])
        high_w, o = carve(o, [32, T // 2])
        maskw, o = carve(o, [128, NCH * T // 2])
        assert o <= 13 * 1600, o
        Vo = Vo_w.rearrange("p (c h d) -> p c h d", c=NCH, h=H)
        own_Vo = own_Vo_w.rearrange("p (h d) -> p h d", h=H)
        keys_st = kst_w.bitcast(BF16).rearrange("p (h k) -> p h k", h=8)
        own_keys_st = own_kst_w.bitcast(BF16).rearrange("p (h k) -> p h k", h=8)
        q1 = q1_w.bitcast(BF16).rearrange("p (h q) -> p h q", h=8)
        q2 = q2_w.bitcast(BF16).rearrange("p (h q) -> p h q", h=8)
        own_q2 = own_q2_w.bitcast(BF16).rearrange("p (h q) -> p h q", h=8)
        kparts = kparts_w.bitcast(BF16).rearrange("p (a k) -> p a k", a=3)
        qparts = qparts_w.bitcast(BF16).rearrange("p (a k) -> p a k", a=3)
        own_kparts = own_kparts_w.bitcast(BF16).rearrange("p (a k) -> p a k", a=3)
        hl = hl_w.bitcast(BF16).rearrange("p (g q) -> p g q", g=2)
        high = high_w.bitcast(BF16)
        maskb = maskw.bitcast(BF16).rearrange("p (c q) -> p c q", c=NCH)
        lat = sb("lat", [T, B, D])
        mB = sb("mB", [128, 4 * GROUP])
        xkT = sb("xkT", [D, S2 + T])
        qeff = sb("qeff", [D, H, T])
        Psum = sb("Psum", [128, 4 * GROUP])
        own_M = mB[0:T, :]
        kf = Psum[:, 0:S2]
        kr = qeff[:, :, :].rearrange("p h q -> p (h q)")[:, 0:S2]
        qf = Psum[:, 0:BT]
        qr = qeff[:, :, :].rearrange("p h q -> p (h q)")[:, 0:BT]
        Vn = xkT[:, 0:NCH * D].rearrange("p (c d) -> p c d", c=NCH)
        vs = lat[:, :, :]
        maski = Psum[:, 0:NCH * T]

        hid, o = carve(0, [128, 4, BT])
        big1, o = carve(o, [128, 1024])
        big2, o = carve(o, [128, 1024])
        big3, o = carve(o, [128, 1024])
        g0, o = carve(o, [128, 512])
        g1, o = carve(o, [128, 512])
        g2, o = carve(o, [128, 512])
        g3, o = carve(o, [128, 512])
        w3a, o = carve(o, [D, E3, H3])
        w3b, o = carve(o, [128, E3, 4, D])
        assert o <= 13 * 1600, o
        acc3 = big1[0:T, :].rearrange("p (b d) -> p b d", b=B)
        q3T, o = carve(0, [D, BT])
        qe3, o = carve(o, [D, BT])
        qkv3, o = carve(o, [T, B, 3 * D])
        q3c, o = carve(o, [D, T])
        P1, o = carve(o, [T, S2])
        PT3, o = carve(o, [128, NCH, T])
        AT3, o = carve(o, [D, T])
        y3, o = carve(o, [T, D])
        st3, o = carve(o, [T, 64])
        assert o <= w3a_off(), o
        S_all, _ = carve(0, [128, 13, 4 * GROUP])
        sq = Psum[:, 0:1024]
        qnt = M[:, 0:800].rearrange("p (t q) -> p t q", t=8)
        n2 = sb("n2", [128, 16])
        rk = sb("rk", [128, 16])
        kbias = sb("kbias", [128, B, NCH])
        kbc = sb("kbc", [128, NCH + 1])
        kmask = sb("kmask", [128, B, NCH], U8)
        shift2 = mB[0:16, :]

        block = ctx.enter_context(nc.Block())

        def bank(i, parts, cols):
            return psum[0:parts, i, 0:cols]

        def slot(s, parts, cols):
            return psum[0:parts, 2 * s:2 * s + 2, 0:cols]

        def bc(v, shape, at):
            return v.unsqueeze(at).broadcast_to(shape)

        def ternary_hidden(bb):
            if bb < 4:
                return hid[0:T, :, :].rearrange("p a b -> p (a b)")[:, bb * 512:(bb + 1) * 512]
            return (g0, g1, g2, g3)[bb - 4][0:T, :]

        class Ring:
            def __init__(self, name, size, plan):
                while len(plan) % size:
                    plan = plan + ["none"]
                self.name, self.size, self.plan = name, size, plan
                self.full = sem(name + "_slot_full")
                self.emptied = {e: sem(f"{name}_slot_emptied_by_{e}") for e in ("act", "dve")}
                self.per = {e: plan.count(e) for e in ("act", "dve")}
                self.nfull = sum(p != "none" for p in plan)

            def before_fill(self, pe, b, n):
                m = n - self.size
                lap = 1 if m >= 0 else 0
                e = self.plan[m % len(self.plan)]
                if e == "none":
                    return
                k = self.plan[:m % len(self.plan) + 1].count(e)
                pe.wait_ge(self.emptied[e], (b + lap) * self.per[e] + k)

            def full_count(self, b, n):
                return b * self.nfull + n + 1

            def emptied_count(self, b, n):
                e = self.plan[n]
                return (b + 1) * self.per[e] + self.plan[:n + 1].count(e)

        def attention_order(layer):
            units = [("max", 0, u, "dve") for u in range(2 * NCH)]
            head = []
            if layer == 1:
                head = [("max", 1, 0, "dve"), ("max", 1, 1, "dve")]
                units[16:16] = [("exp", 1, 0, "act"), ("exp", 1, 1, "act")]
                units[8:8] = [("turn", 1, 0, "dve"), ("turn", 1, 1, "dve"), ("row", 1, 0, "dve")]
            return (head + units
                    + [("turn", 0, 0, "dve"), ("turn", 0, 1, "dve"), ("keys", 0, 0, "act"), ("keys", 0, 1, "act"),
                       ("row", 0, 0, "dve"), ("values", 0, 0, "dve"), ("values", 0, 1, "dve")]
                    + [("exp", 0, u, "act") for u in range(2 * NCH)])

        FINISH = [(1, 5, 9), (1, 4, 7, 10)]
        OWN_WEIGHED, OWN_TAKEN = 19, 22

        ORDER = [attention_order(0), attention_order(1)]

        def position(layer, kind, g, u):
            return [k[0:3] for k in ORDER[layer]].index((kind, g, u))

        rings = [Ring("a0", 3, [k[3] for k in ORDER[0]]), Ring("a1", 3, [k[3] for k in ORDER[1]]),
                 Ring("a2", 2, ["dve", "dve", "dve", "act", "act", "act"] + ["dve"] * 39 + ["dve"] * 3
                      + ["act"] * 2 + ["dve"] * 2 + ["act", "dve"]),
                 Ring("a3", 3, ["act", "act", "dve", "dve", "dve"])]

        @block.sync
        def _(sp):
            sp.dma_start(x[:, :, :], A["x"].rearrange("b t d -> t b d")).then_inc(sem("x_loaded"), 16)
            n = 0
            for tile, name in ((ident, "c_ident"), (identb, "c_identb"), (low_rows, "c_low_rows"),
                               (before, "c_before"), (gates, "gates")):
                sp.dma_start(tile[:, :], A[name]).then_inc(sem("constants_loaded"), 16)
            for name in W:
                t = W[name]
                sl = tuple(slice(None) for _ in t.shape)
                sp.dma_start(t[sl], A["w_" + name]).then_inc(sem("weights_loaded"), 16)
                n += 1
            sp.dma_start(maski.bitcast(I32).rearrange("p (c q) -> p c q", c=NCH)[0:CK, 0:NCH - 1, :],
                         A["mask0"][0:(NCH - 1) * CK, :].rearrange("(c p) q -> p c q", p=CK)
                         ).then_inc(sem("masks_loaded"), 16)
            sp.dma_start(maski.bitcast(I32).rearrange("p (c q) -> p c q", c=NCH)[0:LAST, NCH - 1, :],
                         A["mask0"][(NCH - 1) * CK:S2, :]).then_inc(sem("masks_loaded"), 16)
            sp.wait_ge(sem("key_mask_cleared"), 1)
            with nc.allow_non_contiguous_dma(reason="a small mask, keys onto partitions"):
                for bb in range(B):
                    sp.dma_start(kmask[0:CK, bb, 0:NCH - 1],
                                 A["mask2"][bb, 0:(NCH - 1) * CK].rearrange("(c p) -> p c", p=CK)
                                 ).then_inc(sem("masks_loaded"), 16)
                    sp.dma_start(kmask[0:LAST, bb, NCH - 1:NCH],
                                 A["mask2"][bb, (NCH - 1) * CK:S2].rearrange("(c p) -> p c", c=1)
                                 ).then_inc(sem("masks_loaded"), 16)

            def load_keys(b):
                sp.dma_start(ctxk[0:CK, 0:NCH - 1, :],
                             A["ctx"][b, 0:(NCH - 1) * CK, :].rearrange("(c p) d -> p c d", p=CK)
                             ).then_inc(sem("ctx_keys_loaded"), 16)
                sp.dma_start(ctxk[0:LAST, NCH - 1, :], A["ctx"][b, (NCH - 1) * CK:S2, :]
                             ).then_inc(sem("ctx_keys_loaded"), 16)

            def stack_keys(layer, b, half):
                k0, k1 = (0, 6 * CK) if half == 0 else (6 * CK, S2)
                for par in range(2):
                    for r, part in enumerate(KEY_PART):
                        sp.dma_start(keys_st[64 * par + 8 * r:64 * par + 8 * r + 8, :, k0:k1],
                                     kparts[64 * par:64 * par + 64, part, k0:k1]
                                     ).then_inc(sem(f"a{layer}_keys_stacked_{half}"), 16)

            def stack_tokens(dst, src, parts, first, signal):
                for par in range(2):
                    for r, part in enumerate(parts):
                        sp.dma_start(dst[64 * par + 8 * r:64 * par + 8 * r + 8, :, :],
                                     src[64 * par:64 * par + 64, part, :][:, bass.ds(first, T)]
                                     ).then_inc(sem(signal), 16)

            def count(v, top=1 << 20):
                return v if isinstance(v, int) else sp.snap(sp.to_reg(v), min_val=0, max_val=top)

            def place_shift(layer, g, this_one):
                dst = (q2, own_q2)[g]
                sp.wait_ge(sem(f"a{layer}_shift_ready_{g}"), this_one)
                for par in range(2):
                    sp.dma_start(dst[64 * par + 48:64 * par + 50, :, :], hl[16 * par:16 * par + 16, g, :]
                                 ).then_inc(sem(f"a{layer}_shift_placed_{g}"), 16)

            sp.dma_start(ctxT[:, :], A["ctxT"][0]).then_inc(sem("ctxT_loaded"), 16)
            for layer in (0, 1):
                ring = rings[layer]
                p = f"a{layer}_"
                if layer == 1:
                    sp.wait_ge(ring_before.full, ring_before.full_count(B - 1, position(0, "values", 0, 1)))
                    sp.dma_start(ctxT[:, :], A["ctxT"][0]).then_inc(sem("ctxT_loaded"), 16)
                ring_before = ring
                sp.wait_ge(sem(p + "first_projected"), 1)
                sp.dma_start(ctxT[:, :], A["ctxT"][1]).then_inc(sem("ctxT_loaded"), 16)
                sp.wait_ge(sem(p + "ones_set"), 1)
                sp.wait_ge(sem(p + "keys_split"), 1)
                stack_keys(layer, 0, 0)
                stack_keys(layer, 0, 1)
                sp.wait_ge(sem(p + "query_parts_ready"), 1)
                stack_tokens(q1, qparts, QUERY_PART, 0, p + "queries_stacked")
                if layer == 1:
                    stack_tokens(own_keys_st, own_kparts, KEY_PART, 0, p + "own_keys_stacked")

                def one_sequence(b, next_ctx):
                    this_one, next_one = count(b + 1), count(b + 2)
                    first = count((b + 1) * T, BT)
                    full = {k: count(ring.full_count(b, position(layer, *k)))
                            for k in [("values", 0, 1), ("exp", 0, NCH - 1), ("exp", 0, 2 * NCH - 1)]}
                    if layer == 1:
                        place_shift(1, 1, this_one)
                    place_shift(layer, 0, this_one)
                    sp.wait_ge(ring.full, full["values", 0, 1])
                    sp.dma_start(ctxT[:, :], A["ctxT"][next_ctx]).then_inc(sem("ctxT_loaded"), 16)
                    sp.wait_ge(sem(p + "queries_copied"), this_one)
                    stack_tokens(q1, qparts, QUERY_PART, first, p + "queries_stacked")
                    if layer == 1:
                        stack_tokens(own_keys_st, own_kparts, KEY_PART, first, p + "own_keys_stacked")
                    sp.wait_ge(sem(p + "keys_split"), next_one)
                    sp.wait_ge(ring.full, full["exp", 0, NCH - 1])
                    stack_keys(layer, b + 1, 0)
                    sp.wait_ge(ring.full, full["exp", 0, 2 * NCH - 1])
                    stack_keys(layer, b + 1, 1)

                with sp.Fori(0, B - 2) as b:
                    one_sequence(b, b + 2)
                one_sequence(B - 2, B - 1)
                if layer == 1:
                    place_shift(1, 1, B)
                place_shift(layer, 0, B)
            sp.wait_ge(sem("ctxk_cleared"), 1)
            load_keys(0)
            with sp.Fori(1, B) as b:
                sp.wait_ge(sem("a2_keys_used"), b)
                load_keys(b)
            sp.wait_ge(sem("a2_keys_used"), B)
            load_keys(0)
            sp.dma_start(ctxT[:, :], A["ctxT"][0]).then_inc(sem("ctxT_loaded"), 16)
            sp.wait_ge(sem("arena_free_for_experts"), 1)
            sp.dma_start(w3a, A["e_W1"]).then_inc(sem("experts_loaded"), 16)
            sp.dma_start(w3b, A["e_W2"]).then_inc(sem("experts_loaded"), 16)
            with sp.Fori(1, B) as b:
                sp.wait_ge(sem("a3_ctx_used"), b)
                load_keys(b)
                sp.dma_start(ctxT[:, :], A["ctxT"][b]).then_inc(sem("ctxT_loaded"), 16)
            sp.wait_ge(sem("y_ready"), 1)
            sp.dma_start(out.rearrange("b t d -> t b d"), x[:, :, :]).then_inc(sem("y_stored"), 16)
            sp.wait_ge(sem("y_stored"), 16)

        NW = len(W) * 16
        CTX_LOADS = B + 1

        @block.tensor
        def _(pe):
            def mm(o, l, r, start=True, stop=True, **k):
                return pe.matmul(o, l, r, start=start, stop=stop, skip_group_check=True, **k)

            def turn_xn(n):
                pe.wait_ge(sem("xn_ready"), n + 1)
                n = n if n < 4 else n - 1
                for half in range(2):
                    for i in range(4):
                        m = pe.transpose(bank(half, D, BANK)[:, i * T:(i + 1) * T], xn[:, 4 * half + i, :],
                                         ident[0:T, 0:T])
                    m.then_inc(sem("xnT_in_psum"), 1)
                pe.wait_ge(sem("xnT_ready"), 2 * n + 2)

            def project(first, w, ws, signal):
                for half in range(2):
                    m = mm(bank(first + half, ws, HALF), w, xnT[:, half * HALF:(half + 1) * HALF])
                m.then_inc(sem(signal), 1)

            def attention(layer):
                ring = rings[layer]
                wk, wv = (W["k0"], W["v0"]) if layer == 0 else (W["ka1"], W["va1"])
                wo = W["o0"] if layer == 0 else W["o1"]
                bo = W["bo0"] if layer == 0 else W["bo1"]
                p = f"a{layer}_"
                pe.wait_ge(sem("ctxT_loaded"), 16 * CTX_LOADS * layer + 16)
                for i in range(4):
                    m = mm(bank(i, D, KQ), wk[:, :], ctxT[:, i * KQ:(i + 1) * KQ])
                m.then_inc(sem(p + "first_keys"), 1)
                for c in range(NCH):
                    if c == 8:
                        pe.wait_ge(sem(p + "key_parts_1"), 1)
                    bk = (4, 5, 0)[c // 4]
                    m = mm(bank(bk, ROWS[c], BANK)[:, (c % 4) * D:(c % 4 + 1) * D],
                           ctxT[:, c * CK:c * CK + ROWS[c]], wv[:, :])
                m.then_inc(sem(p + "first_projected"), 1)
                pe.wait_ge(sem(p + "values_turned"), 1)
                nf = 3 + layer

                def finish(b, k):
                    pe.wait_ge(sem(p + "heads_by_dve"), b * nf + k + 1)
                    if k == 0:
                        pe.wait_ge(sem(p + "sums_copied"), (layer + 1) * b + 1)
                    if k < layer + 1:
                        for j in range(4):
                            m = pe.transpose(bank(7, T, BANK)[:, j * 128:(j + 1) * 128],
                                             (summed, own_summed)[k][:, j * T:(j + 1) * T], ident[:, :])
                    elif k == layer + 1:
                        m = pe.transpose(bank(7, D, T), heads[:, :], ident[0:T, 0:T])
                    else:
                        mm(bank(7, T, D), headsT[:, :], wo[:, :], stop=False)
                        m = mm(bank(7, T, D), ones[0:1, 0:T], bo[0:1, :], start=False)
                    m.then_inc(sem(p + "heads_by_pe"), 1)

                with pe.Fori(0, B) as b:
                    def scores(n, g, u, rows_q, q, signal=True):
                        s = n % 3
                        c, hh = u // 2, u % 2
                        r = ROWS[c] if g == 0 else T
                        kst = keys_st if g == 0 else own_keys_st
                        masked = layer == 0
                        if masked:
                            for par in range(2):
                                mm(bank(2 * s + par, r, GROUP), identb[0:r, 0:r],
                                   bc(maskb[0:r, c, :], [r, 4, T], 1), stop=False)
                        for t in range(4):
                            for par in range(2):
                                hp = 4 * hh + t
                                m = mm(bank(2 * s + par, r, GROUP)[:, t * T:(t + 1) * T],
                                       kst[64 * par:64 * par + rows_q, hp, c * CK:c * CK + r],
                                       q[64 * par:64 * par + rows_q, hp, :], start=not masked)
                        m.then_inc(ring.full, 1)

                    def weigh(g, w, done):
                        c, hh = w // 2, w % 2
                        r = ROWS[c] if g == 0 else T
                        size = NCH if g == 0 else 1
                        pe.wait_ge(ring.emptied["act"], ring.emptied_count(b, position(layer, "exp", g, w)))
                        if w == 0:
                            pe.wait_ge(sem(p + "values_placed"), b + 1)
                            if g == 0:
                                pe.wait_ge(sem(p + "sums_copied"), (layer + 1) * b + 1)
                            else:
                                pe.wait_ge(sem(p + "heads_by_dve"), (b + 1) * nf + 1)
                        for par in range(2):
                            for t in range(4):
                                h = 8 * hh + 2 * t + par
                                k = par * GROUP + t * T
                                col = (2 * hh + par) * T
                                m = mm(psum[32 * t:32 * t + 9, 6 + g, col:col + T],
                                       Vo[0:r, c, h, :] if g == 0 else own_Vo[0:r, h, :],
                                       P3[0:r, done % 3, k:k + T],
                                       start=(c, hh, par) == (0, 0, 0), stop=c == size - 1)
                        m.then_inc(sem(p + "probs_used"), 1)

                    done = 0
                    for n, (kind, g, u, _) in enumerate(ORDER[layer]):
                        s = n % 3
                        ring.before_fill(pe, b, n)
                        if kind == "max":
                            if g == 1 and u == 0:
                                pe.wait_ge(sem(p + "own_keys_stacked"), 16 * 12 * (b + 1))
                            if (g, u) == ((0, 0) if layer == 0 else (1, 0)):
                                pe.wait_ge(sem(p + "queries_stacked"), 16 * 12 * (b + 1))
                            if g == 0 and u in (0, NCH):
                                pe.wait_ge(sem(p + f"keys_stacked_{u // NCH}"), 16 * 12 * (b + 1))
                            scores(n, g, u, 48, q1)
                            if g == 0 and u in FINISH[layer]:
                                finish(b, FINISH[layer].index(u))
                            if layer == 1 and g == 0 and u == OWN_WEIGHED:
                                for w in range(2):
                                    weigh(1, w, done)
                                    done += 1
                        elif kind == "turn":
                            r = CK if g == 0 else T
                            src = M if g == 0 else own_M
                            if u == 0:
                                last = 2 * NCH - 1 if g == 0 else 1
                                pe.wait_ge(ring.emptied["dve"], ring.emptied_count(b, position(layer, "max", g, last)))
                            for k in range(8):
                                h = 8 * u + k
                                m = pe.transpose(bank(2 * s + k // 4, T, BANK)[:, (k % 4) * CK:(k % 4) * CK + r],
                                                 src[0:r, h * T:(h + 1) * T], ident[0:r, 0:r])
                            m.then_inc(ring.full, 1)
                        elif kind == "row":
                            pe.wait_ge(sem(p + f"max_ready_{g}"), b + 1)
                            pe.transpose(bank(2 * s, 32, T), mx[:, g, :], ident[0:T, 0:T]).then_inc(ring.full, 1)
                        elif kind == "keys":
                            if u == 0:
                                pe.wait_ge(sem("ctxT_loaded"), 16 * CTX_LOADS * layer + 16 * b + 32)
                            for i in range(2):
                                c0 = (2 * u + i) * KQ
                                m = mm(bank(2 * s + i, D, KQ), wk[:, :], ctxT[:, c0:c0 + KQ])
                            m.then_inc(ring.full, 1)
                        elif kind == "values":
                            for k, c in enumerate(range(8) if u == 0 else range(8, NCH)):
                                m = mm(bank(2 * s + k // 4, ROWS[c], BANK)[:, (k % 4) * D:(k % 4 + 1) * D],
                                       ctxT[:, c * CK:c * CK + ROWS[c]], wv[:, :])
                            m.then_inc(ring.full, 1)
                        else:
                            if u == 0:
                                pe.wait_ge(sem(p + "queries_copied"), b + 1)
                                pe.wait_ge(sem(p + f"shift_placed_{g}"), 32 * (b + 1))
                            scores(n, g, u, 50, (q2, own_q2)[g])
                            if g == 0 and u >= 2:
                                weigh(g, u - 2, done)
                                done += 1
                            if g == 0 and u == 2 * NCH - 1:
                                for w in (u - 1, u):
                                    weigh(g, w, done)
                                    done += 1
                for k in range(nf):
                    finish(B, k)

            pe.wait_ge(sem("constants_loaded"), 5 * 16)
            pe.wait_ge(sem("weights_loaded"), NW)
            turn_xn(0)
            project(2, W["q0"][:, :], D, "q0_projected")
            pe.wait_ge(sem("layer0_setup"), 1)
            attention(0)
            turn_xn(1)
            project(2, wr_bc[:, :], T, "router_scores")
            for k in range(8):
                f, half = k // 2, k % 2
                if k >= 4:
                    pe.wait_ge(sem("ffn0_hidden"), k - 3)
                mm(bank(4 + k % 4, 128, HALF), W["f0W1"][:, f * 128:(f + 1) * 128],
                   xnT[:, half * HALF:(half + 1) * HALF]).then_inc(sem("ffn0_hidden_psum"), 1)
            pe.wait_ge(sem("ffn0_hidden"), 8)
            for bb in range(B):
                o = bank(bb // 4, T, BANK)[:, (bb % 4) * D:(bb % 4 + 1) * D]
                for f in range(4):
                    mm(o, hid[:, f, bb * T:(bb + 1) * T], W["f0W2"][:, f, :], start=f == 0, stop=False)
                m = mm(o, ones[0:1, 0:T], W["f0b2"][0:1, :], start=False)
            m.then_inc(sem("ffn0_out"), 1)
            turn_xn(2)
            project(2, W["q1"][:, :], D, "q1_projected")
            project(4, W["k1"][:, :], D, "k1_projected")
            for bb in range(B):
                m = mm(bank(6 + bb // 4, T, BANK)[:, (bb % 4) * D:(bb % 4 + 1) * D],
                       xnT[:, bb * T:(bb + 1) * T], W["v1"][:, :])
            m.then_inc(sem("v1_projected"), 1)
            pe.wait_ge(sem("layer1_setup"), 1)
            attention(1)
            turn_xn(3)
            pe.wait_ge(sem("slots_by_dve"), STEP["slots_scaled"])
            mm(bank(2, D, 1), g0[0:NSLOT, 0:D], ones[0:NSLOT, 0:1])
            pe.transpose(bank(3, D, NSLOT), g0[0:NSLOT, 0:D], ident[0:NSLOT, 0:NSLOT]).then_inc(sem("slots_by_pe"), 1)
            pe.wait_ge(sem("slots_by_dve"), STEP["slot_mean"])
            mm(bank(2, NSLOT, 1), W["f1w1b"][:, :], small[:, 8:9]).then_inc(sem("slots_by_pe"), 1)
            for half in range(2):
                m = mm(bank(4 + half, NSLOT, HALF), W["f1w1a"][:, :], xnT[:, half * HALF:(half + 1) * HALF])
            m.then_inc(sem("slots_by_pe"), 1)
            pe.wait_ge(sem("f1_hidden"), 2)
            for bb in range(B):
                m = mm(bank(6, T, BANK)[:, bb * NSLOT:(bb + 1) * NSLOT], hid[0:NSLOT, 0, bb * T:(bb + 1) * T],
                       W["f1w2"][:, :])
            m.then_inc(sem("slots_by_pe"), 1)
            pe.wait_ge(sem("slots_by_dve"), STEP["slotsT_ready"])
            for g in range(3):
                m = mm(bank(7, D, 3 * NSLOT)[:, g * NSLOT:(g + 1) * NSLOT], W["f1whh"][:, g * D:(g + 1) * D],
                       g1[:, 0:NSLOT])
            m.then_inc(sem("slots_by_pe"), 1)
            pe.wait_ge(sem("slots_by_dve"), STEP["alpha_ready"])
            for bb in range(B):
                al = big1[0:T, bb * NSLOT:(bb + 1) * NSLOT]
                mm(bank(0, D, BANK)[:, bb * NSLOT:(bb + 1) * NSLOT], xn[:, bb, :], al)
            mm(bank(1, D, BANK), ones[0:T, :], big1[0:T, 0:B * NSLOT]).then_inc(sem("slots_by_pe"), 1)
            for bb in range(B):
                m = pe.transpose(bank(4 + bb // 4, NSLOT, BANK)[:, (bb % 4) * T:(bb % 4 + 1) * T],
                                 big1[0:T, bb * NSLOT:(bb + 1) * NSLOT], ident[0:T, 0:T])
            m.then_inc(sem("slots_by_pe"), 1)
            pe.wait_ge(sem("slots_by_dve"), STEP["gi_ready"])
            for g, bk in enumerate((2, 3, 6)):
                m = mm(bank(bk, D, BANK), W["f1wih"][:, g * D:(g + 1) * D], g3[:, :])
            m.then_inc(sem("slots_by_pe"), 1)
            pe.wait_ge(sem("slots_by_dve"), STEP["slots_new"])
            mm(bank(0, D, BANK), W["f1wv"][:, :], g2[:, :]).then_inc(sem("slots_by_pe"), 1)
            pe.wait_ge(sem("slots_by_act"), STEP["slot_values"])
            for bb in range(B):
                m = mm(bank(2 + bb // 4, NSLOT, BANK)[:, (bb % 4) * D:(bb % 4 + 1) * D],
                       g3[:, bb * NSLOT:(bb + 1) * NSLOT], W["f1wo"][:, :])
            m.then_inc(sem("slots_by_pe"), 1)
            pe.wait_ge(sem("slots_by_act"), STEP["slot_outputs"])
            for bb in range(B):
                o = bank(6 + bb // 4, T, BANK)[:, (bb % 4) * D:(bb % 4 + 1) * D]
                mm(o, hid[0:NSLOT, 1, bb * T:(bb + 1) * T], big2[0:NSLOT, bb * D:(bb + 1) * D], stop=False)
                m = mm(o, ones[0:1, 0:T], W["f1bo"][0:1, :], start=False)
            m.then_inc(sem("ffn1_out"), 1)
            ring = rings[2]
            with pe.Fori(0, B) as b:
                def fill(n):
                    ring.before_fill(pe, b, n)
                    return n % 2

                def filled(m):
                    m.then_inc(ring.full, 1)

                rows = ROWS + [T]
                pe.wait_ge(sem("a2_keys_normalised"), b + 1)
                for half, chunks in enumerate((range(0, 8), range(8, 13))):
                    s = fill(half)
                    for k, c in enumerate(chunks):
                        m = pe.transpose(bank(2 * s + k // 4, D, BANK)[:, (k % 4) * CK:(k % 4) * CK + rows[c]]
                                         if k < 4 or half == 0 else bank(2 * s + 1, D, T),
                                         ctxk[0:rows[c], c, :], ident[0:rows[c], 0:rows[c]])
                    filled(m)
                pe.wait_ge(ring.emptied["dve"], ring.emptied_count(b, 1))
                s = fill(2)
                for i in range(2):
                    m = mm(bank(2 * s + i, T, BANK), xkT[:, S2:S2 + T], W["q2"][:, i * BANK:(i + 1) * BANK])
                filled(m)
                pe.wait_ge(sem("a2_q_normalised"), b + 1)
                s = fill(3)
                for t in range(8):
                    m = pe.transpose(bank(2 * s + t // 4, D, BANK)[:, (t % 4) * T:(t % 4 + 1) * T],
                                     Psum[0:T, t * D:(t + 1) * D], ident[0:T, 0:T])
                filled(m)
                pe.wait_ge(ring.emptied["act"], ring.emptied_count(b, 3))
                for half in range(2):
                    s = fill(4 + half)
                    for t in range(4):
                        for par in range(2):
                            tt = 4 * half + t
                            m = mm(bank(2 * s + par, D, BANK)[:, t * T:(t + 1) * T],
                                   W["k2T"][64 * par:64 * par + 64, tt, :], qnt[64 * par:64 * par + 64, tt, :])
                    filled(m)
                pe.wait_ge(ring.emptied["act"], ring.emptied_count(b, 5))
                n = 6
                for c in range(13):
                    r = rows[c]
                    s = fill(n)
                    for i in range(2):
                        m = mm(bank(2 * s + i, r, BANK), xkT[:, min(c * CK, S2):min(c * CK, S2) + r],
                               W["kv2"][:, i * BANK:(i + 1) * BANK])
                    filled(m)
                    n += 1
                    for half in range(2):
                        s = fill(n)
                        for i in range(2):
                            j = 2 * half + i
                            m = mm(bank(2 * s + i, r, GROUP), xkT[:, min(c * CK, S2):min(c * CK, S2) + r], qeff[:, 4 * j:4 * j + 4, :])
                        filled(m)
                        n += 1
                pe.wait_ge(sem("a2_column_max"), b + 1)
                for half in range(2):
                    s = fill(n)
                    for k in range(8):
                        h = 8 * half + k
                        m = pe.transpose(bank(2 * s + k // 4, T, BANK)[:, (k % 4) * CK:(k % 4 + 1) * CK],
                                         M[0:CK, h * T:(h + 1) * T], ident[0:CK, 0:CK])
                    filled(m)
                    n += 1
                s = fill(n)
                pe.wait_ge(sem("a2_max_ready"), b + 1)
                filled(pe.transpose(bank(2 * s, 16, T), stat[0:T, 0, 0:16], ident[0:T, 0:T]))
                n += 1
                pe.wait_ge(sem("a2_shift_ready"), b + 1)
                for half in range(2):
                    s = fill(n)
                    for i in range(2):
                        j = 2 * half + i
                        m = mm(bank(2 * s + i, 128, GROUP), ones[0:16, :], M[0:16, j * GROUP:(j + 1) * GROUP])
                    filled(m)
                    n += 1
                for c in range(13):
                    r = rows[c]
                    pe.wait_ge(sem("a2_probs_ready"), b * 13 + c + 1)
                    if c == 0:
                        pe.wait_ge(sem("a2_context_normalised"), b + 1)
                    for j in range(4):
                        m = mm(bank(4 + j, D, GROUP), ctxk[0:r, c, :], S_all[0:r, c, j * GROUP:(j + 1) * GROUP],
                               start=c == 0, stop=c == 12)
                m.then_inc(sem("a2_keys_used"), 1)
                pe.wait_ge(sem("a2_sum_step"), b * 12 + 12)
                for half in range(2):
                    s = fill(n)
                    for i in range(2):
                        j = 2 * half + i
                        m = mm(bank(2 * s + i, 128, GROUP), ones[0:CK, :], Psum[0:CK, j * GROUP:(j + 1) * GROUP])
                    filled(m)
                    n += 1
                pe.wait_ge(sem("a2_context_normalised"), b + 2)
                s = fill(n)
                for t in range(8):
                    for par in range(2):
                        h = 2 * t + par
                        m = mm(psum[64 * par:64 * par + 64, 2 * s + t // 4, (t % 4) * T:(t % 4 + 1) * T],
                               W["kv2"][:, 1024 + 64 * h:1024 + 64 * h + 64], mB[:, h * T:(h + 1) * T])
                filled(m)
                n += 1
                pe.wait_ge(ring.emptied["act"], ring.emptied_count(b, n - 1))
                s = fill(n)
                for t in range(8):
                    mm(bank(2 * s, T, D), qnt[:, t, :], W["out2"][:, t, :], start=t == 0, stop=False)
                filled(mm(bank(2 * s, T, D), ones[0:1, 0:T], W["bo2"][0:1, :], start=False))
                assert n + 1 == ring.nfull
            pe.wait_ge(sem("ternary_sums"), 1)
            mm(bank(2, 128, 2), ones[:, :], small[:, 16:18]).then_inc(sem("ternary_scale"), 1)
            turn_xn(5)
            pe.wait_ge(sem("ternary_ready"), 1)
            for bb in range(B):
                if bb >= 2:
                    pe.wait_ge(sem("f2_gelu"), bb - 1)
                mm(bank(2 + bb % 2, T, BANK), xnT[:, bb * T:(bb + 1) * T], W["f2fc"][:, :]
                   ).then_inc(sem("f2_hidden_psum"), 1)
            for bb in range(B):
                pe.wait_ge(sem("f2_normalised"), bb + 1)
                if bb >= 2:
                    pe.wait_ge(sem("f2_turned"), bb - 1)
                for f in range(4):
                    m = pe.transpose(bank(4 + bb % 2, 128, BANK)[:, f * T:(f + 1) * T],
                                     big1[0:T, (bb % 2) * 512 + f * 128:(bb % 2) * 512 + (f + 1) * 128],
                                     ident[0:T, 0:T])
                m.then_inc(sem("f2_turned_psum"), 1)
                pe.wait_ge(sem("f2_turned"), bb + 1)
                o = bank(6 + bb // 4, T, BANK)[:, (bb % 4) * D:(bb % 4 + 1) * D]
                for f in range(4):
                    m = mm(o, big2[:, (bb % 2) * 400 + f * T:(bb % 2) * 400 + (f + 1) * T], W["f2proj"][:, f, :],
                           start=f == 0, stop=f == 3)
            m.then_inc(sem("ffn2_out"), 1)
            turn_xn(6)
            project(2, W["qkv3"][:, 0:D], D, "q3T_psum")
            for bb in range(B):
                if bb >= 4:
                    pe.wait_ge(sem("qkv3_ready"), bb - 3)
                mm(bank(4 + bb % 4, T, 3 * D), xnT[:, bb * T:(bb + 1) * T], W["qkv3"][:, :]
                   ).then_inc(sem("qkv3_psum"), 1)
            pe.wait_ge(sem("q3T_ready"), 1)
            for half in range(2):
                m = mm(bank(half, D, HALF), W["k3T"][:, :], q3T[:, half * HALF:(half + 1) * HALF])
            m.then_inc(sem("qe3_psum"), 1)
            pe.wait_ge(sem("layer3_setup"), 1)
            ring = rings[3]
            with pe.Fori(0, B) as b:
                pe.wait_ge(sem("ctxT_loaded"), 32 * CTX_LOADS + 16 * b + 16)
                pe.wait_ge(sem("ctx_keys_loaded"), 32 * B + 32 * b + 32)
                pe.wait_ge(sem("a3_query_placed"), b + 1)
                for half in range(2):
                    ring.before_fill(pe, b, half)
                    for i in range(2):
                        c0 = (2 * half + i) * KQ
                        m = mm(bank(2 * half + i, T, KQ), q3c[:, :], ctxT[:, c0:c0 + KQ])
                    m.then_inc(ring.full, 1)
                pe.wait_ge(ring.emptied["act"], ring.emptied_count(b, 1))
                for half, chunks in enumerate((range(0, 8), range(8, NCH))):
                    ring.before_fill(pe, b, 2 + half)
                    s = (2 + half) % 3
                    for k, c in enumerate(chunks):
                        m = pe.transpose(bank(2 * s + k // 4, ROWS[c], BANK)[:, (k % 4) * T:(k % 4 + 1) * T],
                                         P1[:, c * CK:c * CK + ROWS[c]], ident[0:T, 0:T])
                    m.then_inc(ring.full, 1)
                pe.wait_ge(ring.emptied["dve"], ring.emptied_count(b, 3))
                for c in range(NCH):
                    m = mm(bank(6, D, T), ctxk[0:ROWS[c], c, :], PT3[0:ROWS[c], c, :], start=c == 0, stop=c == NCH - 1)
                m.then_inc(sem("a3_ctx_used"), 1)
                pe.wait_ge(sem("a3_context_copied"), b + 1)
                ring.before_fill(pe, b, 4)
                mm(bank(2, T, D), AT3[:, :], W["qkv3"][:, 2 * D:3 * D]).then_inc(ring.full, 1)
            turn_xn(7)
            pe.wait_ge(sem("experts_by_dve"), STEP["experts_normalised"])
            pe.transpose(bank(2, D, E3), g0[0:E3, 0:D], ident[0:E3, 0:E3]).then_inc(sem("experts_by_pe"), 1)
            pe.wait_ge(sem("experts_by_dve"), STEP["expert_columns"])
            for bb in range(B):
                m = mm(bank(3, T, 128)[:, bb * 16:(bb + 1) * 16], xnT[:, bb * T:(bb + 1) * T], g1[:, 0:16])
            m.then_inc(sem("experts_by_pe"), 1)
            pe.wait_ge(sem("experts_by_dve"), STEP["expert_weights"])
            for bb in range(B):
                m = pe.transpose(bank(bb // 4, E3, BANK)[:, (bb % 4) * T:(bb % 4 + 1) * T],
                                 g2[0:T, bb * E3:(bb + 1) * E3], ident[0:T, 0:T])
            m.then_inc(sem("experts_by_pe"), 1)
            pe.wait_ge(sem("experts_by_act"), STEP["expert_weights_turned"])
            for bb in range(B):
                m = mm(bank(2 + bb // 4, T, BANK)[:, (bb % 4) * D:(bb % 4 + 1) * D],
                       big2[0:E3, bb * T:(bb + 1) * T],
                       W["f3b2"][:, :])
            m.then_inc(sem("experts_by_pe"), 1)
            pe.wait_ge(sem("experts_loaded"), 32)
            pe.wait_ge(sem("experts_by_dve"), STEP["expert_biases_taken"])
            for e in range(E3):
                for k in range(8):
                    f, half = k // 2, k % 2
                    q = 8 * e + k
                    if q >= 4:
                        pe.wait_ge(sem("f3_gelu"), q - 3)
                    mm(bank(4 + q % 4, 128, HALF), w3a[:, e, f * 128:(f + 1) * 128],
                       xnT[:, half * HALF:(half + 1) * HALF]).then_inc(sem("f3_hidden_psum"), 1)
                pe.wait_ge(sem("f3_gelu"), 8 * e + 8)
                if e >= 2:
                    pe.wait_ge(sem("f3_accumulated"), 2 * (e - 1))
                for bb in range(B):
                    o = bank(2 * (e % 2) + bb // 4, T, BANK)[:, (bb % 4) * D:(bb % 4 + 1) * D]
                    for f in range(4):
                        m = mm(o, hid[:, f, bb * T:(bb + 1) * T], w3b[:, e, f, :], start=f == 0, stop=f == 3)
                m.then_inc(sem("f3_out"), 1)

        @block.scalar
        def _(act):
            own = [0]

            def link(i):
                own[0] += 1
                i.then_inc(sem("act_step"), 1)
                act.wait_ge(sem("act_step"), own[0])

            rooted = [0]

            def take_roots(dst, src):
                rooted[0] += 1
                act.wait_ge(sem("variances_ready"), rooted[0])
                act.activation(dst, src, ACT.Sqrt).then_inc(sem("deviations_ready"), 1)

            def root_of_rows():
                take_roots(stat[0:T, 4, 0:8], stat[0:T, 3, 0:8])

            def turned(n):
                root_of_rows()
                n = n if n < 4 else n - 1
                for half in range(2):
                    act.wait_ge(sem("xnT_in_psum"), 2 * n + half + 1)
                    act.copy(xnT[:, half * HALF:(half + 1) * HALF], bank(half, D, HALF)
                             ).then_inc(sem("xnT_ready"), 1)

            act.wait_ge(sem("constants_loaded"), 5 * 16)
            act.wait_ge(sem("weights_loaded"), NW)
            act.activation(gates[:, :], gates[:, :], ACT.Tanh).then_inc(sem("gates_ready"), 1)
            act.activation(small[:, 24:25], W["g1"][:, :], ACT.Exp, scale=-1.0)
            act.activation(head_gates[:, 0, :], W["g1heads"][:, :], ACT.Exp, scale=-1.0
                           ).then_inc(sem("head_gate_exp"), 1)

            def attention(layer):
                ring = rings[layer]
                p = f"a{layer}_"
                bk = W["bk0"] if layer == 0 else W["bka1"]

                def copy_keys(half, s, last):
                    k0, k1 = half * 2 * KQ, (half + 1) * 2 * KQ
                    act.activation(kf[:, k0:k1].rearrange("p (a k) -> p a k", a=2), slot(s, D, KQ), ACT.Identity,
                                   bias=bk[:, 0:1])
                    return act.activation(kparts[:, 0, k0:k1].rearrange("p (a k) -> p a k", a=2), slot(s, D, KQ),
                                          ACT.Identity, bias=bk[:, 0:1])

                def second_part(count):
                    act.wait_ge(sem(p + "keys_rest"), count)
                    act.copy(kparts[:, 1, :], kr).then_inc(sem(p + "key_parts_2"), 1)

                act.wait_ge(sem(p + "first_keys"), 1)
                act.wait_ge(sem(p + "query_parts_ready"), 1)
                copy_keys(0, 0, False)
                copy_keys(1, 1, True).then_inc(sem(p + "key_parts_1"), 1)
                second_part(1)
                act.sem_inc(ring.emptied["act"], ring.per["act"])
                act.sem_inc(sem(p + "probs_used"), 3)
                per = 2 * NCH + 2 * layer
                with act.Fori(0, B) as b:
                    act.wait_ge(sem(p + "queries_stacked"), 16 * 12 * (b + 1))
                    for dst in (q2, own_q2)[0:layer + 1]:
                        for par in range(2):
                            i = act.copy(dst[64 * par:64 * par + 48, :, :], q1[64 * par:64 * par + 48, :, :])
                    i.then_inc(sem(p + "queries_copied"), 1)
                    act.wait_ge(sem(p + "probs_used"), b * per + 3)
                    act.wait_ge(sem(p + "values_turned"), b + 1)
                    act.copy(Vo[:, :, :, 0:8], Vn.rearrange("p c (h d) -> p c h d", h=H)
                             ).then_inc(sem(p + "values_placed"), 1)
                    done = 0
                    for n, (kind, g, u, _) in enumerate(ORDER[layer]):
                        if kind == "keys":
                            act.wait_ge(ring.full, ring.full_count(b, n))
                            copy_keys(u, n % 3, u == 1).then_inc(ring.emptied["act"], 1)
                        if kind == "exp":
                            r = ROWS[u // 2] if g == 0 else T
                            act.wait_ge(ring.full, ring.full_count(b, n))
                            if done >= 3:
                                act.wait_ge(sem(p + "probs_used"), b * per + done + 1)
                            act.activation(P3[0:r, done % 3, :].rearrange("p (a k) -> p a k", a=2),
                                           slot(n % 3, r, GROUP), ACT.Exp).then_inc(ring.emptied["act"], 1)
                            done += 1
                            if g == 0 and u == 5:
                                second_part(b + 2)

            turned(0)
            attention(0)
            turned(1)
            act.wait_ge(sem("router_columns"), 1)
            act.activation(small[0:T, 0:8], stat[0:T, 0, 0:8], ACT.Exp, scale=-1.0).then_inc(sem("router_exp"), 1)
            for k in range(8):
                f, half = k // 2, k % 2
                act.wait_ge(sem("ffn0_hidden_psum"), k + 1)
                act.activation(hid[:, f, half * HALF:(half + 1) * HALF], bank(4 + k % 4, 128, HALF),
                               ACT.Gelu_apprx_tanh, bias=W["f0b1"][:, f:f + 1]).then_inc(sem("ffn0_hidden"), 1)
            turned(2)
            act.wait_ge(sem("k1_projected"), 1)
            act.wait_ge(sem("q1_split"), 1)
            act.activation(qf.rearrange("p (a k) -> p a k", a=2), slot(2, D, HALF), ACT.Identity,
                           bias=W["bk1"][:, 0:1]).then_inc(sem("k1_ready"), 1)
            attention(1)
            turned(3)
            act.wait_ge(sem("slots_by_dve"), STEP["slot_bias"])
            act.wait_ge(sem("slots_by_pe"), STEP["f1_hidden_psum"])
            for half in range(2):
                act.activation(hid[0:NSLOT, 0, half * HALF:(half + 1) * HALF], bank(4 + half, NSLOT, HALF),
                               ACT.Gelu, bias=small[0:NSLOT, 10:11]).then_inc(sem("f1_hidden"), 1)
            act.wait_ge(sem("slots_by_dve"), STEP["logits_shifted"])
            act.activation(big2[0:T, 0:512], big2[0:T, 0:512], ACT.Exp).then_inc(sem("slots_by_act"), 1)
            act.wait_ge(sem("slots_by_pe"), STEP["alpha_turned"])
            act.copy(hid[0:NSLOT, 1, :].rearrange("p (a k) -> p a k", a=2), slot(2, NSLOT, HALF)
                     ).then_inc(sem("slots_by_act"), 1)
            act.wait_ge(sem("slots_by_dve"), STEP["gate_r_sum"])
            act.activation(g0[:, :], g0[:, :], ACT.Exp, scale=-1.0).then_inc(sem("slots_by_act"), 1)
            act.wait_ge(sem("slots_by_dve"), STEP["gate_z_sum"])
            act.activation(big3[:, 0:512], big3[:, 0:512], ACT.Exp, scale=-1.0).then_inc(sem("slots_by_act"), 1)
            act.wait_ge(sem("slots_by_dve"), STEP["gate_n_sum"])
            act.activation(g3[:, :], g3[:, :], ACT.Tanh).then_inc(sem("slots_by_act"), 1)
            act.wait_ge(sem("slots_by_pe"), STEP["slot_values_psum"])
            act.activation(g3[:, :], bank(0, D, BANK), ACT.Identity, bias=W["f1bv"][:, 0:1]
                           ).then_inc(sem("slots_by_act"), 1)
            act.wait_ge(sem("slots_by_pe"), STEP["slot_outputs_psum"])
            act.copy(big2[0:NSLOT, :].rearrange("p (a k) -> p a k", a=2), slot(1, NSLOT, BANK)
                     ).then_inc(sem("slots_by_act"), 1)
            ring = rings[2]
            root_of_rows()
            root_of_rows()
            act.wait_ge(sem("latents_ready"), 1)
            act.sem_inc(ring.emptied["act"], ring.per["act"])
            with act.Fori(0, B) as b:
                act.wait_ge(sem("a2_variances"), b + 1)
                act.activation(stat[:, 1, 0:NCH], stat[:, 1, 0:NCH], ACT.Sqrt).then_inc(sem("a2_deviations"), 1)

                def vector_norms(r, c):
                    act.wait_ge(sem("a2_squares_summed"), b * 14 + c + 1)
                    act.activation(n2[0:r, :], n2[0:r, :], ACT.Sqrt).then_inc(sem("a2_norms"), 1)

                act.wait_ge(ring.full, ring.full_count(b, 2))
                act.activation(sq[0:T, :].rearrange("p (a k) -> p a k", a=2), slot(0, T, BANK), ACT.Square
                               ).then_inc(sem("a2_squares"), 1)
                vector_norms(T, 0)
                act.wait_ge(ring.full, ring.full_count(b, 3))
                act.activation(M[:, 0:800].rearrange("p (a k) -> p a k", a=2), slot(1, D, HALF), ACT.Copy,
                               scale=small[:, 30:31]).then_inc(ring.emptied["act"], 1)
                for half in range(2):
                    act.wait_ge(ring.full, ring.full_count(b, 4 + half))
                    act.copy(qeff[:, 8 * half:8 * half + 8, :].rearrange("p (t a) q -> p a t q", a=2),
                             slot(half, D, GROUP).rearrange("p a (t q) -> p a t q", t=4)
                             ).then_inc(ring.emptied["act"], 1)
                n = 6
                for c in range(13):
                    r = (ROWS + [T])[c]
                    act.wait_ge(ring.full, ring.full_count(b, n))
                    act.activation(sq[0:r, :].rearrange("p (a k) -> p a k", a=2), slot(n % 2, r, BANK), ACT.Square
                                   ).then_inc(sem("a2_squares"), 1)
                    vector_norms(r, c + 1)
                    n += 3
                n += 3
                for half in range(2):
                    act.wait_ge(ring.full, ring.full_count(b, n))
                    act.copy(mB[:, 2 * half * GROUP:(2 * half + 2) * GROUP].rearrange("p (a k) -> p a k", a=2),
                             slot(n % 2, 128, GROUP)).then_inc(ring.emptied["act"], 1)
                    n += 1
                for c in range(13):
                    r = (ROWS + [T])[c]
                    act.wait_ge(sem("a2_scores_shifted"), b * 13 + c + 1)
                    act.activation(S_all[0:r, c, :], S_all[0:r, c, :], ACT.Exp, bias=kbc[0:r, c:c + 1]
                                   ).then_inc(sem("a2_probs_ready"), 1)
                n += 2
                act.wait_ge(ring.full, ring.full_count(b, n))
                act.copy(M[:, 0:800].rearrange("p (a k) -> p a k", a=2), slot(n % 2, 128, GROUP)
                         ).then_inc(ring.emptied["act"], 1)
            turned(5)
            for bb in range(B):
                act.wait_ge(sem("f2_hidden_psum"), bb + 1)
                act.activation(ternary_hidden(bb), bank(2 + bb % 2, T, BANK), ACT.Gelu).then_inc(sem("f2_gelu"), 1)
            root_of_rows()
            for bb in range(B):
                act.wait_ge(sem("f2_turned_psum"), bb + 1)
                act.copy(big2[:, (bb % 2) * 400:(bb % 2) * 400 + 400], bank(4 + bb % 2, 128, 4 * T)
                         ).then_inc(sem("f2_turned"), 1)
            turned(6)
            act.wait_ge(sem("q3T_psum"), 1)
            act.activation(q3T[:, :].rearrange("p (a k) -> p a k", a=2), slot(1, D, HALF), ACT.Identity,
                           bias=W["bq3"][:, 0:1]).then_inc(sem("q3T_ready"), 1)
            act.wait_ge(sem("qe3_psum"), 1)
            act.copy(qe3[:, :].rearrange("p (a k) -> p a k", a=2), slot(0, D, HALF)).then_inc(sem("qe3_ready"), 1)
            ring = rings[3]
            act.sem_inc(ring.emptied["act"], ring.per["act"])
            with act.Fori(0, B) as b:
                act.wait_ge(sem("a3_shift_ready"), b + 1)
                act.activation(st3[:, 36:37], st3[:, 35:36], ACT.Exp).then_inc(sem("a3_self_exp"), 1)
                for half in range(2):
                    act.activation(P1[:, half * 2 * KQ:(half + 1) * 2 * KQ].rearrange("p (a k) -> p a k", a=2),
                                   slot(half, T, KQ), ACT.Exp, bias=st3[:, 34:35], accum_out=st3[:, 37 + half:38 + half]
                                   ).then_inc(ring.emptied["act"], 1)
                act.wait_ge(sem("a3_ctx_used"), b + 1)
                act.copy(AT3[:, :], bank(6, D, T)).then_inc(sem("a3_context_copied"), 1)
            turned(7)
            act.wait_ge(sem("experts_by_dve"), STEP["squares_ready"])
            act.activation(stat[0:T, 5, 0:8], stat[0:T, 5, 0:8], ACT.Sqrt).then_inc(sem("norms_ready"), 1)
            act.activation(small[0:E3, 40:41], small[0:E3, 40:41], ACT.Sqrt).then_inc(sem("norms_ready"), 1)
            act.wait_ge(sem("experts_by_dve"), STEP["expert_shifted"])
            act.activation(g3[0:T, 0:64], g3[0:T, 0:64], ACT.Exp).then_inc(sem("experts_by_act"), 1)
            act.wait_ge(sem("experts_by_pe"), STEP["expert_weights_psum"])
            act.copy(big2[0:E3, 0:BT].rearrange("p (a k) -> p a k", a=2), slot(0, E3, HALF)
                     ).then_inc(sem("experts_by_act"), 1)
            for e in range(E3):
                for k in range(8):
                    f, half = k // 2, k % 2
                    q = 8 * e + k
                    act.wait_ge(sem("f3_hidden_psum"), q + 1)
                    if e >= 1 and k == 0:
                        act.wait_ge(sem("f3_out"), e)
                    act.activation(hid[:, f, half * HALF:(half + 1) * HALF], bank(4 + q % 4, 128, HALF),
                                   ACT.Gelu, bias=W["f3b1"][:, e, f:f + 1]).then_inc(sem("f3_gelu"), 1)

        @block.gpsimd
        def _(pool):
            def split_keys(layer, copied, count):
                p = f"a{layer}_"
                pool.wait_ge(*copied)
                pool.tensor_tensor(kr, kf, kparts[:, 0, :], ALU.subtract).then_inc(sem(p + "keys_rest"), 1)
                pool.wait_ge(sem(p + "key_parts_2"), count)
                pool.tensor_tensor(kparts[:, 2, :], kr, kparts[:, 1, :], ALU.subtract
                                   ).then_inc(sem(p + "keys_split"), 1)

            for layer in (0, 1):
                ring = rings[layer]
                split_keys(layer, (sem(f"a{layer}_key_parts_1"), 1), 1)
                with pool.Fori(0, B) as b:
                    split_keys(layer, (ring.emptied["act"], ring.emptied_count(b, position(layer, "keys", 0, 1))),
                               b + 2)

            with pool.Fori(0, B) as b:
                for c in range(1, 13):
                    r = (ROWS + [T])[c]
                    pool.wait_ge(sem("a2_probs_ready"), b * 13 + c + 1)
                    if c > 1:
                        pool.wait_ge(sem("a2_sum_step"), b * 12 + c - 1)
                    before_c = S_all[0:r, 0, :] if c == 1 else Psum[0:r, :]
                    pool.tensor_tensor(Psum[0:r, :], before_c, S_all[0:r, c, :], ALU.add
                                       ).then_inc(sem("a2_sum_step"), 1)

        @block.vector
        def _(dve):
            own = [0]

            def link(i):
                own[0] += 1
                i.then_inc(sem("dve_step"), 1)
                dve.wait_ge(sem("dve_step"), own[0])

            roots = [0]

            def invert_roots(at):
                dve.sem_inc(sem("variances_ready"), 1)
                roots[0] += 1
                dve.wait_ge(sem("deviations_ready"), roots[0])
                link(dve.reciprocal(at, at))

            def norm_rows(dst, src, parts, n, width, scratch, st):
                shape = [parts, n, width]
                link(dve.tensor_reduce(st[:, 0, 0:n], src, AX.X, ALU.add))
                link(dve.tensor_scalar(st[:, 1, 0:n], st[:, 0, 0:n], 1.0 / width, None, ALU.mult))
                link(dve.tensor_tensor(dst, src, bc(st[:, 1, 0:n], shape, 2), ALU.subtract))
                link(dve.tensor_tensor(scratch, dst, dst, ALU.mult))
                link(dve.tensor_reduce(st[:, 2, 0:n], scratch, AX.X, ALU.add))
                link(dve.tensor_scalar(st[:, 3, 0:n], st[:, 2, 0:n], 1.0 / width, LN_EPS, ALU.mult, ALU.add))
                invert_roots(st[:, 4, 0:n])
                return dve.tensor_tensor(dst, dst, bc(st[:, 4, 0:n], shape, 2), ALU.mult)

            def norm_x():
                i = norm_rows(xn[:, :, :], x[:, :, :], T, B, D, wideA[:, :, :], stat[0:T])
                link(i)
                dve.sem_inc(sem("xn_ready"), 1)

            def add_residual(psum_pair, gate):
                link(dve.scalar_tensor_tensor(
                    out=x[:, :, :].rearrange("p (a b) d -> p a (b d)", a=2), in0=psum_pair,
                    scalar=gates[0:T, gate:gate + 1],
                    in1=x[:, :, :].rearrange("p (a b) d -> p a (b d)", a=2), op0=ALU.mult, op1=ALU.add))

            dve.memset(kmask[:, :, :].rearrange("p a b -> p (a b)"), 0).then_inc(sem("key_mask_cleared"), 1)
            link(dve.memset(ones[:, :], 1.0))
            link(dve.memset(Vo_w, 1.0))
            link(dve.memset(own_Vo_w, 1.0))
            link(dve.memset(Vn, 0.0))
            link(dve.memset(qparts_w, 0.0))
            link(dve.memset(own_kparts_w, 0.0))
            link(dve.memset(kst_w.bitcast(BF16), 1.0))
            link(dve.memset(own_kst_w.bitcast(BF16), 1.0))
            dve.sem_inc(sem("a0_ones_set"), 1)
            dve.wait_ge(sem("x_loaded"), 16)
            dve.wait_ge(sem("constants_loaded"), 5 * 16)
            dve.wait_ge(sem("weights_loaded"), NW)
            norm_x()
            link(dve.tensor_copy(wr_bc[:, :], W["f0wr"][:, 0:1].broadcast_to([D, T])))
            dve.wait_ge(sem("head_gate_exp"), 1)
            link(dve.tensor_scalar(head_gates[:, 0, :], head_gates[:, 0, :], 1.0, None, ALU.add))
            link(dve.reciprocal(head_gates[:, 0, :], head_gates[:, 0, :]))
            link(dve.tensor_scalar(head_gates[:, 1, :], head_gates[:, 0, :], -1.0, 1.0, ALU.mult, ALU.add))
            link(dve.tensor_scalar(small[:, 25:26], small[:, 24:25], 1.0, None, ALU.add))
            link(dve.reciprocal(small[:, 26:27], small[:, 25:26]))
            link(dve.tensor_tensor(small[:, 27:28], W["bva1"][:, :], W["bv1"][:, :], ALU.subtract))
            link(dve.scalar_tensor_tensor(out=bv1[:, :], in0=small[:, 27:28], scalar=small[:, 26:27],
                                          in1=W["bv1"][:, :], op0=ALU.mult, op1=ALU.add))
            link(dve.tensor_scalar(small[:, 30:31], W["gq2"][:, 0:1], W["gk2"][:, 0:1], DH ** -0.5, ALU.mult, ALU.mult))
            dve.wait_ge(sem("masks_loaded"), 32 + 32 * B)
            link(dve.memset(maskb, 0.0))
            mi = maski.bitcast(I32).rearrange("p (c q) -> p c q", c=NCH)
            link(dve.tensor_scalar(maskb[0:CK, 0:NCH - 1, :], mi[0:CK, 0:NCH - 1, :], 0, OFF, ALU.is_equal, ALU.mult))
            link(dve.tensor_scalar(maskb[0:LAST, NCH - 1, :], mi[0:LAST, NCH - 1, :], 0, OFF, ALU.is_equal, ALU.mult))
            link(dve.tensor_scalar(kbias[:, :, :], kmask[:, :, :], 0, OFF, ALU.is_equal, ALU.mult))

            def split(parts, src, rest):
                link(dve.tensor_copy(parts[:, 0, :], src))
                link(dve.tensor_tensor(rest, src, parts[:, 0, :], ALU.subtract))
                link(dve.tensor_copy(parts[:, 1, :], rest))
                link(dve.tensor_tensor(parts[:, 2, :], rest, parts[:, 1, :], ALU.subtract))

            def attention(layer):
                ring = rings[layer]
                p = f"a{layer}_"
                own_sem = sem(p + "dve_step")
                used = 2 * NCH + 2 * layer
                G = layer + 1
                per = STEPS[layer]
                bv = W["bv0"] if layer == 0 else bv1
                nf = 3 + layer
                link(dve.memset(psum[:, 6:8, :], 1.0))
                link(dve.memset(summed[:, :], 1.0))
                link(dve.memset(own_summed[:, :], 1.0))
                dve.wait_ge(sem(p + "first_projected"), 1)
                link(dve.tensor_copy(Vn[0:CK, 0:8, :].rearrange("p (a c) d -> p a (c d)", a=2), psum[0:CK, 4:6, :]))
                link(dve.tensor_copy(Vn[0:CK, 8:11, :].rearrange("p c d -> p (c d)"), bank(0, CK, 3 * D)))
                link(dve.tensor_copy(Vn[0:LAST, 11, :], bank(0, LAST, BANK)[:, 3 * D:4 * D]))
                dve.sem_inc(sem(p + "values_turned"), 1)
                dve.sem_inc(ring.emptied["dve"], ring.per["dve"])
                dve.sem_inc(sem(p + "sums_copied"), 1)
                dve.sem_inc(sem(p + "heads_by_dve"), 1)

                def finish(b, k, step):
                    dve.wait_ge(sem(p + "heads_by_pe"), b * nf + k + 1)
                    if k < G:
                        turned = bank(7, T, BANK).rearrange("p (h d) -> p h d", h=H)
                        dst = (heads, own_heads)[k]
                        step(dve.reciprocal(shares[:, k, :], turned[:, :, 8]))
                        if layer == 1:
                            step(dve.tensor_tensor(shares[:, k, :], shares[:, k, :], head_gates[0:T, k, :], ALU.mult))
                        i = dve.tensor_tensor(dst.rearrange("p (h d) -> p h d", h=H), turned[:, :, 0:8],
                                              bc(shares[:, k, :], [T, H, HD], 2), ALU.mult)
                        if k == 1:
                            step(i)
                            i = dve.tensor_tensor(heads[:, :], heads[:, :], own_heads[:, :], ALU.add)
                    elif k == G:
                        i = dve.tensor_scalar(headsT[:, :], bank(7, D, T), bv[:, 0:1], None, ALU.add)
                    else:
                        i = dve.tensor_copy(attended[:, bass.ds(b * D, D)], bank(7, T, D))
                    i.then_inc(sem(p + "heads_by_dve"), 1)

                with dve.Fori(0, B) as b:
                    k = [0]

                    def step(i):
                        k[0] += 1
                        i.then_inc(own_sem, 1)
                        dve.wait_ge(own_sem, b * per + k[0])

                    if layer == 1:
                        step(dve.tensor_copy(own_Vo[0:T, :, 0:8],
                                             vs.rearrange("p b (h d) -> p (b h) d", h=H)[:, bass.ds(b * H, H), :]))
                    for n, (kind, g, u, _) in enumerate(ORDER[layer]):
                        s = n % 3
                        if kind in ("exp", "keys"):
                            continue
                        dve.wait_ge(ring.full, ring.full_count(b, n))
                        if kind == "max":
                            r = ROWS[u // 2] if g == 0 else T
                            dst = (M if g == 0 else own_M)[0:r, 800 * (u % 2):800 * (u % 2) + 800].rearrange(
                                "p (a k) -> p a k", a=2)
                            if u < 2:
                                i = dve.tensor_copy(dst, slot(s, r, GROUP))
                            else:
                                dve.wait_ge(ring.emptied["dve"], ring.emptied_count(b, position(layer, "max", g, u - 2)))
                                i = dve.tensor_tensor(dst, slot(s, r, GROUP), dst, ALU.max)
                            i.then_inc(ring.emptied["dve"], 1)
                            if g == 0 and u in FINISH[layer]:
                                finish(b, FINISH[layer].index(u), step)
                            if layer == 1 and g == 0 and u == OWN_TAKEN:
                                dve.wait_ge(sem(p + "probs_used"), b * used + 2 + 3)
                                dve.tensor_copy(own_summed[:, :], bank(7, 128, GROUP)).then_inc(sem(p + "sums_copied"), 1)
                        elif kind == "turn":
                            r = CK if g == 0 else T
                            src = slot(s, T, 4 * CK).rearrange("p a (h k) -> p a h k", h=4)[:, :, :, 0:r]
                            for part in range(2):
                                dst = mx[:, g, :].rearrange("p (a r h) -> p a r h", a=2, r=2)[:, :, part, 4 * u:4 * u + 4]
                                if part == 0:
                                    i = dve.tensor_reduce(dst, src, AX.X, ALU.max, negate=True)
                                    step(i)
                                    first = dst
                                else:
                                    i = dve.tensor_copy(dst, first)
                            i.then_inc(ring.emptied["dve"], 1)
                            if u == 1:
                                dve.wait_ge(ring.emptied["dve"], ring.emptied_count(b, n))
                                if layer == 0:
                                    step(dve.tensor_scalar(flag[:, :], mx[:, 0, :], 1e29, 3e38, ALU.is_gt, ALU.mult))
                                    step(dve.tensor_tensor(mx[:, 0, :], mx[:, 0, :], flag[:, :], ALU.add))
                                dve.sem_inc(sem(p + f"max_ready_{g}"), 1)
                        elif kind == "row":
                            step(dve.tensor_copy(high[:, :], bank(2 * s, 32, T)))
                            step(dve.scalar_tensor_tensor(out=hl[:, g, :], in0=high[:, :], scalar=low_rows[:, 0:1],
                                                          in1=bank(2 * s, 32, T), op0=ALU.mult, op1=ALU.add))
                            dve.sem_inc(ring.emptied["dve"], 1)
                            dve.sem_inc(sem(p + f"shift_ready_{g}"), 1)
                        elif kind == "values":
                            if u == 0:
                                dve.wait_ge(sem(p + "values_placed"), b + 1)
                                dve.tensor_copy(Vn[0:CK, 0:8, :].rearrange("p (a c) d -> p a (c d)", a=2),
                                                slot(s, CK, BANK)).then_inc(ring.emptied["dve"], 1)
                            else:
                                step(dve.tensor_copy(Vn[0:CK, 8:11, :].rearrange("p c d -> p (c d)"),
                                                     bank(2 * s, CK, 3 * D)))
                                step(dve.tensor_copy(Vn[0:LAST, 11, :], bank(2 * s, LAST, BANK)[:, 3 * D:4 * D]))
                                dve.sem_inc(ring.emptied["dve"], 1)
                                dve.sem_inc(sem(p + "values_turned"), 1)
                    dve.wait_ge(sem(p + "probs_used"), (b + 1) * used + 3)
                    dve.tensor_copy(summed[:, :], bank(6, 128, GROUP)).then_inc(sem(p + "sums_copied"), 1)
                    assert k[0] == per, k[0]
                for k in range(nf):
                    finish(B, k, link)
                dve.wait_ge(sem(p + "heads_by_dve"), (B + 1) * nf + 1)
                link(dve.scalar_tensor_tensor(out=x[:, :, :], in0=attended[:, D:].rearrange("p (b d) -> p b d", b=B),
                                              scalar=gates[0:T, layer:layer + 1], in1=x[:, :, :],
                                              op0=ALU.mult, op1=ALU.add))
                dve.wait_ge(ring.emptied["dve"], (B + 1) * ring.per["dve"])
                dve.wait_ge(sem(p + "keys_split"), B + 1)

            dve.wait_ge(sem("gates_ready"), 1)
            dve.wait_ge(sem("q0_projected"), 1)
            link(dve.tensor_scalar(qf.rearrange("p (a k) -> p a k", a=2), slot(1, D, HALF), W["bq0"][:, 0:1],
                                   HD ** -0.5, ALU.add, ALU.mult))
            split(qparts[:, :, 0:BT], qf, qr)
            dve.sem_inc(sem("layer0_setup"), 1)
            dve.sem_inc(sem("a0_query_parts_ready"), 1)
            attention(0)

            norm_x()
            dve.wait_ge(sem("router_scores"), 1)
            flat = wideA[:, :, :].rearrange("p b d -> p (b d)")
            sr = flat[:, 0:BT].rearrange("p (b t) -> p b t", b=B)
            tmp = wideB[:, :, :].rearrange("p b d -> p (b d)")[:, 0:BT].rearrange("p (b t) -> p b t", b=B)
            sh = [T, B, T]
            link(dve.tensor_copy(flat[:, 0:BT].rearrange("p (a k) -> p a k", a=2), slot(1, T, HALF)))
            link(dve.tensor_tensor(tmp, sr, bc(ident[0:T, 0:T], sh, 1), ALU.mult))
            dve.tensor_reduce(stat[0:T, 0, 0:8], tmp, AX.X, ALU.add).then_inc(sem("router_columns"), 1)
            dve.wait_ge(sem("router_columns"), 1)
            link(dve.tensor_tensor(tmp, sr, bc(stat[0:T, 0, 0:8], sh, 2), ALU.is_gt))
            link(dve.tensor_reduce(stat[0:T, 1, 0:8], tmp, AX.X, ALU.add))
            link(dve.tensor_tensor(tmp, sr, bc(stat[0:T, 0, 0:8], sh, 2), ALU.is_equal))
            link(dve.tensor_tensor(tmp, tmp, bc(before[:, :], sh, 1), ALU.mult))
            link(dve.tensor_reduce(stat[0:T, 2, 0:8], tmp, AX.X, ALU.add))
            link(dve.tensor_tensor(stat[0:T, 3, 0:8], stat[0:T, 1, 0:8], stat[0:T, 2, 0:8], ALU.add))
            link(dve.tensor_scalar(stat[0:T, 4, 0:8], stat[0:T, 3, 0:8], T // 2 - 0.5, gates[0:T, 4:5],
                                   ALU.is_lt, ALU.mult))
            dve.wait_ge(sem("router_exp"), 1)
            link(dve.tensor_scalar(stat[0:T, 5, 0:8], small[0:T, 0:8], 1.0, None, ALU.add))
            link(dve.reciprocal(stat[0:T, 6, 0:8], stat[0:T, 5, 0:8]))
            link(dve.tensor_tensor(stat[0:T, 7, 0:8], stat[0:T, 6, 0:8], stat[0:T, 4, 0:8], ALU.mult))
            link(dve.scalar_tensor_tensor(out=x[:, :, :], in0=xn[:, :, :], scalar=gates[0:T, 4:5], in1=x[:, :, :],
                                          op0=ALU.mult, op1=ALU.add))
            dve.wait_ge(sem("ffn0_out"), 1)
            link(dve.tensor_tensor(wideA[:, :, :].rearrange("p (a b) d -> p a b d", a=2),
                                   slot(0, T, BANK).rearrange("p a (b d) -> p a b d", b=4),
                                   stat[0:T, 7, 0:8].rearrange("p (a b) -> p a b", a=2).unsqueeze(3)
                                   .broadcast_to([T, 2, 4, D]), ALU.mult))
            link(dve.tensor_tensor(x[:, :, :], x[:, :, :], wideA[:, :, :], ALU.add))

            norm_x()
            dve.wait_ge(sem("q1_projected"), 1)
            for tile in (Vo_w, own_Vo_w, kst_w.bitcast(BF16), own_kst_w.bitcast(BF16)):
                link(dve.memset(tile, 1.0))
            for tile in (qparts_w, own_kparts_w, Vn):
                link(dve.memset(tile, 0.0))
            dve.sem_inc(sem("a1_ones_set"), 1)
            link(dve.tensor_scalar(qf.rearrange("p (a k) -> p a k", a=2), slot(1, D, HALF), W["bq1"][:, 0:1],
                                   HD ** -0.5, ALU.add, ALU.mult))
            split(qparts[:, :, 0:BT], qf, qr)
            dve.sem_inc(sem("q1_split"), 1)
            dve.wait_ge(sem("k1_ready"), 1)
            split(own_kparts[:, :, 0:BT], qf, qr)
            dve.wait_ge(sem("v1_projected"), 1)
            link(dve.tensor_copy(vs.rearrange("p (a b) d -> p a (b d)", a=2), slot(3, T, BANK)))
            dve.sem_inc(sem("layer1_setup"), 1)
            dve.sem_inc(sem("a1_query_parts_ready"), 1)
            attention(1)

            norm_x()
            link(dve.tensor_scalar(g0[0:NSLOT, 0:D], W["slots"][:, :], W["slot_scale"][:, 0:1], None, ALU.mult))
            dve.sem_inc(sem("slots_by_dve"), 1)
            dve.wait_ge(sem("slots_by_pe"), STEP["slots_turned"])
            link(dve.tensor_scalar(small[:, 8:9], bank(2, D, 1), 1.0 / NSLOT, None, ALU.mult))
            link(dve.tensor_copy(g1[:, 0:NSLOT], bank(3, D, NSLOT)))
            dve.sem_inc(sem("slots_by_dve"), 1)
            dve.sem_inc(sem("slots_by_dve"), 1)
            dve.wait_ge(sem("slots_by_pe"), STEP["slot_bias_psum"])
            link(dve.tensor_tensor(small[0:NSLOT, 10:11], bank(2, NSLOT, 1), W["f1b1"][:, 0:1], ALU.add))
            dve.sem_inc(sem("slots_by_dve"), 1)
            link(dve.scalar_tensor_tensor(out=small[0:T, 11:12], in0=W["tau"][0:T, 0:1], scalar=-1.0,
                                          in1=W["tau"][0:T, 0:1], op0=ALU.mult, op1=ALU.max))
            link(dve.tensor_scalar(small[0:T, 11:12], small[0:T, 11:12], 0.1, None, ALU.add))
            link(dve.reciprocal(small[0:T, 12:13], small[0:T, 11:12]))
            dve.wait_ge(sem("slots_by_pe"), STEP["route_logits"])
            lg = big3[0:T, 0:512].rearrange("p (b s) -> p b s", b=B)
            rest = big2[0:T, 0:512].rearrange("p (b s) -> p b s", b=B)
            chosen = big1[0:T, 0:512].rearrange("p (b s) -> p b s", b=B)
            ls = [T, B, NSLOT]
            link(dve.tensor_tensor(lg, bank(6, T, BANK).rearrange("p (b s) -> p b s", b=B),
                                   bc(W["f1b2"][0:T, :], ls, 1), ALU.add))
            link(dve.tensor_scalar(lg, lg, small[0:T, 12:13], None, ALU.mult))
            top = stat[0:T, 0:2, :].rearrange("p a b -> p (a b)").rearrange("p (b k) -> p b k", b=B)
            for bb in range(B):
                i = dve.max(top[:, bb, :], lg[:, bb, :])
            link(i)
            for bb in range(B):
                i = dve.match_replace(rest[:, bb, :], top[:, bb, :], lg[:, bb, :], -3e38)
            link(i)
            link(dve.tensor_tensor(chosen, rest, lg, ALU.not_equal))
            link(dve.tensor_tensor(rest, lg, top[:, :, 0:1].broadcast_to(ls), ALU.subtract))
            dve.sem_inc(sem("slots_by_dve"), 1)
            dve.wait_ge(sem("slots_by_act"), STEP["logits_exp"])
            link(dve.tensor_tensor(chosen, chosen, rest, ALU.mult))
            link(dve.tensor_reduce(stat[0:T, 3, 0:8], chosen, AX.X, ALU.add))
            link(dve.reciprocal(stat[0:T, 4, 0:8], stat[0:T, 3, 0:8]))
            link(dve.tensor_tensor(chosen, chosen, bc(stat[0:T, 4, 0:8], ls, 2), ALU.mult))
            dve.sem_inc(sem("slots_by_dve"), 1)
            dve.wait_ge(sem("slots_by_pe"), STEP["gh_psum"])
            for g in range(3):
                i = dve.tensor_scalar(g1[:, 64 + g * 64:128 + g * 64], bank(7, D, 192)[:, g * 64:(g + 1) * 64],
                                      W["f1bhh"][:, g:g + 1], None, ALU.add)
            link(i)
            dve.wait_ge(sem("slots_by_pe"), STEP["slot_inputs"])
            link(dve.tensor_scalar(g2[:, :], bank(1, D, BANK), 1e-8, None, ALU.add))
            link(dve.reciprocal(g2[:, :], g2[:, :]))
            link(dve.tensor_tensor(g3[:, :], bank(0, D, BANK), g2[:, :], ALU.mult))
            dve.sem_inc(sem("slots_by_dve"), 1)
            dve.wait_ge(sem("slots_by_pe"), STEP["gx_psum"])
            gs = [D, B, NSLOT]

            def gate_sum(dst, bk, g):
                dve.wait_ge(sem("dve_step"), own[0])
                link(dve.scalar_tensor_tensor(
                    out=dst.rearrange("p (b s) -> p b s", b=B), in0=bank(bk, D, BANK).rearrange("p (b s) -> p b s", b=B),
                    scalar=W["f1bih"][:, g:g + 1], in1=bc(g1[:, 64 + g * 64:128 + g * 64], gs, 1),
                    op0=ALU.add, op1=ALU.add))

            gate_sum(g0[:, :], 2, 0)
            dve.sem_inc(sem("slots_by_dve"), 1)
            gate_sum(big3[:, 0:512], 3, 1)
            dve.sem_inc(sem("slots_by_dve"), 1)
            dve.wait_ge(sem("slots_by_act"), STEP["gate_r_exp"])
            link(dve.tensor_scalar(g0[:, :], g0[:, :], 1.0, None, ALU.add))
            link(dve.reciprocal(g0[:, :], g0[:, :]))
            link(dve.tensor_tensor(g2[:, :].rearrange("p (b s) -> p b s", b=B),
                                   g0[:, :].rearrange("p (b s) -> p b s", b=B), bc(g1[:, 192:256], gs, 1), ALU.mult))
            link(dve.scalar_tensor_tensor(out=g3[:, :], in0=bank(6, D, BANK), scalar=W["f1bih"][:, 2:3], in1=g2[:, :],
                                          op0=ALU.add, op1=ALU.add))
            dve.sem_inc(sem("slots_by_dve"), 1)
            dve.wait_ge(sem("slots_by_act"), STEP["gate_z_exp"])
            link(dve.tensor_scalar(big3[:, 0:512], big3[:, 0:512], 1.0, None, ALU.add))
            link(dve.reciprocal(big3[:, 0:512], big3[:, 0:512]))
            dve.wait_ge(sem("slots_by_act"), STEP["gate_n_tanh"])
            link(dve.tensor_tensor(g2[:, :].rearrange("p (b s) -> p b s", b=B), bc(g1[:, 0:64], gs, 1),
                                   g3[:, :].rearrange("p (b s) -> p b s", b=B), ALU.subtract))
            link(dve.tensor_tensor(g2[:, :], g2[:, :], big3[:, 0:512], ALU.mult))
            link(dve.tensor_tensor(g2[:, :], g2[:, :], g3[:, :], ALU.add))
            dve.sem_inc(sem("slots_by_dve"), 1)
            dve.wait_ge(sem("ffn1_out"), 1)
            add_residual(slot(3, T, BANK), 5)

            norm_x()
            lf = lat[:, :, :]
            link(norm_rows(lf, xn[:, :, :], T, B, D, wideA[:, :, :], stat[0:T]))
            link(dve.tensor_tensor(lf, lf, bc(W["lnlg"][0:T, :], [T, B, D], 1), ALU.mult))
            link(dve.tensor_tensor(lf, lf, bc(W["lnlb"][0:T, :], [T, B, D], 1), ALU.add))
            link(dve.memset(ctxk[:, :, :], 0.0))
            dve.sem_inc(sem("ctxk_cleared"), 1)
            link(dve.memset(kbc[:, :], 0.0))
            link(dve.memset(ones[:, :], 1.0))
            dve.sem_inc(sem("latents_ready"), 1)
            ring = rings[2]
            dve.sem_inc(ring.emptied["dve"], ring.per["dve"])
            dve.sem_inc(sem("a2_context_normalised"), 1)
            per = STEPS[2]
            with dve.Fori(0, B) as b:
                k = [0]

                def step(i):
                    k[0] += 1
                    i.then_inc(sem("a2_dve_step"), 1)
                    dve.wait_ge(sem("a2_dve_step"), b * per + k[0])

                dve.wait_ge(sem("ctx_keys_loaded"), 32 * b + 32)
                kk = ctxk[:, 0:NCH, :]
                ks = [128, NCH, D]
                s1, s2 = stat[:, 0, 0:12], stat[:, 1, 0:12]
                step(dve.tensor_reduce(s1, kk, AX.X, ALU.add))
                step(dve.tensor_scalar(s1, s1, 1.0 / D, None, ALU.mult))
                step(dve.tensor_tensor(kk, kk, bc(s1, ks, 2), ALU.subtract))
                scr = mB[:, 0:1536].rearrange("p (c d) -> p c d", c=NCH)
                step(dve.tensor_tensor(scr, kk, kk, ALU.mult))
                step(dve.tensor_reduce(s2, scr, AX.X, ALU.add))
                step(dve.tensor_scalar(s2, s2, 1.0 / D, LN_EPS, ALU.mult, ALU.add))
                dve.sem_inc(sem("a2_variances"), 1)
                dve.wait_ge(sem("a2_deviations"), b + 1)
                step(dve.reciprocal(s2, s2))
                step(dve.tensor_tensor(kk, kk, bc(s2, ks, 2), ALU.mult))
                step(dve.tensor_tensor(kk, kk, bc(W["lnxg"][:, :], ks, 1), ALU.mult))
                step(dve.tensor_tensor(kk, kk, bc(W["lnxb"][:, :], ks, 1), ALU.add))
                step(dve.tensor_copy(kbc[:, 0:NCH], kbias[:, :, :].rearrange("p b c -> p (b c)")[:, bass.ds(b * NCH, NCH)]))
                step(dve.tensor_copy(ctxk[0:T, NCH, :], lat[:, :, :].rearrange("p b d -> p (b d)")[:, bass.ds(b * D, D)]))
                dve.sem_inc(sem("a2_keys_normalised"), 1)
                dve.wait_ge(ring.full, ring.full_count(b, 0))
                dve.tensor_copy(xkT[:, 0:8 * CK].rearrange("p (a k) -> p a k", a=2), slot(0, D, 4 * CK)
                                ).then_inc(ring.emptied["dve"], 1)
                dve.wait_ge(ring.full, ring.full_count(b, 1))
                dve.tensor_copy(xkT[:, 8 * CK:S2], bank(2, D, S2 - 8 * CK))
                step(dve.tensor_copy(xkT[:, S2:S2 + T], bank(3, D, T)))
                dve.sem_inc(ring.emptied["dve"], 1)

                def inverse_norm(r, c):
                    step(dve.tensor_reduce(n2[0:r, :], sq[0:r, :].rearrange("p (h d) -> p h d", h=H), AX.X, ALU.add))
                    step(dve.tensor_scalar(n2[0:r, :], n2[0:r, :], 1.0 / DH, 1e-16, ALU.mult, ALU.max))
                    dve.sem_inc(sem("a2_squares_summed"), 1)
                    dve.wait_ge(sem("a2_norms"), b * 14 + c + 1)
                    step(dve.reciprocal(rk[0:r, :], n2[0:r, :]))

                dve.wait_ge(ring.full, ring.full_count(b, 2))
                dve.wait_ge(sem("a2_squares"), b * 14 + 1)
                inverse_norm(T, 0)
                step(dve.tensor_tensor(Psum[0:T, 0:1024].rearrange("p (a h d) -> p a h d", a=2, d=DH),
                                       slot(0, T, BANK).rearrange("p a (h d) -> p a h d", d=DH),
                                       rk[0:T, :].rearrange("p (a h) -> p a h", a=2).unsqueeze(3)
                                       .broadcast_to([T, 2, 8, DH]), ALU.mult))
                dve.sem_inc(ring.emptied["dve"], 1)
                dve.sem_inc(sem("a2_q_normalised"), 1)
                n = 6
                for c in range(13):
                    r = (ROWS + [T])[c]
                    dve.wait_ge(sem("a2_squares"), b * 14 + c + 2)
                    inverse_norm(r, c + 1)
                    dve.sem_inc(ring.emptied["dve"], 1)
                    n += 1
                    for half in range(2):
                        dve.wait_ge(ring.full, ring.full_count(b, n))
                        sl = S_all[0:r, c, 2 * half * GROUP:(2 * half + 2) * GROUP]
                        step(dve.tensor_tensor(sl.rearrange("p (a h q) -> p a h q", a=2, q=T),
                                               slot(n % 2, r, GROUP).rearrange("p a (h q) -> p a h q", q=T),
                                               rk[0:r, 8 * half:8 * half + 8].rearrange("p (a h) -> p a h", a=2)
                                               .unsqueeze(3).broadcast_to([r, 2, 4, T]), ALU.mult))
                        dve.sem_inc(ring.emptied["dve"], 1)
                        n += 1
                        msl = M[0:r, 2 * half * GROUP:(2 * half + 2) * GROUP]
                        if c == 0:
                            i = dve.tensor_scalar(msl, sl, kbc[0:r, c:c + 1], None, ALU.add)
                        else:
                            i = dve.scalar_tensor_tensor(out=msl, in0=sl, scalar=kbc[0:r, c:c + 1], in1=msl,
                                                         op0=ALU.add, op1=ALU.max)
                        step(i)
                dve.sem_inc(sem("a2_column_max"), 1)
                for half in range(2):
                    dve.wait_ge(ring.full, ring.full_count(b, n))
                    step(dve.tensor_reduce(stat[0:T, 0, 8 * half:8 * half + 8].rearrange("p (a h) -> p a h", a=2),
                                           slot(n % 2, T, 4 * CK).rearrange("p a (h k) -> p a h k", h=4),
                                           AX.X, ALU.max))
                    dve.sem_inc(ring.emptied["dve"], 1)
                    n += 1
                dve.sem_inc(sem("a2_max_ready"), 1)
                dve.wait_ge(ring.full, ring.full_count(b, n))
                step(dve.tensor_tensor(M[0:16, :].rearrange("p (h q) -> p h q", h=16),
                                       bc(bank(2 * (n % 2), 16, T), [16, 16, T], 1),
                                       bc(ident[0:16, 0:16], [16, 16, T], 2), ALU.mult))
                dve.sem_inc(ring.emptied["dve"], 1)
                dve.sem_inc(sem("a2_shift_ready"), 1)
                n += 1
                dve.wait_ge(ring.emptied["act"], ring.emptied_count(b, n + 1))
                n += 2
                for c in range(13):
                    r = (ROWS + [T])[c]
                    dve.tensor_tensor(S_all[0:r, c, :], S_all[0:r, c, :], mB[0:r, :], ALU.subtract
                                      ).then_inc(sem("a2_scores_shifted"), 1)
                for half in range(2):
                    dve.wait_ge(ring.full, ring.full_count(b, n))
                    sl = M[:, 2 * half * GROUP:(2 * half + 2) * GROUP].rearrange("p (a k) -> p a k", a=2)
                    step(dve.reciprocal(sl, slot(n % 2, 128, GROUP)))
                    dve.sem_inc(ring.emptied["dve"], 1)
                    n += 1
                dve.wait_ge(sem("a2_scores_shifted"), b * 13 + 13)
                step(dve.tensor_tensor(mB[:, :].rearrange("p (a k) -> p a k", a=4), psum[:, 4:8, 0:GROUP],
                                       M[:, :].rearrange("p (a k) -> p a k", a=4), ALU.mult))
                dve.sem_inc(sem("a2_context_normalised"), 1)
                n += 1
                dve.wait_ge(ring.full, ring.full_count(b, n))
                xb = x[:, :, :].rearrange("p b d -> p (b d)")[:, bass.ds(b * D, D)]
                dve.scalar_tensor_tensor(out=xb, in0=bank(2 * (n % 2), T, D), scalar=gates[0:T, 2:3],
                                         in1=xb, op0=ALU.mult, op1=ALU.add).then_inc(ring.emptied["dve"], 1)
                assert k[0] == per, k[0]
            dve.wait_ge(ring.emptied["dve"], (B + 1) * ring.per["dve"])

            link(dve.tensor_reduce(small[:, 16:17], W["f2fc"][:, :], AX.X, ALU.add, apply_absolute_value=True))
            link(dve.tensor_reduce(small[:, 17:18], W["f2proj"][:, :, :], AX.XY, ALU.add, apply_absolute_value=True))
            dve.sem_inc(sem("ternary_sums"), 1)
            dve.wait_ge(sem("ternary_scale"), 1)
            link(dve.tensor_scalar(small[:, 18:20], bank(2, 128, 2), 1.0 / (4 * D * D), 1e-6, ALU.mult, ALU.add))
            link(dve.tensor_scalar(small[:, 20:22], small[:, 18:20], 0.5, None, ALU.mult))
            link(dve.tensor_scalar(small[:, 22:24], small[:, 18:20], -0.5, None, ALU.mult))
            for w, i in ((W["f2fc"][:, :], 0), (W["f2proj"][:, :, :].rearrange("p a b -> p (a b)"), 1)):
                link(dve.tensor_scalar(big3[:, 0:512], w, small[:, 22 + i:23 + i], None, ALU.is_lt))
                link(dve.scalar_tensor_tensor(out=w, in0=w, scalar=small[:, 20 + i:21 + i], in1=big3[:, 0:512],
                                              op0=ALU.is_gt, op1=ALU.subtract))
            dve.sem_inc(sem("ternary_ready"), 1)
            norm_x()
            for bb in range(B):
                dve.wait_ge(sem("f2_gelu"), bb + 1)
                src = ternary_hidden(bb)
                link(dve.tensor_reduce(stat[0:T, 0, bb:bb + 1], src, AX.X, ALU.add))
                link(dve.tensor_scalar(stat[0:T, 1, bb:bb + 1], stat[0:T, 0, bb:bb + 1], 1.0 / F0, None, ALU.mult))
                link(dve.tensor_scalar(src, src, stat[0:T, 1, bb:bb + 1], None, ALU.subtract))
                link(dve.tensor_tensor(big3[0:T, 0:512], src, src, ALU.mult))
                link(dve.tensor_reduce(stat[0:T, 2, bb:bb + 1], big3[0:T, 0:512], AX.X, ALU.add))
            link(dve.tensor_scalar(stat[0:T, 3, 0:8], stat[0:T, 2, 0:8], 1.0 / F0, LN_EPS, ALU.mult, ALU.add))
            invert_roots(stat[0:T, 4, 0:8])
            for bb in range(B):
                src = ternary_hidden(bb)
                dst = big1[0:T, (bb % 2) * 512:(bb % 2 + 1) * 512]
                if bb >= 2:
                    dve.wait_ge(sem("f2_turned_psum"), bb - 1)
                link(dve.scalar_tensor_tensor(out=dst, in0=src, scalar=stat[0:T, 4, bb:bb + 1],
                                              in1=W["f2lnw"][0:T, :], op0=ALU.mult, op1=ALU.mult))
                link(dve.tensor_tensor(dst, dst, W["f2lnb"][0:T, :], ALU.add))
                dve.sem_inc(sem("f2_normalised"), 1)
            dve.wait_ge(sem("ffn2_out"), 1)
            add_residual(slot(3, T, BANK), 6)

            dve.sem_inc(sem("arena_free_for_experts"), 1)
            norm_x()
            for bb in range(B):
                dve.wait_ge(sem("qkv3_psum"), bb + 1)
                dve.tensor_tensor(qkv3[:, bb, :], bank(4 + bb % 4, T, 3 * D), W["b3"][0:T, :], ALU.add
                                  ).then_inc(sem("qkv3_ready"), 1)
            dve.wait_ge(sem("qkv3_ready"), B)
            link(dve.tensor_tensor(wideA[:, :, :], qkv3[:, :, 0:D], qkv3[:, :, D:2 * D], ALU.mult))
            link(dve.tensor_reduce(st3[:, 0:8], wideA[:, :, :], AX.X, ALU.add))
            link(dve.tensor_tensor(wideA[:, :, :], qkv3[:, :, 0:D], bc(W["b3"][0:T, D:2 * D], [T, B, D], 1), ALU.mult))
            link(dve.tensor_reduce(st3[:, 8:16], wideA[:, :, :], AX.X, ALU.add))
            dve.wait_ge(sem("qe3_ready"), 1)
            dve.sem_inc(sem("layer3_setup"), 1)
            ring = rings[3]
            dve.sem_inc(ring.emptied["dve"], ring.per["dve"])
            per = STEPS[3]
            with dve.Fori(0, B) as b:
                k = [0]

                def step(i):
                    k[0] += 1
                    i.then_inc(sem("a3_dve_step"), 1)
                    dve.wait_ge(sem("a3_dve_step"), b * per + k[0])

                dve.tensor_copy(q3c[:, :], qe3[:, bass.ds(b * T, T)]).then_inc(sem("a3_query_placed"), 1)
                dve.tensor_copy(st3[:, 32:33], st3[:, bass.ds(b, 1)])
                step(dve.tensor_copy(st3[:, 33:34], st3[:, bass.ds(b + 8, 1)]))
                dve.wait_ge(ring.full, ring.full_count(b, 0))
                dve.tensor_reduce(st3[:, 40:42], slot(0, T, KQ), AX.X, ALU.max)
                dve.wait_ge(ring.full, ring.full_count(b, 1))
                step(dve.tensor_reduce(st3[:, 42:44], slot(1, T, KQ), AX.X, ALU.max))
                step(dve.tensor_reduce(st3[:, 44:45], st3[:, 40:44], AX.X, ALU.max))
                step(dve.scalar_tensor_tensor(out=st3[:, 45:46], in0=st3[:, 44:45], scalar=st3[:, 33:34],
                                              in1=st3[:, 32:33], op0=ALU.add, op1=ALU.max))
                dve.tensor_tensor(st3[:, 34:35], st3[:, 33:34], st3[:, 45:46], ALU.subtract)
                step(dve.tensor_tensor(st3[:, 35:36], st3[:, 32:33], st3[:, 45:46], ALU.subtract))
                dve.sem_inc(sem("a3_shift_ready"), 1)
                dve.wait_ge(ring.full, ring.full_count(b, 2))
                dve.tensor_copy(PT3[0:CK, 0:8, :].rearrange("p (a c) q -> p a (c q)", a=2), slot(2, CK, GROUP)
                                ).then_inc(ring.emptied["dve"], 1)
                dve.wait_ge(ring.full, ring.full_count(b, 3))
                dve.tensor_copy(PT3[0:CK, 8:11, :].rearrange("p c q -> p (c q)"), bank(0, CK, 3 * T))
                dve.tensor_copy(PT3[0:LAST, 11, :], bank(0, LAST, 4 * T)[:, 3 * T:4 * T]
                                ).then_inc(ring.emptied["dve"], 1)
                dve.wait_ge(sem("a3_self_exp"), b + 1)
                dve.wait_ge(ring.full, ring.full_count(b, 4))
                step(dve.tensor_tensor(st3[:, 46:47], st3[:, 37:38], st3[:, 38:39], ALU.add))
                dve.tensor_tensor(st3[:, 47:48], st3[:, 46:47], st3[:, 36:37], ALU.add)
                step(dve.scalar_tensor_tensor(out=y3[:, :], in0=W["b3"][0:T, 2 * D:3 * D], scalar=st3[:, 46:47],
                                              in1=bank(2, T, D), op0=ALU.mult, op1=ALU.add))
                dve.reciprocal(st3[:, 48:49], st3[:, 47:48])
                vb = qkv3.rearrange("p b d -> p (b d)")[:, bass.ds(b * 3 * D + 2 * D, D)]
                step(dve.scalar_tensor_tensor(out=y3[:, :], in0=vb, scalar=st3[:, 36:37], in1=y3[:, :],
                                              op0=ALU.mult, op1=ALU.add))
                step(dve.tensor_scalar(y3[:, :], y3[:, :], st3[:, 48:49], gates[0:T, 3:4], ALU.mult, ALU.mult))
                xb = x[:, :, :].rearrange("p b d -> p (b d)")[:, bass.ds(b * D, D)]
                dve.tensor_tensor(xb, xb, y3[:, :], ALU.add).then_inc(ring.emptied["dve"], 1)
                assert k[0] == per, k[0]
            dve.wait_ge(ring.emptied["dve"], (B + 1) * ring.per["dve"])

            norm_x()
            eps = 1e-8
            link(dve.tensor_tensor(wideA[:, :, :], xn[:, :, :], xn[:, :, :], ALU.mult))
            link(dve.tensor_reduce(stat[0:T, 5, 0:8], wideA[:, :, :], AX.X, ALU.add))
            em = W["emb"][:, :]
            link(dve.tensor_tensor(g0[0:E3, 128:256], em, em, ALU.mult))
            link(dve.tensor_reduce(small[0:E3, 40:41], g0[0:E3, 128:256], AX.X, ALU.add))
            dve.sem_inc(sem("experts_by_dve"), 1)
            dve.wait_ge(sem("norms_ready"), 2)
            link(dve.tensor_scalar(stat[0:T, 5, 0:8], stat[0:T, 5, 0:8], eps, None, ALU.add))
            link(dve.reciprocal(stat[0:T, 5, 0:8], stat[0:T, 5, 0:8]))
            link(dve.tensor_scalar(small[0:E3, 41:42], small[0:E3, 40:41], eps, None, ALU.add))
            link(dve.reciprocal(small[0:E3, 42:43], small[0:E3, 41:42]))
            link(dve.tensor_scalar(g0[0:E3, 0:D], em, small[0:E3, 42:43], None, ALU.mult))
            dve.sem_inc(sem("experts_by_dve"), 1)
            dve.wait_ge(sem("experts_by_pe"), STEP["experts_turned"])
            dve.tensor_copy(g1[:, 0:8], W["embT"][:, :])
            link(dve.tensor_copy(g1[:, 8:16], bank(2, D, E3)))
            dve.sem_inc(sem("experts_by_dve"), 1)
            dve.wait_ge(sem("experts_by_pe"), STEP["expert_scores"])
            sc = bank(3, T, 128).rearrange("p (b k) -> p b k", b=B)
            es, fs = [T, B, E3], [T, B, E3, E3]
            simv = g2[0:T, 64:128].rearrange("p (b e) -> p b e", b=B)
            cosv = g2[0:T, 128:192].rearrange("p (b e) -> p b e", b=B)
            rank = g2[0:T, 192:256].rearrange("p (b e) -> p b e", b=B)
            rank2 = g2[0:T, 256:320].rearrange("p (b e) -> p b e", b=B)
            pair = g0[0:T, :].rearrange("p (b e f) -> p b e f", b=B, e=E3)
            pair2 = big3[0:T, 0:512].rearrange("p (b e f) -> p b e f", b=B, e=E3)
            link(dve.tensor_copy(simv, sc[:, :, 0:E3]))
            link(dve.tensor_tensor(cosv, sc[:, :, E3:2 * E3], bc(stat[0:T, 5, 0:8], es, 2), ALU.mult))
            link(dve.tensor_scalar(g1[0:T, 16:24], W["onb"][0:T, :], 0.1, None, ALU.mult))
            link(dve.tensor_tensor(cosv, cosv, bc(g1[0:T, 16:24], es, 1), ALU.add))
            def ranks(dst, other, v):
                fbc = v.unsqueeze(2).broadcast_to(fs)
                ebc = v.unsqueeze(3).broadcast_to(fs)
                link(dve.tensor_tensor(pair, fbc, ebc, ALU.is_gt))
                link(dve.tensor_reduce(dst, pair, AX.X, ALU.add))
                link(dve.tensor_tensor(pair, fbc, ebc, ALU.is_equal))
                link(dve.tensor_tensor(pair, pair, W["etri"][0:T, :].rearrange("p (e f) -> p e f", e=E3)
                                       .unsqueeze(1).broadcast_to(fs), ALU.mult))
                link(dve.tensor_reduce(other, pair, AX.X, ALU.add))
                link(dve.tensor_tensor(dst, dst, other, ALU.add))

            ranks(rank, rank2, simv)
            link(dve.tensor_scalar(rank, rank, 6.5, OFF, ALU.is_gt, ALU.mult))
            link(dve.tensor_tensor(cosv, cosv, rank, ALU.add))
            ranks(rank, rank2, cosv)
            link(dve.tensor_scalar(rank, rank, 1.5, None, ALU.is_lt))
            link(dve.tensor_reduce(stat[0:T, 6, 0:8], cosv, AX.X, ALU.max))
            ev = g3[0:T, 0:64].rearrange("p (b e) -> p b e", b=B)
            link(dve.tensor_tensor(ev, cosv, bc(stat[0:T, 6, 0:8], es, 2), ALU.subtract))
            dve.sem_inc(sem("experts_by_dve"), 1)
            dve.wait_ge(sem("experts_by_act"), STEP["expert_exp"])
            wv = g2[0:T, 0:64].rearrange("p (b e) -> p b e", b=B)
            link(dve.tensor_tensor(wv, ev, rank, ALU.mult))
            link(dve.tensor_reduce(stat[0:T, 7, 0:8], wv, AX.X, ALU.add))
            link(dve.reciprocal(stat[0:T, 7, 0:8], stat[0:T, 7, 0:8]))
            link(dve.tensor_scalar(stat[0:T, 7, 0:8], stat[0:T, 7, 0:8], gates[0:T, 7:8], None, ALU.mult))
            link(dve.tensor_tensor(wv, wv, bc(stat[0:T, 7, 0:8], es, 2), ALU.mult))
            dve.sem_inc(sem("experts_by_dve"), 1)
            dve.wait_ge(sem("experts_by_pe"), STEP["expert_biases"])
            link(dve.tensor_tensor(x[:, :, :].rearrange("p (a b) d -> p a (b d)", a=2), slot(1, T, BANK),
                                   x[:, :, :].rearrange("p (a b) d -> p a (b d)", a=2), ALU.add))
            dve.sem_inc(sem("experts_by_dve"), 1)
            for e in range(E3):
                dve.wait_ge(sem("f3_out"), e + 1)
                for half in range(2):
                    src = bank(2 * (e % 2) + half, T, BANK)
                    for i4 in range(4):
                        bb = 4 * half + i4
                        i = dve.scalar_tensor_tensor(out=x[:, bb, :], in0=src[:, i4 * D:(i4 + 1) * D],
                                                     scalar=wv[:, bb, e:e + 1], in1=x[:, bb, :],
                                                     op0=ALU.mult, op1=ALU.add)
                    i.then_inc(sem("f3_accumulated"), 1)
                dve.wait_ge(sem("f3_accumulated"), 2 * (e + 1))
            dve.sem_inc(sem("y_ready"), 1)


def milestones(*names):
    return {name: i + 1 for i, name in enumerate(names)}


STEP = {}
STEP.update(milestones("slots_turned", "slot_bias_psum", "f1_hidden_psum", "route_logits", "gh_psum", "slot_inputs",
                       "alpha_turned", "gx_psum", "slot_values_psum", "slot_outputs_psum"))
STEP.update(milestones("slots_scaled", "slot_mean", "slotsT_ready", "slot_bias", "logits_shifted", "alpha_ready",
                       "gi_ready", "gate_r_sum", "gate_z_sum", "gate_n_sum", "slots_new"))
STEP.update(milestones("logits_exp", "alphaT_ready", "gate_r_exp", "gate_z_exp", "gate_n_tanh", "slot_values",
                       "slot_outputs"))
STEP.update(milestones("experts_turned", "expert_scores", "expert_weights_psum", "expert_biases"))
STEP.update(milestones("squares_ready", "experts_normalised", "expert_columns", "expert_shifted", "expert_weights",
                       "expert_biases_taken"))
STEP.update(milestones("expert_exp", "expert_weights_turned"))


KEY_PART = (0, 0, 0, 1, 1, 2)
QUERY_PART = (0, 1, 2, 0, 1, 0)
STEPS = [9, 16, 114, 9]


def w3a_off():
    return 128 * 0 + 4 * BT + 3 * 1024 + 4 * 512


def kernel(**inputs):
    import numpy as np
    import ml_dtypes
    import concourse.bacc as bacc
    from concourse.bass_utils import run_bass_kernel_spmd

    v = {k: np.asarray(a) for k, a in inputs.items()}

    def col(a, k=1):
        return a.reshape(k, -1).T

    def rep(a, n):
        return np.broadcast_to(a.reshape(1, -1), (n, a.size))

    p = {}
    p["x"] = v["x"]
    p["ctx"] = v["ctx_1024"]
    p["ctxT"] = v["ctx_1024"].transpose(0, 2, 1)
    p["mask0"] = v["mask_1x1xSxS2_ik0"][0, 0].T
    p["mask2"] = v["mask_BxS2_bf1"].view(np.uint8)
    p["gates"] = rep(np.concatenate([v["g_xattn"], v["g_ffn"]]), 128)
    p["c_ident"] = np.eye(128, dtype=np.float32)
    p["c_identb"] = np.eye(128, dtype=ml_dtypes.bfloat16)
    p["c_low_rows"] = np.where(np.arange(32) // 8 % 2 == 1, -1.0, 0.0).astype(np.float32)[:, None]
    t = np.arange(T)
    p["c_before"] = (t[None, :] < t[:, None]).astype(np.float32)

    def pairs(a):
        return a.reshape(a.shape[0], 8, 2, HD).transpose(0, 2, 3, 1).reshape(a.shape[0], 128)

    def places(a):
        n = a.shape[0] // H
        return a.reshape(2, 4, 2, n, -1).transpose(0, 2, 1, 3, 4).reshape(a.shape)

    p["w_q0"] = pairs(v["L0_xattn_Wq"].T)
    p["w_k0"] = pairs(v["L0_xattn_Wk"].T)
    p["w_v0"] = v["L0_xattn_Wv"].T
    p["w_o0"] = places(v["L0_xattn_Wo"].T)
    p["w_bq0"] = pairs(v["L0_xattn_bq"].reshape(1, -1)).T
    p["w_bk0"] = pairs(v["L0_xattn_bk"].reshape(1, -1)).T
    p["w_bv0"] = places(col(v["L0_xattn_bv"]))
    p["w_bo0"] = rep(v["L0_xattn_bo"], 1)
    p["w_f0wr"] = col(v["L0_ffn_w_router"])
    p["w_f0W1"] = v["L0_ffn_W1"]
    p["w_f0b1"] = col(v["L0_ffn_b1"], 4)
    p["w_f0W2"] = v["L0_ffn_W2"].reshape(4, 128, D).transpose(1, 0, 2)
    p["w_f0b2"] = rep(v["L0_ffn_b2"], 1)
    w, b = v["L1_xattn_Wqkv"], v["L1_xattn_bqkv"].reshape(1, -1)
    wa, ba = v["L1_xattn_Wqkv_aux"], v["L1_xattn_bqkv_aux"].reshape(1, -1)
    p["w_q1"] = pairs(w[:, 0:D])
    p["w_k1"] = pairs(w[:, D:2 * D])
    p["w_v1"] = w[:, 2 * D:3 * D]
    p["w_ka1"] = pairs(wa[:, D:2 * D])
    p["w_va1"] = wa[:, 2 * D:3 * D]
    p["w_bq1"] = pairs(b[:, 0:D]).T
    p["w_bk1"] = pairs(b[:, D:2 * D]).T
    p["w_bv1"] = places(b[:, 2 * D:3 * D].T)
    p["w_bka1"] = pairs(ba[:, D:2 * D]).T
    p["w_bva1"] = places(ba[:, 2 * D:3 * D].T)
    p["w_o1"] = places(v["L1_xattn_Wo"])
    p["w_bo1"] = rep(v["L1_xattn_bo"], 1)
    p["w_g1"] = places(np.repeat(v["L1_xattn_g"], HD).reshape(128, 1))
    p["w_g1heads"] = rep(places(v["L1_xattn_g"]), 128)
    p["w_slots"] = v["L1_ffn_slot_init"]
    p["w_slot_scale"] = v["L1_ffn_slot_scale"]
    p["w_f1w1a"] = v["L1_ffn_w1"][:, 0:D].T
    p["w_f1w1b"] = v["L1_ffn_w1"][:, D:2 * D].T
    p["w_f1b1"] = col(v["L1_ffn_b1"])
    p["w_f1w2"] = v["L1_ffn_w2"].T
    p["w_f1b2"] = rep(v["L1_ffn_b2"], T)
    p["w_f1wih"] = v["L1_ffn_gru_wih"].T
    p["w_f1whh"] = v["L1_ffn_gru_whh"].T
    p["w_f1bih"] = col(v["L1_ffn_gru_bih"], 3)
    p["w_f1bhh"] = col(v["L1_ffn_gru_bhh"], 3)
    p["w_f1wv"] = v["L1_ffn_wv"].T
    p["w_f1bv"] = col(v["L1_ffn_bv"])
    p["w_f1wo"] = v["L1_ffn_wo"].T
    p["w_f1bo"] = rep(v["L1_ffn_bo"], 1)
    p["w_tau"] = rep(v["L1_ffn_tau"], T)
    p["w_lnxg"] = rep(v["L2_xattn_ln_x_g"], 128)
    p["w_lnxb"] = rep(v["L2_xattn_ln_x_b"], 128)
    p["w_lnlg"] = rep(v["L2_xattn_ln_l_g"], T)
    p["w_lnlb"] = rep(v["L2_xattn_ln_l_b"], T)
    p["w_gq2"] = np.tile(v["L2_xattn_qn_g"], 2).reshape(128, 1)
    p["w_gk2"] = np.tile(v["L2_xattn_kn_g"], 2).reshape(128, 1)
    p["w_q2"] = v["L2_xattn_Wq"]
    p["w_kv2"] = v["L2_xattn_Wkv"]
    p["w_k2T"] = v["L2_xattn_Wkv"][:, 0:H * DH].reshape(D, 8, 128).transpose(2, 1, 0)
    p["w_out2"] = v["L2_xattn_Wout"].reshape(8, 128, D).transpose(1, 0, 2)
    p["w_bo2"] = rep(v["L2_xattn_bout"], 1)
    p["w_f2fc"] = v["L2_ffn_W_fc"].T
    p["w_f2proj"] = v["L2_ffn_W_proj"].T.reshape(4, 128, D).transpose(1, 0, 2)
    p["w_f2lnw"] = rep(v["L2_ffn_ln_w"], T)
    p["w_f2lnb"] = rep(v["L2_ffn_ln_b"], T)
    p["w_qkv3"] = np.concatenate([v["L3_xattn_Wq"], v["L3_xattn_Wk"], v["L3_xattn_Wv"]], axis=1)
    p["w_k3T"] = v["L3_xattn_Wk"].T
    p["w_bq3"] = col(v["L3_xattn_bq"])
    p["w_b3"] = rep(np.concatenate([v["L3_xattn_bq"], v["L3_xattn_bk"], v["L3_xattn_bv"]]), T)
    p["w_emb"] = v["L3_ffn_uzman_embeddings"]
    p["w_embT"] = v["L3_ffn_uzman_embeddings"].T
    p["w_onb"] = rep(v["L3_ffn_onbellek_durumu"], T)
    e = np.arange(E3)
    p["w_etri"] = rep((e[None, :] < e[:, None]).astype(np.float32), T)
    p["w_f3b1"] = v["L3_ffn_b1"].reshape(E3, 4, 128).transpose(2, 0, 1)
    p["w_f3b2"] = v["L3_ffn_b2"]
    p["e_W1"] = v["L3_ffn_W1"].transpose(1, 0, 2)
    p["e_W2"] = v["L3_ffn_W2"].reshape(E3, 4, 128, D).transpose(2, 0, 1, 3)

    nc = bacc.Bacc("TRN2", target_bir_lowering=False, num_devices=1)
    arrays, A = {}, {}
    for name, a in p.items():
        a = np.ascontiguousarray(a)
        arrays["in_" + name] = a
        A[name] = nc.dram_tensor("in_" + name, a.shape, mybir.dt.from_np(a.dtype), kind="ExternalInput").ap()
    y = nc.dram_tensor("y", (B, T, D), F32, kind="ExternalOutput").ap()
    flamingo(nc, A, y)
    r = run_bass_kernel_spmd(nc, [arrays], core_ids=[0])
    return r.results[0]["y"]
```

```python
from contextlib import ExitStack

import concourse.bass as bass
from concourse import mybir

F32 = mybir.dt.float32
BF16 = mybir.dt.bfloat16
I32 = mybir.dt.int32
U8 = mybir.dt.uint8
ALU = mybir.AluOpType
ACT = mybir.ActivationFunctionType
AX = mybir.AxisListType

B, T, D = 8, 100, 128
H = 16
S2 = 1444
NCH = 12
CK = 121
LAST = S2 - (NCH - 1) * CK
KQ = S2 // 4
HD = 8
DH = 64
F0 = 512
NSLOT = 64
E3, H3 = 8, 512
BT = B * T
HALF = BT // 2
BANK = 512
LN_EPS = 1e-5
OFF = -1e30
GROUP = 4 * T
ROWS = [CK] * (NCH - 1) + [LAST]


def flamingo(nc, A, out):
    ctx = ExitStack()
    with ctx:
        def sb(name, shape, dt=F32):
            return ctx.enter_context(nc.sbuf_tensor(name, shape, dt))

        sems = {}

        def sem(name):
            if name not in sems:
                sems[name] = ctx.enter_context(nc.semaphore(name))
            return sems[name]

        x = sb("x", [T, B, D])
        xn = sb("xn", [T, B, D])
        xnT = sb("xnT", [D, BT])
        wideA = sb("wideA", [T, B, D])
        wideB = sb("wideB", [T, B + 1, D])
        small = sb("small", [128, 64])
        stat = sb("stat", [128, 8, 32])
        gates = sb("gates", [128, 8])

        ident = sb("ident", [128, 128])
        identb = sb("identb", [128, 128], BF16)
        low_rows = sb("low_rows", [32, 1])
        before = sb("before", [T, T])
        ones = sb("ones", [128, 128])

        W = {}
        for name, ap in A.items():
            if name.startswith("w_"):
                W[name[2:]] = sb(name, list(ap.shape))
        wr_bc = sb("wr_bc", [D, T])
        bv1 = sb("bv1", [128, 1])
        head_gates = sb("head_gates", [128, 2, H])
        ctxT = sb("ctxT", [D, (NCH + 1) * D])
        ctxk = sb("ctxk", [128, NCH + 1, D])
        M = sb("M", [128, 4 * GROUP])
        arena = sb("arena", [128, 13 * 1600])

        psum = ctx.enter_context(nc.psum_tensor("psum", [128, 8, BANK], F32))

        def carve(off, shape):
            n = 1
            for s in shape[1:]:
                n *= s
            v = arena[0:shape[0], off:off + n]
            if len(shape) == 3:
                v = v.rearrange("p (a b) -> p a b", a=shape[1])
            if len(shape) == 4:
                v = v.rearrange("p (a b c) -> p a b c", a=shape[1], b=shape[2])
            return v, off + n

        kst_w, o = carve(0, [128, 8 * S2 // 2])
        own_kst_w, o = carve(o, [128, 8 * T // 2])
        q1_w, o = carve(o, [128, 8 * T // 2])
        q2_w, o = carve(o, [128, 8 * T // 2])
        own_q2_w, o = carve(o, [128, 8 * T // 2])
        kparts_w, o = carve(o, [128, 3 * S2 // 2])
        qparts_w, o = carve(o, [128, 3 * (BT + T) // 2])
        own_kparts_w, o = carve(o, [128, 3 * (BT + T) // 2])
        Vo_w, o = carve(o, [128, NCH * H * 9])
        own_Vo_w, o = carve(o, [128, H * 9])
        P3, o = carve(o, [128, 3, 2 * GROUP])
        summed, o = carve(o, [128, GROUP])
        own_summed, o = carve(o, [128, GROUP])
        shares, o = carve(o, [T, 2, H])
        heads, o = carve(o, [T, D])
        own_heads, o = carve(o, [T, D])
        headsT, o = carve(o, [D, T])
        attended, o = carve(o, [T, (B + 1) * D])
        mx, o = carve(o, [T, 2, 32])
        flag, o = carve(o, [T, 32])
        hl_w, o = carve(o, [32, 2 * T // 2])
        high_w, o = carve(o, [32, T // 2])
        maskw, o = carve(o, [128, NCH * T // 2])
        assert o <= 13 * 1600, o
        Vo = Vo_w.rearrange("p (c h d) -> p c h d", c=NCH, h=H)
        own_Vo = own_Vo_w.rearrange("p (h d) -> p h d", h=H)
        keys_st = kst_w.bitcast(BF16).rearrange("p (h k) -> p h k", h=8)
        own_keys_st = own_kst_w.bitcast(BF16).rearrange("p (h k) -> p h k", h=8)
        q1 = q1_w.bitcast(BF16).rearrange("p (h q) -> p h q", h=8)
        q2 = q2_w.bitcast(BF16).rearrange("p (h q) -> p h q", h=8)
        own_q2 = own_q2_w.bitcast(BF16).rearrange("p (h q) -> p h q", h=8)
        kparts = kparts_w.bitcast(BF16).rearrange("p (a k) -> p a k", a=3)
        qparts = qparts_w.bitcast(BF16).rearrange("p (a k) -> p a k", a=3)
        own_kparts = own_kparts_w.bitcast(BF16).rearrange("p (a k) -> p a k", a=3)
        hl = hl_w.bitcast(BF16).rearrange("p (g q) -> p g q", g=2)
        high = high_w.bitcast(BF16)
        maskb = maskw.bitcast(BF16).rearrange("p (c q) -> p c q", c=NCH)
        lat = sb("lat", [T, B + 1, D])
        mB = sb("mB", [128, 4 * GROUP])
        xkT = sb("xkT", [D, S2 + T])
        qeff = sb("qeff", [D, H, T])
        Psum = sb("Psum", [128, 4 * GROUP])
        own_M = mB[0:T, :]
        kf = Psum[:, 0:S2]
        kr = qeff[:, :, :].rearrange("p h q -> p (h q)")[:, 0:S2]
        qf = Psum[:, 0:BT]
        qr = qeff[:, :, :].rearrange("p h q -> p (h q)")[:, 0:BT]
        Vn = xkT[:, 0:NCH * D].rearrange("p (c d) -> p c d", c=NCH)
        vs = lat[:, 0:B, :]
        maski = Psum[:, 0:NCH * T]

        hid, o = carve(0, [128, 4, BT])
        big1, o = carve(o, [128, 1024])
        big2, o = carve(o, [128, 1024])
        big3, o = carve(o, [128, 1024])
        g0, o = carve(o, [128, 512])
        g1, o = carve(o, [128, 512])
        g2, o = carve(o, [128, 512])
        g3, o = carve(o, [128, 512])
        w3a, o = carve(o, [D, E3, H3])
        w3b, o = carve(o, [128, E3, 4, D])
        assert o <= 13 * 1600, o
        acc3 = big1[0:T, :].rearrange("p (b d) -> p b d", b=B)
        q3T, o = carve(0, [D, BT])
        qe3, o = carve(o, [D, BT])
        qkv3, o = carve(o, [T, B, 3 * D])
        q3c, o = carve(o, [D, T])
        P1, o = carve(o, [T, S2])
        PT3, o = carve(o, [128, NCH, T])
        AT3, o = carve(o, [D, T])
        y3, o = carve(o, [T, D])
        st3, o = carve(o, [T, 64])
        assert o <= w3a_off(), o
        S_all, _ = carve(0, [128, 13, 4 * GROUP])
        sq = Psum[:, 0:1024]
        stage = ctxT[:, :].rearrange("p (c d) -> p c d", c=NCH + 1)
        scratch = qeff[:, :, :].rearrange("p h q -> p (h q)")[:, 0:NCH * D].rearrange("p (c d) -> p c d", c=NCH)
        qn = xn[:, :, :].rearrange("p b d -> p (b d)")
        qnt = xnT[:, :].rearrange("p (t q) -> p t q", t=8)
        values2 = wideA[:, :, :].rearrange("p b d -> p (b d)")
        values2T = xnT[:, :].rearrange("p (t q) -> p t q", t=8)
        attended2 = wideB[:, :, :].rearrange("p b d -> p (b d)")
        shares2 = sb("shares2", [T, 16])
        n2 = sb("n2", [128, 2, 16])
        rk = sb("rk", [128, 2, 16])
        kbias = sb("kbias", [128, B, NCH])
        kbc = sb("kbc", [128, NCH + 1])
        kmask = sb("kmask", [128, B, NCH], U8)

        block = ctx.enter_context(nc.Block())

        def bank(i, parts, cols):
            return psum[0:parts, i, 0:cols]

        def slot(s, parts, cols):
            return psum[0:parts, 2 * s:2 * s + 2, 0:cols]

        def bc(v, shape, at):
            return v.unsqueeze(at).broadcast_to(shape)

        def ternary_hidden(bb):
            if bb < 4:
                return hid[0:T, :, :].rearrange("p a b -> p (a b)")[:, bb * 512:(bb + 1) * 512]
            return (g0, g1, g2, g3)[bb - 4][0:T, :]

        class Ring:
            def __init__(self, name, size, plan):
                while len(plan) % size:
                    plan = plan + ["none"]
                self.name, self.size, self.plan = name, size, plan
                self.full = sem(name + "_slot_full")
                self.emptied = {e: sem(f"{name}_slot_emptied_by_{e}") for e in ("act", "dve")}
                self.per = {e: plan.count(e) for e in ("act", "dve")}
                self.nfull = sum(p != "none" for p in plan)

            def before_fill(self, pe, b, n):
                m = n - self.size
                lap = 1 if m >= 0 else 0
                e = self.plan[m % len(self.plan)]
                if e == "none":
                    return
                k = self.plan[:m % len(self.plan) + 1].count(e)
                pe.wait_ge(self.emptied[e], (b + lap) * self.per[e] + k)

            def full_count(self, b, n):
                return b * self.nfull + n + 1

            def emptied_count(self, b, n):
                e = self.plan[n]
                return (b + 1) * self.per[e] + self.plan[:n + 1].count(e)

        class Uses:
            def __init__(self, name, uses, tail):
                self.uses, self.at = uses, {u[0:2]: n for n, u in enumerate(uses)}
                self.full = sem(name + "_slot_full")
                self.emptied = {e: sem(f"{name}_slot_emptied_by_{e}") for e in ("act", "dve")}
                who = [u[3] for u in uses]
                self.per = {e: who.count(e) for e in self.emptied}
                self.head = {e: who[:tail].count(e) for e in self.emptied}
                self.nfull, self.nhead = len(uses), tail

            def slot_of(self, *use):
                return self.uses[self.at[use]][2]

            def before_fill(self, pe, b, *use):
                n = self.at[use]
                same = [m for m, u in enumerate(self.uses) if u[2] == self.uses[n][2]]
                earlier = [m for m in same if m < n]
                m, lap = (earlier[-1], b) if earlier else (same[-1], b - 1)
                pe.wait_ge(self.emptied[self.uses[m][3]], self.emptied_count(lap, *self.uses[m][0:2]))

            def full_count(self, b, *use):
                return (b + 1) * self.nfull + self.at[use] + 1

            def emptied_count(self, b, *use):
                n = self.at[use]
                e = self.uses[n][3]
                return (b + 1) * self.per[e] + sum(u[3] == e for u in self.uses[:n + 1])

        def layer2_uses():
            order = [("norm", 0, "act")]
            for c in range(NCH + 1):
                if c < NCH:
                    order.append(("norm", c + 1, "act"))
                order += [("score", 2 * c, "dve"), ("score", 2 * c + 1, "dve")]
            order += [("turn", 0, "dve"), ("turn", 1, "dve"), ("row", 0, "dve"), ("shift", 0, "act"), ("shift", 1, "act")]
            tail = [("context", 0, "act"), ("context", 1, "act"), ("query", 0, "dve"), ("turned", 0, "act"),
                    ("carried", 0, "act"), ("carried", 1, "act"), ("sum", 0, "dve")]
            return ([(k, i, n % 3, e) for n, (k, i, e) in enumerate(order)]
                    + [(k, i, n % 2, e) for n, (k, i, e) in enumerate(tail)], len(order))

        DVE_SUMS = (6, 9, 12)
        POOL_SUMS = [c for c in range(NCH + 1) if c not in DVE_SUMS]
        VALUES, VALUES_TURNED, PROJECTED = 1, 4, 7
        CENTRE, VARIANCE, SCALE = 0, 3, 5
        TURN, QUERY = 8, 10

        def attention_order(layer):
            units = [("max", 0, u, "dve") for u in range(2 * NCH)]
            head = []
            if layer == 1:
                head = [("max", 1, 0, "dve"), ("max", 1, 1, "dve")]
                units[16:16] = [("exp", 1, 0, "act"), ("exp", 1, 1, "act")]
                units[8:8] = [("turn", 1, 0, "dve"), ("turn", 1, 1, "dve"), ("row", 1, 0, "dve")]
            return (head + units
                    + [("turn", 0, 0, "dve"), ("turn", 0, 1, "dve"), ("keys", 0, 0, "act"), ("keys", 0, 1, "act"),
                       ("row", 0, 0, "dve"), ("values", 0, 0, "dve"), ("values", 0, 1, "dve")]
                    + [("exp", 0, u, "act") for u in range(2 * NCH)])

        FINISH = [(1, 5, 9), (1, 4, 7, 10)]
        OWN_WEIGHED, OWN_TAKEN = 19, 22

        ORDER = [attention_order(0), attention_order(1)]

        def position(layer, kind, g, u):
            return [k[0:3] for k in ORDER[layer]].index((kind, g, u))

        rings = [Ring("a0", 3, [k[3] for k in ORDER[0]]), Ring("a1", 3, [k[3] for k in ORDER[1]]),
                 Uses("a2", *layer2_uses()),
                 Ring("a3", 3, ["act", "act", "dve", "dve", "dve"])]

        @block.sync
        def _(sp):
            sp.dma_start(x[:, :, :], A["x"].rearrange("b t d -> t b d")).then_inc(sem("x_loaded"), 16)
            n = 0
            for tile, name in ((ident, "c_ident"), (identb, "c_identb"), (low_rows, "c_low_rows"),
                               (before, "c_before"), (gates, "gates")):
                sp.dma_start(tile[:, :], A[name]).then_inc(sem("constants_loaded"), 16)
            for name in W:
                t = W[name]
                sl = tuple(slice(None) for _ in t.shape)
                sp.dma_start(t[sl], A["w_" + name]).then_inc(sem("weights_loaded"), 16)
                n += 1
            sp.dma_start(maski.bitcast(I32).rearrange("p (c q) -> p c q", c=NCH)[0:CK, 0:NCH - 1, :],
                         A["mask0"][0:(NCH - 1) * CK, :].rearrange("(c p) q -> p c q", p=CK)
                         ).then_inc(sem("masks_loaded"), 16)
            sp.dma_start(maski.bitcast(I32).rearrange("p (c q) -> p c q", c=NCH)[0:LAST, NCH - 1, :],
                         A["mask0"][(NCH - 1) * CK:S2, :]).then_inc(sem("masks_loaded"), 16)
            sp.wait_ge(sem("key_mask_cleared"), 1)
            with nc.allow_non_contiguous_dma(reason="a small mask, keys onto partitions"):
                for bb in range(B):
                    sp.dma_start(kmask[0:CK, bb, 0:NCH - 1],
                                 A["mask2"][bb, 0:(NCH - 1) * CK].rearrange("(c p) -> p c", p=CK)
                                 ).then_inc(sem("masks_loaded"), 16)
                    sp.dma_start(kmask[0:LAST, bb, NCH - 1:NCH],
                                 A["mask2"][bb, (NCH - 1) * CK:S2].rearrange("(c p) -> p c", c=1)
                                 ).then_inc(sem("masks_loaded"), 16)

            def load_keys(b, ctxk=ctxk):
                sp.dma_start(ctxk[0:CK, 0:NCH - 1, :],
                             A["ctx"][b, 0:(NCH - 1) * CK, :].rearrange("(c p) d -> p c d", p=CK)
                             ).then_inc(sem("ctx_keys_loaded"), 16)
                sp.dma_start(ctxk[0:LAST, NCH - 1, :], A["ctx"][b, (NCH - 1) * CK:S2, :]
                             ).then_inc(sem("ctx_keys_loaded"), 16)

            def stack_keys(layer, b, half):
                k0, k1 = (0, 6 * CK) if half == 0 else (6 * CK, S2)
                for par in range(2):
                    for r, part in enumerate(KEY_PART):
                        sp.dma_start(keys_st[64 * par + 8 * r:64 * par + 8 * r + 8, :, k0:k1],
                                     kparts[64 * par:64 * par + 64, part, k0:k1]
                                     ).then_inc(sem(f"a{layer}_keys_stacked_{half}"), 16)

            def stack_tokens(dst, src, parts, first, signal):
                for par in range(2):
                    for r, part in enumerate(parts):
                        sp.dma_start(dst[64 * par + 8 * r:64 * par + 8 * r + 8, :, :],
                                     src[64 * par:64 * par + 64, part, :][:, bass.ds(first, T)]
                                     ).then_inc(sem(signal), 16)

            def count(v, top=1 << 20):
                return v if isinstance(v, int) else sp.snap(sp.to_reg(v), min_val=0, max_val=top)

            def place_shift(layer, g, this_one):
                dst = (q2, own_q2)[g]
                sp.wait_ge(sem(f"a{layer}_shift_ready_{g}"), this_one)
                for par in range(2):
                    sp.dma_start(dst[64 * par + 48:64 * par + 50, :, :], hl[16 * par:16 * par + 16, g, :]
                                 ).then_inc(sem(f"a{layer}_shift_placed_{g}"), 16)

            sp.dma_start(ctxT[:, 0:S2], A["ctxT"][0]).then_inc(sem("ctxT_loaded"), 16)
            for layer in (0, 1):
                ring = rings[layer]
                p = f"a{layer}_"
                if layer == 1:
                    sp.wait_ge(ring_before.full, ring_before.full_count(B - 1, position(0, "values", 0, 1)))
                    sp.dma_start(ctxT[:, 0:S2], A["ctxT"][0]).then_inc(sem("ctxT_loaded"), 16)
                ring_before = ring
                sp.wait_ge(sem(p + "first_projected"), 1)
                sp.dma_start(ctxT[:, 0:S2], A["ctxT"][1]).then_inc(sem("ctxT_loaded"), 16)
                sp.wait_ge(sem(p + "ones_set"), 1)
                sp.wait_ge(sem(p + "keys_split"), 1)
                stack_keys(layer, 0, 0)
                stack_keys(layer, 0, 1)
                sp.wait_ge(sem(p + "query_parts_ready"), 1)
                stack_tokens(q1, qparts, QUERY_PART, 0, p + "queries_stacked")
                if layer == 1:
                    stack_tokens(own_keys_st, own_kparts, KEY_PART, 0, p + "own_keys_stacked")

                def one_sequence(b, next_ctx):
                    this_one, next_one = count(b + 1), count(b + 2)
                    first = count((b + 1) * T, BT)
                    full = {k: count(ring.full_count(b, position(layer, *k)))
                            for k in [("values", 0, 1), ("exp", 0, NCH - 1), ("exp", 0, 2 * NCH - 1)]}
                    if layer == 1:
                        place_shift(1, 1, this_one)
                    place_shift(layer, 0, this_one)
                    sp.wait_ge(ring.full, full["values", 0, 1])
                    sp.dma_start(ctxT[:, 0:S2], A["ctxT"][next_ctx]).then_inc(sem("ctxT_loaded"), 16)
                    sp.wait_ge(sem(p + "queries_copied"), this_one)
                    stack_tokens(q1, qparts, QUERY_PART, first, p + "queries_stacked")
                    if layer == 1:
                        stack_tokens(own_keys_st, own_kparts, KEY_PART, first, p + "own_keys_stacked")
                    sp.wait_ge(sem(p + "keys_split"), next_one)
                    sp.wait_ge(ring.full, full["exp", 0, NCH - 1])
                    stack_keys(layer, b + 1, 0)
                    sp.wait_ge(ring.full, full["exp", 0, 2 * NCH - 1])
                    stack_keys(layer, b + 1, 1)

                with sp.Fori(0, B - 2) as b:
                    one_sequence(b, b + 2)
                one_sequence(B - 2, B - 1)
                if layer == 1:
                    place_shift(1, 1, B)
                place_shift(layer, 0, B)
            sp.wait_ge(sem("stage_cleared"), 1)
            load_keys(0, stage)
            with sp.Fori(1, B) as b:
                sp.wait_ge(sem("a2_stage_copied"), b)
                load_keys(b, stage)
            sp.wait_ge(sem("a2_stage_copied"), B)
            load_keys(0, stage)
            sp.wait_ge(sem("a2_stage_copied"), B + 1)
            load_keys(0)
            sp.dma_start(ctxT[:, 0:S2], A["ctxT"][0]).then_inc(sem("ctxT_loaded"), 16)
            sp.wait_ge(sem("arena_free_for_experts"), 1)
            sp.dma_start(w3a, A["e_W1"]).then_inc(sem("experts_loaded"), 16)
            sp.dma_start(w3b, A["e_W2"]).then_inc(sem("experts_loaded"), 16)
            with sp.Fori(1, B) as b:
                sp.wait_ge(sem("a3_ctx_used"), b)
                load_keys(b)
                sp.dma_start(ctxT[:, 0:S2], A["ctxT"][b]).then_inc(sem("ctxT_loaded"), 16)
            sp.wait_ge(sem("y_ready"), 1)
            sp.dma_start(out.rearrange("b t d -> t b d"), x[:, :, :]).then_inc(sem("y_stored"), 16)
            sp.wait_ge(sem("y_stored"), 16)

        NW = len(W) * 16
        CTX_LOADS = B + 1

        @block.tensor
        def _(pe):
            def mm(o, l, r, start=True, stop=True, **k):
                return pe.matmul(o, l, r, start=start, stop=stop, skip_group_check=True, **k)

            def turn_xn(n):
                pe.wait_ge(sem("xn_ready"), n + 1)
                n = n if n < 4 else n - 1
                for half in range(2):
                    for i in range(4):
                        m = pe.transpose(bank(half, D, BANK)[:, i * T:(i + 1) * T], xn[:, 4 * half + i, :],
                                         ident[0:T, 0:T])
                    m.then_inc(sem("xnT_in_psum"), 1)
                pe.wait_ge(sem("xnT_ready"), 2 * n + 2)

            def project(first, w, ws, signal):
                for half in range(2):
                    m = mm(bank(first + half, ws, HALF), w, xnT[:, half * HALF:(half + 1) * HALF])
                m.then_inc(sem(signal), 1)

            def attention(layer):
                ring = rings[layer]
                wk, wv = (W["k0"], W["v0"]) if layer == 0 else (W["ka1"], W["va1"])
                wo = W["o0"] if layer == 0 else W["o1"]
                bo = W["bo0"] if layer == 0 else W["bo1"]
                p = f"a{layer}_"
                pe.wait_ge(sem("ctxT_loaded"), 16 * CTX_LOADS * layer + 16)
                for i in range(4):
                    m = mm(bank(i, D, KQ), wk[:, :], ctxT[:, i * KQ:(i + 1) * KQ])
                m.then_inc(sem(p + "first_keys"), 1)
                for c in range(NCH):
                    if c == 8:
                        pe.wait_ge(sem(p + "key_parts_1"), 1)
                    bk = (4, 5, 0)[c // 4]
                    m = mm(bank(bk, ROWS[c], BANK)[:, (c % 4) * D:(c % 4 + 1) * D],
                           ctxT[:, c * CK:c * CK + ROWS[c]], wv[:, :])
                m.then_inc(sem(p + "first_projected"), 1)
                pe.wait_ge(sem(p + "values_turned"), 1)
                nf = 3 + layer

                def finish(b, k):
                    pe.wait_ge(sem(p + "heads_by_dve"), b * nf + k + 1)
                    if k == 0:
                        pe.wait_ge(sem(p + "sums_copied"), (layer + 1) * b + 1)
                    if k < layer + 1:
                        for j in range(4):
                            m = pe.transpose(bank(7, T, BANK)[:, j * 128:(j + 1) * 128],
                                             (summed, own_summed)[k][:, j * T:(j + 1) * T], ident[:, :])
                    elif k == layer + 1:
                        m = pe.transpose(bank(7, D, T), heads[:, :], ident[0:T, 0:T])
                    else:
                        mm(bank(7, T, D), headsT[:, :], wo[:, :], stop=False)
                        m = mm(bank(7, T, D), ones[0:1, 0:T], bo[0:1, :], start=False)
                    m.then_inc(sem(p + "heads_by_pe"), 1)

                with pe.Fori(0, B) as b:
                    def scores(n, g, u, rows_q, q, signal=True):
                        s = n % 3
                        c, hh = u // 2, u % 2
                        r = ROWS[c] if g == 0 else T
                        kst = keys_st if g == 0 else own_keys_st
                        masked = layer == 0
                        if masked:
                            for par in range(2):
                                mm(bank(2 * s + par, r, GROUP), identb[0:r, 0:r],
                                   bc(maskb[0:r, c, :], [r, 4, T], 1), stop=False)
                        for t in range(4):
                            for par in range(2):
                                hp = 4 * hh + t
                                m = mm(bank(2 * s + par, r, GROUP)[:, t * T:(t + 1) * T],
                                       kst[64 * par:64 * par + rows_q, hp, c * CK:c * CK + r],
                                       q[64 * par:64 * par + rows_q, hp, :], start=not masked)
                        m.then_inc(ring.full, 1)

                    def weigh(g, w, done):
                        c, hh = w // 2, w % 2
                        r = ROWS[c] if g == 0 else T
                        size = NCH if g == 0 else 1
                        pe.wait_ge(ring.emptied["act"], ring.emptied_count(b, position(layer, "exp", g, w)))
                        if w == 0:
                            pe.wait_ge(sem(p + "values_placed"), b + 1)
                            if g == 0:
                                pe.wait_ge(sem(p + "sums_copied"), (layer + 1) * b + 1)
                            else:
                                pe.wait_ge(sem(p + "heads_by_dve"), (b + 1) * nf + 1)
                        for par in range(2):
                            for t in range(4):
                                h = 8 * hh + 2 * t + par
                                k = par * GROUP + t * T
                                col = (2 * hh + par) * T
                                m = mm(psum[32 * t:32 * t + 9, 6 + g, col:col + T],
                                       Vo[0:r, c, h, :] if g == 0 else own_Vo[0:r, h, :],
                                       P3[0:r, done % 3, k:k + T],
                                       start=(c, hh, par) == (0, 0, 0), stop=c == size - 1)
                        m.then_inc(sem(p + "probs_used"), 1)

                    done = 0
                    for n, (kind, g, u, _) in enumerate(ORDER[layer]):
                        s = n % 3
                        ring.before_fill(pe, b, n)
                        if kind == "max":
                            if g == 1 and u == 0:
                                pe.wait_ge(sem(p + "own_keys_stacked"), 16 * 12 * (b + 1))
                            if (g, u) == ((0, 0) if layer == 0 else (1, 0)):
                                pe.wait_ge(sem(p + "queries_stacked"), 16 * 12 * (b + 1))
                            if g == 0 and u in (0, NCH):
                                pe.wait_ge(sem(p + f"keys_stacked_{u // NCH}"), 16 * 12 * (b + 1))
                            scores(n, g, u, 48, q1)
                            if g == 0 and u in FINISH[layer]:
                                finish(b, FINISH[layer].index(u))
                            if layer == 1 and g == 0 and u == OWN_WEIGHED:
                                for w in range(2):
                                    weigh(1, w, done)
                                    done += 1
                        elif kind == "turn":
                            r = CK if g == 0 else T
                            src = M if g == 0 else own_M
                            if u == 0:
                                last = 2 * NCH - 1 if g == 0 else 1
                                pe.wait_ge(ring.emptied["dve"], ring.emptied_count(b, position(layer, "max", g, last)))
                            for k in range(8):
                                h = 8 * u + k
                                m = pe.transpose(bank(2 * s + k // 4, T, BANK)[:, (k % 4) * CK:(k % 4) * CK + r],
                                                 src[0:r, h * T:(h + 1) * T], ident[0:r, 0:r])
                            m.then_inc(ring.full, 1)
                        elif kind == "row":
                            pe.wait_ge(sem(p + f"max_ready_{g}"), b + 1)
                            pe.transpose(bank(2 * s, 32, T), mx[:, g, :], ident[0:T, 0:T]).then_inc(ring.full, 1)
                        elif kind == "keys":
                            if u == 0:
                                pe.wait_ge(sem("ctxT_loaded"), 16 * CTX_LOADS * layer + 16 * b + 32)
                            for i in range(2):
                                c0 = (2 * u + i) * KQ
                                m = mm(bank(2 * s + i, D, KQ), wk[:, :], ctxT[:, c0:c0 + KQ])
                            m.then_inc(ring.full, 1)
                        elif kind == "values":
                            for k, c in enumerate(range(8) if u == 0 else range(8, NCH)):
                                m = mm(bank(2 * s + k // 4, ROWS[c], BANK)[:, (k % 4) * D:(k % 4 + 1) * D],
                                       ctxT[:, c * CK:c * CK + ROWS[c]], wv[:, :])
                            m.then_inc(ring.full, 1)
                        else:
                            if u == 0:
                                pe.wait_ge(sem(p + "queries_copied"), b + 1)
                                pe.wait_ge(sem(p + f"shift_placed_{g}"), 32 * (b + 1))
                            scores(n, g, u, 50, (q2, own_q2)[g])
                            if g == 0 and u >= 2:
                                weigh(g, u - 2, done)
                                done += 1
                            if g == 0 and u == 2 * NCH - 1:
                                for w in (u - 1, u):
                                    weigh(g, w, done)
                                    done += 1
                for k in range(nf):
                    finish(B, k)

            pe.wait_ge(sem("constants_loaded"), 5 * 16)
            pe.wait_ge(sem("weights_loaded"), NW)
            turn_xn(0)
            project(2, W["q0"][:, :], D, "q0_projected")
            pe.wait_ge(sem("layer0_setup"), 1)
            attention(0)
            turn_xn(1)
            project(2, wr_bc[:, :], T, "router_scores")
            for k in range(8):
                f, half = k // 2, k % 2
                if k >= 4:
                    pe.wait_ge(sem("ffn0_hidden"), k - 3)
                mm(bank(4 + k % 4, 128, HALF), W["f0W1"][:, f * 128:(f + 1) * 128],
                   xnT[:, half * HALF:(half + 1) * HALF]).then_inc(sem("ffn0_hidden_psum"), 1)
            pe.wait_ge(sem("ffn0_hidden"), 8)
            for bb in range(B):
                o = bank(bb // 4, T, BANK)[:, (bb % 4) * D:(bb % 4 + 1) * D]
                for f in range(4):
                    mm(o, hid[:, f, bb * T:(bb + 1) * T], W["f0W2"][:, f, :], start=f == 0, stop=False)
                m = mm(o, ones[0:1, 0:T], W["f0b2"][0:1, :], start=False)
            m.then_inc(sem("ffn0_out"), 1)
            turn_xn(2)
            project(2, W["q1"][:, :], D, "q1_projected")
            project(4, W["k1"][:, :], D, "k1_projected")
            for bb in range(B):
                m = mm(bank(6 + bb // 4, T, BANK)[:, (bb % 4) * D:(bb % 4 + 1) * D],
                       xnT[:, bb * T:(bb + 1) * T], W["v1"][:, :])
            m.then_inc(sem("v1_projected"), 1)
            pe.wait_ge(sem("layer1_setup"), 1)
            attention(1)
            turn_xn(3)
            pe.wait_ge(sem("slots_by_dve"), STEP["slots_scaled"])
            mm(bank(2, D, 1), g0[0:NSLOT, 0:D], ones[0:NSLOT, 0:1])
            pe.transpose(bank(3, D, NSLOT), g0[0:NSLOT, 0:D], ident[0:NSLOT, 0:NSLOT]).then_inc(sem("slots_by_pe"), 1)
            pe.wait_ge(sem("slots_by_dve"), STEP["slot_mean"])
            mm(bank(2, NSLOT, 1), W["f1w1b"][:, :], small[:, 8:9]).then_inc(sem("slots_by_pe"), 1)
            for half in range(2):
                m = mm(bank(4 + half, NSLOT, HALF), W["f1w1a"][:, :], xnT[:, half * HALF:(half + 1) * HALF])
            m.then_inc(sem("slots_by_pe"), 1)
            pe.wait_ge(sem("f1_hidden"), 2)
            for bb in range(B):
                m = mm(bank(6, T, BANK)[:, bb * NSLOT:(bb + 1) * NSLOT], hid[0:NSLOT, 0, bb * T:(bb + 1) * T],
                       W["f1w2"][:, :])
            m.then_inc(sem("slots_by_pe"), 1)
            pe.wait_ge(sem("slots_by_dve"), STEP["slotsT_ready"])
            for g in range(3):
                m = mm(bank(7, D, 3 * NSLOT)[:, g * NSLOT:(g + 1) * NSLOT], W["f1whh"][:, g * D:(g + 1) * D],
                       g1[:, 0:NSLOT])
            m.then_inc(sem("slots_by_pe"), 1)
            pe.wait_ge(sem("slots_by_dve"), STEP["alpha_ready"])
            for bb in range(B):
                al = big1[0:T, bb * NSLOT:(bb + 1) * NSLOT]
                mm(bank(0, D, BANK)[:, bb * NSLOT:(bb + 1) * NSLOT], xn[:, bb, :], al)
            mm(bank(1, D, BANK), ones[0:T, :], big1[0:T, 0:B * NSLOT]).then_inc(sem("slots_by_pe"), 1)
            for bb in range(B):
                m = pe.transpose(bank(4 + bb // 4, NSLOT, BANK)[:, (bb % 4) * T:(bb % 4 + 1) * T],
                                 big1[0:T, bb * NSLOT:(bb + 1) * NSLOT], ident[0:T, 0:T])
            m.then_inc(sem("slots_by_pe"), 1)
            pe.wait_ge(sem("slots_by_dve"), STEP["gi_ready"])
            for g, bk in enumerate((2, 3, 6)):
                m = mm(bank(bk, D, BANK), W["f1wih"][:, g * D:(g + 1) * D], g3[:, :])
            m.then_inc(sem("slots_by_pe"), 1)
            pe.wait_ge(sem("slots_by_dve"), STEP["slots_new"])
            mm(bank(0, D, BANK), W["f1wv"][:, :], g2[:, :]).then_inc(sem("slots_by_pe"), 1)
            pe.wait_ge(sem("slots_by_act"), STEP["slot_values"])
            for bb in range(B):
                m = mm(bank(2 + bb // 4, NSLOT, BANK)[:, (bb % 4) * D:(bb % 4 + 1) * D],
                       g3[:, bb * NSLOT:(bb + 1) * NSLOT], W["f1wo"][:, :])
            m.then_inc(sem("slots_by_pe"), 1)
            pe.wait_ge(sem("slots_by_act"), STEP["slot_outputs"])
            for bb in range(B):
                o = bank(6 + bb // 4, T, BANK)[:, (bb % 4) * D:(bb % 4 + 1) * D]
                mm(o, hid[0:NSLOT, 1, bb * T:(bb + 1) * T], big2[0:NSLOT, bb * D:(bb + 1) * D], stop=False)
                m = mm(o, ones[0:1, 0:T], W["f1bo"][0:1, :], start=False)
            m.then_inc(sem("ffn1_out"), 1)
            ring = rings[2]
            rows = ROWS + [T]

            def columns2(c):
                return xkT[:, min(c * CK, S2):min(c * CK, S2) + rows[c]]

            def fill(b, *use):
                ring.before_fill(pe, b, *use)
                return ring.slot_of(*use)

            def filled(m):
                m.then_inc(ring.full, 1)

            def turn_context(b):
                pe.wait_ge(sem("a2_keys_normalised"), b + 2)
                for half, chunks in enumerate((range(0, 8), range(8, 13))):
                    s = fill(b, "context", half)
                    for k, c in enumerate(chunks):
                        m = pe.transpose(bank(2 * s + k // 4, D, BANK)[:, (k % 4) * CK:(k % 4) * CK + rows[c]],
                                         stage[0:rows[c], c, :], ident[0:rows[c], 0:rows[c]])
                    filled(m)

            def project_queries(b):
                pe.wait_ge(ring.emptied["act"], ring.emptied_count(b, "context", 1))
                s = fill(b, "query", 0)
                for i in range(2):
                    m = mm(bank(2 * s + i, T, BANK), xkT[:, S2:S2 + T], W["q2"][:, i * BANK:(i + 1) * BANK])
                filled(m)

            def carry_queries(b):
                pe.wait_ge(sem("a2_q_normalised"), b + 2)
                s = fill(b, "turned", 0)
                for t in range(8):
                    m = pe.transpose(bank(2 * s + t // 4, D, BANK)[:, (t % 4) * T:(t % 4 + 1) * T],
                                     qn[:, t * D:(t + 1) * D], ident[0:T, 0:T])
                filled(m)
                pe.wait_ge(ring.emptied["act"], ring.emptied_count(b, "turned", 0))
                for half in range(2):
                    s = fill(b, "carried", half)
                    for t in range(4):
                        for par in range(2):
                            tt = 4 * half + t
                            m = mm(bank(2 * s + par, D, BANK)[:, t * T:(t + 1) * T],
                                   W["k2T"][64 * par:64 * par + 64, tt, :], qnt[64 * par:64 * par + 64, tt, :])
                    filled(m)

            def finish2(b, k):
                if k == 0:
                    pe.wait_ge(sem("a2_contexts_copied_by_dve"), b + 1)
                    pe.wait_ge(sem("a2_contexts_copied_by_act"), b + 1)
                    for h in range(H):
                        m = mm(bank(6 + h // 8, T, BANK)[:, (h % 8) * DH:(h % 8 + 1) * DH],
                               mB[:, h * T:(h + 1) * T], W["kv2"][:, H * DH + h * DH:H * DH + (h + 1) * DH])
                elif k == 1:
                    pe.wait_ge(sem("a2_heads_by_dve"), 2 * b + 1)
                    for t in range(8):
                        m = pe.transpose(bank(6 + t // 4, D, BANK)[:, (t % 4) * T:(t % 4 + 1) * T],
                                         values2[:, t * D:(t + 1) * D], ident[0:T, 0:T])
                else:
                    pe.wait_ge(sem("a2_heads_by_act"), b + 1)
                    for t in range(8):
                        mm(bank(6, T, D), values2T[:, t, :], W["out2"][:, t, :], start=t == 0, stop=False)
                    m = mm(bank(6, T, D), ones[0:1, 0:T], W["bo2"][0:1, :], start=False)
                m.then_inc(sem("a2_heads_by_pe"), 1)

            pe.sem_inc(ring.full, ring.nhead)
            turn_context(-1)
            project_queries(-1)
            carry_queries(-1)
            pe.wait_ge(ring.emptied["act"], ring.emptied_count(-1, "carried", 1))
            pe.sem_inc(ring.full, 1)
            with pe.Fori(0, B) as b:
                def norms(c):
                    s = fill(b, "norm", c)
                    if s == 2 and c <= 2:
                        pe.wait_ge(sem("a2_contexts_copied_by_dve"), b + 1)
                    for i in range(2):
                        m = mm(bank(2 * s + i, rows[c], BANK), columns2(c), W["kv2"][:, i * BANK:(i + 1) * BANK])
                    filled(m)

                norms(0)
                pe.wait_ge(ring.emptied["act"], ring.emptied_count(b - 1, "carried", 1))
                for c in range(13):
                    if c < NCH:
                        norms(c + 1)
                    for half in range(2):
                        s = fill(b, "score", 2 * c + half)
                        if s == 2 and c == 0:
                            pe.wait_ge(sem("a2_contexts_copied_by_dve"), b + 1)
                        for i in range(2):
                            j = 2 * half + i
                            m = mm(bank(2 * s + i, rows[c], GROUP), columns2(c), qeff[:, 4 * j:4 * j + 4, :])
                        filled(m)
                    if c in (VALUES, VALUES_TURNED, PROJECTED):
                        finish2(b, (VALUES, VALUES_TURNED, PROJECTED).index(c))
                pe.wait_ge(sem("a2_column_max"), b + 1)
                for half in range(2):
                    s = fill(b, "turn", half)
                    for k in range(8):
                        h = 8 * half + k
                        m = pe.transpose(bank(2 * s + k // 4, T, BANK)[:, (k % 4) * CK:(k % 4 + 1) * CK],
                                         M[0:CK, h * T:(h + 1) * T], ident[0:CK, 0:CK])
                    filled(m)
                pe.wait_ge(sem("a2_max_ready"), b + 1)
                s = fill(b, "row", 0)
                filled(pe.transpose(bank(2 * s, 16, T), stat[0:T, 0, 0:16], ident[0:T, 0:T]))
                pe.wait_ge(sem("a2_shift_ready"), b + 1)
                for half in range(2):
                    s = fill(b, "shift", half)
                    for i in range(2):
                        j = 2 * half + i
                        m = mm(bank(2 * s + i, 128, GROUP), ones[0:16, :], M[0:16, j * GROUP:(j + 1) * GROUP])
                    filled(m)
                last = [u for u in ring.uses[0:ring.nhead] if u[2] == 2][-1]
                for c in range(13):
                    r = rows[c]
                    pe.wait_ge(sem("a2_probs_ready"), b * 13 + c + 1)
                    if c == 0:
                        pe.wait_ge(ring.emptied[last[3]], ring.emptied_count(b, *last[0:2]))
                        pe.wait_ge(sem("a2_heads_by_dve"), 2 * b + 2)
                        pe.wait_ge(sem("a2_stage_copied"), b + 1)
                    for j in range(4):
                        m = mm(bank(4 + j, D, GROUP), ctxk[0:r, c, :], S_all[0:r, c, j * GROUP:(j + 1) * GROUP],
                               start=c == 0, stop=c == 12)
                    if c == 12:
                        m.then_inc(sem("a2_keys_used"), 1)
                    if c == TURN:
                        turn_context(b)
                    if c == QUERY:
                        project_queries(b)
                carry_queries(b)
                pe.wait_ge(sem("a2_pool_summed"), (len(POOL_SUMS) - 1) * (b + 1))
                pe.wait_ge(sem("a2_dve_summed"), b + 1)
                s = fill(b, "sum", 0)
                for h in range(H):
                    for part, tile in enumerate((Psum, M)):
                        m = mm(bank(2 * s, T, H)[:, h:h + 1], tile[0:CK, h * T:(h + 1) * T], ones[0:CK, 0:1],
                               start=h + part == 0, stop=part == 1)
                filled(m)
            for k in range(3):
                finish2(B, k)
            pe.wait_ge(sem("ternary_sums"), 1)
            mm(bank(2, 128, 2), ones[:, :], small[:, 16:18]).then_inc(sem("ternary_scale"), 1)
            turn_xn(5)
            pe.wait_ge(sem("ternary_ready"), 1)
            for bb in range(B):
                if bb >= 2:
                    pe.wait_ge(sem("f2_gelu"), bb - 1)
                mm(bank(2 + bb % 2, T, BANK), xnT[:, bb * T:(bb + 1) * T], W["f2fc"][:, :]
                   ).then_inc(sem("f2_hidden_psum"), 1)
            for bb in range(B):
                pe.wait_ge(sem("f2_normalised"), bb + 1)
                if bb >= 2:
                    pe.wait_ge(sem("f2_turned"), bb - 1)
                for f in range(4):
                    m = pe.transpose(bank(4 + bb % 2, 128, BANK)[:, f * T:(f + 1) * T],
                                     big1[0:T, (bb % 2) * 512 + f * 128:(bb % 2) * 512 + (f + 1) * 128],
                                     ident[0:T, 0:T])
                m.then_inc(sem("f2_turned_psum"), 1)
                pe.wait_ge(sem("f2_turned"), bb + 1)
                o = bank(6 + bb // 4, T, BANK)[:, (bb % 4) * D:(bb % 4 + 1) * D]
                for f in range(4):
                    m = mm(o, big2[:, (bb % 2) * 400 + f * T:(bb % 2) * 400 + (f + 1) * T], W["f2proj"][:, f, :],
                           start=f == 0, stop=f == 3)
            m.then_inc(sem("ffn2_out"), 1)
            turn_xn(6)
            project(2, W["qkv3"][:, 0:D], D, "q3T_psum")
            for bb in range(B):
                if bb >= 4:
                    pe.wait_ge(sem("qkv3_ready"), bb - 3)
                mm(bank(4 + bb % 4, T, 3 * D), xnT[:, bb * T:(bb + 1) * T], W["qkv3"][:, :]
                   ).then_inc(sem("qkv3_psum"), 1)
            pe.wait_ge(sem("q3T_ready"), 1)
            for half in range(2):
                m = mm(bank(half, D, HALF), W["k3T"][:, :], q3T[:, half * HALF:(half + 1) * HALF])
            m.then_inc(sem("qe3_psum"), 1)
            pe.wait_ge(sem("layer3_setup"), 1)
            ring = rings[3]
            with pe.Fori(0, B) as b:
                pe.wait_ge(sem("ctxT_loaded"), 32 * CTX_LOADS + 16 * b + 16)
                pe.wait_ge(sem("ctx_keys_loaded"), 32 * (B + 1) + 32 * b + 32)
                pe.wait_ge(sem("a3_query_placed"), b + 1)
                for half in range(2):
                    ring.before_fill(pe, b, half)
                    for i in range(2):
                        c0 = (2 * half + i) * KQ
                        m = mm(bank(2 * half + i, T, KQ), q3c[:, :], ctxT[:, c0:c0 + KQ])
                    m.then_inc(ring.full, 1)
                pe.wait_ge(ring.emptied["act"], ring.emptied_count(b, 1))
                for half, chunks in enumerate((range(0, 8), range(8, NCH))):
                    ring.before_fill(pe, b, 2 + half)
                    s = (2 + half) % 3
                    for k, c in enumerate(chunks):
                        m = pe.transpose(bank(2 * s + k // 4, ROWS[c], BANK)[:, (k % 4) * T:(k % 4 + 1) * T],
                                         P1[:, c * CK:c * CK + ROWS[c]], ident[0:T, 0:T])
                    m.then_inc(ring.full, 1)
                pe.wait_ge(ring.emptied["dve"], ring.emptied_count(b, 3))
                for c in range(NCH):
                    m = mm(bank(6, D, T), ctxk[0:ROWS[c], c, :], PT3[0:ROWS[c], c, :], start=c == 0, stop=c == NCH - 1)
                m.then_inc(sem("a3_ctx_used"), 1)
                pe.wait_ge(sem("a3_context_copied"), b + 1)
                ring.before_fill(pe, b, 4)
                mm(bank(2, T, D), AT3[:, :], W["qkv3"][:, 2 * D:3 * D]).then_inc(ring.full, 1)
            turn_xn(7)
            pe.wait_ge(sem("experts_by_dve"), STEP["experts_normalised"])
            pe.transpose(bank(2, D, E3), g0[0:E3, 0:D], ident[0:E3, 0:E3]).then_inc(sem("experts_by_pe"), 1)
            pe.wait_ge(sem("experts_by_dve"), STEP["expert_columns"])
            for bb in range(B):
                m = mm(bank(3, T, 128)[:, bb * 16:(bb + 1) * 16], xnT[:, bb * T:(bb + 1) * T], g1[:, 0:16])
            m.then_inc(sem("experts_by_pe"), 1)
            pe.wait_ge(sem("experts_by_dve"), STEP["expert_weights"])
            for bb in range(B):
                m = pe.transpose(bank(bb // 4, E3, BANK)[:, (bb % 4) * T:(bb % 4 + 1) * T],
                                 g2[0:T, bb * E3:(bb + 1) * E3], ident[0:T, 0:T])
            m.then_inc(sem("experts_by_pe"), 1)
            pe.wait_ge(sem("experts_by_act"), STEP["expert_weights_turned"])
            for bb in range(B):
                m = mm(bank(2 + bb // 4, T, BANK)[:, (bb % 4) * D:(bb % 4 + 1) * D],
                       big2[0:E3, bb * T:(bb + 1) * T],
                       W["f3b2"][:, :])
            m.then_inc(sem("experts_by_pe"), 1)
            pe.wait_ge(sem("experts_loaded"), 32)
            pe.wait_ge(sem("experts_by_dve"), STEP["expert_biases_taken"])
            for e in range(E3):
                for k in range(8):
                    f, half = k // 2, k % 2
                    q = 8 * e + k
                    if q >= 4:
                        pe.wait_ge(sem("f3_gelu"), q - 3)
                    mm(bank(4 + q % 4, 128, HALF), w3a[:, e, f * 128:(f + 1) * 128],
                       xnT[:, half * HALF:(half + 1) * HALF]).then_inc(sem("f3_hidden_psum"), 1)
                pe.wait_ge(sem("f3_gelu"), 8 * e + 8)
                if e >= 2:
                    pe.wait_ge(sem("f3_accumulated"), 2 * (e - 1))
                for bb in range(B):
                    o = bank(2 * (e % 2) + bb // 4, T, BANK)[:, (bb % 4) * D:(bb % 4 + 1) * D]
                    for f in range(4):
                        m = mm(o, hid[:, f, bb * T:(bb + 1) * T], w3b[:, e, f, :], start=f == 0, stop=f == 3)
                m.then_inc(sem("f3_out"), 1)

        @block.scalar
        def _(act):
            own = [0]

            def link(i):
                own[0] += 1
                i.then_inc(sem("act_step"), 1)
                act.wait_ge(sem("act_step"), own[0])

            rooted = [0]

            def take_roots(dst, src):
                rooted[0] += 1
                act.wait_ge(sem("variances_ready"), rooted[0])
                act.activation(dst, src, ACT.Sqrt).then_inc(sem("deviations_ready"), 1)

            def root_of_rows():
                take_roots(stat[0:T, 4, 0:8], stat[0:T, 3, 0:8])

            def turned(n):
                root_of_rows()
                n = n if n < 4 else n - 1
                for half in range(2):
                    act.wait_ge(sem("xnT_in_psum"), 2 * n + half + 1)
                    act.copy(xnT[:, half * HALF:(half + 1) * HALF], bank(half, D, HALF)
                             ).then_inc(sem("xnT_ready"), 1)

            act.wait_ge(sem("constants_loaded"), 5 * 16)
            act.wait_ge(sem("weights_loaded"), NW)
            act.activation(gates[:, :], gates[:, :], ACT.Tanh).then_inc(sem("gates_ready"), 1)
            act.activation(small[:, 24:25], W["g1"][:, :], ACT.Exp, scale=-1.0)
            act.activation(head_gates[:, 0, :], W["g1heads"][:, :], ACT.Exp, scale=-1.0
                           ).then_inc(sem("head_gate_exp"), 1)

            def attention(layer):
                ring = rings[layer]
                p = f"a{layer}_"
                bk = W["bk0"] if layer == 0 else W["bka1"]

                def copy_keys(half, s, last):
                    k0, k1 = half * 2 * KQ, (half + 1) * 2 * KQ
                    act.activation(kf[:, k0:k1].rearrange("p (a k) -> p a k", a=2), slot(s, D, KQ), ACT.Identity,
                                   bias=bk[:, 0:1])
                    return act.activation(kparts[:, 0, k0:k1].rearrange("p (a k) -> p a k", a=2), slot(s, D, KQ),
                                          ACT.Identity, bias=bk[:, 0:1])

                def second_part(count):
                    act.wait_ge(sem(p + "keys_rest"), count)
                    act.copy(kparts[:, 1, :], kr).then_inc(sem(p + "key_parts_2"), 1)

                act.wait_ge(sem(p + "first_keys"), 1)
                act.wait_ge(sem(p + "query_parts_ready"), 1)
                copy_keys(0, 0, False)
                copy_keys(1, 1, True).then_inc(sem(p + "key_parts_1"), 1)
                second_part(1)
                act.sem_inc(ring.emptied["act"], ring.per["act"])
                act.sem_inc(sem(p + "probs_used"), 3)
                per = 2 * NCH + 2 * layer
                with act.Fori(0, B) as b:
                    act.wait_ge(sem(p + "queries_stacked"), 16 * 12 * (b + 1))
                    for dst in (q2, own_q2)[0:layer + 1]:
                        for par in range(2):
                            i = act.copy(dst[64 * par:64 * par + 48, :, :], q1[64 * par:64 * par + 48, :, :])
                    i.then_inc(sem(p + "queries_copied"), 1)
                    act.wait_ge(sem(p + "probs_used"), b * per + 3)
                    act.wait_ge(sem(p + "values_turned"), b + 1)
                    act.copy(Vo[:, :, :, 0:8], Vn.rearrange("p c (h d) -> p c h d", h=H)
                             ).then_inc(sem(p + "values_placed"), 1)
                    done = 0
                    for n, (kind, g, u, _) in enumerate(ORDER[layer]):
                        if kind == "keys":
                            act.wait_ge(ring.full, ring.full_count(b, n))
                            copy_keys(u, n % 3, u == 1).then_inc(ring.emptied["act"], 1)
                        if kind == "exp":
                            r = ROWS[u // 2] if g == 0 else T
                            act.wait_ge(ring.full, ring.full_count(b, n))
                            if done >= 3:
                                act.wait_ge(sem(p + "probs_used"), b * per + done + 1)
                            act.activation(P3[0:r, done % 3, :].rearrange("p (a k) -> p a k", a=2),
                                           slot(n % 3, r, GROUP), ACT.Exp).then_inc(ring.emptied["act"], 1)
                            done += 1
                            if g == 0 and u == 5:
                                second_part(b + 2)

            turned(0)
            attention(0)
            turned(1)
            act.wait_ge(sem("router_columns"), 1)
            act.activation(small[0:T, 0:8], stat[0:T, 0, 0:8], ACT.Exp, scale=-1.0).then_inc(sem("router_exp"), 1)
            for k in range(8):
                f, half = k // 2, k % 2
                act.wait_ge(sem("ffn0_hidden_psum"), k + 1)
                act.activation(hid[:, f, half * HALF:(half + 1) * HALF], bank(4 + k % 4, 128, HALF),
                               ACT.Gelu_apprx_tanh, bias=W["f0b1"][:, f:f + 1]).then_inc(sem("ffn0_hidden"), 1)
            turned(2)
            act.wait_ge(sem("k1_projected"), 1)
            act.wait_ge(sem("q1_split"), 1)
            act.activation(qf.rearrange("p (a k) -> p a k", a=2), slot(2, D, HALF), ACT.Identity,
                           bias=W["bk1"][:, 0:1]).then_inc(sem("k1_ready"), 1)
            attention(1)
            turned(3)
            act.wait_ge(sem("slots_by_dve"), STEP["slot_bias"])
            act.wait_ge(sem("slots_by_pe"), STEP["f1_hidden_psum"])
            for half in range(2):
                act.activation(hid[0:NSLOT, 0, half * HALF:(half + 1) * HALF], bank(4 + half, NSLOT, HALF),
                               ACT.Gelu, bias=small[0:NSLOT, 10:11]).then_inc(sem("f1_hidden"), 1)
            act.wait_ge(sem("slots_by_dve"), STEP["logits_shifted"])
            act.activation(big2[0:T, 0:512], big2[0:T, 0:512], ACT.Exp).then_inc(sem("slots_by_act"), 1)
            act.wait_ge(sem("slots_by_pe"), STEP["alpha_turned"])
            act.copy(hid[0:NSLOT, 1, :].rearrange("p (a k) -> p a k", a=2), slot(2, NSLOT, HALF)
                     ).then_inc(sem("slots_by_act"), 1)
            act.wait_ge(sem("slots_by_dve"), STEP["gate_r_sum"])
            act.activation(g0[:, :], g0[:, :], ACT.Exp, scale=-1.0).then_inc(sem("slots_by_act"), 1)
            act.wait_ge(sem("slots_by_dve"), STEP["gate_z_sum"])
            act.activation(big3[:, 0:512], big3[:, 0:512], ACT.Exp, scale=-1.0).then_inc(sem("slots_by_act"), 1)
            act.wait_ge(sem("slots_by_dve"), STEP["gate_n_sum"])
            act.activation(g3[:, :], g3[:, :], ACT.Tanh).then_inc(sem("slots_by_act"), 1)
            act.wait_ge(sem("slots_by_pe"), STEP["slot_values_psum"])
            act.activation(g3[:, :], bank(0, D, BANK), ACT.Identity, bias=W["f1bv"][:, 0:1]
                           ).then_inc(sem("slots_by_act"), 1)
            act.wait_ge(sem("slots_by_pe"), STEP["slot_outputs_psum"])
            act.copy(big2[0:NSLOT, :].rearrange("p (a k) -> p a k", a=2), slot(1, NSLOT, BANK)
                     ).then_inc(sem("slots_by_act"), 1)
            ring = rings[2]
            root_of_rows()
            root_of_rows()
            act.wait_ge(sem("latents_ready"), 1)
            act.sem_inc(ring.emptied["act"], ring.head["act"])
            act.sem_inc(sem("a2_contexts_copied_by_act"), 1)
            pair = "p (a k) -> p a k"

            def event(b, c):
                return 14 * b + c + 2

            def take_norms(b, r, c, at):
                act.wait_ge(sem("a2_squares_summed"), event(b, c))
                act.activation(n2[0:r, at, :], n2[0:r, at, :], ACT.Sqrt).then_inc(sem("a2_norms"), 1)

            def square_context(b):
                act.wait_ge(sem("a2_stage_centred"), b + 2)
                act.activation(scratch, stage[:, 0:NCH, :], ACT.Square).then_inc(sem("a2_stage_squared"), 1)

            def root_variances(b):
                act.wait_ge(sem("a2_variances"), b + 2)
                act.activation(stat[:, 6, 0:NCH], stat[:, 6, 0:NCH], ACT.Sqrt).then_inc(sem("a2_deviations"), 1)

            def copy_context(b):
                act.wait_ge(ring.full, ring.full_count(b, "context", 0))
                act.copy(xkT[:, 0:8 * CK].rearrange(pair, a=2), slot(ring.slot_of("context", 0), D, 4 * CK)
                         ).then_inc(ring.emptied["act"], 1)
                act.wait_ge(ring.full, ring.full_count(b, "context", 1))
                s = ring.slot_of("context", 1)
                act.copy(xkT[:, S2:S2 + T], bank(2 * s + 1, D, T))
                act.copy(xkT[:, 8 * CK:S2], bank(2 * s, D, S2 - 8 * CK)).then_inc(ring.emptied["act"], 1)

            def square_queries(b):
                act.wait_ge(ring.full, ring.full_count(b, "query", 0))
                act.activation(values2.rearrange(pair, a=2), slot(ring.slot_of("query", 0), T, BANK), ACT.Square
                               ).then_inc(sem("a2_query_squares"), 1)

            def carry(b):
                take_norms(b, T, 13, 0)
                act.wait_ge(ring.full, ring.full_count(b, "turned", 0))
                act.activation(xnT[:, :].rearrange(pair, a=2), slot(ring.slot_of("turned", 0), D, HALF), ACT.Copy,
                               scale=small[:, 30:31]).then_inc(ring.emptied["act"], 1)
                for half in range(2):
                    act.wait_ge(ring.full, ring.full_count(b, "carried", half))
                    act.copy(qeff[:, 8 * half:8 * half + 8, :].rearrange("p (t a) q -> p a t q", a=2),
                             slot(ring.slot_of("carried", half), D, GROUP).rearrange("p a (t q) -> p a t q", t=4)
                             ).then_inc(ring.emptied["act"], 1)

            def place_context():
                act.copy(ctxk[:, :, :], stage).then_inc(sem("a2_stage_copied"), 1)

            def copy_values(b):
                act.wait_ge(sem("a2_heads_by_pe"), 3 * b + 2)
                act.copy(xnT[:, :].rearrange(pair, a=2), slot(3, D, HALF)).then_inc(sem("a2_heads_by_act"), 1)

            square_context(-1)
            root_variances(-1)
            copy_context(-1)
            square_queries(-1)
            carry(-1)
            place_context()
            with act.Fori(0, B) as b:
                rows = ROWS + [T]
                for c in range(13):
                    act.wait_ge(ring.full, ring.full_count(b, "norm", c))
                    act.activation(sq[0:rows[c], :].rearrange(pair, a=2), slot(ring.slot_of("norm", c), rows[c], BANK),
                                   ACT.Square).then_inc(ring.emptied["act"], 1)
                    take_norms(b, rows[c], c, c % 2)
                    if c == VALUES_TURNED + 1:
                        copy_values(b)
                for half in range(2):
                    act.wait_ge(ring.full, ring.full_count(b, "shift", half))
                    act.copy(mB[:, 2 * half * GROUP:(2 * half + 2) * GROUP].rearrange(pair, a=2),
                             slot(ring.slot_of("shift", half), 128, GROUP)).then_inc(ring.emptied["act"], 1)
                for c in range(13):
                    act.wait_ge(sem("a2_scores_shifted"), b * 13 + c + 1)
                    act.activation(S_all[0:rows[c], c, :], S_all[0:rows[c], c, :], ACT.Exp,
                                   bias=kbc[0:rows[c], c:c + 1]).then_inc(sem("a2_probs_ready"), 1)
                    if c == CENTRE + 1:
                        square_context(b)
                    if c == VARIANCE + 1:
                        root_variances(b)
                    if c == TURN + 1:
                        copy_context(b)
                    if c == QUERY + 1:
                        square_queries(b)
                carry(b)
                act.wait_ge(sem("a2_keys_used"), b + 1)
                act.copy(mB[:, 2 * GROUP:4 * GROUP].rearrange(pair, a=2), slot(3, D, GROUP)
                         ).then_inc(sem("a2_contexts_copied_by_act"), 1)
                place_context()
            copy_values(B)
            turned(5)
            for bb in range(B):
                act.wait_ge(sem("f2_hidden_psum"), bb + 1)
                act.activation(ternary_hidden(bb), bank(2 + bb % 2, T, BANK), ACT.Gelu).then_inc(sem("f2_gelu"), 1)
            root_of_rows()
            for bb in range(B):
                act.wait_ge(sem("f2_turned_psum"), bb + 1)
                act.copy(big2[:, (bb % 2) * 400:(bb % 2) * 400 + 400], bank(4 + bb % 2, 128, 4 * T)
                         ).then_inc(sem("f2_turned"), 1)
            turned(6)
            act.wait_ge(sem("q3T_psum"), 1)
            act.activation(q3T[:, :].rearrange("p (a k) -> p a k", a=2), slot(1, D, HALF), ACT.Identity,
                           bias=W["bq3"][:, 0:1]).then_inc(sem("q3T_ready"), 1)
            act.wait_ge(sem("qe3_psum"), 1)
            act.copy(qe3[:, :].rearrange("p (a k) -> p a k", a=2), slot(0, D, HALF)).then_inc(sem("qe3_ready"), 1)
            ring = rings[3]
            act.sem_inc(ring.emptied["act"], ring.per["act"])
            with act.Fori(0, B) as b:
                act.wait_ge(sem("a3_shift_ready"), b + 1)
                act.activation(st3[:, 36:37], st3[:, 35:36], ACT.Exp).then_inc(sem("a3_self_exp"), 1)
                for half in range(2):
                    act.activation(P1[:, half * 2 * KQ:(half + 1) * 2 * KQ].rearrange("p (a k) -> p a k", a=2),
                                   slot(half, T, KQ), ACT.Exp, bias=st3[:, 34:35], accum_out=st3[:, 37 + half:38 + half]
                                   ).then_inc(ring.emptied["act"], 1)
                act.wait_ge(sem("a3_ctx_used"), b + 1)
                act.copy(AT3[:, :], bank(6, D, T)).then_inc(sem("a3_context_copied"), 1)
            turned(7)
            act.wait_ge(sem("experts_by_dve"), STEP["squares_ready"])
            act.activation(stat[0:T, 5, 0:8], stat[0:T, 5, 0:8], ACT.Sqrt).then_inc(sem("norms_ready"), 1)
            act.activation(small[0:E3, 40:41], small[0:E3, 40:41], ACT.Sqrt).then_inc(sem("norms_ready"), 1)
            act.wait_ge(sem("experts_by_dve"), STEP["expert_shifted"])
            act.activation(g3[0:T, 0:64], g3[0:T, 0:64], ACT.Exp).then_inc(sem("experts_by_act"), 1)
            act.wait_ge(sem("experts_by_pe"), STEP["expert_weights_psum"])
            act.copy(big2[0:E3, 0:BT].rearrange("p (a k) -> p a k", a=2), slot(0, E3, HALF)
                     ).then_inc(sem("experts_by_act"), 1)
            for e in range(E3):
                for k in range(8):
                    f, half = k // 2, k % 2
                    q = 8 * e + k
                    act.wait_ge(sem("f3_hidden_psum"), q + 1)
                    if e >= 1 and k == 0:
                        act.wait_ge(sem("f3_out"), e)
                    act.activation(hid[:, f, half * HALF:(half + 1) * HALF], bank(4 + q % 4, 128, HALF),
                                   ACT.Gelu, bias=W["f3b1"][:, e, f:f + 1]).then_inc(sem("f3_gelu"), 1)

        @block.gpsimd
        def _(pool):
            def split_keys(layer, copied, count):
                p = f"a{layer}_"
                pool.wait_ge(*copied)
                pool.tensor_tensor(kr, kf, kparts[:, 0, :], ALU.subtract).then_inc(sem(p + "keys_rest"), 1)
                pool.wait_ge(sem(p + "key_parts_2"), count)
                pool.tensor_tensor(kparts[:, 2, :], kr, kparts[:, 1, :], ALU.subtract
                                   ).then_inc(sem(p + "keys_split"), 1)

            for layer in (0, 1):
                ring = rings[layer]
                split_keys(layer, (sem(f"a{layer}_key_parts_1"), 1), 1)
                with pool.Fori(0, B) as b:
                    split_keys(layer, (ring.emptied["act"], ring.emptied_count(b, position(layer, "keys", 0, 1))),
                               b + 2)

            def gain_and_bias(b):
                pool.wait_ge(sem("a2_stage_scaled"), b + 2)
                kk, ks = stage[:, 0:NCH, :], [128, NCH, D]
                pool.tensor_tensor(kk, kk, bc(W["lnxg"][:, :], ks, 1), ALU.mult).then_inc(sem("a2_gained"), 1)
                pool.wait_ge(sem("a2_gained"), b + 2)
                pool.tensor_tensor(kk, kk, bc(W["lnxb"][:, :], ks, 1), ALU.add).then_inc(sem("a2_keys_normalised"), 1)

            gain_and_bias(-1)
            with pool.Fori(0, B) as b:
                for k, c in enumerate(POOL_SUMS[1:]):
                    r = (ROWS + [T])[c]
                    pool.wait_ge(sem("a2_probs_ready"), b * 13 + c + 1)
                    if k > 0:
                        pool.wait_ge(sem("a2_pool_summed"), b * (len(POOL_SUMS) - 1) + k)
                    before_c = S_all[0:r, 0, :] if k == 0 else Psum[0:r, :]
                    pool.tensor_tensor(Psum[0:r, :], before_c, S_all[0:r, c, :], ALU.add
                                       ).then_inc(sem("a2_pool_summed"), 1)
                    if c == SCALE - 1:
                        gain_and_bias(b)

        @block.vector
        def _(dve):
            own = [0]

            def link(i):
                own[0] += 1
                i.then_inc(sem("dve_step"), 1)
                dve.wait_ge(sem("dve_step"), own[0])

            roots = [0]

            def invert_roots(at):
                dve.sem_inc(sem("variances_ready"), 1)
                roots[0] += 1
                dve.wait_ge(sem("deviations_ready"), roots[0])
                link(dve.reciprocal(at, at))

            def norm_rows(dst, src, parts, n, width, scratch, st):
                shape = [parts, n, width]
                link(dve.tensor_reduce(st[:, 0, 0:n], src, AX.X, ALU.add))
                link(dve.tensor_scalar(st[:, 1, 0:n], st[:, 0, 0:n], 1.0 / width, None, ALU.mult))
                link(dve.tensor_tensor(dst, src, bc(st[:, 1, 0:n], shape, 2), ALU.subtract))
                link(dve.tensor_tensor(scratch, dst, dst, ALU.mult))
                link(dve.tensor_reduce(st[:, 2, 0:n], scratch, AX.X, ALU.add))
                link(dve.tensor_scalar(st[:, 3, 0:n], st[:, 2, 0:n], 1.0 / width, LN_EPS, ALU.mult, ALU.add))
                invert_roots(st[:, 4, 0:n])
                return dve.tensor_tensor(dst, dst, bc(st[:, 4, 0:n], shape, 2), ALU.mult)

            def norm_x():
                i = norm_rows(xn[:, :, :], x[:, :, :], T, B, D, wideA[:, :, :], stat[0:T])
                link(i)
                dve.sem_inc(sem("xn_ready"), 1)

            def add_residual(psum_pair, gate):
                link(dve.scalar_tensor_tensor(
                    out=x[:, :, :].rearrange("p (a b) d -> p a (b d)", a=2), in0=psum_pair,
                    scalar=gates[0:T, gate:gate + 1],
                    in1=x[:, :, :].rearrange("p (a b) d -> p a (b d)", a=2), op0=ALU.mult, op1=ALU.add))

            dve.memset(kmask[:, :, :].rearrange("p a b -> p (a b)"), 0).then_inc(sem("key_mask_cleared"), 1)
            link(dve.memset(ones[:, :], 1.0))
            link(dve.memset(Vo_w, 1.0))
            link(dve.memset(own_Vo_w, 1.0))
            link(dve.memset(Vn, 0.0))
            link(dve.memset(qparts_w, 0.0))
            link(dve.memset(own_kparts_w, 0.0))
            link(dve.memset(kst_w.bitcast(BF16), 1.0))
            link(dve.memset(own_kst_w.bitcast(BF16), 1.0))
            dve.sem_inc(sem("a0_ones_set"), 1)
            dve.wait_ge(sem("x_loaded"), 16)
            dve.wait_ge(sem("constants_loaded"), 5 * 16)
            dve.wait_ge(sem("weights_loaded"), NW)
            norm_x()
            link(dve.tensor_copy(wr_bc[:, :], W["f0wr"][:, 0:1].broadcast_to([D, T])))
            dve.wait_ge(sem("head_gate_exp"), 1)
            link(dve.tensor_scalar(head_gates[:, 0, :], head_gates[:, 0, :], 1.0, None, ALU.add))
            link(dve.reciprocal(head_gates[:, 0, :], head_gates[:, 0, :]))
            link(dve.tensor_scalar(head_gates[:, 1, :], head_gates[:, 0, :], -1.0, 1.0, ALU.mult, ALU.add))
            link(dve.tensor_scalar(small[:, 25:26], small[:, 24:25], 1.0, None, ALU.add))
            link(dve.reciprocal(small[:, 26:27], small[:, 25:26]))
            link(dve.tensor_tensor(small[:, 27:28], W["bva1"][:, :], W["bv1"][:, :], ALU.subtract))
            link(dve.scalar_tensor_tensor(out=bv1[:, :], in0=small[:, 27:28], scalar=small[:, 26:27],
                                          in1=W["bv1"][:, :], op0=ALU.mult, op1=ALU.add))
            link(dve.tensor_scalar(small[:, 30:31], W["gq2"][:, 0:1], W["gk2"][:, 0:1], DH ** -0.5, ALU.mult, ALU.mult))
            dve.wait_ge(sem("masks_loaded"), 32 + 32 * B)
            link(dve.memset(maskb, 0.0))
            mi = maski.bitcast(I32).rearrange("p (c q) -> p c q", c=NCH)
            link(dve.tensor_scalar(maskb[0:CK, 0:NCH - 1, :], mi[0:CK, 0:NCH - 1, :], 0, OFF, ALU.is_equal, ALU.mult))
            link(dve.tensor_scalar(maskb[0:LAST, NCH - 1, :], mi[0:LAST, NCH - 1, :], 0, OFF, ALU.is_equal, ALU.mult))
            link(dve.tensor_scalar(kbias[:, :, :], kmask[:, :, :], 0, OFF, ALU.is_equal, ALU.mult))

            def split(parts, src, rest):
                link(dve.tensor_copy(parts[:, 0, :], src))
                link(dve.tensor_tensor(rest, src, parts[:, 0, :], ALU.subtract))
                link(dve.tensor_copy(parts[:, 1, :], rest))
                link(dve.tensor_tensor(parts[:, 2, :], rest, parts[:, 1, :], ALU.subtract))

            def attention(layer):
                ring = rings[layer]
                p = f"a{layer}_"
                own_sem = sem(p + "dve_step")
                used = 2 * NCH + 2 * layer
                G = layer + 1
                per = STEPS[layer]
                bv = W["bv0"] if layer == 0 else bv1
                nf = 3 + layer
                link(dve.memset(psum[:, 6:8, :], 1.0))
                link(dve.memset(summed[:, :], 1.0))
                link(dve.memset(own_summed[:, :], 1.0))
                dve.wait_ge(sem(p + "first_projected"), 1)
                link(dve.tensor_copy(Vn[0:CK, 0:8, :].rearrange("p (a c) d -> p a (c d)", a=2), psum[0:CK, 4:6, :]))
                link(dve.tensor_copy(Vn[0:CK, 8:11, :].rearrange("p c d -> p (c d)"), bank(0, CK, 3 * D)))
                link(dve.tensor_copy(Vn[0:LAST, 11, :], bank(0, LAST, BANK)[:, 3 * D:4 * D]))
                dve.sem_inc(sem(p + "values_turned"), 1)
                dve.sem_inc(ring.emptied["dve"], ring.per["dve"])
                dve.sem_inc(sem(p + "sums_copied"), 1)
                dve.sem_inc(sem(p + "heads_by_dve"), 1)

                def finish(b, k, step):
                    dve.wait_ge(sem(p + "heads_by_pe"), b * nf + k + 1)
                    if k < G:
                        turned = bank(7, T, BANK).rearrange("p (h d) -> p h d", h=H)
                        dst = (heads, own_heads)[k]
                        step(dve.reciprocal(shares[:, k, :], turned[:, :, 8]))
                        if layer == 1:
                            step(dve.tensor_tensor(shares[:, k, :], shares[:, k, :], head_gates[0:T, k, :], ALU.mult))
                        i = dve.tensor_tensor(dst.rearrange("p (h d) -> p h d", h=H), turned[:, :, 0:8],
                                              bc(shares[:, k, :], [T, H, HD], 2), ALU.mult)
                        if k == 1:
                            step(i)
                            i = dve.tensor_tensor(heads[:, :], heads[:, :], own_heads[:, :], ALU.add)
                    elif k == G:
                        i = dve.tensor_scalar(headsT[:, :], bank(7, D, T), bv[:, 0:1], None, ALU.add)
                    else:
                        i = dve.tensor_copy(attended[:, bass.ds(b * D, D)], bank(7, T, D))
                    i.then_inc(sem(p + "heads_by_dve"), 1)

                with dve.Fori(0, B) as b:
                    k = [0]

                    def step(i):
                        k[0] += 1
                        i.then_inc(own_sem, 1)
                        dve.wait_ge(own_sem, b * per + k[0])

                    if layer == 1:
                        step(dve.tensor_copy(own_Vo[0:T, :, 0:8],
                                             vs.rearrange("p b (h d) -> p (b h) d", h=H)[:, bass.ds(b * H, H), :]))
                    for n, (kind, g, u, _) in enumerate(ORDER[layer]):
                        s = n % 3
                        if kind in ("exp", "keys"):
                            continue
                        dve.wait_ge(ring.full, ring.full_count(b, n))
                        if kind == "max":
                            r = ROWS[u // 2] if g == 0 else T
                            dst = (M if g == 0 else own_M)[0:r, 800 * (u % 2):800 * (u % 2) + 800].rearrange(
                                "p (a k) -> p a k", a=2)
                            if u < 2:
                                i = dve.tensor_copy(dst, slot(s, r, GROUP))
                            else:
                                dve.wait_ge(ring.emptied["dve"], ring.emptied_count(b, position(layer, "max", g, u - 2)))
                                i = dve.tensor_tensor(dst, slot(s, r, GROUP), dst, ALU.max)
                            i.then_inc(ring.emptied["dve"], 1)
                            if g == 0 and u in FINISH[layer]:
                                finish(b, FINISH[layer].index(u), step)
                            if layer == 1 and g == 0 and u == OWN_TAKEN:
                                dve.wait_ge(sem(p + "probs_used"), b * used + 2 + 3)
                                dve.tensor_copy(own_summed[:, :], bank(7, 128, GROUP)).then_inc(sem(p + "sums_copied"), 1)
                        elif kind == "turn":
                            r = CK if g == 0 else T
                            src = slot(s, T, 4 * CK).rearrange("p a (h k) -> p a h k", h=4)[:, :, :, 0:r]
                            for part in range(2):
                                dst = mx[:, g, :].rearrange("p (a r h) -> p a r h", a=2, r=2)[:, :, part, 4 * u:4 * u + 4]
                                if part == 0:
                                    i = dve.tensor_reduce(dst, src, AX.X, ALU.max, negate=True)
                                    step(i)
                                    first = dst
                                else:
                                    i = dve.tensor_copy(dst, first)
                            i.then_inc(ring.emptied["dve"], 1)
                            if u == 1:
                                dve.wait_ge(ring.emptied["dve"], ring.emptied_count(b, n))
                                if layer == 0:
                                    step(dve.tensor_scalar(flag[:, :], mx[:, 0, :], 1e29, 3e38, ALU.is_gt, ALU.mult))
                                    step(dve.tensor_tensor(mx[:, 0, :], mx[:, 0, :], flag[:, :], ALU.add))
                                dve.sem_inc(sem(p + f"max_ready_{g}"), 1)
                        elif kind == "row":
                            step(dve.tensor_copy(high[:, :], bank(2 * s, 32, T)))
                            step(dve.scalar_tensor_tensor(out=hl[:, g, :], in0=high[:, :], scalar=low_rows[:, 0:1],
                                                          in1=bank(2 * s, 32, T), op0=ALU.mult, op1=ALU.add))
                            dve.sem_inc(ring.emptied["dve"], 1)
                            dve.sem_inc(sem(p + f"shift_ready_{g}"), 1)
                        elif kind == "values":
                            if u == 0:
                                dve.wait_ge(sem(p + "values_placed"), b + 1)
                                dve.tensor_copy(Vn[0:CK, 0:8, :].rearrange("p (a c) d -> p a (c d)", a=2),
                                                slot(s, CK, BANK)).then_inc(ring.emptied["dve"], 1)
                            else:
                                step(dve.tensor_copy(Vn[0:CK, 8:11, :].rearrange("p c d -> p (c d)"),
                                                     bank(2 * s, CK, 3 * D)))
                                step(dve.tensor_copy(Vn[0:LAST, 11, :], bank(2 * s, LAST, BANK)[:, 3 * D:4 * D]))
                                dve.sem_inc(ring.emptied["dve"], 1)
                                dve.sem_inc(sem(p + "values_turned"), 1)
                    dve.wait_ge(sem(p + "probs_used"), (b + 1) * used + 3)
                    dve.tensor_copy(summed[:, :], bank(6, 128, GROUP)).then_inc(sem(p + "sums_copied"), 1)
                    assert k[0] == per, k[0]
                for k in range(nf):
                    finish(B, k, link)
                dve.wait_ge(sem(p + "heads_by_dve"), (B + 1) * nf + 1)
                link(dve.scalar_tensor_tensor(out=x[:, :, :], in0=attended[:, D:].rearrange("p (b d) -> p b d", b=B),
                                              scalar=gates[0:T, layer:layer + 1], in1=x[:, :, :],
                                              op0=ALU.mult, op1=ALU.add))
                dve.wait_ge(ring.emptied["dve"], (B + 1) * ring.per["dve"])
                dve.wait_ge(sem(p + "keys_split"), B + 1)

            dve.wait_ge(sem("gates_ready"), 1)
            dve.wait_ge(sem("q0_projected"), 1)
            link(dve.tensor_scalar(qf.rearrange("p (a k) -> p a k", a=2), slot(1, D, HALF), W["bq0"][:, 0:1],
                                   HD ** -0.5, ALU.add, ALU.mult))
            split(qparts[:, :, 0:BT], qf, qr)
            dve.sem_inc(sem("layer0_setup"), 1)
            dve.sem_inc(sem("a0_query_parts_ready"), 1)
            attention(0)

            norm_x()
            dve.wait_ge(sem("router_scores"), 1)
            flat = wideA[:, :, :].rearrange("p b d -> p (b d)")
            sr = flat[:, 0:BT].rearrange("p (b t) -> p b t", b=B)
            tmp = wideB[:, :, :].rearrange("p b d -> p (b d)")[:, 0:BT].rearrange("p (b t) -> p b t", b=B)
            sh = [T, B, T]
            link(dve.tensor_copy(flat[:, 0:BT].rearrange("p (a k) -> p a k", a=2), slot(1, T, HALF)))
            link(dve.tensor_tensor(tmp, sr, bc(ident[0:T, 0:T], sh, 1), ALU.mult))
            dve.tensor_reduce(stat[0:T, 0, 0:8], tmp, AX.X, ALU.add).then_inc(sem("router_columns"), 1)
            dve.wait_ge(sem("router_columns"), 1)
            link(dve.tensor_tensor(tmp, sr, bc(stat[0:T, 0, 0:8], sh, 2), ALU.is_gt))
            link(dve.tensor_reduce(stat[0:T, 1, 0:8], tmp, AX.X, ALU.add))
            link(dve.tensor_tensor(tmp, sr, bc(stat[0:T, 0, 0:8], sh, 2), ALU.is_equal))
            link(dve.tensor_tensor(tmp, tmp, bc(before[:, :], sh, 1), ALU.mult))
            link(dve.tensor_reduce(stat[0:T, 2, 0:8], tmp, AX.X, ALU.add))
            link(dve.tensor_tensor(stat[0:T, 3, 0:8], stat[0:T, 1, 0:8], stat[0:T, 2, 0:8], ALU.add))
            link(dve.tensor_scalar(stat[0:T, 4, 0:8], stat[0:T, 3, 0:8], T // 2 - 0.5, gates[0:T, 4:5],
                                   ALU.is_lt, ALU.mult))
            dve.wait_ge(sem("router_exp"), 1)
            link(dve.tensor_scalar(stat[0:T, 5, 0:8], small[0:T, 0:8], 1.0, None, ALU.add))
            link(dve.reciprocal(stat[0:T, 6, 0:8], stat[0:T, 5, 0:8]))
            link(dve.tensor_tensor(stat[0:T, 7, 0:8], stat[0:T, 6, 0:8], stat[0:T, 4, 0:8], ALU.mult))
            link(dve.scalar_tensor_tensor(out=x[:, :, :], in0=xn[:, :, :], scalar=gates[0:T, 4:5], in1=x[:, :, :],
                                          op0=ALU.mult, op1=ALU.add))
            dve.wait_ge(sem("ffn0_out"), 1)
            link(dve.tensor_tensor(wideA[:, :, :].rearrange("p (a b) d -> p a b d", a=2),
                                   slot(0, T, BANK).rearrange("p a (b d) -> p a b d", b=4),
                                   stat[0:T, 7, 0:8].rearrange("p (a b) -> p a b", a=2).unsqueeze(3)
                                   .broadcast_to([T, 2, 4, D]), ALU.mult))
            link(dve.tensor_tensor(x[:, :, :], x[:, :, :], wideA[:, :, :], ALU.add))

            norm_x()
            dve.wait_ge(sem("q1_projected"), 1)
            for tile in (Vo_w, own_Vo_w, kst_w.bitcast(BF16), own_kst_w.bitcast(BF16)):
                link(dve.memset(tile, 1.0))
            for tile in (qparts_w, own_kparts_w, Vn):
                link(dve.memset(tile, 0.0))
            dve.sem_inc(sem("a1_ones_set"), 1)
            link(dve.tensor_scalar(qf.rearrange("p (a k) -> p a k", a=2), slot(1, D, HALF), W["bq1"][:, 0:1],
                                   HD ** -0.5, ALU.add, ALU.mult))
            split(qparts[:, :, 0:BT], qf, qr)
            dve.sem_inc(sem("q1_split"), 1)
            dve.wait_ge(sem("k1_ready"), 1)
            split(own_kparts[:, :, 0:BT], qf, qr)
            dve.wait_ge(sem("v1_projected"), 1)
            link(dve.tensor_copy(vs.rearrange("p (a b) d -> p a (b d)", a=2), slot(3, T, BANK)))
            dve.sem_inc(sem("layer1_setup"), 1)
            dve.sem_inc(sem("a1_query_parts_ready"), 1)
            attention(1)

            norm_x()
            link(dve.tensor_scalar(g0[0:NSLOT, 0:D], W["slots"][:, :], W["slot_scale"][:, 0:1], None, ALU.mult))
            dve.sem_inc(sem("slots_by_dve"), 1)
            dve.wait_ge(sem("slots_by_pe"), STEP["slots_turned"])
            link(dve.tensor_scalar(small[:, 8:9], bank(2, D, 1), 1.0 / NSLOT, None, ALU.mult))
            link(dve.tensor_copy(g1[:, 0:NSLOT], bank(3, D, NSLOT)))
            dve.sem_inc(sem("slots_by_dve"), 1)
            dve.sem_inc(sem("slots_by_dve"), 1)
            dve.wait_ge(sem("slots_by_pe"), STEP["slot_bias_psum"])
            link(dve.tensor_tensor(small[0:NSLOT, 10:11], bank(2, NSLOT, 1), W["f1b1"][:, 0:1], ALU.add))
            dve.sem_inc(sem("slots_by_dve"), 1)
            link(dve.scalar_tensor_tensor(out=small[0:T, 11:12], in0=W["tau"][0:T, 0:1], scalar=-1.0,
                                          in1=W["tau"][0:T, 0:1], op0=ALU.mult, op1=ALU.max))
            link(dve.tensor_scalar(small[0:T, 11:12], small[0:T, 11:12], 0.1, None, ALU.add))
            link(dve.reciprocal(small[0:T, 12:13], small[0:T, 11:12]))
            dve.wait_ge(sem("slots_by_pe"), STEP["route_logits"])
            lg = big3[0:T, 0:512].rearrange("p (b s) -> p b s", b=B)
            rest = big2[0:T, 0:512].rearrange("p (b s) -> p b s", b=B)
            chosen = big1[0:T, 0:512].rearrange("p (b s) -> p b s", b=B)
            ls = [T, B, NSLOT]
            link(dve.tensor_tensor(lg, bank(6, T, BANK).rearrange("p (b s) -> p b s", b=B),
                                   bc(W["f1b2"][0:T, :], ls, 1), ALU.add))
            link(dve.tensor_scalar(lg, lg, small[0:T, 12:13], None, ALU.mult))
            top = stat[0:T, 0:2, :].rearrange("p a b -> p (a b)").rearrange("p (b k) -> p b k", b=B)
            for bb in range(B):
                i = dve.max(top[:, bb, :], lg[:, bb, :])
            link(i)
            for bb in range(B):
                i = dve.match_replace(rest[:, bb, :], top[:, bb, :], lg[:, bb, :], -3e38)
            link(i)
            link(dve.tensor_tensor(chosen, rest, lg, ALU.not_equal))
            link(dve.tensor_tensor(rest, lg, top[:, :, 0:1].broadcast_to(ls), ALU.subtract))
            dve.sem_inc(sem("slots_by_dve"), 1)
            dve.wait_ge(sem("slots_by_act"), STEP["logits_exp"])
            link(dve.tensor_tensor(chosen, chosen, rest, ALU.mult))
            link(dve.tensor_reduce(stat[0:T, 3, 0:8], chosen, AX.X, ALU.add))
            link(dve.reciprocal(stat[0:T, 4, 0:8], stat[0:T, 3, 0:8]))
            link(dve.tensor_tensor(chosen, chosen, bc(stat[0:T, 4, 0:8], ls, 2), ALU.mult))
            dve.sem_inc(sem("slots_by_dve"), 1)
            dve.wait_ge(sem("slots_by_pe"), STEP["gh_psum"])
            for g in range(3):
                i = dve.tensor_scalar(g1[:, 64 + g * 64:128 + g * 64], bank(7, D, 192)[:, g * 64:(g + 1) * 64],
                                      W["f1bhh"][:, g:g + 1], None, ALU.add)
            link(i)
            dve.wait_ge(sem("slots_by_pe"), STEP["slot_inputs"])
            link(dve.tensor_scalar(g2[:, :], bank(1, D, BANK), 1e-8, None, ALU.add))
            link(dve.reciprocal(g2[:, :], g2[:, :]))
            link(dve.tensor_tensor(g3[:, :], bank(0, D, BANK), g2[:, :], ALU.mult))
            dve.sem_inc(sem("slots_by_dve"), 1)
            dve.wait_ge(sem("slots_by_pe"), STEP["gx_psum"])
            gs = [D, B, NSLOT]

            def gate_sum(dst, bk, g):
                dve.wait_ge(sem("dve_step"), own[0])
                link(dve.scalar_tensor_tensor(
                    out=dst.rearrange("p (b s) -> p b s", b=B), in0=bank(bk, D, BANK).rearrange("p (b s) -> p b s", b=B),
                    scalar=W["f1bih"][:, g:g + 1], in1=bc(g1[:, 64 + g * 64:128 + g * 64], gs, 1),
                    op0=ALU.add, op1=ALU.add))

            gate_sum(g0[:, :], 2, 0)
            dve.sem_inc(sem("slots_by_dve"), 1)
            gate_sum(big3[:, 0:512], 3, 1)
            dve.sem_inc(sem("slots_by_dve"), 1)
            dve.wait_ge(sem("slots_by_act"), STEP["gate_r_exp"])
            link(dve.tensor_scalar(g0[:, :], g0[:, :], 1.0, None, ALU.add))
            link(dve.reciprocal(g0[:, :], g0[:, :]))
            link(dve.tensor_tensor(g2[:, :].rearrange("p (b s) -> p b s", b=B),
                                   g0[:, :].rearrange("p (b s) -> p b s", b=B), bc(g1[:, 192:256], gs, 1), ALU.mult))
            link(dve.scalar_tensor_tensor(out=g3[:, :], in0=bank(6, D, BANK), scalar=W["f1bih"][:, 2:3], in1=g2[:, :],
                                          op0=ALU.add, op1=ALU.add))
            dve.sem_inc(sem("slots_by_dve"), 1)
            dve.wait_ge(sem("slots_by_act"), STEP["gate_z_exp"])
            link(dve.tensor_scalar(big3[:, 0:512], big3[:, 0:512], 1.0, None, ALU.add))
            link(dve.reciprocal(big3[:, 0:512], big3[:, 0:512]))
            dve.wait_ge(sem("slots_by_act"), STEP["gate_n_tanh"])
            link(dve.tensor_tensor(g2[:, :].rearrange("p (b s) -> p b s", b=B), bc(g1[:, 0:64], gs, 1),
                                   g3[:, :].rearrange("p (b s) -> p b s", b=B), ALU.subtract))
            link(dve.tensor_tensor(g2[:, :], g2[:, :], big3[:, 0:512], ALU.mult))
            link(dve.tensor_tensor(g2[:, :], g2[:, :], g3[:, :], ALU.add))
            dve.sem_inc(sem("slots_by_dve"), 1)
            dve.wait_ge(sem("ffn1_out"), 1)
            add_residual(slot(3, T, BANK), 5)

            norm_x()
            lf = lat[:, 0:B, :]
            link(dve.memset(lat[:, B, :], 0.0))
            link(norm_rows(lf, xn[:, :, :], T, B, D, wideA[:, :, :], stat[0:T]))
            link(dve.tensor_tensor(lf, lf, bc(W["lnlg"][0:T, :], [T, B, D], 1), ALU.mult))
            link(dve.tensor_tensor(lf, lf, bc(W["lnlb"][0:T, :], [T, B, D], 1), ALU.add))
            link(dve.memset(ctxT[:, :], 0.0))
            dve.sem_inc(sem("stage_cleared"), 1)
            link(dve.memset(kbc[:, :], 0.0))
            link(dve.memset(ones[:, :], 1.0))
            link(dve.memset(mB[:, :], 1.0))
            link(dve.memset(shares2[:, :], 1.0))
            dve.sem_inc(sem("latents_ready"), 1)
            ring = rings[2]
            dve.sem_inc(ring.emptied["dve"], ring.head["dve"])
            dve.sem_inc(sem("a2_contexts_copied_by_dve"), 1)
            per = STEPS[2]
            kk, ks = stage[:, 0:NCH, :], [128, NCH, D]
            s1, s2 = stat[:, 5, 0:NCH], stat[:, 6, 0:NCH]
            pair = "p (a k) -> p a k"

            def event(b, c):
                return 14 * b + c + 2

            def sum_squares(b, r, c, at, squares, step):
                step(dve.tensor_reduce(n2[0:r, at, :], squares[0:r, :].rearrange("p (h d) -> p h d", h=H), AX.X, ALU.add))
                step(dve.tensor_scalar(n2[0:r, at, :], n2[0:r, at, :], 1.0 / DH, 1e-16, ALU.mult, ALU.max))
                dve.sem_inc(sem("a2_squares_summed"), 1)

            def invert_norms(b, r, c, at, step):
                dve.wait_ge(sem("a2_norms"), event(b, c))
                step(dve.reciprocal(rk[0:r, at, :], n2[0:r, at, :]))

            def centre(b, step):
                dve.wait_ge(sem("ctx_keys_loaded"), 32 * b + 64)
                dve.tensor_copy(stage[0:T, NCH, :], lat[:, :, :].rearrange("p b d -> p (b d)")[:, bass.ds((b + 1) * D, D)])
                step(dve.tensor_reduce(s1, kk, AX.X, ALU.add))
                step(dve.tensor_scalar(s1, s1, 1.0 / D, None, ALU.mult))
                step(dve.tensor_tensor(kk, kk, bc(s1, ks, 2), ALU.subtract))
                dve.sem_inc(sem("a2_stage_centred"), 1)

            def variance(b, step):
                dve.wait_ge(sem("a2_stage_squared"), b + 2)
                step(dve.tensor_reduce(s2, scratch, AX.X, ALU.add))
                step(dve.tensor_scalar(s2, s2, 1.0 / D, LN_EPS, ALU.mult, ALU.add))
                dve.sem_inc(sem("a2_variances"), 1)

            def scale(b, step):
                dve.wait_ge(sem("a2_deviations"), b + 2)
                step(dve.reciprocal(s2, s2))
                step(dve.tensor_tensor(kk, kk, bc(s2, ks, 2), ALU.mult))
                dve.sem_inc(sem("a2_stage_scaled"), 1)

            def normalise_queries(b, step):
                dve.wait_ge(sem("a2_query_squares"), b + 2)
                sum_squares(b, T, 13, 0, values2, step)
                invert_norms(b, T, 13, 0, step)
                step(dve.tensor_tensor(qn.rearrange("p (a h d) -> p a h d", a=2, d=DH),
                                       slot(ring.slot_of("query", 0), T, BANK).rearrange("p a (h d) -> p a h d", d=DH),
                                       rk[0:T, 0, :].rearrange("p (a h) -> p a h", a=2).unsqueeze(3)
                                       .broadcast_to([T, 2, 8, DH]), ALU.mult))
                dve.sem_inc(ring.emptied["dve"], 1)
                dve.sem_inc(sem("a2_q_normalised"), 1)

            def divide_values(b):
                dve.wait_ge(sem("a2_heads_by_pe"), 3 * b + 1)
                dve.tensor_tensor(values2.rearrange("p (a h d) -> p a h d", a=2, d=DH),
                                  slot(3, T, BANK).rearrange("p a (h d) -> p a h d", d=DH),
                                  shares2[:, :].rearrange("p (a h) -> p a h", a=2).unsqueeze(3)
                                  .broadcast_to([T, 2, 8, DH]), ALU.mult).then_inc(sem("a2_heads_by_dve"), 1)

            def take_output(b):
                dve.wait_ge(sem("a2_heads_by_pe"), 3 * b + 3)
                dve.tensor_copy(attended2[:, bass.ds(b * D, D)], bank(6, T, D)).then_inc(sem("a2_heads_by_dve"), 1)

            centre(-1, link)
            variance(-1, link)
            scale(-1, link)
            normalise_queries(-1, link)
            dve.sem_inc(ring.emptied["dve"], 1)
            with dve.Fori(0, B) as b:
                k = [0]

                def step(i):
                    k[0] += 1
                    i.then_inc(sem("a2_dve_step"), 1)
                    dve.wait_ge(sem("a2_dve_step"), b * per + k[0])

                def square_sums(c):
                    dve.wait_ge(ring.emptied["act"], ring.emptied_count(b, "norm", c))
                    sum_squares(b, rows[c], c, c % 2, sq, step)

                rows = ROWS + [T]
                step(dve.tensor_copy(kbc[:, 0:NCH], kbias[:, :, :].rearrange("p b c -> p (b c)")[:, bass.ds(b * NCH, NCH)]))
                square_sums(0)
                invert_norms(b, rows[0], 0, 0, step)
                for c in range(13):
                    r = rows[c]
                    if c < NCH:
                        square_sums(c + 1)
                    for half in range(2):
                        dve.wait_ge(ring.full, ring.full_count(b, "score", 2 * c + half))
                        sl = S_all[0:r, c, 2 * half * GROUP:(2 * half + 2) * GROUP]
                        dve.tensor_tensor(sl.rearrange("p (a h q) -> p a h q", a=2, q=T),
                                          slot(ring.slot_of("score", 2 * c + half), r, GROUP)
                                          .rearrange("p a (h q) -> p a h q", q=T),
                                          rk[0:r, c % 2, 8 * half:8 * half + 8].rearrange("p (a h) -> p a h", a=2)
                                          .unsqueeze(3).broadcast_to([r, 2, 4, T]), ALU.mult
                                          ).then_inc(ring.emptied["dve"], 1)
                    dve.wait_ge(ring.emptied["dve"], ring.emptied_count(b, "score", 2 * c + 1))
                    if c == 0:
                        step(dve.tensor_scalar(M[0:r, :], S_all[0:r, c, :], kbc[0:r, c:c + 1], None, ALU.add))
                    else:
                        step(dve.scalar_tensor_tensor(out=M[0:r, :], in0=S_all[0:r, c, :], scalar=kbc[0:r, c:c + 1],
                                                      in1=M[0:r, :], op0=ALU.add, op1=ALU.max))
                    if c < NCH:
                        invert_norms(b, rows[c + 1], c + 1, (c + 1) % 2, step)
                    if c == VALUES:
                        divide_values(b)
                    if c == PROJECTED:
                        take_output(b)
                dve.sem_inc(sem("a2_column_max"), 1)
                for half in range(2):
                    dve.wait_ge(ring.full, ring.full_count(b, "turn", half))
                    step(dve.tensor_reduce(stat[0:T, 0, 8 * half:8 * half + 8].rearrange("p (a h) -> p a h", a=2),
                                           slot(ring.slot_of("turn", half), T, 4 * CK)
                                           .rearrange("p a (h k) -> p a h k", h=4), AX.X, ALU.max))
                    dve.sem_inc(ring.emptied["dve"], 1)
                dve.sem_inc(sem("a2_max_ready"), 1)
                dve.wait_ge(ring.full, ring.full_count(b, "row", 0))
                step(dve.tensor_tensor(M[0:16, :].rearrange("p (h q) -> p h q", h=16),
                                       bc(bank(2 * ring.slot_of("row", 0), 16, T), [16, 16, T], 1),
                                       bc(ident[0:16, 0:16], [16, 16, T], 2), ALU.mult))
                dve.sem_inc(ring.emptied["dve"], 1)
                dve.sem_inc(sem("a2_shift_ready"), 1)
                dve.wait_ge(ring.emptied["act"], ring.emptied_count(b, "shift", 1))
                for c in range(13):
                    r = rows[c]
                    dve.tensor_tensor(S_all[0:r, c, :], S_all[0:r, c, :], mB[0:r, :], ALU.subtract
                                      ).then_inc(sem("a2_scores_shifted"), 1)
                    if c == CENTRE:
                        centre(b, step)
                    if c == VARIANCE:
                        variance(b, step)
                    if c == SCALE:
                        scale(b, step)
                    if c == DVE_SUMS[1] + 2:
                        r = rows[DVE_SUMS[0]]
                        dve.wait_ge(sem("a2_probs_ready"), b * 13 + DVE_SUMS[1] + 1)
                        step(dve.tensor_tensor(M[0:r, :], S_all[0:r, DVE_SUMS[0], :], S_all[0:r, DVE_SUMS[1], :], ALU.add))
                normalise_queries(b, step)
                r = rows[DVE_SUMS[2]]
                dve.wait_ge(sem("a2_probs_ready"), b * 13 + DVE_SUMS[2] + 1)
                dve.tensor_tensor(M[0:r, :], M[0:r, :], S_all[0:r, DVE_SUMS[2], :], ALU.add
                                  ).then_inc(sem("a2_dve_summed"), 1)
                dve.wait_ge(sem("a2_keys_used"), b + 1)
                dve.tensor_copy(mB[:, 0:2 * GROUP].rearrange(pair, a=2), slot(2, D, GROUP)
                                ).then_inc(sem("a2_contexts_copied_by_dve"), 1)
                dve.wait_ge(ring.full, ring.full_count(b, "sum", 0))
                dve.reciprocal(shares2[:, :], bank(2 * ring.slot_of("sum", 0), T, H)).then_inc(ring.emptied["dve"], 1)
                dve.wait_ge(ring.emptied["dve"], ring.emptied_count(b, "sum", 0))
                assert k[0] == per, k[0]
            divide_values(B)
            take_output(B)
            dve.wait_ge(sem("a2_heads_by_dve"), 2 * (B + 1))
            link(dve.scalar_tensor_tensor(out=x[:, :, :], in0=wideB[:, 1:, :], scalar=gates[0:T, 2:3], in1=x[:, :, :],
                                          op0=ALU.mult, op1=ALU.add))

            link(dve.tensor_reduce(small[:, 16:17], W["f2fc"][:, :], AX.X, ALU.add, apply_absolute_value=True))
            link(dve.tensor_reduce(small[:, 17:18], W["f2proj"][:, :, :], AX.XY, ALU.add, apply_absolute_value=True))
            dve.sem_inc(sem("ternary_sums"), 1)
            dve.wait_ge(sem("ternary_scale"), 1)
            link(dve.tensor_scalar(small[:, 18:20], bank(2, 128, 2), 1.0 / (4 * D * D), 1e-6, ALU.mult, ALU.add))
            link(dve.tensor_scalar(small[:, 20:22], small[:, 18:20], 0.5, None, ALU.mult))
            link(dve.tensor_scalar(small[:, 22:24], small[:, 18:20], -0.5, None, ALU.mult))
            for w, i in ((W["f2fc"][:, :], 0), (W["f2proj"][:, :, :].rearrange("p a b -> p (a b)"), 1)):
                link(dve.tensor_scalar(big3[:, 0:512], w, small[:, 22 + i:23 + i], None, ALU.is_lt))
                link(dve.scalar_tensor_tensor(out=w, in0=w, scalar=small[:, 20 + i:21 + i], in1=big3[:, 0:512],
                                              op0=ALU.is_gt, op1=ALU.subtract))
            dve.sem_inc(sem("ternary_ready"), 1)
            norm_x()
            for bb in range(B):
                dve.wait_ge(sem("f2_gelu"), bb + 1)
                src = ternary_hidden(bb)
                link(dve.tensor_reduce(stat[0:T, 0, bb:bb + 1], src, AX.X, ALU.add))
                link(dve.tensor_scalar(stat[0:T, 1, bb:bb + 1], stat[0:T, 0, bb:bb + 1], 1.0 / F0, None, ALU.mult))
                link(dve.tensor_scalar(src, src, stat[0:T, 1, bb:bb + 1], None, ALU.subtract))
                link(dve.tensor_tensor(big3[0:T, 0:512], src, src, ALU.mult))
                link(dve.tensor_reduce(stat[0:T, 2, bb:bb + 1], big3[0:T, 0:512], AX.X, ALU.add))
            link(dve.tensor_scalar(stat[0:T, 3, 0:8], stat[0:T, 2, 0:8], 1.0 / F0, LN_EPS, ALU.mult, ALU.add))
            invert_roots(stat[0:T, 4, 0:8])
            for bb in range(B):
                src = ternary_hidden(bb)
                dst = big1[0:T, (bb % 2) * 512:(bb % 2 + 1) * 512]
                if bb >= 2:
                    dve.wait_ge(sem("f2_turned_psum"), bb - 1)
                link(dve.scalar_tensor_tensor(out=dst, in0=src, scalar=stat[0:T, 4, bb:bb + 1],
                                              in1=W["f2lnw"][0:T, :], op0=ALU.mult, op1=ALU.mult))
                link(dve.tensor_tensor(dst, dst, W["f2lnb"][0:T, :], ALU.add))
                dve.sem_inc(sem("f2_normalised"), 1)
            dve.wait_ge(sem("ffn2_out"), 1)
            add_residual(slot(3, T, BANK), 6)

            dve.sem_inc(sem("arena_free_for_experts"), 1)
            norm_x()
            for bb in range(B):
                dve.wait_ge(sem("qkv3_psum"), bb + 1)
                dve.tensor_tensor(qkv3[:, bb, :], bank(4 + bb % 4, T, 3 * D), W["b3"][0:T, :], ALU.add
                                  ).then_inc(sem("qkv3_ready"), 1)
            dve.wait_ge(sem("qkv3_ready"), B)
            link(dve.tensor_tensor(wideA[:, :, :], qkv3[:, :, 0:D], qkv3[:, :, D:2 * D], ALU.mult))
            link(dve.tensor_reduce(st3[:, 0:8], wideA[:, :, :], AX.X, ALU.add))
            link(dve.tensor_tensor(wideA[:, :, :], qkv3[:, :, 0:D], bc(W["b3"][0:T, D:2 * D], [T, B, D], 1), ALU.mult))
            link(dve.tensor_reduce(st3[:, 8:16], wideA[:, :, :], AX.X, ALU.add))
            dve.wait_ge(sem("qe3_ready"), 1)
            dve.sem_inc(sem("layer3_setup"), 1)
            ring = rings[3]
            dve.sem_inc(ring.emptied["dve"], ring.per["dve"])
            per = STEPS[3]
            with dve.Fori(0, B) as b:
                k = [0]

                def step(i):
                    k[0] += 1
                    i.then_inc(sem("a3_dve_step"), 1)
                    dve.wait_ge(sem("a3_dve_step"), b * per + k[0])

                dve.tensor_copy(q3c[:, :], qe3[:, bass.ds(b * T, T)]).then_inc(sem("a3_query_placed"), 1)
                dve.tensor_copy(st3[:, 32:33], st3[:, bass.ds(b, 1)])
                step(dve.tensor_copy(st3[:, 33:34], st3[:, bass.ds(b + 8, 1)]))
                dve.wait_ge(ring.full, ring.full_count(b, 0))
                dve.tensor_reduce(st3[:, 40:42], slot(0, T, KQ), AX.X, ALU.max)
                dve.wait_ge(ring.full, ring.full_count(b, 1))
                step(dve.tensor_reduce(st3[:, 42:44], slot(1, T, KQ), AX.X, ALU.max))
                step(dve.tensor_reduce(st3[:, 44:45], st3[:, 40:44], AX.X, ALU.max))
                step(dve.scalar_tensor_tensor(out=st3[:, 45:46], in0=st3[:, 44:45], scalar=st3[:, 33:34],
                                              in1=st3[:, 32:33], op0=ALU.add, op1=ALU.max))
                dve.tensor_tensor(st3[:, 34:35], st3[:, 33:34], st3[:, 45:46], ALU.subtract)
                step(dve.tensor_tensor(st3[:, 35:36], st3[:, 32:33], st3[:, 45:46], ALU.subtract))
                dve.sem_inc(sem("a3_shift_ready"), 1)
                dve.wait_ge(ring.full, ring.full_count(b, 2))
                dve.tensor_copy(PT3[0:CK, 0:8, :].rearrange("p (a c) q -> p a (c q)", a=2), slot(2, CK, GROUP)
                                ).then_inc(ring.emptied["dve"], 1)
                dve.wait_ge(ring.full, ring.full_count(b, 3))
                dve.tensor_copy(PT3[0:CK, 8:11, :].rearrange("p c q -> p (c q)"), bank(0, CK, 3 * T))
                dve.tensor_copy(PT3[0:LAST, 11, :], bank(0, LAST, 4 * T)[:, 3 * T:4 * T]
                                ).then_inc(ring.emptied["dve"], 1)
                dve.wait_ge(sem("a3_self_exp"), b + 1)
                dve.wait_ge(ring.full, ring.full_count(b, 4))
                step(dve.tensor_tensor(st3[:, 46:47], st3[:, 37:38], st3[:, 38:39], ALU.add))
                dve.tensor_tensor(st3[:, 47:48], st3[:, 46:47], st3[:, 36:37], ALU.add)
                step(dve.scalar_tensor_tensor(out=y3[:, :], in0=W["b3"][0:T, 2 * D:3 * D], scalar=st3[:, 46:47],
                                              in1=bank(2, T, D), op0=ALU.mult, op1=ALU.add))
                dve.reciprocal(st3[:, 48:49], st3[:, 47:48])
                vb = qkv3.rearrange("p b d -> p (b d)")[:, bass.ds(b * 3 * D + 2 * D, D)]
                step(dve.scalar_tensor_tensor(out=y3[:, :], in0=vb, scalar=st3[:, 36:37], in1=y3[:, :],
                                              op0=ALU.mult, op1=ALU.add))
                step(dve.tensor_scalar(y3[:, :], y3[:, :], st3[:, 48:49], gates[0:T, 3:4], ALU.mult, ALU.mult))
                xb = x[:, :, :].rearrange("p b d -> p (b d)")[:, bass.ds(b * D, D)]
                dve.tensor_tensor(xb, xb, y3[:, :], ALU.add).then_inc(ring.emptied["dve"], 1)
                assert k[0] == per, k[0]
            dve.wait_ge(ring.emptied["dve"], (B + 1) * ring.per["dve"])

            norm_x()
            eps = 1e-8
            link(dve.tensor_tensor(wideA[:, :, :], xn[:, :, :], xn[:, :, :], ALU.mult))
            link(dve.tensor_reduce(stat[0:T, 5, 0:8], wideA[:, :, :], AX.X, ALU.add))
            em = W["emb"][:, :]
            link(dve.tensor_tensor(g0[0:E3, 128:256], em, em, ALU.mult))
            link(dve.tensor_reduce(small[0:E3, 40:41], g0[0:E3, 128:256], AX.X, ALU.add))
            dve.sem_inc(sem("experts_by_dve"), 1)
            dve.wait_ge(sem("norms_ready"), 2)
            link(dve.tensor_scalar(stat[0:T, 5, 0:8], stat[0:T, 5, 0:8], eps, None, ALU.add))
            link(dve.reciprocal(stat[0:T, 5, 0:8], stat[0:T, 5, 0:8]))
            link(dve.tensor_scalar(small[0:E3, 41:42], small[0:E3, 40:41], eps, None, ALU.add))
            link(dve.reciprocal(small[0:E3, 42:43], small[0:E3, 41:42]))
            link(dve.tensor_scalar(g0[0:E3, 0:D], em, small[0:E3, 42:43], None, ALU.mult))
            dve.sem_inc(sem("experts_by_dve"), 1)
            dve.wait_ge(sem("experts_by_pe"), STEP["experts_turned"])
            dve.tensor_copy(g1[:, 0:8], W["embT"][:, :])
            link(dve.tensor_copy(g1[:, 8:16], bank(2, D, E3)))
            dve.sem_inc(sem("experts_by_dve"), 1)
            dve.wait_ge(sem("experts_by_pe"), STEP["expert_scores"])
            sc = bank(3, T, 128).rearrange("p (b k) -> p b k", b=B)
            es, fs = [T, B, E3], [T, B, E3, E3]
            simv = g2[0:T, 64:128].rearrange("p (b e) -> p b e", b=B)
            cosv = g2[0:T, 128:192].rearrange("p (b e) -> p b e", b=B)
            rank = g2[0:T, 192:256].rearrange("p (b e) -> p b e", b=B)
            rank2 = g2[0:T, 256:320].rearrange("p (b e) -> p b e", b=B)
            pair = g0[0:T, :].rearrange("p (b e f) -> p b e f", b=B, e=E3)
            pair2 = big3[0:T, 0:512].rearrange("p (b e f) -> p b e f", b=B, e=E3)
            link(dve.tensor_copy(simv, sc[:, :, 0:E3]))
            link(dve.tensor_tensor(cosv, sc[:, :, E3:2 * E3], bc(stat[0:T, 5, 0:8], es, 2), ALU.mult))
            link(dve.tensor_scalar(g1[0:T, 16:24], W["onb"][0:T, :], 0.1, None, ALU.mult))
            link(dve.tensor_tensor(cosv, cosv, bc(g1[0:T, 16:24], es, 1), ALU.add))
            def ranks(dst, other, v):
                fbc = v.unsqueeze(2).broadcast_to(fs)
                ebc = v.unsqueeze(3).broadcast_to(fs)
                link(dve.tensor_tensor(pair, fbc, ebc, ALU.is_gt))
                link(dve.tensor_reduce(dst, pair, AX.X, ALU.add))
                link(dve.tensor_tensor(pair, fbc, ebc, ALU.is_equal))
                link(dve.tensor_tensor(pair, pair, W["etri"][0:T, :].rearrange("p (e f) -> p e f", e=E3)
                                       .unsqueeze(1).broadcast_to(fs), ALU.mult))
                link(dve.tensor_reduce(other, pair, AX.X, ALU.add))
                link(dve.tensor_tensor(dst, dst, other, ALU.add))

            ranks(rank, rank2, simv)
            link(dve.tensor_scalar(rank, rank, 6.5, OFF, ALU.is_gt, ALU.mult))
            link(dve.tensor_tensor(cosv, cosv, rank, ALU.add))
            ranks(rank, rank2, cosv)
            link(dve.tensor_scalar(rank, rank, 1.5, None, ALU.is_lt))
            link(dve.tensor_reduce(stat[0:T, 6, 0:8], cosv, AX.X, ALU.max))
            ev = g3[0:T, 0:64].rearrange("p (b e) -> p b e", b=B)
            link(dve.tensor_tensor(ev, cosv, bc(stat[0:T, 6, 0:8], es, 2), ALU.subtract))
            dve.sem_inc(sem("experts_by_dve"), 1)
            dve.wait_ge(sem("experts_by_act"), STEP["expert_exp"])
            wv = g2[0:T, 0:64].rearrange("p (b e) -> p b e", b=B)
            link(dve.tensor_tensor(wv, ev, rank, ALU.mult))
            link(dve.tensor_reduce(stat[0:T, 7, 0:8], wv, AX.X, ALU.add))
            link(dve.reciprocal(stat[0:T, 7, 0:8], stat[0:T, 7, 0:8]))
            link(dve.tensor_scalar(stat[0:T, 7, 0:8], stat[0:T, 7, 0:8], gates[0:T, 7:8], None, ALU.mult))
            link(dve.tensor_tensor(wv, wv, bc(stat[0:T, 7, 0:8], es, 2), ALU.mult))
            dve.sem_inc(sem("experts_by_dve"), 1)
            dve.wait_ge(sem("experts_by_pe"), STEP["expert_biases"])
            link(dve.tensor_tensor(x[:, :, :].rearrange("p (a b) d -> p a (b d)", a=2), slot(1, T, BANK),
                                   x[:, :, :].rearrange("p (a b) d -> p a (b d)", a=2), ALU.add))
            dve.sem_inc(sem("experts_by_dve"), 1)
            for e in range(E3):
                dve.wait_ge(sem("f3_out"), e + 1)
                for half in range(2):
                    src = bank(2 * (e % 2) + half, T, BANK)
                    for i4 in range(4):
                        bb = 4 * half + i4
                        i = dve.scalar_tensor_tensor(out=x[:, bb, :], in0=src[:, i4 * D:(i4 + 1) * D],
                                                     scalar=wv[:, bb, e:e + 1], in1=x[:, bb, :],
                                                     op0=ALU.mult, op1=ALU.add)
                    i.then_inc(sem("f3_accumulated"), 1)
                dve.wait_ge(sem("f3_accumulated"), 2 * (e + 1))
            dve.sem_inc(sem("y_ready"), 1)


def milestones(*names):
    return {name: i + 1 for i, name in enumerate(names)}


STEP = {}
STEP.update(milestones("slots_turned", "slot_bias_psum", "f1_hidden_psum", "route_logits", "gh_psum", "slot_inputs",
                       "alpha_turned", "gx_psum", "slot_values_psum", "slot_outputs_psum"))
STEP.update(milestones("slots_scaled", "slot_mean", "slotsT_ready", "slot_bias", "logits_shifted", "alpha_ready",
                       "gi_ready", "gate_r_sum", "gate_z_sum", "gate_n_sum", "slots_new"))
STEP.update(milestones("logits_exp", "alphaT_ready", "gate_r_exp", "gate_z_exp", "gate_n_tanh", "slot_values",
                       "slot_outputs"))
STEP.update(milestones("experts_turned", "expert_scores", "expert_weights_psum", "expert_biases"))
STEP.update(milestones("squares_ready", "experts_normalised", "expert_columns", "expert_shifted", "expert_weights",
                       "expert_biases_taken"))
STEP.update(milestones("expert_exp", "expert_weights_turned"))


KEY_PART = (0, 0, 0, 1, 1, 2)
QUERY_PART = (0, 1, 2, 0, 1, 0)
STEPS = [9, 16, 68, 9]


def w3a_off():
    return 128 * 0 + 4 * BT + 3 * 1024 + 4 * 512


def kernel(**inputs):
    import numpy as np
    import ml_dtypes
    import concourse.bacc as bacc
    from concourse.bass_utils import run_bass_kernel_spmd

    v = {k: np.asarray(a) for k, a in inputs.items()}

    def col(a, k=1):
        return a.reshape(k, -1).T

    def rep(a, n):
        return np.broadcast_to(a.reshape(1, -1), (n, a.size))

    p = {}
    p["x"] = v["x"]
    p["ctx"] = v["ctx_1024"]
    p["ctxT"] = v["ctx_1024"].transpose(0, 2, 1)
    p["mask0"] = v["mask_1x1xSxS2_ik0"][0, 0].T
    p["mask2"] = v["mask_BxS2_bf1"].view(np.uint8)
    p["gates"] = rep(np.concatenate([v["g_xattn"], v["g_ffn"]]), 128)
    p["c_ident"] = np.eye(128, dtype=np.float32)
    p["c_identb"] = np.eye(128, dtype=ml_dtypes.bfloat16)
    p["c_low_rows"] = np.where(np.arange(32) // 8 % 2 == 1, -1.0, 0.0).astype(np.float32)[:, None]
    t = np.arange(T)
    p["c_before"] = (t[None, :] < t[:, None]).astype(np.float32)

    def pairs(a):
        return a.reshape(a.shape[0], 8, 2, HD).transpose(0, 2, 3, 1).reshape(a.shape[0], 128)

    def places(a):
        n = a.shape[0] // H
        return a.reshape(2, 4, 2, n, -1).transpose(0, 2, 1, 3, 4).reshape(a.shape)

    p["w_q0"] = pairs(v["L0_xattn_Wq"].T)
    p["w_k0"] = pairs(v["L0_xattn_Wk"].T)
    p["w_v0"] = v["L0_xattn_Wv"].T
    p["w_o0"] = places(v["L0_xattn_Wo"].T)
    p["w_bq0"] = pairs(v["L0_xattn_bq"].reshape(1, -1)).T
    p["w_bk0"] = pairs(v["L0_xattn_bk"].reshape(1, -1)).T
    p["w_bv0"] = places(col(v["L0_xattn_bv"]))
    p["w_bo0"] = rep(v["L0_xattn_bo"], 1)
    p["w_f0wr"] = col(v["L0_ffn_w_router"])
    p["w_f0W1"] = v["L0_ffn_W1"]
    p["w_f0b1"] = col(v["L0_ffn_b1"], 4)
    p["w_f0W2"] = v["L0_ffn_W2"].reshape(4, 128, D).transpose(1, 0, 2)
    p["w_f0b2"] = rep(v["L0_ffn_b2"], 1)
    w, b = v["L1_xattn_Wqkv"], v["L1_xattn_bqkv"].reshape(1, -1)
    wa, ba = v["L1_xattn_Wqkv_aux"], v["L1_xattn_bqkv_aux"].reshape(1, -1)
    p["w_q1"] = pairs(w[:, 0:D])
    p["w_k1"] = pairs(w[:, D:2 * D])
    p["w_v1"] = w[:, 2 * D:3 * D]
    p["w_ka1"] = pairs(wa[:, D:2 * D])
    p["w_va1"] = wa[:, 2 * D:3 * D]
    p["w_bq1"] = pairs(b[:, 0:D]).T
    p["w_bk1"] = pairs(b[:, D:2 * D]).T
    p["w_bv1"] = places(b[:, 2 * D:3 * D].T)
    p["w_bka1"] = pairs(ba[:, D:2 * D]).T
    p["w_bva1"] = places(ba[:, 2 * D:3 * D].T)
    p["w_o1"] = places(v["L1_xattn_Wo"])
    p["w_bo1"] = rep(v["L1_xattn_bo"], 1)
    p["w_g1"] = places(np.repeat(v["L1_xattn_g"], HD).reshape(128, 1))
    p["w_g1heads"] = rep(places(v["L1_xattn_g"]), 128)
    p["w_slots"] = v["L1_ffn_slot_init"]
    p["w_slot_scale"] = v["L1_ffn_slot_scale"]
    p["w_f1w1a"] = v["L1_ffn_w1"][:, 0:D].T
    p["w_f1w1b"] = v["L1_ffn_w1"][:, D:2 * D].T
    p["w_f1b1"] = col(v["L1_ffn_b1"])
    p["w_f1w2"] = v["L1_ffn_w2"].T
    p["w_f1b2"] = rep(v["L1_ffn_b2"], T)
    p["w_f1wih"] = v["L1_ffn_gru_wih"].T
    p["w_f1whh"] = v["L1_ffn_gru_whh"].T
    p["w_f1bih"] = col(v["L1_ffn_gru_bih"], 3)
    p["w_f1bhh"] = col(v["L1_ffn_gru_bhh"], 3)
    p["w_f1wv"] = v["L1_ffn_wv"].T
    p["w_f1bv"] = col(v["L1_ffn_bv"])
    p["w_f1wo"] = v["L1_ffn_wo"].T
    p["w_f1bo"] = rep(v["L1_ffn_bo"], 1)
    p["w_tau"] = rep(v["L1_ffn_tau"], T)
    p["w_lnxg"] = rep(v["L2_xattn_ln_x_g"], 128)
    p["w_lnxb"] = rep(v["L2_xattn_ln_x_b"], 128)
    p["w_lnlg"] = rep(v["L2_xattn_ln_l_g"], T)
    p["w_lnlb"] = rep(v["L2_xattn_ln_l_b"], T)
    p["w_gq2"] = np.tile(v["L2_xattn_qn_g"], 2).reshape(128, 1)
    p["w_gk2"] = np.tile(v["L2_xattn_kn_g"], 2).reshape(128, 1)
    p["w_q2"] = v["L2_xattn_Wq"]
    p["w_kv2"] = v["L2_xattn_Wkv"]
    p["w_k2T"] = v["L2_xattn_Wkv"][:, 0:H * DH].reshape(D, 8, 128).transpose(2, 1, 0)
    p["w_out2"] = v["L2_xattn_Wout"].reshape(8, 128, D).transpose(1, 0, 2)
    p["w_bo2"] = rep(v["L2_xattn_bout"], 1)
    p["w_f2fc"] = v["L2_ffn_W_fc"].T
    p["w_f2proj"] = v["L2_ffn_W_proj"].T.reshape(4, 128, D).transpose(1, 0, 2)
    p["w_f2lnw"] = rep(v["L2_ffn_ln_w"], T)
    p["w_f2lnb"] = rep(v["L2_ffn_ln_b"], T)
    p["w_qkv3"] = np.concatenate([v["L3_xattn_Wq"], v["L3_xattn_Wk"], v["L3_xattn_Wv"]], axis=1)
    p["w_k3T"] = v["L3_xattn_Wk"].T
    p["w_bq3"] = col(v["L3_xattn_bq"])
    p["w_b3"] = rep(np.concatenate([v["L3_xattn_bq"], v["L3_xattn_bk"], v["L3_xattn_bv"]]), T)
    p["w_emb"] = v["L3_ffn_uzman_embeddings"]
    p["w_embT"] = v["L3_ffn_uzman_embeddings"].T
    p["w_onb"] = rep(v["L3_ffn_onbellek_durumu"], T)
    e = np.arange(E3)
    p["w_etri"] = rep((e[None, :] < e[:, None]).astype(np.float32), T)
    p["w_f3b1"] = v["L3_ffn_b1"].reshape(E3, 4, 128).transpose(2, 0, 1)
    p["w_f3b2"] = v["L3_ffn_b2"]
    p["e_W1"] = v["L3_ffn_W1"].transpose(1, 0, 2)
    p["e_W2"] = v["L3_ffn_W2"].reshape(E3, 4, 128, D).transpose(2, 0, 1, 3)

    nc = bacc.Bacc("TRN2", target_bir_lowering=False, num_devices=1)
    arrays, A = {}, {}
    for name, a in p.items():
        a = np.ascontiguousarray(a)
        arrays["in_" + name] = a
        A[name] = nc.dram_tensor("in_" + name, a.shape, mybir.dt.from_np(a.dtype), kind="ExternalInput").ap()
    y = nc.dram_tensor("y", (B, T, D), F32, kind="ExternalOutput").ap()
    flamingo(nc, A, y)
    r = run_bass_kernel_spmd(nc, [arrays], core_ids=[0])
    return r.results[0]["y"]
```

```python
from contextlib import ExitStack

import concourse.bass as bass
from concourse import mybir

F32 = mybir.dt.float32
BF16 = mybir.dt.bfloat16
I32 = mybir.dt.int32
U8 = mybir.dt.uint8
ALU = mybir.AluOpType
ACT = mybir.ActivationFunctionType
AX = mybir.AxisListType

B, T, D = 8, 100, 128
H = 16
S2 = 1444
NCH = 12
CK = 121
LAST = S2 - (NCH - 1) * CK
KQ = S2 // 4
HD = 8
DH = 64
F0 = 512
NSLOT = 64
E3, H3 = 8, 512
BT = B * T
HALF = BT // 2
BANK = 512
LN_EPS = 1e-5
OFF = -1e30
GROUP = 4 * T
ROWS = [CK] * (NCH - 1) + [LAST]


FIRST_WEIGHTS = ("q0", "k0", "v0", "o0", "bq0", "bk0", "bv0", "bo0")
PAIR_OF_ONES = 1.0 + 0x3F80 / 2 ** 23


def flamingo(nc, A, out):
    ctx = ExitStack()
    with ctx:
        def sb(name, shape, dt=F32):
            return ctx.enter_context(nc.sbuf_tensor(name, shape, dt))

        sems = {}

        def sem(name):
            if name not in sems:
                sems[name] = ctx.enter_context(nc.semaphore(name))
            return sems[name]

        x = sb("x", [T, B, D])
        xn = sb("xn", [T, B, D])
        xnT = sb("xnT", [D, BT])
        wideA = sb("wideA", [T, B, D])
        wideB = sb("wideB", [T, B + 1, D])
        small = sb("small", [128, 64])
        stat = sb("stat", [128, 8, 32])
        gates = sb("gates", [128, 8])

        ident = sb("ident", [128, 128])
        identb = sb("identb", [128, 128], BF16)
        low_rows = sb("low_rows", [32, 1])
        before = sb("before", [T, T])
        ones = sb("ones", [128, 128])

        W = {}
        for name, ap in A.items():
            if name.startswith("w_"):
                W[name[2:]] = sb(name, list(ap.shape))
        wr_bc = sb("wr_bc", [D, T])
        bv1 = sb("bv1", [128, 1])
        head_gates = sb("head_gates", [128, 2, H])
        ctxT = sb("ctxT", [D, (NCH + 1) * D])
        ctxk = sb("ctxk", [128, NCH + 1, D])
        M = sb("M", [128, 4 * GROUP])
        arena = sb("arena", [128, 13 * 1600])

        psum = ctx.enter_context(nc.psum_tensor("psum", [128, 8, BANK], F32))

        def carve(off, shape):
            n = 1
            for s in shape[1:]:
                n *= s
            v = arena[0:shape[0], off:off + n]
            if len(shape) == 3:
                v = v.rearrange("p (a b) -> p a b", a=shape[1])
            if len(shape) == 4:
                v = v.rearrange("p (a b c) -> p a b c", a=shape[1], b=shape[2])
            return v, off + n

        kst_w, o = carve(0, [128, 8 * S2 // 2])
        own_kst_w, o = carve(o, [128, 8 * T // 2])
        q1_w, o = carve(o, [128, 8 * 2 * T // 2])
        q2_w, o = carve(o, [128, 8 * 2 * T // 2])
        own_q2_w, o = carve(o, [128, 8 * 2 * T // 2])
        kparts_w, o = carve(o, [128, 3 * S2 // 2])
        qparts_w, o = carve(o, [128, 3 * (BT + T) // 2])
        own_kparts_w, o = carve(o, [128, 3 * (BT + T) // 2])
        Vo_w, o = carve(o, [128, NCH * H * 9])
        own_Vo_w, o = carve(o, [128, H * 9])
        P3, o = carve(o, [128, 3, 2 * GROUP])
        summed, o = carve(o, [128, GROUP])
        own_summed, o = carve(o, [128, GROUP])
        shares, o = carve(o, [T, 2, H])
        heads, o = carve(o, [T, D])
        own_heads, o = carve(o, [T, D])
        headsT, o = carve(o, [D, T])
        mx, o = carve(o, [T, 2, 32])
        flag, o = carve(o, [T, 32])
        hl_w, o = carve(o, [32, 2 * T // 2])
        high_w, o = carve(o, [32, T // 2])
        maskw, o = carve(o, [128, NCH * T // 2])
        assert o <= 13 * 1600, o
        Vo = Vo_w.rearrange("p (c h d) -> p c h d", c=NCH, h=H)
        own_Vo = own_Vo_w.rearrange("p (h d) -> p h d", h=H)
        attended = wideB[:, :, :].rearrange("p b d -> p (b d)")
        keys_st = kst_w.bitcast(BF16).rearrange("p (h k) -> p h k", h=8)
        own_keys_st = own_kst_w.bitcast(BF16).rearrange("p (h k) -> p h k", h=8)
        q1 = q1_w.bitcast(BF16).rearrange("p (h q) -> p h q", h=8)
        q2 = q2_w.bitcast(BF16).rearrange("p (h q) -> p h q", h=8)
        own_q2 = own_q2_w.bitcast(BF16).rearrange("p (h q) -> p h q", h=8)
        kparts = kparts_w.bitcast(BF16).rearrange("p (a k) -> p a k", a=3)
        qparts = qparts_w.bitcast(BF16).rearrange("p (a k) -> p a k", a=3)
        own_kparts = own_kparts_w.bitcast(BF16).rearrange("p (a k) -> p a k", a=3)
        hl = hl_w.bitcast(BF16).rearrange("p (g q) -> p g q", g=2)
        high = high_w.bitcast(BF16)
        maskb = maskw.bitcast(BF16).rearrange("p (c q) -> p c q", c=NCH)
        lat = sb("lat", [T, B + 1, D])
        mB = sb("mB", [128, 4 * GROUP])
        xkT = sb("xkT", [D, S2 + T])
        qeff = sb("qeff", [D, H, T])
        Psum = sb("Psum", [128, 4 * GROUP])
        own_M = mB[0:T, :]
        kf = Psum[:, 0:S2]
        kr = qeff[:, :, :].rearrange("p h q -> p (h q)")[:, 0:S2]
        qf = Psum[:, 0:BT]
        qr = qeff[:, :, :].rearrange("p h q -> p (h q)")[:, 0:BT]
        Vn = xkT[:, 0:NCH * D].rearrange("p (c d) -> p c d", c=NCH)
        vs = lat[:, 0:B, :]
        maski = Psum[:, 0:NCH * T]

        hid, o = carve(0, [128, 4, BT])
        big1, o = carve(o, [128, 1024])
        big2, o = carve(o, [128, 1024])
        big3, o = carve(o, [128, 1024])
        g0, o = carve(o, [128, 512])
        g1, o = carve(o, [128, 512])
        g2, o = carve(o, [128, 512])
        g3, o = carve(o, [128, 512])
        w3a, o = carve(o, [D, E3, H3])
        w3b, o = carve(o, [128, E3, 4, D])
        assert o <= 13 * 1600, o
        acc3 = big1[0:T, :].rearrange("p (b d) -> p b d", b=B)
        q3T, o = carve(0, [D, BT])
        qe3, o = carve(o, [D, BT + T])
        qkv3, o = carve(o, [T, B, 3 * D])
        q3c, o = carve(o, [D, T])
        P1, o = carve(o, [T, S2])
        PT3, o = carve(o, [128, NCH, T])
        AT3, o = carve(o, [D, T])
        y3, o = carve(o, [T, D])
        st3, o = carve(o, [T, 64])
        assert o <= w3a_off(), o
        S_all, _ = carve(0, [128, 13, 4 * GROUP])
        sq = Psum[:, 0:1024]
        stage = ctxT[:, :].rearrange("p (c d) -> p c d", c=NCH + 1)
        scratch = qeff[:, :, :].rearrange("p h q -> p (h q)")[:, 0:NCH * D].rearrange("p (c d) -> p c d", c=NCH)
        qn = xn[:, :, :].rearrange("p b d -> p (b d)")
        qnt = xnT[:, :].rearrange("p (t q) -> p t q", t=8)
        values2 = wideA[:, :, :].rearrange("p b d -> p (b d)")
        values2T = xnT[:, :].rearrange("p (t q) -> p t q", t=8)
        attended2 = wideB[:, :, :].rearrange("p b d -> p (b d)")
        shares2 = sb("shares2", [T, 16])
        warm = sb("warm", [1, 1])
        n2 = sb("n2", [128, 2, 16])
        rk = sb("rk", [128, 2, 16])
        kbias = sb("kbias", [128, B, NCH])
        kbc = sb("kbc", [128, NCH + 1])
        kmask = sb("kmask", [128, B, NCH], U8)

        block = ctx.enter_context(nc.Block())

        def bank(i, parts, cols):
            return psum[0:parts, i, 0:cols]

        def slot(s, parts, cols):
            return psum[0:parts, 2 * s:2 * s + 2, 0:cols]

        def bc(v, shape, at):
            return v.unsqueeze(at).broadcast_to(shape)

        def ternary_hidden(bb):
            if bb < 4:
                return hid[0:T, :, :].rearrange("p a b -> p (a b)")[:, bb * 512:(bb + 1) * 512]
            return (g0, g1, g2, g3)[bb - 4][0:T, :]

        class Ring:
            def __init__(self, name, size, plan):
                while len(plan) % size:
                    plan = plan + ["none"]
                self.name, self.size, self.plan = name, size, plan
                self.full = sem(name + "_slot_full")
                self.emptied = {e: sem(f"{name}_slot_emptied_by_{e}") for e in ("act", "dve")}
                self.per = {e: plan.count(e) for e in ("act", "dve")}
                self.nfull = sum(p != "none" for p in plan)

            def before_fill(self, pe, b, n):
                m = n - self.size
                lap = 1 if m >= 0 else 0
                e = self.plan[m % len(self.plan)]
                if e == "none":
                    return
                k = self.plan[:m % len(self.plan) + 1].count(e)
                pe.wait_ge(self.emptied[e], (b + lap) * self.per[e] + k)

            def full_count(self, b, n):
                return b * self.nfull + n + 1

            def emptied_count(self, b, n):
                e = self.plan[n]
                return (b + 1) * self.per[e] + self.plan[:n + 1].count(e)

        class Uses:
            def __init__(self, name, uses, tail):
                self.uses, self.at = uses, {u[0:2]: n for n, u in enumerate(uses)}
                self.full = sem(name + "_slot_full")
                self.emptied = {e: sem(f"{name}_slot_emptied_by_{e}") for e in ("act", "dve")}
                who = [u[3] for u in uses]
                self.per = {e: who.count(e) for e in self.emptied}
                self.head = {e: who[:tail].count(e) for e in self.emptied}
                self.nfull, self.nhead = len(uses), tail

            def slot_of(self, *use):
                return self.uses[self.at[use]][2]

            def before_fill(self, pe, b, *use):
                n = self.at[use]
                same = [m for m, u in enumerate(self.uses) if u[2] == self.uses[n][2]]
                earlier = [m for m in same if m < n]
                m, lap = (earlier[-1], b) if earlier else (same[-1], b - 1)
                pe.wait_ge(self.emptied[self.uses[m][3]], self.emptied_count(lap, *self.uses[m][0:2]))

            def full_count(self, b, *use):
                return (b + 1) * self.nfull + self.at[use] + 1

            def emptied_count(self, b, *use):
                n = self.at[use]
                e = self.uses[n][3]
                return (b + 1) * self.per[e] + sum(u[3] == e for u in self.uses[:n + 1])

        def layer2_uses():
            order = [("norm", 0, "act")]
            for c in range(NCH + 1):
                if c < NCH:
                    order.append(("norm", c + 1, "act"))
                order += [("score", 2 * c, "dve"), ("score", 2 * c + 1, "act")]
            order += [("turn", 0, "dve"), ("turn", 1, "dve"), ("row", 0, "dve"), ("shift", 0, "act"), ("shift", 1, "act")]
            tail = [("context", 0, "act"), ("context", 1, "act"), ("query", 0, "dve"), ("turned", 0, "act"),
                    ("carried", 0, "act"), ("carried", 1, "act"), ("sum", 0, "dve")]
            return ([(k, i, n % 3, e) for n, (k, i, e) in enumerate(order)]
                    + [(k, i, n % 2, e) for n, (k, i, e) in enumerate(tail)], len(order))

        DVE_SUMS = (6, 9, 12)
        POOL_SUMS = [c for c in range(NCH + 1) if c not in DVE_SUMS]
        VALUES, VALUES_TURNED, PROJECTED = 1, 4, 7
        CENTRE, VARIANCE, SCALE = 0, 3, 5
        ACT_HEADS = 4
        TURN, QUERY = 8, 10

        def attention_order(layer):
            units = [("max", 0, u, "dve") for u in range(2 * NCH)]
            head = []
            if layer == 1:
                head = [("max", 1, 0, "dve"), ("max", 1, 1, "dve")]
                units[16:16] = [("exp", 1, 0, "act"), ("exp", 1, 1, "act")]
                units[8:8] = [("turn", 1, 0, "dve"), ("turn", 1, 1, "dve"), ("row", 1, 0, "dve")]
            return (head + units
                    + [("turn", 0, 0, "dve"), ("turn", 0, 1, "dve"), ("keys", 0, 0, "act"), ("keys", 0, 1, "act"),
                       ("row", 0, 0, "dve"), ("values", 0, 0, "dve"), ("values", 0, 1, "dve")]
                    + [("exp", 0, u, "act") for u in range(2 * NCH)])

        FINISH = [(1, 5, 9), (1, 4, 7, 10)]
        OWN_WEIGHED, OWN_TAKEN = 19, 22

        ORDER = [attention_order(0), attention_order(1)]

        def position(layer, kind, g, u):
            return [k[0:3] for k in ORDER[layer]].index((kind, g, u))

        rings = [Ring("a0", 3, [k[3] for k in ORDER[0]]), Ring("a1", 3, [k[3] for k in ORDER[1]]),
                 Uses("a2", *layer2_uses())]

        @block.sync
        def _(sp):
            sp.dma_start(x[:, :, :], A["x"].rearrange("b t d -> t b d")).then_inc(sem("first_loaded"), 16)
            for tile, name in ((ident, "c_ident"), (identb, "c_identb"), (low_rows, "c_low_rows"),
                               (before, "c_before"), (gates, "gates")):
                sp.dma_start(tile[:, :], A[name]).then_inc(sem("first_loaded"), 16)

            def load_weight(name, signal):
                t = W[name]
                sl = tuple(slice(None) for _ in t.shape)
                sp.dma_start(t[sl], A["w_" + name]).then_inc(sem(signal), 16)

            for name in FIRST_WEIGHTS:
                load_weight(name, "first_loaded")
            sp.dma_start(maski.bitcast(I32).rearrange("p (c q) -> p c q", c=NCH)[0:CK, 0:NCH - 1, :],
                         A["mask0"][0:(NCH - 1) * CK, :].rearrange("(c p) q -> p c q", p=CK)
                         ).then_inc(sem("first_loaded"), 16)
            sp.dma_start(maski.bitcast(I32).rearrange("p (c q) -> p c q", c=NCH)[0:LAST, NCH - 1, :],
                         A["mask0"][(NCH - 1) * CK:S2, :]).then_inc(sem("first_loaded"), 16)
            sp.dma_start(ctxT[:, 0:S2], A["ctxT"][0]).then_inc(sem("ctxT_loaded"), 16)
            for name in W:
                if name not in FIRST_WEIGHTS:
                    load_weight(name, "later_loaded")
            sp.wait_ge(sem("stages_by_dve"), STEP["key_mask_cleared"])
            with nc.allow_non_contiguous_dma(reason="a small mask, keys onto partitions"):
                for bb in range(B):
                    sp.dma_start(kmask[0:CK, bb, 0:NCH - 1],
                                 A["mask2"][bb, 0:(NCH - 1) * CK].rearrange("(c p) -> p c", p=CK)
                                 ).then_inc(sem("later_loaded"), 16)
                    sp.dma_start(kmask[0:LAST, bb, NCH - 1:NCH],
                                 A["mask2"][bb, (NCH - 1) * CK:S2].rearrange("(c p) -> p c", c=1)
                                 ).then_inc(sem("later_loaded"), 16)

            def load_keys(b, ctxk=ctxk):
                sp.dma_start(ctxk[0:CK, 0:NCH - 1, :],
                             A["ctx"][b, 0:(NCH - 1) * CK, :].rearrange("(c p) d -> p c d", p=CK)
                             ).then_inc(sem("ctx_keys_loaded"), 16)
                sp.dma_start(ctxk[0:LAST, NCH - 1, :], A["ctx"][b, (NCH - 1) * CK:S2, :]
                             ).then_inc(sem("ctx_keys_loaded"), 16)

            def stack_keys(layer, b, half):
                k0, k1 = (0, 6 * CK) if half == 0 else (6 * CK, S2)
                for r, part in enumerate(KEY_PART):
                    sp.dma_start(keys_st[16 * r:16 * r + 16, :, k0:k1], kparts[:, part, k0:k1]
                                 ).then_inc(sem(f"a{layer}_keys_stacked_{half}"), 16)

            def stack_queries(first, signal):
                for par in range(2):
                    for r, part in enumerate(QUERY_PART):
                        sp.dma_start(q1[16 * r + 8 * par:16 * r + 8 * par + 8, :, par * T:(par + 1) * T],
                                     qparts[64 * par:64 * par + 64, part, :][:, bass.ds(first, T)]
                                     ).then_inc(sem(signal), 16)

            def stack_own_keys(first, signal):
                for r, part in enumerate(KEY_PART):
                    sp.dma_start(own_keys_st[16 * r:16 * r + 16, :, :], own_kparts[:, part, :][:, bass.ds(first, T)]
                                 ).then_inc(sem(signal), 16)

            def count(v, top=1 << 20):
                return v if isinstance(v, int) else sp.snap(sp.to_reg(v), min_val=0, max_val=top)

            def place_shift(layer, g, this_one):
                dst = (q2, own_q2)[g]
                sp.wait_ge(sem(f"a{layer}_shift_ready_{g}"), this_one)
                for par in range(2):
                    sp.dma_start(dst[SHIFT + 2 * par:SHIFT + 2 * par + 2, :, par * T:(par + 1) * T], hl[16 * par:16 * par + 16, g, :]
                                 ).then_inc(sem(f"a{layer}_shift_placed_{g}"), 16)

            for layer in (0, 1):
                ring = rings[layer]
                p = f"a{layer}_"
                if layer == 1:
                    sp.wait_ge(ring_before.full, ring_before.full_count(B - 1, position(0, "values", 0, 1)))
                    sp.dma_start(ctxT[:, 0:S2], A["ctxT"][0]).then_inc(sem("ctxT_loaded"), 16)
                ring_before = ring
                sp.wait_ge(sem(p + "first_projected"), 1)
                sp.dma_start(ctxT[:, 0:S2], A["ctxT"][1]).then_inc(sem("ctxT_loaded"), 16)
                sp.wait_ge(sem(p + "ones_set"), 1)
                sp.wait_ge(sem(p + "keys_split"), 1)
                stack_keys(layer, 0, 0)
                stack_keys(layer, 0, 1)
                sp.wait_ge(sem(p + "query_parts_ready"), 1)
                stack_queries(0, p + "queries_stacked")
                if layer == 1:
                    stack_own_keys(0, p + "own_keys_stacked")

                def one_sequence(b, next_ctx):
                    this_one, next_one = count(b + 1), count(b + 2)
                    first = count((b + 1) * T, BT)
                    full = {k: count(ring.full_count(b, position(layer, *k)))
                            for k in [("values", 0, 1), ("exp", 0, NCH - 1), ("exp", 0, 2 * NCH - 1)]}
                    if layer == 1:
                        place_shift(1, 1, this_one)
                    place_shift(layer, 0, this_one)
                    sp.wait_ge(ring.full, full["values", 0, 1])
                    sp.dma_start(ctxT[:, 0:S2], A["ctxT"][next_ctx]).then_inc(sem("ctxT_loaded"), 16)
                    sp.wait_ge(sem(p + "queries_copied"), this_one)
                    stack_queries(first, p + "queries_stacked")
                    if layer == 1:
                        stack_own_keys(first, p + "own_keys_stacked")
                    sp.wait_ge(sem(p + "keys_split"), next_one)
                    sp.wait_ge(ring.full, full["exp", 0, NCH - 1])
                    stack_keys(layer, b + 1, 0)
                    sp.wait_ge(ring.full, full["exp", 0, 2 * NCH - 1])
                    stack_keys(layer, b + 1, 1)

                with sp.Fori(0, B - 2) as b:
                    one_sequence(b, b + 2)
                one_sequence(B - 2, B - 1)
                if layer == 1:
                    place_shift(1, 1, B)
                place_shift(layer, 0, B)
            sp.wait_ge(sem("stages_by_dve"), STEP["stage_cleared"])
            load_keys(0, stage)
            with sp.Fori(1, B) as b:
                sp.wait_ge(sem("a2_stage_copied"), b)
                load_keys(b, stage)
            sp.wait_ge(sem("a2_stage_copied"), B)
            load_keys(0, stage)
            sp.wait_ge(sem("a2_stage_copied"), B + 1)
            load_keys(0)
            sp.dma_start(ctxT[:, 0:S2], A["ctxT"][0]).then_inc(sem("ctxT_loaded"), 16)
            sp.wait_ge(sem("stages_by_dve"), STEP["arena_free_for_experts"])
            sp.dma_start(w3a, A["e_W1"]).then_inc(sem("experts_loaded"), 16)
            sp.dma_start(w3b, A["e_W2"]).then_inc(sem("experts_loaded"), 16)
            with sp.Fori(1, B) as b:
                sp.wait_ge(sem("a3_scores"), b)
                sp.dma_start(ctxT[:, 0:S2], A["ctxT"][b]).then_inc(sem("ctxT_loaded"), 16)
                sp.wait_ge(sem("a3_ctx_used"), b)
                load_keys(b)
            sp.wait_ge(sem("a3_scores"), B)
            sp.dma_start(ctxT[:, 0:S2], A["ctxT"][0]).then_inc(sem("ctxT_loaded"), 16)
            sp.wait_ge(sem("stages_by_dve"), STEP["y_ready"])
            sp.dma_start(out.rearrange("b t d -> t b d"), x[:, :, :]).then_inc(sem("y_stored"), 16)
            sp.wait_ge(sem("y_stored"), 16)

        FIRST_LOADS = 16 * (1 + 5 + len(FIRST_WEIGHTS) + 2)
        LATER_LOADS = 16 * (len(W) - len(FIRST_WEIGHTS) + 2 * B)
        CTX_LOADS = B + 1

        @block.tensor
        def _(pe):
            def mm(o, l, r, start=True, stop=True, **k):
                return pe.matmul(o, l, r, start=start, stop=stop, skip_group_check=True, **k)

            def turn_xn(n):
                pe.wait_ge(sem("xn_ready"), n + 1)
                n = n if n < 4 else n - 1
                for half in range(2):
                    for i in range(4):
                        m = pe.transpose(bank(half, D, BANK)[:, i * T:(i + 1) * T], xn[:, 4 * half + i, :],
                                         ident[0:T, 0:T])
                    m.then_inc(sem("xnT_in_psum"), 1)
                pe.wait_ge(sem("xnT_ready"), 2 * n + 2)

            def project(first, w, ws, signal):
                for half in range(2):
                    m = mm(bank(first + half, ws, HALF), w, xnT[:, half * HALF:(half + 1) * HALF])
                m.then_inc(sem(signal), 1)

            def attention(layer):
                ring = rings[layer]
                wk, wv = (W["k0"], W["v0"]) if layer == 0 else (W["ka1"], W["va1"])
                wo = W["o0"] if layer == 0 else W["o1"]
                bo = W["bo0"] if layer == 0 else W["bo1"]
                p = f"a{layer}_"
                pe.wait_ge(sem("ctxT_loaded"), 16 * CTX_LOADS * layer + 16)
                for i in range(4):
                    m = mm(bank(i, D, KQ), wk[:, :], ctxT[:, i * KQ:(i + 1) * KQ])
                m.then_inc(sem(p + "first_keys"), 1)
                for c in range(NCH):
                    if c == 8:
                        pe.wait_ge(sem(p + "key_parts_1"), 1)
                    bk = (4, 5, 0)[c // 4]
                    m = mm(bank(bk, ROWS[c], BANK)[:, (c % 4) * D:(c % 4 + 1) * D],
                           ctxT[:, c * CK:c * CK + ROWS[c]], wv[:, :])
                m.then_inc(sem(p + "first_projected"), 1)
                pe.wait_ge(sem(p + "values_turned"), 1)
                nf = 3 + layer

                def finish(b, k):
                    pe.wait_ge(sem(p + "heads_by_dve"), b * nf + k + 1)
                    if k == 0:
                        pe.wait_ge(sem(p + "sums_copied"), (layer + 1) * b + 1)
                    if k < layer + 1:
                        for j in range(4):
                            m = pe.transpose(bank(7, T, BANK)[:, j * 128:(j + 1) * 128],
                                             (summed, own_summed)[k][:, j * T:(j + 1) * T], ident[:, :])
                    elif k == layer + 1:
                        m = pe.transpose(bank(7, D, T), heads[:, :], ident[0:T, 0:T])
                    else:
                        mm(bank(7, T, D), headsT[:, :], wo[:, :], stop=False)
                        m = mm(bank(7, T, D), ones[0:1, 0:T], bo[0:1, :], start=False)
                    m.then_inc(sem(p + "heads_by_pe"), 1)

                with pe.Fori(0, B) as b:
                    def scores(n, g, u, q):
                        s = n % 3
                        c, hh = u // 2, u % 2
                        r = ROWS[c] if g == 0 else T
                        kst = keys_st if g == 0 else own_keys_st
                        masked = layer == 0
                        if masked:
                            for i in range(2):
                                mm(bank(2 * s + i, r, GROUP), identb[0:r, 0:r],
                                   bc(maskb[0:r, c, :], [r, 4, T], 1), stop=False)
                        for t in range(4):
                            m = mm(bank(2 * s + t // 2, r, GROUP)[:, (t % 2) * 2 * T:(t % 2 + 1) * 2 * T],
                                   kst[0:STACK, 4 * hh + t, c * CK:c * CK + r], q[0:STACK, 4 * hh + t, :],
                                   start=not masked)
                        m.then_inc(ring.full, 1)

                    def weigh(g, w, done):
                        c, hh = w // 2, w % 2
                        r = ROWS[c] if g == 0 else T
                        size = NCH if g == 0 else 1
                        pe.wait_ge(ring.emptied["act"], ring.emptied_count(b, position(layer, "exp", g, w)))
                        if w == 0:
                            pe.wait_ge(sem(p + "values_placed"), b + 1)
                            if g == 0:
                                pe.wait_ge(sem(p + "sums_copied"), (layer + 1) * b + 1)
                            else:
                                pe.wait_ge(sem(p + "heads_by_dve"), (b + 1) * nf + 1)
                        for par in range(2):
                            for t in range(4):
                                h = 8 * hh + 2 * t + par
                                k = (2 * t + par) * T
                                col = (2 * hh + par) * T
                                m = mm(psum[32 * t:32 * t + 9, 6 + g, col:col + T],
                                       Vo[0:r, c, h, :] if g == 0 else own_Vo[0:r, h, :],
                                       P3[0:r, done % 3, k:k + T],
                                       start=(c, hh, par) == (0, 0, 0), stop=c == size - 1)
                        m.then_inc(sem(p + "probs_used"), 1)

                    done = 0
                    for n, (kind, g, u, _) in enumerate(ORDER[layer]):
                        s = n % 3
                        ring.before_fill(pe, b, n)
                        if kind == "max":
                            if g == 1 and u == 0:
                                pe.wait_ge(sem(p + "own_keys_stacked"), 16 * 6 * (b + 1))
                            if (g, u) == ((0, 0) if layer == 0 else (1, 0)):
                                pe.wait_ge(sem(p + "queries_stacked"), 16 * 12 * (b + 1))
                            if g == 0 and u in (0, NCH):
                                pe.wait_ge(sem(p + f"keys_stacked_{u // NCH}"), 16 * 6 * (b + 1))
                            scores(n, g, u, q1)
                            if g == 0 and u in FINISH[layer]:
                                finish(b, FINISH[layer].index(u))
                            if layer == 1 and g == 0 and u == OWN_WEIGHED:
                                for w in range(2):
                                    weigh(1, w, done)
                                    done += 1
                        elif kind == "turn":
                            r = CK if g == 0 else T
                            src = M if g == 0 else own_M
                            if u == 0:
                                last = 2 * NCH - 1 if g == 0 else 1
                                pe.wait_ge(ring.emptied["dve"], ring.emptied_count(b, position(layer, "max", g, last)))
                            for k in range(8):
                                h = 8 * u + k
                                m = pe.transpose(bank(2 * s + k // 4, T, BANK)[:, (k % 4) * CK:(k % 4) * CK + r],
                                                 src[0:r, h * T:(h + 1) * T], ident[0:r, 0:r])
                            m.then_inc(ring.full, 1)
                        elif kind == "row":
                            pe.wait_ge(sem(p + f"max_ready_{g}"), b + 1)
                            pe.transpose(bank(2 * s, 32, T), mx[:, g, :], ident[0:T, 0:T]).then_inc(ring.full, 1)
                        elif kind == "keys":
                            if u == 0:
                                pe.wait_ge(sem("ctxT_loaded"), 16 * CTX_LOADS * layer + 16 * b + 32)
                            for i in range(2):
                                c0 = (2 * u + i) * KQ
                                m = mm(bank(2 * s + i, D, KQ), wk[:, :], ctxT[:, c0:c0 + KQ])
                            m.then_inc(ring.full, 1)
                        elif kind == "values":
                            for k, c in enumerate(range(8) if u == 0 else range(8, NCH)):
                                m = mm(bank(2 * s + k // 4, ROWS[c], BANK)[:, (k % 4) * D:(k % 4 + 1) * D],
                                       ctxT[:, c * CK:c * CK + ROWS[c]], wv[:, :])
                            m.then_inc(ring.full, 1)
                        else:
                            if u == 0:
                                pe.wait_ge(sem(p + "queries_copied"), b + 1)
                                pe.wait_ge(sem(p + f"shift_placed_{g}"), 32 * (b + 1))
                            scores(n, g, u, (q2, own_q2)[g])
                            if g == 0 and u >= 2:
                                weigh(g, u - 2, done)
                                done += 1
                            if g == 0 and u == 2 * NCH - 1:
                                for w in (u - 1, u):
                                    weigh(g, w, done)
                                    done += 1
                for k in range(nf):
                    finish(B, k)

            pe.wait_ge(sem("first_loaded"), FIRST_LOADS)
            turn_xn(0)
            project(2, W["q0"][:, :], D, "q0_projected")
            pe.wait_ge(sem("stages_by_dve"), STEP["layer0_setup"])
            attention(0)
            pe.wait_ge(sem("later_loaded"), LATER_LOADS)
            turn_xn(1)
            project(2, wr_bc[:, :], T, "router_scores")
            for k in range(8):
                f, half = k // 2, k % 2
                if k >= 4:
                    pe.wait_ge(sem("ffn0_hidden"), k - 3)
                mm(bank(4 + k % 4, 128, HALF), W["f0W1"][:, f * 128:(f + 1) * 128],
                   xnT[:, half * HALF:(half + 1) * HALF]).then_inc(sem("ffn0_hidden_psum"), 1)
            pe.wait_ge(sem("ffn0_hidden"), 8)
            for bb in range(B):
                o = bank(bb // 4, T, BANK)[:, (bb % 4) * D:(bb % 4 + 1) * D]
                for f in range(4):
                    mm(o, hid[:, f, bb * T:(bb + 1) * T], W["f0W2"][:, f, :], start=f == 0, stop=False)
                m = mm(o, ones[0:1, 0:T], W["f0b2"][0:1, :], start=False)
            m.then_inc(sem("ffn0_out"), 1)
            turn_xn(2)
            project(2, W["q1"][:, :], D, "q1_projected")
            project(4, W["k1"][:, :], D, "k1_projected")
            for bb in range(B):
                m = mm(bank(6 + bb // 4, T, BANK)[:, (bb % 4) * D:(bb % 4 + 1) * D],
                       xnT[:, bb * T:(bb + 1) * T], W["v1"][:, :])
            m.then_inc(sem("v1_projected"), 1)
            pe.wait_ge(sem("stages_by_dve"), STEP["layer1_setup"])
            attention(1)
            turn_xn(3)
            pe.wait_ge(sem("slots_by_dve"), STEP["slots_scaled"])
            mm(bank(2, D, 1), g0[0:NSLOT, 0:D], ones[0:NSLOT, 0:1])
            pe.transpose(bank(3, D, NSLOT), g0[0:NSLOT, 0:D], ident[0:NSLOT, 0:NSLOT]).then_inc(sem("slots_by_pe"), 1)
            pe.wait_ge(sem("slots_by_dve"), STEP["slot_mean"])
            mm(bank(2, NSLOT, 1), W["f1w1b"][:, :], small[:, 8:9]).then_inc(sem("slots_by_pe"), 1)
            for half in range(2):
                m = mm(bank(4 + half, NSLOT, HALF), W["f1w1a"][:, :], xnT[:, half * HALF:(half + 1) * HALF])
            m.then_inc(sem("slots_by_pe"), 1)
            pe.wait_ge(sem("f1_hidden"), 2)
            for bb in range(B):
                m = mm(bank(6, T, BANK)[:, bb * NSLOT:(bb + 1) * NSLOT], hid[0:NSLOT, 0, bb * T:(bb + 1) * T],
                       W["f1w2"][:, :])
            m.then_inc(sem("slots_by_pe"), 1)
            pe.wait_ge(sem("slots_by_dve"), STEP["slotsT_ready"])
            for g in range(3):
                m = mm(bank(7, D, 3 * NSLOT)[:, g * NSLOT:(g + 1) * NSLOT], W["f1whh"][:, g * D:(g + 1) * D],
                       g1[:, 0:NSLOT])
            m.then_inc(sem("slots_by_pe"), 1)
            pe.wait_ge(sem("slots_by_dve"), STEP["alpha_ready"])
            for bb in range(B):
                al = big1[0:T, bb * NSLOT:(bb + 1) * NSLOT]
                mm(bank(0, D, BANK)[:, bb * NSLOT:(bb + 1) * NSLOT], xn[:, bb, :], al)
            mm(bank(1, D, BANK), ones[0:T, :], big1[0:T, 0:B * NSLOT]).then_inc(sem("slots_by_pe"), 1)
            for bb in range(B):
                m = pe.transpose(bank(4 + bb // 4, NSLOT, BANK)[:, (bb % 4) * T:(bb % 4 + 1) * T],
                                 big1[0:T, bb * NSLOT:(bb + 1) * NSLOT], ident[0:T, 0:T])
            m.then_inc(sem("slots_by_pe"), 1)
            pe.wait_ge(sem("slots_by_dve"), STEP["gi_ready"])
            for g, bk in enumerate((2, 3, 6)):
                m = mm(bank(bk, D, BANK), W["f1wih"][:, g * D:(g + 1) * D], g3[:, :])
            m.then_inc(sem("slots_by_pe"), 1)
            pe.wait_ge(sem("slots_by_dve"), STEP["slots_new"])
            mm(bank(0, D, BANK), W["f1wv"][:, :], g2[:, :]).then_inc(sem("slots_by_pe"), 1)
            pe.wait_ge(sem("slots_by_act"), STEP["slot_values"])
            for bb in range(B):
                m = mm(bank(2 + bb // 4, NSLOT, BANK)[:, (bb % 4) * D:(bb % 4 + 1) * D],
                       g3[:, bb * NSLOT:(bb + 1) * NSLOT], W["f1wo"][:, :])
            m.then_inc(sem("slots_by_pe"), 1)
            pe.wait_ge(sem("slots_by_act"), STEP["slot_outputs"])
            for bb in range(B):
                o = bank(6 + bb // 4, T, BANK)[:, (bb % 4) * D:(bb % 4 + 1) * D]
                mm(o, hid[0:NSLOT, 1, bb * T:(bb + 1) * T], big2[0:NSLOT, bb * D:(bb + 1) * D], stop=False)
                m = mm(o, ones[0:1, 0:T], W["f1bo"][0:1, :], start=False)
            m.then_inc(sem("ffn1_out"), 1)
            ring = rings[2]
            rows = ROWS + [T]

            def columns2(c):
                return xkT[:, min(c * CK, S2):min(c * CK, S2) + rows[c]]

            def fill(b, *use):
                ring.before_fill(pe, b, *use)
                return ring.slot_of(*use)

            def filled(m):
                m.then_inc(ring.full, 1)

            def turn_context(b):
                pe.wait_ge(sem("a2_keys_normalised"), b + 2)
                for half, chunks in enumerate((range(0, 8), range(8, 13))):
                    s = fill(b, "context", half)
                    for k, c in enumerate(chunks):
                        m = pe.transpose(bank(2 * s + k // 4, D, BANK)[:, (k % 4) * CK:(k % 4) * CK + rows[c]],
                                         stage[0:rows[c], c, :], ident[0:rows[c], 0:rows[c]])
                    filled(m)

            def project_queries(b):
                pe.wait_ge(ring.emptied["act"], ring.emptied_count(b, "context", 1))
                s = fill(b, "query", 0)
                for i in range(2):
                    m = mm(bank(2 * s + i, T, BANK), xkT[:, S2:S2 + T], W["q2"][:, i * BANK:(i + 1) * BANK])
                filled(m)

            def carry_queries(b):
                pe.wait_ge(sem("a2_q_normalised"), b + 2)
                s = fill(b, "turned", 0)
                for t in range(8):
                    m = pe.transpose(bank(2 * s + t // 4, D, BANK)[:, (t % 4) * T:(t % 4 + 1) * T],
                                     qn[:, t * D:(t + 1) * D], ident[0:T, 0:T])
                filled(m)
                pe.wait_ge(ring.emptied["act"], ring.emptied_count(b, "turned", 0))
                for half in range(2):
                    s = fill(b, "carried", half)
                    for t in range(4):
                        for par in range(2):
                            tt = 4 * half + t
                            m = mm(bank(2 * s + par, D, BANK)[:, t * T:(t + 1) * T],
                                   W["k2T"][64 * par:64 * par + 64, tt, :], qnt[64 * par:64 * par + 64, tt, :])
                    filled(m)

            def finish2(b, k):
                if k == 0:
                    pe.wait_ge(sem("a2_contexts_copied_by_dve"), b + 1)
                    pe.wait_ge(sem("a2_contexts_copied_by_act"), b + 1)
                    for h in range(H):
                        m = mm(bank(6 + h // 8, T, BANK)[:, (h % 8) * DH:(h % 8 + 1) * DH],
                               mB[:, h * T:(h + 1) * T], W["kv2"][:, H * DH + h * DH:H * DH + (h + 1) * DH])
                elif k == 1:
                    pe.wait_ge(sem("a2_heads_by_dve"), 2 * b + 1)
                    for t in range(8):
                        m = pe.transpose(bank(6 + t // 4, D, BANK)[:, (t % 4) * T:(t % 4 + 1) * T],
                                         values2[:, t * D:(t + 1) * D], ident[0:T, 0:T])
                else:
                    pe.wait_ge(sem("a2_heads_by_act"), b + 1)
                    for t in range(8):
                        mm(bank(6, T, D), values2T[:, t, :], W["out2"][:, t, :], start=t == 0, stop=False)
                    m = mm(bank(6, T, D), ones[0:1, 0:T], W["bo2"][0:1, :], start=False)
                m.then_inc(sem("a2_heads_by_pe"), 1)

            pe.sem_inc(ring.full, ring.nhead)
            pe.wait_ge(sem("stages_by_dve"), STEP["latents_ready"])
            turn_context(-1)
            project_queries(-1)
            carry_queries(-1)
            pe.wait_ge(ring.emptied["act"], ring.emptied_count(-1, "carried", 1))
            pe.sem_inc(ring.full, 1)
            with pe.Fori(0, B) as b:
                def norms(c):
                    s = fill(b, "norm", c)
                    if s == 2 and c <= 2:
                        pe.wait_ge(sem("a2_contexts_copied_by_dve"), b + 1)
                    for i in range(2):
                        m = mm(bank(2 * s + i, rows[c], BANK), columns2(c), W["kv2"][:, i * BANK:(i + 1) * BANK])
                    filled(m)

                norms(0)
                pe.wait_ge(ring.emptied["act"], ring.emptied_count(b - 1, "carried", 1))
                for c in range(13):
                    if c < NCH:
                        norms(c + 1)
                    for half in range(2):
                        s = fill(b, "score", 2 * c + half)
                        if s == 2 and c == 0:
                            pe.wait_ge(sem("a2_contexts_copied_by_dve"), b + 1)
                        for i in range(2):
                            j = 2 * half + i
                            m = mm(bank(2 * s + i, rows[c], GROUP), columns2(c), qeff[:, 4 * j:4 * j + 4, :])
                        filled(m)
                    if c in (VALUES, VALUES_TURNED, PROJECTED):
                        finish2(b, (VALUES, VALUES_TURNED, PROJECTED).index(c))
                for half in range(2):
                    pe.wait_ge(sem("a2_column_max"), 2 * b + half + 1)
                    s = fill(b, "turn", half)
                    for k in range(8):
                        h = 8 * half + k
                        m = pe.transpose(bank(2 * s + k // 4, T, BANK)[:, (k % 4) * CK:(k % 4 + 1) * CK],
                                         M[0:CK, h * T:(h + 1) * T], ident[0:CK, 0:CK])
                    filled(m)
                pe.wait_ge(sem("a2_max_ready"), b + 1)
                s = fill(b, "row", 0)
                filled(pe.transpose(bank(2 * s, 16, T), stat[0:T, 0, 0:16], ident[0:T, 0:T]))
                for half in range(2):
                    pe.wait_ge(sem("a2_shift_ready"), 2 * b + half + 1)
                    s = fill(b, "shift", half)
                    for i in range(2):
                        j = 2 * half + i
                        m = mm(bank(2 * s + i, 128, GROUP), ones[0:16, :], M[0:16, j * GROUP:(j + 1) * GROUP])
                    filled(m)
                last = [u for u in ring.uses[0:ring.nhead] if u[2] == 2][-1]
                for c in range(13):
                    r = rows[c]
                    pe.wait_ge(sem("a2_probs_ready"), b * 13 + c + 1)
                    if c == 0:
                        pe.wait_ge(ring.emptied[last[3]], ring.emptied_count(b, *last[0:2]))
                        pe.wait_ge(sem("a2_heads_by_dve"), 2 * b + 2)
                        pe.wait_ge(sem("a2_stage_copied"), b + 1)
                    for j in range(4):
                        m = mm(bank(4 + j, D, GROUP), ctxk[0:r, c, :], S_all[0:r, c, j * GROUP:(j + 1) * GROUP],
                               start=c == 0, stop=c == 12)
                    if c == 12:
                        m.then_inc(sem("a2_keys_used"), 1)
                    if c == TURN:
                        turn_context(b)
                    if c == QUERY:
                        project_queries(b)
                carry_queries(b)
                pe.wait_ge(sem("a2_pool_summed"), (len(POOL_SUMS) - 1) * (b + 1))
                pe.wait_ge(sem("a2_dve_summed"), b + 1)
                s = fill(b, "sum", 0)
                for h in range(H):
                    for part, tile in enumerate((Psum, M)):
                        m = mm(bank(2 * s, T, H)[:, h:h + 1], tile[0:CK, h * T:(h + 1) * T], ones[0:CK, 0:1],
                               start=h + part == 0, stop=part == 1)
                filled(m)
            for k in range(3):
                finish2(B, k)
            pe.wait_ge(sem("stages_by_dve"), STEP["ternary_sums"])
            mm(bank(2, 128, 2), ones[:, :], small[:, 16:18]).then_inc(sem("ternary_scale"), 1)
            turn_xn(5)
            pe.wait_ge(sem("stages_by_dve"), STEP["ternary_ready"])
            for bb in range(B):
                if bb >= 2:
                    pe.wait_ge(sem("f2_gelu"), bb - 1)
                mm(bank(2 + bb % 2, T, BANK), xnT[:, bb * T:(bb + 1) * T], W["f2fc"][:, :]
                   ).then_inc(sem("f2_hidden_psum"), 1)
            for bb in range(B):
                pe.wait_ge(sem("f2_normalised"), bb + 1)
                if bb >= 2:
                    pe.wait_ge(sem("f2_turned"), bb - 1)
                for f in range(4):
                    m = pe.transpose(bank(4 + bb % 2, 128, BANK)[:, f * T:(f + 1) * T],
                                     big1[0:T, (bb % 2) * 512 + f * 128:(bb % 2) * 512 + (f + 1) * 128],
                                     ident[0:T, 0:T])
                m.then_inc(sem("f2_turned_psum"), 1)
                pe.wait_ge(sem("f2_turned"), bb + 1)
                o = bank(6 + bb // 4, T, BANK)[:, (bb % 4) * D:(bb % 4 + 1) * D]
                for f in range(4):
                    m = mm(o, big2[:, (bb % 2) * 400 + f * T:(bb % 2) * 400 + (f + 1) * T], W["f2proj"][:, f, :],
                           start=f == 0, stop=f == 3)
            m.then_inc(sem("ffn2_out"), 1)
            turn_xn(6)
            project(2, W["qkv3"][:, 0:D], D, "q3T_psum")
            for bb in range(B):
                if bb >= 4:
                    pe.wait_ge(sem("qkv3_ready"), bb - 3)
                mm(bank(4 + bb % 4, T, 3 * D), xnT[:, bb * T:(bb + 1) * T], W["qkv3"][:, :]
                   ).then_inc(sem("qkv3_psum"), 1)
            pe.wait_ge(sem("stages_by_act"), STEP["q3T_ready"])
            for half in range(2):
                m = mm(bank(half, D, HALF), W["k3T"][:, :], q3T[:, half * HALF:(half + 1) * HALF])
            m.then_inc(sem("qe3_psum"), 1)
            pe.wait_ge(sem("stages_by_dve"), STEP["layer3_setup"])

            def scores3(b):
                pe.wait_ge(sem("ctxT_loaded"), 32 * CTX_LOADS + 16 * b + 16)
                pe.wait_ge(sem("a3_query_placed"), b + 1)
                for i in range(4):
                    m = mm(bank(i, T, KQ), q3c[:, :], ctxT[:, i * KQ:(i + 1) * KQ])
                m.then_inc(sem("a3_scores"), 1)

            scores3(0)
            with pe.Fori(0, B) as b:
                pe.wait_ge(sem("a3_exp"), b + 1)
                pe.wait_ge(sem("a3_turned_copied"), b + 1)
                for c in range(NCH):
                    m = pe.transpose(bank(4 + c // 4, ROWS[c], BANK)[:, (c % 4) * T:(c % 4 + 1) * T],
                                     P1[:, c * CK:c * CK + ROWS[c]], ident[0:T, 0:T])
                m.then_inc(sem("a3_turned"), 1)
                scores3(b + 1)
                pe.wait_ge(sem("a3_turned_copied"), b + 2)
                pe.wait_ge(sem("ctx_keys_loaded"), 32 * (B + 1) + 32 * b + 32)
                pe.wait_ge(sem("a3_output_taken"), b + 1)
                for c in range(NCH):
                    m = mm(bank(7, D, T), ctxk[0:ROWS[c], c, :], PT3[0:ROWS[c], c, :], start=c == 0, stop=c == NCH - 1)
                m.then_inc(sem("a3_ctx_used"), 1)
                pe.wait_ge(sem("a3_context_copied"), b + 1)
                mm(bank(7, T, D), AT3[:, :], W["qkv3"][:, 2 * D:3 * D]).then_inc(sem("a3_output"), 1)
            turn_xn(7)
            pe.wait_ge(sem("experts_by_dve"), STEP["experts_normalised"])
            pe.transpose(bank(2, D, E3), g0[0:E3, 0:D], ident[0:E3, 0:E3]).then_inc(sem("experts_by_pe"), 1)
            pe.wait_ge(sem("experts_by_dve"), STEP["expert_columns"])
            for bb in range(B):
                m = mm(bank(3, T, 128)[:, bb * 16:(bb + 1) * 16], xnT[:, bb * T:(bb + 1) * T], g1[:, 0:16])
            m.then_inc(sem("experts_by_pe"), 1)

            def expert_hidden(e):
                for k in range(8):
                    f, half = k // 2, k % 2
                    q = 8 * e + k
                    if q >= 4:
                        pe.wait_ge(sem("f3_gelu"), q - 3)
                    mm(bank(4 + q % 4, 128, HALF), w3a[:, e, f * 128:(f + 1) * 128],
                       xnT[:, half * HALF:(half + 1) * HALF]).then_inc(sem("f3_hidden_psum"), 1)

            pe.wait_ge(sem("experts_loaded"), 32)
            expert_hidden(0)
            pe.wait_ge(sem("experts_by_dve"), STEP["expert_weights"])
            for bb in range(B):
                m = pe.transpose(bank(bb // 4, E3, BANK)[:, (bb % 4) * T:(bb % 4 + 1) * T],
                                 g2[0:T, bb * E3:(bb + 1) * E3], ident[0:T, 0:T])
            m.then_inc(sem("experts_by_pe"), 1)
            pe.wait_ge(sem("experts_by_act"), STEP["expert_weights_turned"])
            for bb in range(B):
                m = mm(bank(2 + bb // 4, T, BANK)[:, (bb % 4) * D:(bb % 4 + 1) * D],
                       big2[0:E3, bb * T:(bb + 1) * T],
                       W["f3b2"][:, :])
            m.then_inc(sem("experts_by_pe"), 1)
            pe.wait_ge(sem("experts_by_dve"), STEP["expert_biases_taken"])
            for e in range(E3):
                if e > 0:
                    expert_hidden(e)
                pe.wait_ge(sem("f3_gelu"), 8 * e + 8)
                if e >= 2:
                    pe.wait_ge(sem("f3_accumulated"), 2 * (e - 1))
                for bb in range(B):
                    o = bank(2 * (e % 2) + bb // 4, T, BANK)[:, (bb % 4) * D:(bb % 4 + 1) * D]
                    for f in range(4):
                        m = mm(o, hid[:, f, bb * T:(bb + 1) * T], w3b[:, e, f, :], start=f == 0, stop=f == 3)
                m.then_inc(sem("f3_out"), 1)

        @block.scalar
        def _(act):
            own = [0]

            def link(i):
                own[0] += 1
                i.then_inc(sem("act_step"), 1)
                act.wait_ge(sem("act_step"), own[0])

            rooted = [0]

            def take_roots(dst, src):
                rooted[0] += 1
                act.wait_ge(sem("variances_ready"), rooted[0])
                act.activation(dst, src, ACT.Sqrt).then_inc(sem("deviations_ready"), 1)

            def root_of_rows():
                take_roots(stat[0:T, 4, 0:8], stat[0:T, 3, 0:8])

            def turned(n):
                root_of_rows()
                n = n if n < 4 else n - 1
                for half in range(2):
                    act.wait_ge(sem("xnT_in_psum"), 2 * n + half + 1)
                    act.copy(xnT[:, half * HALF:(half + 1) * HALF], bank(half, D, HALF)
                             ).then_inc(sem("xnT_ready"), 1)

            act.wait_ge(sem("first_loaded"), FIRST_LOADS)
            act.activation(gates[:, :], gates[:, :], ACT.Tanh).then_inc(sem("stages_by_act"), 1)

            def attention(layer):
                ring = rings[layer]
                p = f"a{layer}_"
                bk = W["bk0"] if layer == 0 else W["bka1"]

                def copy_keys(half, s, last):
                    k0, k1 = half * 2 * KQ, (half + 1) * 2 * KQ
                    act.activation(kf[:, k0:k1].rearrange("p (a k) -> p a k", a=2), slot(s, D, KQ), ACT.Identity,
                                   bias=bk[:, 0:1])
                    return act.activation(kparts[:, 0, k0:k1].rearrange("p (a k) -> p a k", a=2), slot(s, D, KQ),
                                          ACT.Identity, bias=bk[:, 0:1])

                def second_part(count):
                    act.wait_ge(sem(p + "keys_rest"), count)
                    act.copy(kparts[:, 1, :], kr).then_inc(sem(p + "key_parts_2"), 1)

                act.wait_ge(sem(p + "first_keys"), 1)
                act.wait_ge(sem(p + "query_parts_ready"), 1)
                copy_keys(0, 0, False)
                copy_keys(1, 1, True).then_inc(sem(p + "key_parts_1"), 1)
                second_part(1)
                if layer == 0:
                    act.wait_ge(sem("later_loaded"), LATER_LOADS)
                    act.activation(small[:, 24:25], W["g1"][:, :], ACT.Exp, scale=-1.0)
                    act.activation(head_gates[:, 0, :], W["g1heads"][:, :], ACT.Exp, scale=-1.0
                                   ).then_inc(sem("stages_by_act"), 1)
                act.sem_inc(ring.emptied["act"], ring.per["act"])
                act.sem_inc(sem(p + "probs_used"), 3)
                per = 2 * NCH + 2 * layer
                with act.Fori(0, B) as b:
                    act.wait_ge(sem(p + "queries_stacked"), 16 * 12 * (b + 1))
                    for dst in (q2, own_q2)[0:layer + 1]:
                        i = act.copy(dst[0:SHIFT, :, :], q1[0:SHIFT, :, :])
                    i.then_inc(sem(p + "queries_copied"), 1)
                    act.wait_ge(sem(p + "probs_used"), b * per + 3)
                    act.wait_ge(sem(p + "values_turned"), b + 1)
                    act.copy(Vo[:, :, :, 0:8], Vn.rearrange("p c (h d) -> p c h d", h=H)
                             ).then_inc(sem(p + "values_placed"), 1)
                    done = 0
                    for n, (kind, g, u, _) in enumerate(ORDER[layer]):
                        if kind == "keys":
                            act.wait_ge(ring.full, ring.full_count(b, n))
                            copy_keys(u, n % 3, u == 1).then_inc(ring.emptied["act"], 1)
                        if kind == "exp":
                            r = ROWS[u // 2] if g == 0 else T
                            act.wait_ge(ring.full, ring.full_count(b, n))
                            if done >= 3:
                                act.wait_ge(sem(p + "probs_used"), b * per + done + 1)
                            act.activation(P3[0:r, done % 3, :].rearrange("p (a k) -> p a k", a=2),
                                           slot(n % 3, r, GROUP), ACT.Exp).then_inc(ring.emptied["act"], 1)
                            done += 1
                            if g == 0 and u == 5:
                                second_part(b + 2)

            turned(0)
            attention(0)
            turned(1)
            act.wait_ge(sem("router_columns"), 1)
            act.activation(small[0:T, 0:8], stat[0:T, 0, 0:8], ACT.Exp, scale=-1.0).then_inc(sem("stages_by_act"), 1)
            for k in range(8):
                f, half = k // 2, k % 2
                act.wait_ge(sem("ffn0_hidden_psum"), k + 1)
                act.activation(hid[:, f, half * HALF:(half + 1) * HALF], bank(4 + k % 4, 128, HALF),
                               ACT.Gelu_apprx_tanh, bias=W["f0b1"][:, f:f + 1]).then_inc(sem("ffn0_hidden"), 1)
            turned(2)
            act.wait_ge(sem("k1_projected"), 1)
            act.wait_ge(sem("stages_by_dve"), STEP["q1_split"])
            act.activation(qf.rearrange("p (a k) -> p a k", a=2), slot(2, D, HALF), ACT.Identity,
                           bias=W["bk1"][:, 0:1]).then_inc(sem("stages_by_act"), 1)
            attention(1)
            def square_context(b):
                act.wait_ge(sem("a2_stage_centred"), b + 2)
                act.activation(scratch, stage[:, 0:NCH, :], ACT.Square).then_inc(sem("a2_stage_squared"), 1)

            def root_variances(b):
                act.wait_ge(sem("a2_variances"), b + 2)
                act.activation(stat[:, 6, 0:NCH], stat[:, 6, 0:NCH], ACT.Sqrt).then_inc(sem("a2_deviations"), 1)

            turned(3)
            act.wait_ge(sem("slots_by_dve"), STEP["slot_bias"])
            act.wait_ge(sem("slots_by_pe"), STEP["f1_hidden_psum"])
            for half in range(2):
                act.activation(hid[0:NSLOT, 0, half * HALF:(half + 1) * HALF], bank(4 + half, NSLOT, HALF),
                               ACT.Gelu, bias=small[0:NSLOT, 10:11]).then_inc(sem("f1_hidden"), 1)
            act.wait_ge(sem("slots_by_dve"), STEP["logits_shifted"])
            act.activation(big2[0:T, 0:512], big2[0:T, 0:512], ACT.Exp).then_inc(sem("slots_by_act"), 1)
            square_context(-1)
            act.wait_ge(sem("slots_by_pe"), STEP["alpha_turned"])
            act.copy(hid[0:NSLOT, 1, :].rearrange("p (a k) -> p a k", a=2), slot(2, NSLOT, HALF)
                     ).then_inc(sem("slots_by_act"), 1)
            root_variances(-1)
            act.wait_ge(sem("slots_by_dve"), STEP["gate_r_sum"])
            act.activation(g0[:, :], g0[:, :], ACT.Exp, scale=-1.0).then_inc(sem("slots_by_act"), 1)
            act.wait_ge(sem("slots_by_dve"), STEP["gate_z_sum"])
            act.activation(big3[:, 0:512], big3[:, 0:512], ACT.Exp, scale=-1.0).then_inc(sem("slots_by_act"), 1)
            act.wait_ge(sem("slots_by_dve"), STEP["gate_n_sum"])
            act.activation(g3[:, :], g3[:, :], ACT.Tanh).then_inc(sem("slots_by_act"), 1)
            act.wait_ge(sem("slots_by_pe"), STEP["slot_values_psum"])
            act.activation(g3[:, :], bank(0, D, BANK), ACT.Identity, bias=W["f1bv"][:, 0:1]
                           ).then_inc(sem("slots_by_act"), 1)
            act.wait_ge(sem("slots_by_pe"), STEP["slot_outputs_psum"])
            act.copy(big2[0:NSLOT, :].rearrange("p (a k) -> p a k", a=2), slot(1, NSLOT, BANK)
                     ).then_inc(sem("slots_by_act"), 1)
            ring = rings[2]
            root_of_rows()
            root_of_rows()
            act.wait_ge(sem("stages_by_dve"), STEP["latents_ready"])
            act.sem_inc(ring.emptied["act"], ring.head["act"])
            act.sem_inc(sem("a2_contexts_copied_by_act"), 1)
            pair = "p (a k) -> p a k"

            def event(b, c):
                return 14 * b + c + 2

            def take_norms(b, r, c, at):
                act.wait_ge(sem("a2_squares_summed"), event(b, c))
                act.activation(n2[0:r, at, :], n2[0:r, at, :], ACT.Sqrt).then_inc(sem("a2_norms"), 1)

            def copy_context(b):
                act.wait_ge(ring.full, ring.full_count(b, "context", 0))
                act.copy(xkT[:, 0:8 * CK].rearrange(pair, a=2), slot(ring.slot_of("context", 0), D, 4 * CK)
                         ).then_inc(ring.emptied["act"], 1)
                act.wait_ge(ring.full, ring.full_count(b, "context", 1))
                s = ring.slot_of("context", 1)
                act.copy(xkT[:, S2:S2 + T], bank(2 * s + 1, D, T))
                act.copy(xkT[:, 8 * CK:S2], bank(2 * s, D, S2 - 8 * CK)).then_inc(ring.emptied["act"], 1)

            def square_queries(b):
                act.wait_ge(ring.full, ring.full_count(b, "query", 0))
                act.activation(values2.rearrange(pair, a=2), slot(ring.slot_of("query", 0), T, BANK), ACT.Square
                               ).then_inc(sem("a2_query_squares"), 1)

            def carry(b):
                take_norms(b, T, 13, 0)
                act.wait_ge(ring.full, ring.full_count(b, "turned", 0))
                act.activation(xnT[:, :].rearrange(pair, a=2), slot(ring.slot_of("turned", 0), D, HALF), ACT.Copy,
                               scale=small[:, 30:31]).then_inc(ring.emptied["act"], 1)
                for half in range(2):
                    act.wait_ge(ring.full, ring.full_count(b, "carried", half))
                    act.copy(qeff[:, 8 * half:8 * half + 8, :].rearrange("p (t a) q -> p a t q", a=2),
                             slot(ring.slot_of("carried", half), D, GROUP).rearrange("p a (t q) -> p a t q", t=4)
                             ).then_inc(ring.emptied["act"], 1)

            def place_context():
                act.copy(ctxk[:, :, :], stage).then_inc(sem("a2_stage_copied"), 1)

            def copy_values(b):
                act.wait_ge(sem("a2_heads_by_pe"), 3 * b + 2)
                act.copy(xnT[:, :].rearrange(pair, a=2), slot(3, D, HALF)).then_inc(sem("a2_heads_by_act"), 1)

            copy_context(-1)
            square_queries(-1)
            carry(-1)
            place_context()
            with act.Fori(0, B) as b:
                rows = ROWS + [T]

                def square_keys(c):
                    act.wait_ge(ring.full, ring.full_count(b, "norm", c))
                    act.activation(sq[0:rows[c], :].rearrange(pair, a=2), slot(ring.slot_of("norm", c), rows[c], BANK),
                                   ACT.Square).then_inc(ring.emptied["act"], 1)

                square_keys(0)
                take_norms(b, rows[0], 0, 0)
                for c in range(13):
                    r = rows[c]
                    if c < NCH:
                        square_keys(c + 1)
                    act.wait_ge(sem("a2_norms_inverted"), event(b, c))
                    for half, heads_of in ((0, range(ACT_HEADS)), (1, range(8))):
                        act.wait_ge(ring.full, ring.full_count(b, "score", 2 * c + half))
                        s = ring.slot_of("score", 2 * c + half)
                        for k in heads_of:
                            h = 8 * half + k
                            i = act.activation(S_all[0:r, c, h * T:(h + 1) * T],
                                               bank(2 * s + k // 4, r, GROUP)[:, (k % 4) * T:(k % 4 + 1) * T],
                                               ACT.Copy, scale=rk[0:r, c % 2, h:h + 1])
                        i.then_inc(sem("a2_scaled_by_act") if half == 0 else ring.emptied["act"], 1)
                    if c < NCH:
                        take_norms(b, rows[c + 1], c + 1, (c + 1) % 2)
                    if c == VALUES_TURNED + 1:
                        copy_values(b)
                act.activation(warm[:, :], ones[0:1, 0:1], ACT.Exp)
                for half in range(2):
                    act.wait_ge(ring.full, ring.full_count(b, "shift", half))
                    act.copy(mB[:, 2 * half * GROUP:(2 * half + 2) * GROUP].rearrange(pair, a=2),
                             slot(ring.slot_of("shift", half), 128, GROUP)).then_inc(ring.emptied["act"], 1)
                for half in range(2):
                    act.wait_ge(sem("a2_scores_shifted"), b * 14 + half + 1)
                    cols = slice(2 * half * GROUP, 2 * (half + 1) * GROUP)
                    i = act.activation(S_all[0:rows[0], 0, cols], S_all[0:rows[0], 0, cols], ACT.Exp,
                                       bias=kbc[0:rows[0], 0:1])
                i.then_inc(sem("a2_probs_ready"), 1)
                for c in range(13):
                    if c > 0:
                        act.wait_ge(sem("a2_scores_shifted"), b * 14 + c + 2)
                        act.activation(S_all[0:rows[c], c, :], S_all[0:rows[c], c, :], ACT.Exp,
                                       bias=kbc[0:rows[c], c:c + 1]).then_inc(sem("a2_probs_ready"), 1)
                    if c == CENTRE + 1:
                        square_context(b)
                    if c == VARIANCE + 1:
                        root_variances(b)
                    if c == TURN + 1:
                        copy_context(b)
                    if c == QUERY + 1:
                        square_queries(b)
                carry(b)
                act.wait_ge(sem("a2_keys_used"), b + 1)
                act.copy(mB[:, 2 * GROUP:4 * GROUP].rearrange(pair, a=2), slot(3, D, GROUP)
                         ).then_inc(sem("a2_contexts_copied_by_act"), 1)
                place_context()
            copy_values(B)
            turned(5)
            for bb in range(B):
                act.wait_ge(sem("f2_hidden_psum"), bb + 1)
                act.activation(ternary_hidden(bb), bank(2 + bb % 2, T, BANK), ACT.Gelu).then_inc(sem("f2_gelu"), 1)
            root_of_rows()
            for bb in range(B):
                act.wait_ge(sem("f2_turned_psum"), bb + 1)
                act.copy(big2[:, (bb % 2) * 400:(bb % 2) * 400 + 400], bank(4 + bb % 2, 128, 4 * T)
                         ).then_inc(sem("f2_turned"), 1)
            turned(6)
            act.wait_ge(sem("q3T_psum"), 1)
            act.activation(q3T[:, :].rearrange("p (a k) -> p a k", a=2), slot(1, D, HALF), ACT.Identity,
                           bias=W["bq3"][:, 0:1]).then_inc(sem("stages_by_act"), 1)
            act.wait_ge(sem("qe3_psum"), 1)
            act.copy(qe3[:, 0:BT].rearrange("p (a k) -> p a k", a=2), slot(0, D, HALF)).then_inc(sem("stages_by_act"), 1)
            with act.Fori(0, B) as b:
                act.wait_ge(sem("a3_shift_ready"), b + 1)
                act.activation(st3[:, 36:37], st3[:, 35:36], ACT.Exp)
                for half in range(2):
                    i = act.activation(P1[:, half * 2 * KQ:(half + 1) * 2 * KQ].rearrange("p (a k) -> p a k", a=2),
                                       slot(half, T, KQ), ACT.Exp, bias=st3[:, 34:35],
                                       accum_out=st3[:, 37 + half:38 + half])
                i.then_inc(sem("a3_exp"), 1)
                act.wait_ge(sem("a3_ctx_used"), b + 1)
                act.copy(AT3[:, :], bank(7, D, T)).then_inc(sem("a3_context_copied"), 1)
            turned(7)
            act.wait_ge(sem("experts_by_dve"), STEP["squares_ready"])
            act.activation(stat[0:T, 5, 0:8], stat[0:T, 5, 0:8], ACT.Sqrt).then_inc(sem("norms_ready"), 1)
            act.activation(small[0:E3, 40:41], small[0:E3, 40:41], ACT.Sqrt).then_inc(sem("norms_ready"), 1)

            def expert_hidden(e):
                for k in range(8):
                    f, half = k // 2, k % 2
                    q = 8 * e + k
                    act.wait_ge(sem("f3_hidden_psum"), q + 1)
                    if e >= 1 and k == 0:
                        act.wait_ge(sem("f3_out"), e)
                    act.activation(hid[:, f, half * HALF:(half + 1) * HALF], bank(4 + q % 4, 128, HALF),
                                   ACT.Gelu, bias=W["f3b1"][:, e, f:f + 1]).then_inc(sem("f3_gelu"), 1)

            expert_hidden(0)
            act.wait_ge(sem("experts_by_dve"), STEP["expert_shifted"])
            act.activation(g3[0:T, 0:64], g3[0:T, 0:64], ACT.Exp).then_inc(sem("experts_by_act"), 1)
            act.wait_ge(sem("experts_by_pe"), STEP["expert_weights_psum"])
            act.copy(big2[0:E3, 0:BT].rearrange("p (a k) -> p a k", a=2), slot(0, E3, HALF)
                     ).then_inc(sem("experts_by_act"), 1)
            for e in range(1, E3):
                expert_hidden(e)

        @block.gpsimd
        def _(pool):
            def split_keys(layer, copied, count):
                p = f"a{layer}_"
                pool.wait_ge(*copied)
                pool.tensor_tensor(kr, kf, kparts[:, 0, :], ALU.subtract).then_inc(sem(p + "keys_rest"), 1)
                pool.wait_ge(sem(p + "key_parts_2"), count)
                pool.tensor_tensor(kparts[:, 2, :], kr, kparts[:, 1, :], ALU.subtract
                                   ).then_inc(sem(p + "keys_split"), 1)

            for layer in (0, 1):
                ring = rings[layer]
                split_keys(layer, (sem(f"a{layer}_key_parts_1"), 1), 1)
                with pool.Fori(0, B) as b:
                    split_keys(layer, (ring.emptied["act"], ring.emptied_count(b, position(layer, "keys", 0, 1))),
                               b + 2)

            def gain_and_bias(b):
                pool.wait_ge(sem("a2_stage_scaled"), b + 2)
                kk, ks = stage[:, 0:NCH, :], [128, NCH, D]
                pool.tensor_tensor(kk, kk, bc(W["lnxg"][:, :], ks, 1), ALU.mult).then_inc(sem("a2_gained"), 1)
                pool.wait_ge(sem("a2_gained"), b + 2)
                pool.tensor_tensor(kk, kk, bc(W["lnxb"][:, :], ks, 1), ALU.add).then_inc(sem("a2_keys_normalised"), 1)

            gain_and_bias(-1)
            with pool.Fori(0, B) as b:
                for k, c in enumerate(POOL_SUMS[1:]):
                    r = (ROWS + [T])[c]
                    pool.wait_ge(sem("a2_probs_ready"), b * 13 + c + 1)
                    if k > 0:
                        pool.wait_ge(sem("a2_pool_summed"), b * (len(POOL_SUMS) - 1) + k)
                    before_c = S_all[0:r, 0, :] if k == 0 else Psum[0:r, :]
                    pool.tensor_tensor(Psum[0:r, :], before_c, S_all[0:r, c, :], ALU.add
                                       ).then_inc(sem("a2_pool_summed"), 1)
                    if c == SCALE - 1:
                        gain_and_bias(b)

        @block.vector
        def _(dve):
            own = [0]

            def link(i):
                own[0] += 1
                i.then_inc(sem("dve_step"), 1)
                dve.wait_ge(sem("dve_step"), own[0])

            roots = [0]

            def invert_roots(at):
                dve.sem_inc(sem("variances_ready"), 1)
                roots[0] += 1
                dve.wait_ge(sem("deviations_ready"), roots[0])
                link(dve.reciprocal(at, at))

            def norm_rows(dst, src, parts, n, width, scratch, st):
                shape = [parts, n, width]
                link(dve.tensor_reduce(st[:, 0, 0:n], src, AX.X, ALU.add))
                link(dve.tensor_scalar(st[:, 1, 0:n], st[:, 0, 0:n], 1.0 / width, None, ALU.mult))
                link(dve.tensor_tensor(dst, src, bc(st[:, 1, 0:n], shape, 2), ALU.subtract))
                link(dve.tensor_tensor(scratch, dst, dst, ALU.mult))
                link(dve.tensor_reduce(st[:, 2, 0:n], scratch, AX.X, ALU.add))
                link(dve.tensor_scalar(st[:, 3, 0:n], st[:, 2, 0:n], 1.0 / width, LN_EPS, ALU.mult, ALU.add))
                invert_roots(st[:, 4, 0:n])
                return dve.tensor_tensor(dst, dst, bc(st[:, 4, 0:n], shape, 2), ALU.mult)

            def norm_x():
                i = norm_rows(xn[:, :, :], x[:, :, :], T, B, D, wideA[:, :, :], stat[0:T])
                link(i)
                dve.sem_inc(sem("xn_ready"), 1)

            def add_residual(psum_pair, gate):
                link(dve.scalar_tensor_tensor(
                    out=x[:, :, :].rearrange("p (a b) d -> p a (b d)", a=2), in0=psum_pair,
                    scalar=gates[0:T, gate:gate + 1],
                    in1=x[:, :, :].rearrange("p (a b) d -> p a (b d)", a=2), op0=ALU.mult, op1=ALU.add))

            dve.memset(kmask[:, :, :].rearrange("p a b -> p (a b)"), 0).then_inc(sem("stages_by_dve"), 1)
            link(dve.memset(ones[:, :], 1.0))
            link(dve.memset(Vo_w, 1.0))
            link(dve.memset(own_Vo_w, 1.0))
            link(dve.memset(Vn, 0.0))
            link(dve.memset(qparts_w, 0.0))
            link(dve.memset(own_kparts_w, 0.0))
            for tile in (q1_w, q2_w, own_q2_w):
                link(dve.memset(tile, 0.0))
            link(dve.memset(kst_w, PAIR_OF_ONES))
            link(dve.memset(own_kst_w, PAIR_OF_ONES))
            dve.sem_inc(sem("a0_ones_set"), 1)
            dve.wait_ge(sem("first_loaded"), FIRST_LOADS)
            norm_x()
            link(dve.memset(maskb, 0.0))
            mi = maski.bitcast(I32).rearrange("p (c q) -> p c q", c=NCH)
            link(dve.tensor_scalar(maskb[0:CK, 0:NCH - 1, :], mi[0:CK, 0:NCH - 1, :], 0, OFF, ALU.is_equal, ALU.mult))
            link(dve.tensor_scalar(maskb[0:LAST, NCH - 1, :], mi[0:LAST, NCH - 1, :], 0, OFF, ALU.is_equal, ALU.mult))

            def split(parts, src, rest):
                link(dve.tensor_copy(parts[:, 0, :], src))
                link(dve.tensor_tensor(rest, src, parts[:, 0, :], ALU.subtract))
                link(dve.tensor_copy(parts[:, 1, :], rest))
                link(dve.tensor_tensor(parts[:, 2, :], rest, parts[:, 1, :], ALU.subtract))

            def prepare_later_layers():
                dve.wait_ge(sem("later_loaded"), LATER_LOADS)
                link(dve.tensor_copy(wr_bc[:, :], W["f0wr"][:, 0:1].broadcast_to([D, T])))
                dve.wait_ge(sem("stages_by_act"), STEP["head_gate_exp"])
                link(dve.tensor_scalar(head_gates[:, 0, :], head_gates[:, 0, :], 1.0, None, ALU.add))
                link(dve.reciprocal(head_gates[:, 0, :], head_gates[:, 0, :]))
                link(dve.tensor_scalar(head_gates[:, 1, :], head_gates[:, 0, :], -1.0, 1.0, ALU.mult, ALU.add))
                link(dve.tensor_scalar(small[:, 25:26], small[:, 24:25], 1.0, None, ALU.add))
                link(dve.reciprocal(small[:, 26:27], small[:, 25:26]))
                link(dve.tensor_tensor(small[:, 27:28], W["bva1"][:, :], W["bv1"][:, :], ALU.subtract))
                link(dve.scalar_tensor_tensor(out=bv1[:, :], in0=small[:, 27:28], scalar=small[:, 26:27],
                                              in1=W["bv1"][:, :], op0=ALU.mult, op1=ALU.add))
                link(dve.tensor_scalar(small[:, 30:31], W["gq2"][:, 0:1], W["gk2"][:, 0:1], DH ** -0.5, ALU.mult, ALU.mult))
                link(dve.tensor_scalar(kbias[:, :, :], kmask[:, :, :], 0, OFF, ALU.is_equal, ALU.mult))

            def attention(layer):
                ring = rings[layer]
                p = f"a{layer}_"
                own_sem = sem(p + "dve_step")
                used = 2 * NCH + 2 * layer
                G = layer + 1
                per = STEPS[layer]
                bv = W["bv0"] if layer == 0 else bv1
                nf = 3 + layer
                link(dve.memset(psum[:, 6:8, :], 1.0))
                link(dve.memset(summed[:, :], 1.0))
                link(dve.memset(own_summed[:, :], 1.0))
                dve.wait_ge(sem(p + "first_projected"), 1)
                link(dve.tensor_copy(Vn[0:CK, 0:8, :].rearrange("p (a c) d -> p a (c d)", a=2), psum[0:CK, 4:6, :]))
                link(dve.tensor_copy(Vn[0:CK, 8:11, :].rearrange("p c d -> p (c d)"), bank(0, CK, 3 * D)))
                link(dve.tensor_copy(Vn[0:LAST, 11, :], bank(0, LAST, BANK)[:, 3 * D:4 * D]))
                dve.sem_inc(sem(p + "values_turned"), 1)
                dve.sem_inc(ring.emptied["dve"], ring.per["dve"])
                dve.sem_inc(sem(p + "sums_copied"), 1)
                dve.sem_inc(sem(p + "heads_by_dve"), 1)
                if layer == 0:
                    prepare_later_layers()

                def finish(b, k, step):
                    dve.wait_ge(sem(p + "heads_by_pe"), b * nf + k + 1)
                    if k < G:
                        turned = bank(7, T, BANK).rearrange("p (h d) -> p h d", h=H)
                        dst = (heads, own_heads)[k]
                        step(dve.reciprocal(shares[:, k, :], turned[:, :, 8]))
                        if layer == 1:
                            step(dve.tensor_tensor(shares[:, k, :], shares[:, k, :], head_gates[0:T, k, :], ALU.mult))
                        i = dve.tensor_tensor(dst.rearrange("p (h d) -> p h d", h=H), turned[:, :, 0:8],
                                              bc(shares[:, k, :], [T, H, HD], 2), ALU.mult)
                        if k == 1:
                            step(i)
                            i = dve.tensor_tensor(heads[:, :], heads[:, :], own_heads[:, :], ALU.add)
                    elif k == G:
                        i = dve.tensor_scalar(headsT[:, :], bank(7, D, T), bv[:, 0:1], None, ALU.add)
                    else:
                        i = dve.tensor_copy(attended[:, bass.ds(b * D, D)], bank(7, T, D))
                    i.then_inc(sem(p + "heads_by_dve"), 1)

                with dve.Fori(0, B) as b:
                    k = [0]

                    def step(i):
                        k[0] += 1
                        i.then_inc(own_sem, 1)
                        dve.wait_ge(own_sem, b * per + k[0])

                    if layer == 1:
                        step(dve.tensor_copy(own_Vo[0:T, :, 0:8],
                                             vs.rearrange("p b (h d) -> p (b h) d", h=H)[:, bass.ds(b * H, H), :]))
                    for n, (kind, g, u, _) in enumerate(ORDER[layer]):
                        s = n % 3
                        if kind in ("exp", "keys"):
                            continue
                        dve.wait_ge(ring.full, ring.full_count(b, n))
                        if kind == "max":
                            r = ROWS[u // 2] if g == 0 else T
                            dst = (M if g == 0 else own_M)[0:r, 800 * (u % 2):800 * (u % 2) + 800].rearrange(
                                "p (a k) -> p a k", a=2)
                            if u < 2:
                                i = dve.tensor_copy(dst, slot(s, r, GROUP))
                            else:
                                dve.wait_ge(ring.emptied["dve"], ring.emptied_count(b, position(layer, "max", g, u - 2)))
                                i = dve.tensor_tensor(dst, slot(s, r, GROUP), dst, ALU.max)
                            i.then_inc(ring.emptied["dve"], 1)
                            if g == 0 and u in FINISH[layer]:
                                finish(b, FINISH[layer].index(u), step)
                            if layer == 1 and g == 0 and u == OWN_TAKEN:
                                dve.wait_ge(sem(p + "probs_used"), b * used + 2 + 3)
                                dve.tensor_copy(own_summed[:, :], bank(7, 128, GROUP)).then_inc(sem(p + "sums_copied"), 1)
                        elif kind == "turn":
                            r = CK if g == 0 else T
                            places = mx[:, g, :].rearrange("p (a r h) -> p r h a", a=2, r=2)
                            for a in range(2):
                                src = bank(2 * s + a, T, 4 * CK).rearrange("p (h a k) -> p h a k", h=2, a=2)[:, :, :, 0:r]
                                i = dve.tensor_reduce(places[:, 0, 4 * u + 2 * a:4 * u + 2 * a + 2, :], src, AX.X,
                                                      ALU.max, negate=True)
                            step(i)
                            dve.tensor_copy(places[:, 1, 4 * u:4 * u + 4, :], places[:, 0, 4 * u:4 * u + 4, :]
                                            ).then_inc(ring.emptied["dve"], 1)
                            if u == 1:
                                dve.wait_ge(ring.emptied["dve"], ring.emptied_count(b, n))
                                if layer == 0:
                                    step(dve.tensor_scalar(flag[:, :], mx[:, 0, :], 1e29, 3e38, ALU.is_gt, ALU.mult))
                                    step(dve.tensor_tensor(mx[:, 0, :], mx[:, 0, :], flag[:, :], ALU.add))
                                dve.sem_inc(sem(p + f"max_ready_{g}"), 1)
                        elif kind == "row":
                            step(dve.tensor_copy(high[:, :], bank(2 * s, 32, T)))
                            step(dve.scalar_tensor_tensor(out=hl[:, g, :], in0=high[:, :], scalar=low_rows[:, 0:1],
                                                          in1=bank(2 * s, 32, T), op0=ALU.mult, op1=ALU.add))
                            dve.sem_inc(ring.emptied["dve"], 1)
                            dve.sem_inc(sem(p + f"shift_ready_{g}"), 1)
                        elif kind == "values":
                            if u == 0:
                                dve.wait_ge(sem(p + "values_placed"), b + 1)
                                dve.tensor_copy(Vn[0:CK, 0:8, :].rearrange("p (a c) d -> p a (c d)", a=2),
                                                slot(s, CK, BANK)).then_inc(ring.emptied["dve"], 1)
                            else:
                                step(dve.tensor_copy(Vn[0:CK, 8:11, :].rearrange("p c d -> p (c d)"),
                                                     bank(2 * s, CK, 3 * D)))
                                step(dve.tensor_copy(Vn[0:LAST, 11, :], bank(2 * s, LAST, BANK)[:, 3 * D:4 * D]))
                                dve.sem_inc(ring.emptied["dve"], 1)
                                dve.sem_inc(sem(p + "values_turned"), 1)
                    dve.wait_ge(sem(p + "probs_used"), (b + 1) * used + 3)
                    dve.tensor_copy(summed[:, :], bank(6, 128, GROUP)).then_inc(sem(p + "sums_copied"), 1)
                    assert k[0] == per, k[0]
                for k in range(nf):
                    finish(B, k, link)
                dve.wait_ge(sem(p + "heads_by_dve"), (B + 1) * nf + 1)
                link(dve.scalar_tensor_tensor(out=x[:, :, :], in0=attended[:, D:].rearrange("p (b d) -> p b d", b=B),
                                              scalar=gates[0:T, layer:layer + 1], in1=x[:, :, :],
                                              op0=ALU.mult, op1=ALU.add))
                dve.wait_ge(ring.emptied["dve"], (B + 1) * ring.per["dve"])
                dve.wait_ge(sem(p + "keys_split"), B + 1)

            dve.wait_ge(sem("stages_by_act"), STEP["gates_ready"])
            dve.wait_ge(sem("q0_projected"), 1)
            link(dve.tensor_scalar(qf.rearrange("p (a k) -> p a k", a=2), slot(1, D, HALF), W["bq0"][:, 0:1],
                                   HD ** -0.5, ALU.add, ALU.mult))
            split(qparts[:, :, 0:BT], qf, qr)
            dve.sem_inc(sem("stages_by_dve"), 1)
            dve.sem_inc(sem("a0_query_parts_ready"), 1)
            attention(0)

            norm_x()
            dve.wait_ge(sem("router_scores"), 1)
            flat = wideA[:, :, :].rearrange("p b d -> p (b d)")
            sr = flat[:, 0:BT].rearrange("p (b t) -> p b t", b=B)
            tmp = wideB[:, :, :].rearrange("p b d -> p (b d)")[:, 0:BT].rearrange("p (b t) -> p b t", b=B)
            sh = [T, B, T]
            link(dve.tensor_copy(flat[:, 0:BT].rearrange("p (a k) -> p a k", a=2), slot(1, T, HALF)))
            link(dve.tensor_tensor(tmp, sr, bc(ident[0:T, 0:T], sh, 1), ALU.mult))
            dve.tensor_reduce(stat[0:T, 0, 0:8], tmp, AX.X, ALU.add).then_inc(sem("router_columns"), 1)
            dve.wait_ge(sem("router_columns"), 1)
            link(dve.tensor_tensor(tmp, sr, bc(stat[0:T, 0, 0:8], sh, 2), ALU.is_gt))
            link(dve.tensor_reduce(stat[0:T, 1, 0:8], tmp, AX.X, ALU.add))
            link(dve.tensor_tensor(tmp, sr, bc(stat[0:T, 0, 0:8], sh, 2), ALU.is_equal))
            link(dve.tensor_tensor(tmp, tmp, bc(before[:, :], sh, 1), ALU.mult))
            link(dve.tensor_reduce(stat[0:T, 2, 0:8], tmp, AX.X, ALU.add))
            link(dve.tensor_tensor(stat[0:T, 3, 0:8], stat[0:T, 1, 0:8], stat[0:T, 2, 0:8], ALU.add))
            link(dve.tensor_scalar(stat[0:T, 4, 0:8], stat[0:T, 3, 0:8], T // 2 - 0.5, gates[0:T, 4:5],
                                   ALU.is_lt, ALU.mult))
            dve.wait_ge(sem("stages_by_act"), STEP["router_exp"])
            link(dve.tensor_scalar(stat[0:T, 5, 0:8], small[0:T, 0:8], 1.0, None, ALU.add))
            link(dve.reciprocal(stat[0:T, 6, 0:8], stat[0:T, 5, 0:8]))
            link(dve.tensor_tensor(stat[0:T, 7, 0:8], stat[0:T, 6, 0:8], stat[0:T, 4, 0:8], ALU.mult))
            link(dve.scalar_tensor_tensor(out=x[:, :, :], in0=xn[:, :, :], scalar=gates[0:T, 4:5], in1=x[:, :, :],
                                          op0=ALU.mult, op1=ALU.add))
            dve.wait_ge(sem("ffn0_out"), 1)
            link(dve.tensor_tensor(wideA[:, :, :].rearrange("p (a b) d -> p a b d", a=2),
                                   slot(0, T, BANK).rearrange("p a (b d) -> p a b d", b=4),
                                   stat[0:T, 7, 0:8].rearrange("p (a b) -> p a b", a=2).unsqueeze(3)
                                   .broadcast_to([T, 2, 4, D]), ALU.mult))
            link(dve.tensor_tensor(x[:, :, :], x[:, :, :], wideA[:, :, :], ALU.add))

            norm_x()
            link(dve.memset(kst_w[:, 0:4 * BT], PAIR_OF_ONES))
            dve.sem_inc(sem("a1_ones_set"), 1)
            dve.wait_ge(sem("q1_projected"), 1)
            link(dve.tensor_scalar(qf.rearrange("p (a k) -> p a k", a=2), slot(1, D, HALF), W["bq1"][:, 0:1],
                                   HD ** -0.5, ALU.add, ALU.mult))
            split(qparts[:, :, 0:BT], qf, qr)
            dve.sem_inc(sem("stages_by_dve"), 1)
            dve.wait_ge(sem("stages_by_act"), STEP["k1_ready"])
            split(own_kparts[:, :, 0:BT], qf, qr)
            dve.wait_ge(sem("v1_projected"), 1)
            link(dve.tensor_copy(vs.rearrange("p (a b) d -> p a (b d)", a=2), slot(3, T, BANK)))
            dve.sem_inc(sem("stages_by_dve"), 1)
            dve.sem_inc(sem("a1_query_parts_ready"), 1)
            attention(1)

            kk, ks = stage[:, 0:NCH, :], [128, NCH, D]
            s1, s2 = stat[:, 5, 0:NCH], stat[:, 6, 0:NCH]

            def place_latents(b):
                return dve.tensor_copy(stage[0:T, NCH, :],
                                       lat[:, :, :].rearrange("p b d -> p (b d)")[:, bass.ds((b + 1) * D, D)])

            def centre(b, step):
                dve.wait_ge(sem("ctx_keys_loaded"), 32 * b + 64)
                step(dve.tensor_reduce(s1, kk, AX.X, ALU.add))
                step(dve.tensor_scalar(s1, s1, 1.0 / D, None, ALU.mult))
                step(dve.tensor_tensor(kk, kk, bc(s1, ks, 2), ALU.subtract))
                dve.sem_inc(sem("a2_stage_centred"), 1)

            def variance(b, step):
                dve.wait_ge(sem("a2_stage_squared"), b + 2)
                step(dve.tensor_reduce(s2, scratch, AX.X, ALU.add))
                step(dve.tensor_scalar(s2, s2, 1.0 / D, LN_EPS, ALU.mult, ALU.add))
                dve.sem_inc(sem("a2_variances"), 1)

            def scale(b, step):
                dve.wait_ge(sem("a2_deviations"), b + 2)
                step(dve.reciprocal(s2, s2))
                step(dve.tensor_tensor(kk, kk, bc(s2, ks, 2), ALU.mult))
                dve.sem_inc(sem("a2_stage_scaled"), 1)

            norm_x()
            link(dve.tensor_scalar(g0[0:NSLOT, 0:D], W["slots"][:, :], W["slot_scale"][:, 0:1], None, ALU.mult))
            dve.sem_inc(sem("slots_by_dve"), 1)
            dve.wait_ge(sem("slots_by_pe"), STEP["slots_turned"])
            link(dve.tensor_scalar(small[:, 8:9], bank(2, D, 1), 1.0 / NSLOT, None, ALU.mult))
            link(dve.tensor_copy(g1[:, 0:NSLOT], bank(3, D, NSLOT)))
            dve.sem_inc(sem("slots_by_dve"), 1)
            dve.sem_inc(sem("slots_by_dve"), 1)
            dve.wait_ge(sem("slots_by_pe"), STEP["slot_bias_psum"])
            link(dve.tensor_tensor(small[0:NSLOT, 10:11], bank(2, NSLOT, 1), W["f1b1"][:, 0:1], ALU.add))
            dve.sem_inc(sem("slots_by_dve"), 1)
            link(dve.scalar_tensor_tensor(out=small[0:T, 11:12], in0=W["tau"][0:T, 0:1], scalar=-1.0,
                                          in1=W["tau"][0:T, 0:1], op0=ALU.mult, op1=ALU.max))
            link(dve.tensor_scalar(small[0:T, 11:12], small[0:T, 11:12], 0.1, None, ALU.add))
            link(dve.reciprocal(small[0:T, 12:13], small[0:T, 11:12]))
            link(dve.memset(ctxT[:, :], 0.0))
            dve.sem_inc(sem("stages_by_dve"), 1)
            link(dve.memset(lat[:, B, :], 0.0))
            link(dve.memset(kbc[:, :], 0.0))
            link(dve.memset(mB[:, :], 1.0))
            link(dve.memset(shares2[:, :], 1.0))
            dve.wait_ge(sem("slots_by_pe"), STEP["route_logits"])
            lg = big3[0:T, 0:512].rearrange("p (b s) -> p b s", b=B)
            rest = big2[0:T, 0:512].rearrange("p (b s) -> p b s", b=B)
            chosen = big1[0:T, 0:512].rearrange("p (b s) -> p b s", b=B)
            ls = [T, B, NSLOT]
            link(dve.tensor_tensor(lg, bank(6, T, BANK).rearrange("p (b s) -> p b s", b=B),
                                   bc(W["f1b2"][0:T, :], ls, 1), ALU.add))
            link(dve.tensor_scalar(lg, lg, small[0:T, 12:13], None, ALU.mult))
            top = stat[0:T, 0:2, :].rearrange("p a b -> p (a b)").rearrange("p (b k) -> p b k", b=B)
            for bb in range(B):
                i = dve.max(top[:, bb, :], lg[:, bb, :])
            link(i)
            for bb in range(B):
                i = dve.match_replace(rest[:, bb, :], top[:, bb, :], lg[:, bb, :], -3e38)
            link(i)
            link(dve.tensor_tensor(chosen, rest, lg, ALU.not_equal))
            link(dve.tensor_tensor(rest, lg, top[:, :, 0:1].broadcast_to(ls), ALU.subtract))
            dve.sem_inc(sem("slots_by_dve"), 1)
            dve.wait_ge(sem("slots_by_act"), STEP["logits_exp"])
            link(dve.tensor_tensor(chosen, chosen, rest, ALU.mult))
            link(dve.tensor_reduce(stat[0:T, 3, 0:8], chosen, AX.X, ALU.add))
            link(dve.reciprocal(stat[0:T, 4, 0:8], stat[0:T, 3, 0:8]))
            link(dve.tensor_tensor(chosen, chosen, bc(stat[0:T, 4, 0:8], ls, 2), ALU.mult))
            dve.sem_inc(sem("slots_by_dve"), 1)
            dve.wait_ge(sem("slots_by_pe"), STEP["gh_psum"])
            for g in range(3):
                i = dve.tensor_scalar(g1[:, 64 + g * 64:128 + g * 64], bank(7, D, 192)[:, g * 64:(g + 1) * 64],
                                      W["f1bhh"][:, g:g + 1], None, ALU.add)
            link(i)
            centre(-1, link)
            dve.wait_ge(sem("slots_by_pe"), STEP["slot_inputs"])
            link(dve.tensor_scalar(g2[:, :], bank(1, D, BANK), 1e-8, None, ALU.add))
            link(dve.reciprocal(g2[:, :], g2[:, :]))
            link(dve.tensor_tensor(g3[:, :], bank(0, D, BANK), g2[:, :], ALU.mult))
            dve.sem_inc(sem("slots_by_dve"), 1)
            variance(-1, link)
            dve.wait_ge(sem("slots_by_pe"), STEP["gx_psum"])
            gs = [D, B, NSLOT]

            def gate_sum(dst, bk, g):
                dve.wait_ge(sem("dve_step"), own[0])
                link(dve.scalar_tensor_tensor(
                    out=dst.rearrange("p (b s) -> p b s", b=B), in0=bank(bk, D, BANK).rearrange("p (b s) -> p b s", b=B),
                    scalar=W["f1bih"][:, g:g + 1], in1=bc(g1[:, 64 + g * 64:128 + g * 64], gs, 1),
                    op0=ALU.add, op1=ALU.add))

            gate_sum(g0[:, :], 2, 0)
            dve.sem_inc(sem("slots_by_dve"), 1)
            gate_sum(big3[:, 0:512], 3, 1)
            dve.sem_inc(sem("slots_by_dve"), 1)
            dve.wait_ge(sem("slots_by_act"), STEP["gate_r_exp"])
            link(dve.tensor_scalar(g0[:, :], g0[:, :], 1.0, None, ALU.add))
            link(dve.reciprocal(g0[:, :], g0[:, :]))
            link(dve.tensor_tensor(g2[:, :].rearrange("p (b s) -> p b s", b=B),
                                   g0[:, :].rearrange("p (b s) -> p b s", b=B), bc(g1[:, 192:256], gs, 1), ALU.mult))
            link(dve.scalar_tensor_tensor(out=g3[:, :], in0=bank(6, D, BANK), scalar=W["f1bih"][:, 2:3], in1=g2[:, :],
                                          op0=ALU.add, op1=ALU.add))
            dve.sem_inc(sem("slots_by_dve"), 1)
            dve.wait_ge(sem("slots_by_act"), STEP["gate_z_exp"])
            link(dve.tensor_scalar(big3[:, 0:512], big3[:, 0:512], 1.0, None, ALU.add))
            link(dve.reciprocal(big3[:, 0:512], big3[:, 0:512]))
            dve.wait_ge(sem("slots_by_act"), STEP["gate_n_tanh"])
            link(dve.tensor_tensor(g2[:, :].rearrange("p (b s) -> p b s", b=B), bc(g1[:, 0:64], gs, 1),
                                   g3[:, :].rearrange("p (b s) -> p b s", b=B), ALU.subtract))
            link(dve.tensor_tensor(g2[:, :], g2[:, :], big3[:, 0:512], ALU.mult))
            link(dve.tensor_tensor(g2[:, :], g2[:, :], g3[:, :], ALU.add))
            dve.sem_inc(sem("slots_by_dve"), 1)
            scale(-1, link)
            dve.wait_ge(sem("ffn1_out"), 1)
            add_residual(slot(3, T, BANK), 5)

            norm_x()
            lf = lat[:, 0:B, :]
            link(norm_rows(lf, xn[:, :, :], T, B, D, wideA[:, :, :], stat[0:T]))
            link(dve.tensor_tensor(lf, lf, bc(W["lnlg"][0:T, :], [T, B, D], 1), ALU.mult))
            link(dve.tensor_tensor(lf, lf, bc(W["lnlb"][0:T, :], [T, B, D], 1), ALU.add))
            link(place_latents(-1))
            dve.sem_inc(sem("stages_by_dve"), 1)
            ring = rings[2]
            dve.sem_inc(ring.emptied["dve"], ring.head["dve"])
            dve.sem_inc(sem("a2_contexts_copied_by_dve"), 1)
            per = STEPS[2]
            pair = "p (a k) -> p a k"

            def event(b, c):
                return 14 * b + c + 2

            def sum_squares(b, r, c, at, squares, step):
                step(dve.tensor_reduce(n2[0:r, at, :], squares[0:r, :].rearrange("p (h d) -> p h d", h=H), AX.X, ALU.add))
                step(dve.tensor_scalar(n2[0:r, at, :], n2[0:r, at, :], 1.0 / DH, 1e-16, ALU.mult, ALU.max))
                dve.sem_inc(sem("a2_squares_summed"), 1)

            def invert_norms(b, r, c, at, step):
                dve.wait_ge(sem("a2_norms"), event(b, c))
                step(dve.reciprocal(rk[0:r, at, :], n2[0:r, at, :]))
                dve.sem_inc(sem("a2_norms_inverted"), 1)

            def normalise_queries(b, step):
                dve.wait_ge(sem("a2_query_squares"), b + 2)
                sum_squares(b, T, 13, 0, values2, step)
                invert_norms(b, T, 13, 0, step)
                step(dve.tensor_tensor(qn.rearrange("p (a h d) -> p a h d", a=2, d=DH),
                                       slot(ring.slot_of("query", 0), T, BANK).rearrange("p a (h d) -> p a h d", d=DH),
                                       rk[0:T, 0, :].rearrange("p (a h) -> p a h", a=2).unsqueeze(3)
                                       .broadcast_to([T, 2, 8, DH]), ALU.mult))
                dve.sem_inc(ring.emptied["dve"], 1)
                dve.sem_inc(sem("a2_q_normalised"), 1)

            def divide_values(b):
                dve.wait_ge(sem("a2_heads_by_pe"), 3 * b + 1)
                dve.tensor_tensor(values2.rearrange("p (a h d) -> p a h d", a=2, d=DH),
                                  slot(3, T, BANK).rearrange("p a (h d) -> p a h d", d=DH),
                                  shares2[:, :].rearrange("p (a h) -> p a h", a=2).unsqueeze(3)
                                  .broadcast_to([T, 2, 8, DH]), ALU.mult).then_inc(sem("a2_heads_by_dve"), 1)

            def take_output(b):
                dve.wait_ge(sem("a2_heads_by_pe"), 3 * b + 3)
                dve.tensor_copy(attended2[:, bass.ds(b * D, D)], bank(6, T, D)).then_inc(sem("a2_heads_by_dve"), 1)

            normalise_queries(-1, link)
            dve.sem_inc(ring.emptied["dve"], 1)
            with dve.Fori(0, B) as b:
                k = [0]

                def step(i):
                    k[0] += 1
                    i.then_inc(sem("a2_dve_step"), 1)
                    dve.wait_ge(sem("a2_dve_step"), b * per + k[0])

                def square_sums(c):
                    dve.wait_ge(ring.emptied["act"], ring.emptied_count(b, "norm", c))
                    sum_squares(b, rows[c], c, c % 2, sq, step)

                rows = ROWS + [T]
                step(dve.tensor_copy(kbc[:, 0:NCH], kbias[:, :, :].rearrange("p b c -> p (b c)")[:, bass.ds(b * NCH, NCH)]))
                square_sums(0)
                invert_norms(b, rows[0], 0, 0, step)
                for c in range(13):
                    r = rows[c]
                    if c < NCH:
                        square_sums(c + 1)
                    dve.wait_ge(ring.full, ring.full_count(b, "score", 2 * c))
                    mine = S_all[0:r, c, ACT_HEADS * T:8 * T]
                    step(dve.tensor_tensor(mine.rearrange("p (h q) -> p h q", q=T),
                                           bank(2 * ring.slot_of("score", 2 * c) + 1, r, GROUP)
                                           .rearrange("p (h q) -> p h q", q=T),
                                           bc(rk[0:r, c % 2, ACT_HEADS:8], [r, 8 - ACT_HEADS, T], 2), ALU.mult))
                    dve.wait_ge(sem("a2_scaled_by_act"), b * (NCH + 1) + c + 1)
                    dve.sem_inc(ring.emptied["dve"], 1)
                    halves = [(M[0:r, j * 2 * GROUP:(j + 1) * 2 * GROUP], S_all[0:r, c, j * 2 * GROUP:(j + 1) * 2 * GROUP])
                              for j in range(2)]
                    for j, (m, new) in enumerate(halves):
                        if j == 1:
                            dve.wait_ge(ring.emptied["act"], ring.emptied_count(b, "score", 2 * c + 1))
                        if c == 0:
                            i = dve.tensor_scalar(m, new, kbc[0:r, c:c + 1], None, ALU.add)
                        else:
                            i = dve.scalar_tensor_tensor(out=m, in0=new, scalar=kbc[0:r, c:c + 1], in1=m,
                                                         op0=ALU.add, op1=ALU.max)
                            if c == 12 and j == 0:
                                i.then_inc(sem("a2_column_max"), 1)
                    step(i)
                    if c < NCH:
                        invert_norms(b, rows[c + 1], c + 1, (c + 1) % 2, step)
                    if c == VALUES:
                        divide_values(b)
                    if c == PROJECTED:
                        take_output(b)
                dve.sem_inc(sem("a2_column_max"), 1)
                for half in range(2):
                    dve.wait_ge(ring.full, ring.full_count(b, "turn", half))
                    step(dve.tensor_reduce(stat[0:T, 0, 8 * half:8 * half + 8].rearrange("p (a h) -> p a h", a=2),
                                           slot(ring.slot_of("turn", half), T, 4 * CK)
                                           .rearrange("p a (h k) -> p a h k", h=4), AX.X, ALU.max))
                    dve.sem_inc(ring.emptied["dve"], 1)
                dve.sem_inc(sem("a2_max_ready"), 1)
                dve.wait_ge(ring.full, ring.full_count(b, "row", 0))
                for half in range(2):
                    step(dve.tensor_tensor(M[0:16, 8 * half * T:8 * (half + 1) * T].rearrange("p (h q) -> p h q", h=8),
                                           bc(bank(2 * ring.slot_of("row", 0), 16, T), [16, 8, T], 1),
                                           bc(ident[0:16, 8 * half:8 * (half + 1)], [16, 8, T], 2), ALU.mult))
                    dve.sem_inc(sem("a2_shift_ready"), 1)
                dve.sem_inc(ring.emptied["dve"], 1)
                for half in range(2):
                    dve.wait_ge(ring.emptied["act"], ring.emptied_count(b, "shift", half))
                    cols = slice(2 * half * GROUP, 2 * (half + 1) * GROUP)
                    dve.tensor_tensor(S_all[0:rows[0], 0, cols], S_all[0:rows[0], 0, cols], mB[0:rows[0], cols],
                                      ALU.subtract).then_inc(sem("a2_scores_shifted"), 1)
                for c in range(13):
                    r = rows[c]
                    if c > 0:
                        dve.tensor_tensor(S_all[0:r, c, :], S_all[0:r, c, :], mB[0:r, :], ALU.subtract
                                          ).then_inc(sem("a2_scores_shifted"), 1)
                    if c == CENTRE:
                        centre(b, step)
                        place_latents(b)
                    if c == VARIANCE:
                        variance(b, step)
                    if c == SCALE:
                        scale(b, step)
                    if c == DVE_SUMS[1] + 2:
                        r = rows[DVE_SUMS[0]]
                        dve.wait_ge(sem("a2_probs_ready"), b * 13 + DVE_SUMS[1] + 1)
                        step(dve.tensor_tensor(M[0:r, :], S_all[0:r, DVE_SUMS[0], :], S_all[0:r, DVE_SUMS[1], :], ALU.add))
                normalise_queries(b, step)
                r = rows[DVE_SUMS[2]]
                dve.wait_ge(sem("a2_probs_ready"), b * 13 + DVE_SUMS[2] + 1)
                dve.tensor_tensor(M[0:r, :], M[0:r, :], S_all[0:r, DVE_SUMS[2], :], ALU.add
                                  ).then_inc(sem("a2_dve_summed"), 1)
                dve.wait_ge(sem("a2_keys_used"), b + 1)
                dve.tensor_copy(mB[:, 0:2 * GROUP].rearrange(pair, a=2), slot(2, D, GROUP)
                                ).then_inc(sem("a2_contexts_copied_by_dve"), 1)
                dve.wait_ge(ring.full, ring.full_count(b, "sum", 0))
                dve.reciprocal(shares2[:, :], bank(2 * ring.slot_of("sum", 0), T, H)).then_inc(ring.emptied["dve"], 1)
                dve.wait_ge(ring.emptied["dve"], ring.emptied_count(b, "sum", 0))
                assert k[0] == per, k[0]
            divide_values(B)
            take_output(B)
            dve.wait_ge(sem("a2_heads_by_dve"), 2 * (B + 1))
            link(dve.scalar_tensor_tensor(out=x[:, :, :], in0=wideB[:, 1:, :], scalar=gates[0:T, 2:3], in1=x[:, :, :],
                                          op0=ALU.mult, op1=ALU.add))

            link(dve.tensor_reduce(small[:, 16:17], W["f2fc"][:, :], AX.X, ALU.add, apply_absolute_value=True))
            link(dve.tensor_reduce(small[:, 17:18], W["f2proj"][:, :, :], AX.XY, ALU.add, apply_absolute_value=True))
            dve.sem_inc(sem("stages_by_dve"), 1)
            dve.wait_ge(sem("ternary_scale"), 1)
            link(dve.tensor_scalar(small[:, 18:20], bank(2, 128, 2), 1.0 / (4 * D * D), 1e-6, ALU.mult, ALU.add))
            link(dve.tensor_scalar(small[:, 20:22], small[:, 18:20], 0.5, None, ALU.mult))
            link(dve.tensor_scalar(small[:, 22:24], small[:, 18:20], -0.5, None, ALU.mult))
            for w, i in ((W["f2fc"][:, :], 0), (W["f2proj"][:, :, :].rearrange("p a b -> p (a b)"), 1)):
                link(dve.tensor_scalar(big3[:, 0:512], w, small[:, 22 + i:23 + i], None, ALU.is_lt))
                link(dve.scalar_tensor_tensor(out=w, in0=w, scalar=small[:, 20 + i:21 + i], in1=big3[:, 0:512],
                                              op0=ALU.is_gt, op1=ALU.subtract))
            dve.sem_inc(sem("stages_by_dve"), 1)
            norm_x()
            for bb in range(B):
                dve.wait_ge(sem("f2_gelu"), bb + 1)
                src = ternary_hidden(bb)
                link(dve.tensor_reduce(stat[0:T, 0, bb:bb + 1], src, AX.X, ALU.add))
                link(dve.tensor_scalar(stat[0:T, 1, bb:bb + 1], stat[0:T, 0, bb:bb + 1], 1.0 / F0, None, ALU.mult))
                link(dve.tensor_scalar(src, src, stat[0:T, 1, bb:bb + 1], None, ALU.subtract))
                link(dve.tensor_tensor(big3[0:T, 0:512], src, src, ALU.mult))
                link(dve.tensor_reduce(stat[0:T, 2, bb:bb + 1], big3[0:T, 0:512], AX.X, ALU.add))
            link(dve.tensor_scalar(stat[0:T, 3, 0:8], stat[0:T, 2, 0:8], 1.0 / F0, LN_EPS, ALU.mult, ALU.add))
            invert_roots(stat[0:T, 4, 0:8])
            for bb in range(B):
                src = ternary_hidden(bb)
                dst = big1[0:T, (bb % 2) * 512:(bb % 2 + 1) * 512]
                if bb >= 2:
                    dve.wait_ge(sem("f2_turned_psum"), bb - 1)
                link(dve.scalar_tensor_tensor(out=dst, in0=src, scalar=stat[0:T, 4, bb:bb + 1],
                                              in1=W["f2lnw"][0:T, :], op0=ALU.mult, op1=ALU.mult))
                link(dve.tensor_tensor(dst, dst, W["f2lnb"][0:T, :], ALU.add))
                dve.sem_inc(sem("f2_normalised"), 1)
            dve.wait_ge(sem("ffn2_out"), 1)
            add_residual(slot(3, T, BANK), 6)

            dve.sem_inc(sem("stages_by_dve"), 1)
            norm_x()
            for bb in range(B):
                dve.wait_ge(sem("qkv3_psum"), bb + 1)
                dve.tensor_tensor(qkv3[:, bb, :], bank(4 + bb % 4, T, 3 * D), W["b3"][0:T, :], ALU.add
                                  ).then_inc(sem("qkv3_ready"), 1)
            dve.wait_ge(sem("qkv3_ready"), B)
            link(dve.tensor_tensor(wideA[:, :, :], qkv3[:, :, 0:D], qkv3[:, :, D:2 * D], ALU.mult))
            link(dve.tensor_reduce(st3[:, 0:8], wideA[:, :, :], AX.X, ALU.add))
            link(dve.tensor_tensor(wideA[:, :, :], qkv3[:, :, 0:D], bc(W["b3"][0:T, D:2 * D], [T, B, D], 1), ALU.mult))
            link(dve.tensor_reduce(st3[:, 8:16], wideA[:, :, :], AX.X, ALU.add))
            dve.wait_ge(sem("stages_by_act"), STEP["qe3_ready"])
            dve.sem_inc(sem("stages_by_dve"), 1)
            def shift3(b, step):
                dve.tensor_copy(st3[:, 32:33], st3[:, bass.ds(b, 1)])
                step(dve.tensor_copy(st3[:, 33:34], st3[:, bass.ds(b + 8, 1)]))
                dve.wait_ge(sem("a3_scores"), b + 1)
                step(dve.tensor_reduce(st3[:, 40:44], psum[0:T, 0:4, 0:KQ], AX.X, ALU.max))
                step(dve.tensor_reduce(st3[:, 44:45], st3[:, 40:44], AX.X, ALU.max))
                step(dve.scalar_tensor_tensor(out=st3[:, 45:46], in0=st3[:, 44:45], scalar=st3[:, 33:34],
                                              in1=st3[:, 32:33], op0=ALU.add, op1=ALU.max))
                dve.tensor_tensor(st3[:, 34:35], st3[:, 33:34], st3[:, 45:46], ALU.subtract)
                step(dve.tensor_tensor(st3[:, 35:36], st3[:, 32:33], st3[:, 45:46], ALU.subtract))
                dve.sem_inc(sem("a3_shift_ready"), 1)

            per = STEPS[3]
            link(dve.memset(st3[:, 16:32], 0.0))
            link(dve.memset(qe3[:, BT:BT + T], 0.0))
            dve.wait_ge(sem("stages_by_act"), STEP["qe3_ready"])
            dve.tensor_copy(q3c[:, :], qe3[:, 0:T]).then_inc(sem("a3_query_placed"), 1)
            shift3(0, link)
            dve.sem_inc(sem("a3_turned_copied"), 1)
            dve.sem_inc(sem("a3_output_taken"), 1)
            with dve.Fori(0, B) as b:
                k = [0]

                def step(i):
                    k[0] += 1
                    i.then_inc(sem("a3_dve_step"), 1)
                    dve.wait_ge(sem("a3_dve_step"), b * per + k[0])

                dve.wait_ge(sem("a3_exp"), b + 1)
                dve.tensor_copy(q3c[:, :], qe3[:, bass.ds((b + 1) * T, T)]).then_inc(sem("a3_query_placed"), 1)
                dve.tensor_copy(st3[:, 49:50], st3[:, 36:37])
                step(dve.tensor_tensor(st3[:, 46:47], st3[:, 37:38], st3[:, 38:39], ALU.add))
                step(dve.tensor_tensor(st3[:, 47:48], st3[:, 46:47], st3[:, 36:37], ALU.add))
                step(dve.reciprocal(st3[:, 48:49], st3[:, 47:48]))
                dve.wait_ge(sem("a3_turned"), b + 1)
                dve.tensor_copy(PT3[0:CK, 0:8, :].rearrange("p (a c) q -> p a (c q)", a=2), slot(2, CK, GROUP))
                dve.tensor_copy(PT3[0:CK, 8:11, :].rearrange("p c q -> p (c q)"), bank(6, CK, 3 * T))
                dve.tensor_copy(PT3[0:LAST, 11, :], bank(6, LAST, 4 * T)[:, 3 * T:4 * T]
                                ).then_inc(sem("a3_turned_copied"), 1)
                shift3(b + 1, step)
                dve.wait_ge(sem("a3_output"), b + 1)
                step(dve.scalar_tensor_tensor(out=y3[:, :], in0=W["b3"][0:T, 2 * D:3 * D], scalar=st3[:, 46:47],
                                              in1=bank(7, T, D), op0=ALU.mult, op1=ALU.add))
                dve.sem_inc(sem("a3_output_taken"), 1)
                vb = qkv3.rearrange("p b d -> p (b d)")[:, bass.ds(b * 3 * D + 2 * D, D)]
                step(dve.scalar_tensor_tensor(out=y3[:, :], in0=vb, scalar=st3[:, 49:50], in1=y3[:, :],
                                              op0=ALU.mult, op1=ALU.add))
                step(dve.tensor_scalar(y3[:, :], y3[:, :], st3[:, 48:49], gates[0:T, 3:4], ALU.mult, ALU.mult))
                xb = x[:, :, :].rearrange("p b d -> p (b d)")[:, bass.ds(b * D, D)]
                step(dve.tensor_tensor(xb, xb, y3[:, :], ALU.add))
                assert k[0] == per, k[0]

            norm_x()
            eps = 1e-8
            link(dve.tensor_tensor(wideA[:, :, :], xn[:, :, :], xn[:, :, :], ALU.mult))
            link(dve.tensor_reduce(stat[0:T, 5, 0:8], wideA[:, :, :], AX.X, ALU.add))
            em = W["emb"][:, :]
            link(dve.tensor_tensor(g0[0:E3, 128:256], em, em, ALU.mult))
            link(dve.tensor_reduce(small[0:E3, 40:41], g0[0:E3, 128:256], AX.X, ALU.add))
            dve.sem_inc(sem("experts_by_dve"), 1)
            dve.wait_ge(sem("norms_ready"), 2)
            link(dve.tensor_scalar(stat[0:T, 5, 0:8], stat[0:T, 5, 0:8], eps, None, ALU.add))
            link(dve.reciprocal(stat[0:T, 5, 0:8], stat[0:T, 5, 0:8]))
            link(dve.tensor_scalar(small[0:E3, 41:42], small[0:E3, 40:41], eps, None, ALU.add))
            link(dve.reciprocal(small[0:E3, 42:43], small[0:E3, 41:42]))
            link(dve.tensor_scalar(g0[0:E3, 0:D], em, small[0:E3, 42:43], None, ALU.mult))
            dve.sem_inc(sem("experts_by_dve"), 1)
            dve.wait_ge(sem("experts_by_pe"), STEP["experts_turned"])
            dve.tensor_copy(g1[:, 0:8], W["embT"][:, :])
            link(dve.tensor_copy(g1[:, 8:16], bank(2, D, E3)))
            dve.sem_inc(sem("experts_by_dve"), 1)
            dve.wait_ge(sem("experts_by_pe"), STEP["expert_scores"])
            sc = bank(3, T, 128).rearrange("p (b k) -> p b k", b=B)
            es, fs = [T, B, E3], [T, B, E3, E3]
            simv = g2[0:T, 64:128].rearrange("p (b e) -> p b e", b=B)
            cosv = g2[0:T, 128:192].rearrange("p (b e) -> p b e", b=B)
            rank = g2[0:T, 192:256].rearrange("p (b e) -> p b e", b=B)
            rank2 = g2[0:T, 256:320].rearrange("p (b e) -> p b e", b=B)
            pair = g0[0:T, :].rearrange("p (b e f) -> p b e f", b=B, e=E3)
            pair2 = big3[0:T, 0:512].rearrange("p (b e f) -> p b e f", b=B, e=E3)
            link(dve.tensor_copy(simv, sc[:, :, 0:E3]))
            link(dve.tensor_tensor(cosv, sc[:, :, E3:2 * E3], bc(stat[0:T, 5, 0:8], es, 2), ALU.mult))
            link(dve.tensor_scalar(g1[0:T, 16:24], W["onb"][0:T, :], 0.1, None, ALU.mult))
            link(dve.tensor_tensor(cosv, cosv, bc(g1[0:T, 16:24], es, 1), ALU.add))
            def ranks(dst, other, v):
                fbc = v.unsqueeze(2).broadcast_to(fs)
                ebc = v.unsqueeze(3).broadcast_to(fs)
                link(dve.tensor_tensor(pair, fbc, ebc, ALU.is_gt))
                link(dve.tensor_reduce(dst, pair, AX.X, ALU.add))
                link(dve.tensor_tensor(pair, fbc, ebc, ALU.is_equal))
                link(dve.tensor_tensor(pair, pair, W["etri"][0:T, :].rearrange("p (e f) -> p e f", e=E3)
                                       .unsqueeze(1).broadcast_to(fs), ALU.mult))
                link(dve.tensor_reduce(other, pair, AX.X, ALU.add))
                link(dve.tensor_tensor(dst, dst, other, ALU.add))

            ranks(rank, rank2, simv)
            link(dve.tensor_scalar(rank, rank, 6.5, OFF, ALU.is_gt, ALU.mult))
            link(dve.tensor_tensor(cosv, cosv, rank, ALU.add))
            ranks(rank, rank2, cosv)
            link(dve.tensor_scalar(rank, rank, 1.5, None, ALU.is_lt))
            link(dve.tensor_reduce(stat[0:T, 6, 0:8], cosv, AX.X, ALU.max))
            ev = g3[0:T, 0:64].rearrange("p (b e) -> p b e", b=B)
            link(dve.tensor_tensor(ev, cosv, bc(stat[0:T, 6, 0:8], es, 2), ALU.subtract))
            dve.sem_inc(sem("experts_by_dve"), 1)
            dve.wait_ge(sem("experts_by_act"), STEP["expert_exp"])
            wv = g2[0:T, 0:64].rearrange("p (b e) -> p b e", b=B)
            link(dve.tensor_tensor(wv, ev, rank, ALU.mult))
            link(dve.tensor_reduce(stat[0:T, 7, 0:8], wv, AX.X, ALU.add))
            link(dve.reciprocal(stat[0:T, 7, 0:8], stat[0:T, 7, 0:8]))
            link(dve.tensor_scalar(stat[0:T, 7, 0:8], stat[0:T, 7, 0:8], gates[0:T, 7:8], None, ALU.mult))
            link(dve.tensor_tensor(wv, wv, bc(stat[0:T, 7, 0:8], es, 2), ALU.mult))
            dve.sem_inc(sem("experts_by_dve"), 1)
            dve.wait_ge(sem("experts_by_pe"), STEP["expert_biases"])
            link(dve.tensor_tensor(x[:, :, :].rearrange("p (a b) d -> p a (b d)", a=2), slot(1, T, BANK),
                                   x[:, :, :].rearrange("p (a b) d -> p a (b d)", a=2), ALU.add))
            dve.sem_inc(sem("experts_by_dve"), 1)
            for e in range(E3):
                dve.wait_ge(sem("f3_out"), e + 1)
                for half in range(2):
                    src = bank(2 * (e % 2) + half, T, BANK)
                    for i4 in range(4):
                        bb = 4 * half + i4
                        i = dve.scalar_tensor_tensor(out=x[:, bb, :], in0=src[:, i4 * D:(i4 + 1) * D],
                                                     scalar=wv[:, bb, e:e + 1], in1=x[:, bb, :],
                                                     op0=ALU.mult, op1=ALU.add)
                    i.then_inc(sem("f3_accumulated"), 1)
                dve.wait_ge(sem("f3_accumulated"), 2 * (e + 1))
            dve.sem_inc(sem("stages_by_dve"), 1)


def milestones(*names):
    return {name: i + 1 for i, name in enumerate(names)}


STEP = {}
STEP.update(milestones("key_mask_cleared", "layer0_setup", "q1_split", "layer1_setup", "stage_cleared", "latents_ready",
                       "ternary_sums", "ternary_ready", "arena_free_for_experts", "layer3_setup",
                       "y_ready"))
STEP.update(milestones("gates_ready", "head_gate_exp", "router_exp", "k1_ready", "q3T_ready", "qe3_ready"))
STEP.update(milestones("slots_turned", "slot_bias_psum", "f1_hidden_psum", "route_logits", "gh_psum", "slot_inputs",
                       "alpha_turned", "gx_psum", "slot_values_psum", "slot_outputs_psum"))
STEP.update(milestones("slots_scaled", "slot_mean", "slotsT_ready", "slot_bias", "logits_shifted", "alpha_ready",
                       "gi_ready", "gate_r_sum", "gate_z_sum", "gate_n_sum", "slots_new"))
STEP.update(milestones("logits_exp", "alphaT_ready", "gate_r_exp", "gate_z_exp", "gate_n_tanh", "slot_values",
                       "slot_outputs"))
STEP.update(milestones("experts_turned", "expert_scores", "expert_weights_psum", "expert_biases"))
STEP.update(milestones("squares_ready", "experts_normalised", "expert_columns", "expert_shifted", "expert_weights",
                       "expert_biases_taken"))
STEP.update(milestones("expert_exp", "expert_weights_turned"))


SHIFT, STACK = 16 * 6, 16 * 6 + 4
KEY_PART = (0, 0, 0, 1, 1, 2)
QUERY_PART = (0, 1, 2, 0, 1, 0)
STEPS = [9, 16, 82, 12]


def w3a_off():
    return 128 * 0 + 4 * BT + 3 * 1024 + 4 * 512


def kernel(**inputs):
    import numpy as np
    import ml_dtypes
    import concourse.bacc as bacc
    from concourse.bass_utils import run_bass_kernel_spmd

    v = {k: np.asarray(a) for k, a in inputs.items()}

    def col(a, k=1):
        return a.reshape(k, -1).T

    def rep(a, n):
        return np.broadcast_to(a.reshape(1, -1), (n, a.size))

    p = {}
    p["x"] = v["x"]
    p["ctx"] = v["ctx_1024"]
    p["ctxT"] = v["ctx_1024"].transpose(0, 2, 1)
    p["mask0"] = v["mask_1x1xSxS2_ik0"][0, 0].T
    p["mask2"] = v["mask_BxS2_bf1"].view(np.uint8)
    p["gates"] = rep(np.concatenate([v["g_xattn"], v["g_ffn"]]), 128)
    p["c_ident"] = np.eye(128, dtype=np.float32)
    p["c_identb"] = np.eye(128, dtype=ml_dtypes.bfloat16)
    p["c_low_rows"] = np.where(np.arange(32) // 8 % 2 == 1, -1.0, 0.0).astype(np.float32)[:, None]
    t = np.arange(T)
    p["c_before"] = (t[None, :] < t[:, None]).astype(np.float32)

    def pairs(a):
        return a.reshape(a.shape[0], 8, 2, HD).transpose(0, 2, 3, 1).reshape(a.shape[0], 128)

    def places(a):
        n = a.shape[0] // H
        return a.reshape(2, 4, 2, n, -1).transpose(0, 2, 1, 3, 4).reshape(a.shape)

    p["w_q0"] = pairs(v["L0_xattn_Wq"].T)
    p["w_k0"] = pairs(v["L0_xattn_Wk"].T)
    p["w_v0"] = v["L0_xattn_Wv"].T
    p["w_o0"] = places(v["L0_xattn_Wo"].T)
    p["w_bq0"] = pairs(v["L0_xattn_bq"].reshape(1, -1)).T
    p["w_bk0"] = pairs(v["L0_xattn_bk"].reshape(1, -1)).T
    p["w_bv0"] = places(col(v["L0_xattn_bv"]))
    p["w_bo0"] = rep(v["L0_xattn_bo"], 1)
    p["w_f0wr"] = col(v["L0_ffn_w_router"])
    p["w_f0W1"] = v["L0_ffn_W1"]
    p["w_f0b1"] = col(v["L0_ffn_b1"], 4)
    p["w_f0W2"] = v["L0_ffn_W2"].reshape(4, 128, D).transpose(1, 0, 2)
    p["w_f0b2"] = rep(v["L0_ffn_b2"], 1)
    w, b = v["L1_xattn_Wqkv"], v["L1_xattn_bqkv"].reshape(1, -1)
    wa, ba = v["L1_xattn_Wqkv_aux"], v["L1_xattn_bqkv_aux"].reshape(1, -1)
    p["w_q1"] = pairs(w[:, 0:D])
    p["w_k1"] = pairs(w[:, D:2 * D])
    p["w_v1"] = w[:, 2 * D:3 * D]
    p["w_ka1"] = pairs(wa[:, D:2 * D])
    p["w_va1"] = wa[:, 2 * D:3 * D]
    p["w_bq1"] = pairs(b[:, 0:D]).T
    p["w_bk1"] = pairs(b[:, D:2 * D]).T
    p["w_bv1"] = places(b[:, 2 * D:3 * D].T)
    p["w_bka1"] = pairs(ba[:, D:2 * D]).T
    p["w_bva1"] = places(ba[:, 2 * D:3 * D].T)
    p["w_o1"] = places(v["L1_xattn_Wo"])
    p["w_bo1"] = rep(v["L1_xattn_bo"], 1)
    p["w_g1"] = places(np.repeat(v["L1_xattn_g"], HD).reshape(128, 1))
    p["w_g1heads"] = rep(places(v["L1_xattn_g"]), 128)
    p["w_slots"] = v["L1_ffn_slot_init"]
    p["w_slot_scale"] = v["L1_ffn_slot_scale"]
    p["w_f1w1a"] = v["L1_ffn_w1"][:, 0:D].T
    p["w_f1w1b"] = v["L1_ffn_w1"][:, D:2 * D].T
    p["w_f1b1"] = col(v["L1_ffn_b1"])
    p["w_f1w2"] = v["L1_ffn_w2"].T
    p["w_f1b2"] = rep(v["L1_ffn_b2"], T)
    p["w_f1wih"] = v["L1_ffn_gru_wih"].T
    p["w_f1whh"] = v["L1_ffn_gru_whh"].T
    p["w_f1bih"] = col(v["L1_ffn_gru_bih"], 3)
    p["w_f1bhh"] = col(v["L1_ffn_gru_bhh"], 3)
    p["w_f1wv"] = v["L1_ffn_wv"].T
    p["w_f1bv"] = col(v["L1_ffn_bv"])
    p["w_f1wo"] = v["L1_ffn_wo"].T
    p["w_f1bo"] = rep(v["L1_ffn_bo"], 1)
    p["w_tau"] = rep(v["L1_ffn_tau"], T)
    p["w_lnxg"] = rep(v["L2_xattn_ln_x_g"], 128)
    p["w_lnxb"] = rep(v["L2_xattn_ln_x_b"], 128)
    p["w_lnlg"] = rep(v["L2_xattn_ln_l_g"], T)
    p["w_lnlb"] = rep(v["L2_xattn_ln_l_b"], T)
    p["w_gq2"] = np.tile(v["L2_xattn_qn_g"], 2).reshape(128, 1)
    p["w_gk2"] = np.tile(v["L2_xattn_kn_g"], 2).reshape(128, 1)
    p["w_q2"] = v["L2_xattn_Wq"]
    p["w_kv2"] = v["L2_xattn_Wkv"]
    p["w_k2T"] = v["L2_xattn_Wkv"][:, 0:H * DH].reshape(D, 8, 128).transpose(2, 1, 0)
    p["w_out2"] = v["L2_xattn_Wout"].reshape(8, 128, D).transpose(1, 0, 2)
    p["w_bo2"] = rep(v["L2_xattn_bout"], 1)
    p["w_f2fc"] = v["L2_ffn_W_fc"].T
    p["w_f2proj"] = v["L2_ffn_W_proj"].T.reshape(4, 128, D).transpose(1, 0, 2)
    p["w_f2lnw"] = rep(v["L2_ffn_ln_w"], T)
    p["w_f2lnb"] = rep(v["L2_ffn_ln_b"], T)
    p["w_qkv3"] = np.concatenate([v["L3_xattn_Wq"], v["L3_xattn_Wk"], v["L3_xattn_Wv"]], axis=1)
    p["w_k3T"] = v["L3_xattn_Wk"].T
    p["w_bq3"] = col(v["L3_xattn_bq"])
    p["w_b3"] = rep(np.concatenate([v["L3_xattn_bq"], v["L3_xattn_bk"], v["L3_xattn_bv"]]), T)
    p["w_emb"] = v["L3_ffn_uzman_embeddings"]
    p["w_embT"] = v["L3_ffn_uzman_embeddings"].T
    p["w_onb"] = rep(v["L3_ffn_onbellek_durumu"], T)
    e = np.arange(E3)
    p["w_etri"] = rep((e[None, :] < e[:, None]).astype(np.float32), T)
    p["w_f3b1"] = v["L3_ffn_b1"].reshape(E3, 4, 128).transpose(2, 0, 1)
    p["w_f3b2"] = v["L3_ffn_b2"]
    p["e_W1"] = v["L3_ffn_W1"].transpose(1, 0, 2)
    p["e_W2"] = v["L3_ffn_W2"].reshape(E3, 4, 128, D).transpose(2, 0, 1, 3)

    nc = bacc.Bacc("TRN2", target_bir_lowering=False, num_devices=1)
    arrays, A = {}, {}
    for name, a in p.items():
        a = np.ascontiguousarray(a)
        arrays["in_" + name] = a
        A[name] = nc.dram_tensor("in_" + name, a.shape, mybir.dt.from_np(a.dtype), kind="ExternalInput").ap()
    y = nc.dram_tensor("y", (B, T, D), F32, kind="ExternalOutput").ap()
    flamingo(nc, A, y)
    r = run_bass_kernel_spmd(nc, [arrays], core_ids=[0])
    return r.results[0]["y"]
```
